# Optimizing a Trainium2 kernel written in Bass

```python
import numpy as np
import jax
import jax.numpy as jnp

def _softmax(x, axis=-1):
    return jax.nn.softmax(x, axis=axis)

def _gelu(x):
    return jax.nn.gelu(x, approximate=True)

def _silu(x):
    return jax.nn.silu(x)

def _sigmoid(x):
    return jax.nn.sigmoid(x)

def _layernorm(x, axis=-1, eps=1e-05):
    m = jnp.mean(x, axis=axis, keepdims=True)
    v = jnp.var(x, axis=axis, keepdims=True)
    return (x - m) / jnp.sqrt(v + eps)

def _scatter_add(tgt, idx, src, axis=0):
    return tgt.at[idx].add(src)

def _segment_sum(src, seg, n):
    return jax.ops.segment_sum(src, seg, n)
kernel_name = 'mk_adaln_attn_ffn_d2_seqx_r4_5e972f'

def setup_inputs(seed: int=0):
    np.random.seed(seed)
    _w = jnp.asarray

    def _rec_inputs():
        import jax
        import jax.numpy as jnp
        _rk = jax.random.key(seed)
        x = 7.22e-05 + 1 * jax.random.normal(jax.random.fold_in(_rk, 1), (4, 512, 256), jnp.float32)
        _lenS = 512 - jax.random.randint(jax.random.fold_in(_rk, 7), (4,), 0, max(1, 512 // 4) + 1, jnp.int32)
        _lenS2 = 512 - jax.random.randint(jax.random.fold_in(_rk, 8), (4,), 0, max(1, 512 // 4) + 1, jnp.int32)
        cond_64 = -0.104238 + 1.01173 * jax.random.normal(jax.random.fold_in(_rk, 11), (4, 64), jnp.float32)
        fside_16xSxS_0 = -5.72187e-05 + 0.999849 * jax.random.normal(jax.random.fold_in(_rk, 13), (16, 512, 512), jnp.float32)
        _validS = jnp.arange(512)[None, :] < _lenS[:, None]
        _validS2 = jnp.arange(512)[None, :] < _lenS2[:, None]
        _causal = jnp.tril(jnp.ones((512, 512), dtype=bool))
        mask_BxS_bf1 = jnp.ones((4, 512), dtype=bool)
        mask_BxS_bk0 = jnp.logical_not(jnp.broadcast_to(_validS[:, :], (4, 512)))
        return (x, cond_64, fside_16xSxS_0, mask_BxS_bf1, mask_BxS_bk0)
    x, cond_64, fside_16xSxS_0, mask_BxS_bf1, mask_BxS_bk0 = _rec_inputs()

    def _L0_cond_setup():
        import jax, jax.numpy as jnp
        import numpy as np
        B, S, H = (4, 512, 256)
        E = 8
        M = 128
        K = 2
        N_SHARED = 2
        SM = M * N_SHARED
        G = 64
        GE_TEMP = 1.0
        ALPHA = 0.001
        SEQ_AUX = True
        NORM_TOPK = True
        COS_TEMP = 0.78
        CONS_ALPHA = 0.01
        LEAKY_SLOPE = 0.01
        EPS_COS = 1e-08

        def _leaky(x):
            return jnp.where(x >= 0, x, LEAKY_SLOPE * x)

        def _moe_forward(hidden_states, g, wt, wg, w_gate, w_up, w_down, sw_gate, sw_up, sw_down):
            b, s, h = hidden_states.shape
            x = hidden_states.reshape(-1, h)
            T = x.shape[0]
            logits_h = x @ wt.T
            logits_g = g @ wg.T
            logits_g = jnp.repeat(logits_g, s, axis=0)
            logits = (logits_h + logits_g / GE_TEMP) / (1.0 + 1.0 / GE_TEMP)
            scores = jax.nn.softmax(logits, axis=-1)
            topk_w, topk_idx = jax.lax.top_k(scores, K)
            if K > 1 and NORM_TOPK:
                topk_w = topk_w / (topk_w.sum(-1, keepdims=True) + 1e-20)
            onehot = jax.nn.one_hot(topk_idx.reshape(b, s * K), E, dtype=jnp.float32)
            ce = onehot.sum(1) / (s * K / E)
            aux_loss = (ce * scores.reshape(b, s, E).mean(1)).sum(1).mean() * ALPHA
            gp = _leaky(jnp.einsum('th,ehm->etm', x, w_gate))
            up = jnp.einsum('th,ehm->etm', x, w_up)
            y_all = jnp.einsum('etm,emh->eth', gp * up, w_down)
            y_sel = y_all[topk_idx, jnp.arange(T)[:, None], :]
            y = (y_sel * topk_w[..., None]).sum(1).reshape(b, s, h)
            p = _leaky(hidden_states @ sw_gate) * (hidden_states @ sw_up) @ sw_down
            y = y + p
            num = jnp.sum(y * p, -1)
            den = jnp.maximum(jnp.linalg.norm(y, axis=-1), EPS_COS) * jnp.maximum(jnp.linalg.norm(p, axis=-1), EPS_COS)
            closs = CONS_ALPHA * jnp.mean(num / den / (1.0 + COS_TEMP))
            return (y, aux_loss + closs)
        key = jax.random.key(seed)
        ks = jax.random.split(key, 12)
        sh = 1.0 / np.sqrt(H)
        sm = 1.0 / np.sqrt(M)
        ssm = 1.0 / np.sqrt(SM)
        sg = 1.0 / np.sqrt(G)
        return {'hidden_states': jax.random.normal(ks[0], (B, S, H), jnp.float32), 'g': jax.random.normal(ks[1], (B, G), jnp.float32), 'wt': jax.random.uniform(ks[2], (E, H), jnp.float32, -sh, sh), 'wg': jax.random.uniform(ks[3], (E, G), jnp.float32, -sg, sg), 'w_gate': jax.random.uniform(ks[4], (E, H, M), jnp.float32, -sh, sh), 'w_up': jax.random.uniform(ks[5], (E, H, M), jnp.float32, -sh, sh), 'w_down': jax.random.uniform(ks[6], (E, M, H), jnp.float32, -sm, sm), 'sw_gate': jax.random.uniform(ks[7], (H, SM), jnp.float32, -sh, sh), 'sw_up': jax.random.uniform(ks[8], (H, SM), jnp.float32, -sh, sh), 'sw_down': jax.random.uniform(ks[9], (SM, H), jnp.float32, -ssm, ssm)}
    _L0_cond_all = _L0_cond_setup()
    _L0_cond_in = {k: v for k, v in _L0_cond_all.items() if k in ('wt', 'wg', 'w_gate', 'w_up', 'w_down', 'sw_gate', 'sw_up', 'sw_down')}
    del _L0_cond_all

    def _L0_attn_setup():
        import jax, jax.numpy as jnp
        import numpy as np
        B, S, D, K = (4, 1024, 256, 64)
        key = jax.random.key(seed)
        kx, kq, kk, kv, ko = jax.random.split(key, 5)
        scale = 1.0 / np.sqrt(D)
        return {'x': jax.random.normal(kx, (B, S, D), dtype=jnp.float32), 'Wq': jax.random.uniform(kq, (K, D), dtype=jnp.float32, minval=-scale, maxval=scale), 'Wk': jax.random.uniform(kk, (K, D), dtype=jnp.float32, minval=-scale, maxval=scale), 'Wv': jax.random.uniform(kv, (K, D), dtype=jnp.float32, minval=-scale, maxval=scale), 'Wo': jax.random.uniform(ko, (D, K), dtype=jnp.float32, minval=-1.0 / np.sqrt(K), maxval=1.0 / np.sqrt(K))}
    _L0_attn_all = _L0_attn_setup()
    _L0_attn_in = {k: v for k, v in _L0_attn_all.items() if k in ('Wq', 'Wk', 'Wv', 'Wo')}
    del _L0_attn_all

    def _L0_cond2_setup():
        import jax, jax.numpy as jnp
        import numpy as np
        DIM = 256
        HEADS = 16
        DIM_HEAD = 64
        SCALE = 8.0

        def ln(x, g, eps=1e-05):
            mean = x.mean(axis=-1, keepdims=True)
            var = ((x - mean) ** 2).mean(axis=-1, keepdims=True)
            return (x - mean) * jax.lax.rsqrt(var + eps) * g

        def l2norm(t):
            n = jnp.maximum(jnp.linalg.norm(t, axis=-1, keepdims=True), 1e-12)
            return t / n

        def rel_pos_bias(n, w0, b0, g0, w1, b1, g1, w2, b2, dtype):
            pos = jnp.arange(-n + 1, n, dtype=dtype)[:, None]
            h = jax.nn.silu(ln(pos @ w0 + b0, g0))
            h = jax.nn.silu(ln(h @ w1 + b1, g1))
            h = h @ w2 + b2
            i = jnp.arange(n)
            idx = i[:, None] - i[None, :] + n - 1
            bias = h[idx]
            return jnp.transpose(bias, (2, 0, 1))
        key = jax.random.key(seed)
        ks = jax.random.split(key, 16)
        b, n = (2, 512)
        inner = HEADS * DIM_HEAD
        s = 0.02
        return {'x': jax.random.normal(ks[0], (b, n, DIM), jnp.float32), 'mask': jnp.ones((b, n), dtype=bool), 'g_norm': jnp.ones((DIM,), jnp.float32), 'Wq': jax.random.normal(ks[1], (DIM, inner), jnp.float32) * s, 'Wkv': jax.random.normal(ks[2], (DIM, 2 * DIM_HEAD), jnp.float32) * s, 'q_scale': jnp.ones((DIM_HEAD,), jnp.float32), 'k_scale': jnp.ones((DIM_HEAD,), jnp.float32), 'null_kv': jax.random.normal(ks[3], (2, DIM_HEAD), jnp.float32), 'null_attn_bias': jax.random.normal(ks[4], (HEADS,), jnp.float32), 'w0': jax.random.normal(ks[5], (1, DIM), jnp.float32) * s, 'b0': jnp.zeros((DIM,), jnp.float32), 'g0': jnp.ones((DIM,), jnp.float32), 'w1': jax.random.normal(ks[6], (DIM, DIM), jnp.float32) * s, 'b1': jnp.zeros((DIM,), jnp.float32), 'g1': jnp.ones((DIM,), jnp.float32), 'w2': jax.random.normal(ks[7], (DIM, HEADS), jnp.float32) * s, 'b2': jnp.zeros((HEADS,), jnp.float32), 'Wout': jax.random.normal(ks[8], (inner, DIM), jnp.float32) * s, 'g_out': jnp.ones((DIM,), jnp.float32)}
    _L0_cond2_all = _L0_cond2_setup()
    _L0_cond2_in = {k: v for k, v in _L0_cond2_all.items() if k in ('g_norm', 'Wq', 'Wkv', 'q_scale', 'k_scale', 'null_attn_bias', 'w0', 'b0', 'g0', 'w1', 'b1', 'g1', 'w2', 'b2', 'Wout', 'g_out')}
    del _L0_cond2_all

    def _L0_ffn_setup():
        import jax, jax.numpy as jnp
        import numpy as np
        B, S, D = (1, 512, 256)
        I = 512
        E = 8
        K = 2
        LIMIT = 7.0
        ALPHA = 1.702
        EPS = 1e-05

        def _swiglu(h):
            x_glu = jnp.minimum(h[..., ::2], LIMIT)
            x_lin = jnp.clip(h[..., 1::2], -LIMIT, LIMIT)
            return x_glu * jax.nn.sigmoid(ALPHA * x_glu) * (x_lin + 1.0)

        def _moe(t, gate_w, gate_b, mlp1_w, mlp1_b, mlp2_w, mlp2_b):
            T = t.shape[0]
            logits = t @ gate_w + gate_b
            top_v, top_i = jax.lax.top_k(logits, K)
            probs = jax.nn.softmax(top_v, axis=-1)
            w = jnp.zeros((T, E), t.dtype).at[jnp.arange(T)[:, None], top_i].set(probs)

            def body(acc, ew):
                w1, b1, w2, b2, we = ew
                h = _swiglu(t @ w1 + b1)
                y = h @ w2 + b2
                return (acc + we[:, None] * y, None)
            acc0 = jnp.zeros((T, t.shape[1]), t.dtype)
            acc, _ = jax.lax.scan(body, acc0, (mlp1_w, mlp1_b, mlp2_w, mlp2_b, w.T))
            return acc
        key = jax.random.key(seed)
        ks = jax.random.split(key, 4)
        s = 0.02
        return {'x': jax.random.normal(ks[0], (B, S, D), jnp.float32), 'norm_scale': jnp.ones((D,), jnp.float32), 'gate_w': jax.random.normal(ks[1], (D, E), jnp.float32) * s, 'gate_b': jnp.zeros((E,), jnp.float32), 'mlp1_w': jax.random.normal(ks[2], (E, D, 2 * I), jnp.float32) * s, 'mlp1_b': jnp.zeros((E, 2 * I), jnp.float32), 'mlp2_w': jax.random.normal(ks[3], (E, I, D), jnp.float32) * s, 'mlp2_b': jnp.zeros((E, D), jnp.float32)}
    _L0_ffn_all = _L0_ffn_setup()
    _L0_ffn_in = {k: v for k, v in _L0_ffn_all.items() if k in ('norm_scale', 'gate_w', 'gate_b', 'mlp1_w', 'mlp1_b', 'mlp2_w', 'mlp2_b')}
    del _L0_ffn_all

    def _L1_cond_setup():
        import jax, jax.numpy as jnp
        import numpy as np
        B, N, DIM, H, DH = (2, 512, 256, 16, 64)
        INNER = H * DH
        EPS = 1e-05

        def layernorm(x, g):
            mean = jnp.mean(x, axis=-1, keepdims=True)
            var = jnp.var(x, axis=-1, keepdims=True)
            return (x - mean) * jax.lax.rsqrt(var + EPS) * g
        key = jax.random.key(seed)
        ks = jax.random.split(key, 10)
        x = jax.random.normal(ks[0], (B, N, DIM), dtype=jnp.float32)
        attn_bias = jax.random.normal(ks[1], (H, N, N), dtype=jnp.float32)
        mask = jax.random.randint(ks[2], (B, N), 0, 2).astype(bool)
        g_in = jnp.ones((DIM,), dtype=jnp.float32)
        null_attn_bias = jax.random.normal(ks[3], (H,), dtype=jnp.float32)
        null_kv = jax.random.normal(ks[4], (2, DH), dtype=jnp.float32)
        Wq = jax.random.normal(ks[5], (DIM, INNER), dtype=jnp.float32) * 0.02
        Wkv = jax.random.normal(ks[6], (DIM, 2 * DH), dtype=jnp.float32) * 0.02
        Wo = jax.random.normal(ks[7], (INNER, DIM), dtype=jnp.float32) * 0.02
        g_out = jnp.ones((DIM,), dtype=jnp.float32)
        return {'x': x, 'attn_bias': attn_bias, 'mask': mask, 'g_in': g_in, 'null_attn_bias': null_attn_bias, 'null_kv': null_kv, 'Wq': Wq, 'Wkv': Wkv, 'Wo': Wo, 'g_out': g_out}
    _L1_cond_all = _L1_cond_setup()
    _L1_cond_in = {k: v for k, v in _L1_cond_all.items() if k in ('g_in', 'null_attn_bias', 'Wq', 'Wkv', 'Wo', 'g_out')}
    del _L1_cond_all

    def _L1_attn_setup():
        import math
        import jax, jax.numpy as jnp
        import numpy as np
        D_MODEL = 256
        N_HEADS = 16
        HEAD_DIM = D_MODEL // N_HEADS
        ROPE_THETA = 10000.0

        def _apply_rope(t, offset=0):
            B, H, T, Dh = t.shape
            inv_freq = 1.0 / ROPE_THETA ** (jnp.arange(0, Dh, 2, dtype=jnp.float32) / Dh)
            pos = jnp.arange(T, dtype=jnp.float32) + offset
            ang = pos[:, None] * inv_freq[None, :]
            cos = jnp.concatenate([jnp.cos(ang), jnp.cos(ang)], axis=-1)
            sin = jnp.concatenate([jnp.sin(ang), jnp.sin(ang)], axis=-1)
            t1, t2 = (t[..., :Dh // 2], t[..., Dh // 2:])
            rot = jnp.concatenate([-t2, t1], axis=-1)
            return t * cos + rot * sin

        def _forward(x, Wq, Wk, Wv, Wo):
            B, T, _ = x.shape
            scale = 1.0 / math.sqrt(HEAD_DIM)

            def split_heads(y):
                return y.reshape(B, T, N_HEADS, HEAD_DIM).transpose(0, 2, 1, 3)
            q = split_heads(x @ Wq.T)
            k = split_heads(x @ Wk.T)
            v = split_heads(x @ Wv.T)
            q = _apply_rope(q)
            k = _apply_rope(k)
            scores = jnp.einsum('bhtd,bhsd->bhts', q, k) * scale
            causal = jnp.triu(jnp.ones((T, T), dtype=bool), k=1)
            scores = jnp.where(causal[None, None], -jnp.inf, scores)
            attn = jax.nn.softmax(scores, axis=-1)
            attn = jnp.nan_to_num(attn, nan=0.0)
            out = jnp.einsum('bhts,bhsd->bhtd', attn, v)
            out = out.transpose(0, 2, 1, 3).reshape(B, T, N_HEADS * HEAD_DIM)
            return out @ Wo.T
        key = jax.random.key(seed)
        ks = jax.random.split(key, 5)
        B, T = (4, 512)
        w_scale = math.sqrt(2.0 / (D_MODEL + D_MODEL))
        return {'x': jax.random.normal(ks[0], (B, T, D_MODEL), dtype=jnp.float32), 'Wq': jax.random.normal(ks[1], (D_MODEL, D_MODEL), dtype=jnp.float32) * w_scale, 'Wk': jax.random.normal(ks[2], (D_MODEL, D_MODEL), dtype=jnp.float32) * w_scale, 'Wv': jax.random.normal(ks[3], (D_MODEL, D_MODEL), dtype=jnp.float32) * w_scale, 'Wo': jax.random.normal(ks[4], (D_MODEL, D_MODEL), dtype=jnp.float32) * w_scale}
    _L1_attn_all = _L1_attn_setup()
    _L1_attn_in = {k: v for k, v in _L1_attn_all.items() if k in ('Wq', 'Wk', 'Wv', 'Wo')}
    del _L1_attn_all

    def _L1_cond2_setup():
        import jax, jax.numpy as jnp
        import numpy as np
        DIM = 256
        HEADS = 16
        DIM_HEAD = 64
        SCALE = 8.0

        def ln(x, g, eps=1e-05):
            mean = x.mean(axis=-1, keepdims=True)
            var = ((x - mean) ** 2).mean(axis=-1, keepdims=True)
            return (x - mean) * jax.lax.rsqrt(var + eps) * g

        def l2norm(t):
            n = jnp.maximum(jnp.linalg.norm(t, axis=-1, keepdims=True), 1e-12)
            return t / n

        def rel_pos_bias(n, w0, b0, g0, w1, b1, g1, w2, b2, dtype):
            pos = jnp.arange(-n + 1, n, dtype=dtype)[:, None]
            h = jax.nn.silu(ln(pos @ w0 + b0, g0))
            h = jax.nn.silu(ln(h @ w1 + b1, g1))
            h = h @ w2 + b2
            i = jnp.arange(n)
            idx = i[:, None] - i[None, :] + n - 1
            bias = h[idx]
            return jnp.transpose(bias, (2, 0, 1))
        key = jax.random.key(seed)
        ks = jax.random.split(key, 16)
        b, n = (2, 512)
        inner = HEADS * DIM_HEAD
        s = 0.02
        return {'x': jax.random.normal(ks[0], (b, n, DIM), jnp.float32), 'mask': jnp.ones((b, n), dtype=bool), 'g_norm': jnp.ones((DIM,), jnp.float32), 'Wq': jax.random.normal(ks[1], (DIM, inner), jnp.float32) * s, 'Wkv': jax.random.normal(ks[2], (DIM, 2 * DIM_HEAD), jnp.float32) * s, 'q_scale': jnp.ones((DIM_HEAD,), jnp.float32), 'k_scale': jnp.ones((DIM_HEAD,), jnp.float32), 'null_kv': jax.random.normal(ks[3], (2, DIM_HEAD), jnp.float32), 'null_attn_bias': jax.random.normal(ks[4], (HEADS,), jnp.float32), 'w0': jax.random.normal(ks[5], (1, DIM), jnp.float32) * s, 'b0': jnp.zeros((DIM,), jnp.float32), 'g0': jnp.ones((DIM,), jnp.float32), 'w1': jax.random.normal(ks[6], (DIM, DIM), jnp.float32) * s, 'b1': jnp.zeros((DIM,), jnp.float32), 'g1': jnp.ones((DIM,), jnp.float32), 'w2': jax.random.normal(ks[7], (DIM, HEADS), jnp.float32) * s, 'b2': jnp.zeros((HEADS,), jnp.float32), 'Wout': jax.random.normal(ks[8], (inner, DIM), jnp.float32) * s, 'g_out': jnp.ones((DIM,), jnp.float32)}
    _L1_cond2_all = _L1_cond2_setup()
    _L1_cond2_in = {k: v for k, v in _L1_cond2_all.items() if k in ('g_norm', 'Wq', 'Wkv', 'q_scale', 'k_scale', 'null_attn_bias', 'w0', 'b0', 'g0', 'w1', 'b1', 'g1', 'w2', 'b2', 'Wout', 'g_out')}
    del _L1_cond2_all

    def _L1_ffn_setup():
        import jax, jax.numpy as jnp
        import numpy as np
        QMAX = 127.0

        def _ste_round(v):
            return v + jax.lax.stop_gradient(jnp.round(v) - v)

        def _act_fake_quant(x, clip_factor):
            scale = jax.nn.sigmoid(clip_factor) * jnp.max(jnp.abs(x)) / QMAX
            return jnp.clip(_ste_round(x / scale), -QMAX - 1.0, QMAX) * scale

        def _weight_fake_quant(w):
            scale = jnp.max(jnp.abs(w), axis=1, keepdims=True) / QMAX
            return jnp.clip(_ste_round(w / scale), -QMAX - 1.0, QMAX) * scale
        key = jax.random.key(seed)
        k1, k2, k3, k4 = jax.random.split(key, 4)
        B, S, H, I = (8, 2048, 256, 704)
        return {'x': jax.random.normal(k1, (B, S, H), dtype=jnp.float32), 'clip_x': jnp.full((1,), 4.0, dtype=jnp.float32), 'clip_down': jnp.full((1,), 4.0, dtype=jnp.float32), 'w_gate': jax.random.normal(k2, (I, H), dtype=jnp.float32) * 0.02, 'w_up': jax.random.normal(k3, (I, H), dtype=jnp.float32) * 0.02, 'w_down': jax.random.normal(k4, (H, I), dtype=jnp.float32) * 0.02}
    _L1_ffn_all = _L1_ffn_setup()
    _L1_ffn_in = {k: v for k, v in _L1_ffn_all.items() if k in ('clip_x', 'clip_down', 'w_gate', 'w_up', 'w_down')}
    del _L1_ffn_all
    return {'x': x, 'cond_64': cond_64, 'fside_16xSxS_0': fside_16xSxS_0, 'mask_BxS_bf1': mask_BxS_bf1, 'mask_BxS_bk0': mask_BxS_bk0, 'L0_cond_wt': _L0_cond_in['wt'], 'L0_cond_wg': _L0_cond_in['wg'], 'L0_cond_w_gate': _L0_cond_in['w_gate'], 'L0_cond_w_up': _L0_cond_in['w_up'], 'L0_cond_w_down': _L0_cond_in['w_down'], 'L0_cond_sw_gate': _L0_cond_in['sw_gate'], 'L0_cond_sw_up': _L0_cond_in['sw_up'], 'L0_cond_sw_down': _L0_cond_in['sw_down'], 'L0_attn_Wq': _L0_attn_in['Wq'], 'L0_attn_Wk': _L0_attn_in['Wk'], 'L0_attn_Wv': _L0_attn_in['Wv'], 'L0_attn_Wo': _L0_attn_in['Wo'], 'L0_cond2_g_norm': _L0_cond2_in['g_norm'], 'L0_cond2_Wq': _L0_cond2_in['Wq'], 'L0_cond2_Wkv': _L0_cond2_in['Wkv'], 'L0_cond2_q_scale': _L0_cond2_in['q_scale'], 'L0_cond2_k_scale': _L0_cond2_in['k_scale'], 'L0_cond2_null_attn_bias': _L0_cond2_in['null_attn_bias'], 'L0_cond2_w0': _L0_cond2_in['w0'], 'L0_cond2_b0': _L0_cond2_in['b0'], 'L0_cond2_g0': _L0_cond2_in['g0'], 'L0_cond2_w1': _L0_cond2_in['w1'], 'L0_cond2_b1': _L0_cond2_in['b1'], 'L0_cond2_g1': _L0_cond2_in['g1'], 'L0_cond2_w2': _L0_cond2_in['w2'], 'L0_cond2_b2': _L0_cond2_in['b2'], 'L0_cond2_Wout': _L0_cond2_in['Wout'], 'L0_cond2_g_out': _L0_cond2_in['g_out'], 'L0_ffn_norm_scale': _L0_ffn_in['norm_scale'], 'L0_ffn_gate_w': _L0_ffn_in['gate_w'], 'L0_ffn_gate_b': _L0_ffn_in['gate_b'], 'L0_ffn_mlp1_w': _L0_ffn_in['mlp1_w'], 'L0_ffn_mlp1_b': _L0_ffn_in['mlp1_b'], 'L0_ffn_mlp2_w': _L0_ffn_in['mlp2_w'], 'L0_ffn_mlp2_b': _L0_ffn_in['mlp2_b'], 'L1_cond_g_in': _L1_cond_in['g_in'], 'L1_cond_null_attn_bias': _L1_cond_in['null_attn_bias'], 'L1_cond_Wq': _L1_cond_in['Wq'], 'L1_cond_Wkv': _L1_cond_in['Wkv'], 'L1_cond_Wo': _L1_cond_in['Wo'], 'L1_cond_g_out': _L1_cond_in['g_out'], 'L1_attn_Wq': _L1_attn_in['Wq'], 'L1_attn_Wk': _L1_attn_in['Wk'], 'L1_attn_Wv': _L1_attn_in['Wv'], 'L1_attn_Wo': _L1_attn_in['Wo'], 'L1_cond2_g_norm': _L1_cond2_in['g_norm'], 'L1_cond2_Wq': _L1_cond2_in['Wq'], 'L1_cond2_Wkv': _L1_cond2_in['Wkv'], 'L1_cond2_q_scale': _L1_cond2_in['q_scale'], 'L1_cond2_k_scale': _L1_cond2_in['k_scale'], 'L1_cond2_null_attn_bias': _L1_cond2_in['null_attn_bias'], 'L1_cond2_w0': _L1_cond2_in['w0'], 'L1_cond2_b0': _L1_cond2_in['b0'], 'L1_cond2_g0': _L1_cond2_in['g0'], 'L1_cond2_w1': _L1_cond2_in['w1'], 'L1_cond2_b1': _L1_cond2_in['b1'], 'L1_cond2_g1': _L1_cond2_in['g1'], 'L1_cond2_w2': _L1_cond2_in['w2'], 'L1_cond2_b2': _L1_cond2_in['b2'], 'L1_cond2_Wout': _L1_cond2_in['Wout'], 'L1_cond2_g_out': _L1_cond2_in['g_out'], 'L1_ffn_clip_x': _L1_ffn_in['clip_x'], 'L1_ffn_clip_down': _L1_ffn_in['clip_down'], 'L1_ffn_w_gate': _L1_ffn_in['w_gate'], 'L1_ffn_w_up': _L1_ffn_in['w_up'], 'L1_ffn_w_down': _L1_ffn_in['w_down']}

def reference(x, cond_64, fside_16xSxS_0, mask_BxS_bf1, mask_BxS_bk0, L0_cond_wt, L0_cond_wg, L0_cond_w_gate, L0_cond_w_up, L0_cond_w_down, L0_cond_sw_gate, L0_cond_sw_up, L0_cond_sw_down, L0_attn_Wq, L0_attn_Wk, L0_attn_Wv, L0_attn_Wo, L0_cond2_g_norm, L0_cond2_Wq, L0_cond2_Wkv, L0_cond2_q_scale, L0_cond2_k_scale, L0_cond2_null_attn_bias, L0_cond2_w0, L0_cond2_b0, L0_cond2_g0, L0_cond2_w1, L0_cond2_b1, L0_cond2_g1, L0_cond2_w2, L0_cond2_b2, L0_cond2_Wout, L0_cond2_g_out, L0_ffn_norm_scale, L0_ffn_gate_w, L0_ffn_gate_b, L0_ffn_mlp1_w, L0_ffn_mlp1_b, L0_ffn_mlp2_w, L0_ffn_mlp2_b, L1_cond_g_in, L1_cond_null_attn_bias, L1_cond_Wq, L1_cond_Wkv, L1_cond_Wo, L1_cond_g_out, L1_attn_Wq, L1_attn_Wk, L1_attn_Wv, L1_attn_Wo, L1_cond2_g_norm, L1_cond2_Wq, L1_cond2_Wkv, L1_cond2_q_scale, L1_cond2_k_scale, L1_cond2_null_attn_bias, L1_cond2_w0, L1_cond2_b0, L1_cond2_g0, L1_cond2_w1, L1_cond2_b1, L1_cond2_g1, L1_cond2_w2, L1_cond2_b2, L1_cond2_Wout, L1_cond2_g_out, L1_ffn_clip_x, L1_ffn_clip_down, L1_ffn_w_gate, L1_ffn_w_up, L1_ffn_w_down):
    import jax
    import jax.numpy as jnp

    def _L0_cond_ref(hidden_states, g, wt, wg, w_gate, w_up, w_down, sw_gate, sw_up, sw_down):
        import jax, jax.numpy as jnp
        import numpy as np
        B, S, H = (4, 512, 256)
        E = 8
        M = 128
        K = 2
        N_SHARED = 2
        SM = M * N_SHARED
        G = 64
        GE_TEMP = 1.0
        ALPHA = 0.001
        SEQ_AUX = True
        NORM_TOPK = True
        COS_TEMP = 0.78
        CONS_ALPHA = 0.01
        LEAKY_SLOPE = 0.01
        EPS_COS = 1e-08

        def _leaky(x):
            return jnp.where(x >= 0, x, LEAKY_SLOPE * x)

        def _moe_forward(hidden_states, g, wt, wg, w_gate, w_up, w_down, sw_gate, sw_up, sw_down):
            b, s, h = hidden_states.shape
            x = hidden_states.reshape(-1, h)
            T = x.shape[0]
            logits_h = x @ wt.T
            logits_g = g @ wg.T
            logits_g = jnp.repeat(logits_g, s, axis=0)
            logits = (logits_h + logits_g / GE_TEMP) / (1.0 + 1.0 / GE_TEMP)
            scores = jax.nn.softmax(logits, axis=-1)
            topk_w, topk_idx = jax.lax.top_k(scores, K)
            if K > 1 and NORM_TOPK:
                topk_w = topk_w / (topk_w.sum(-1, keepdims=True) + 1e-20)
            onehot = jax.nn.one_hot(topk_idx.reshape(b, s * K), E, dtype=jnp.float32)
            ce = onehot.sum(1) / (s * K / E)
            aux_loss = (ce * scores.reshape(b, s, E).mean(1)).sum(1).mean() * ALPHA
            gp = _leaky(jnp.einsum('th,ehm->etm', x, w_gate))
            up = jnp.einsum('th,ehm->etm', x, w_up)
            y_all = jnp.einsum('etm,emh->eth', gp * up, w_down)
            y_sel = y_all[topk_idx, jnp.arange(T)[:, None], :]
            y = (y_sel * topk_w[..., None]).sum(1).reshape(b, s, h)
            p = _leaky(hidden_states @ sw_gate) * (hidden_states @ sw_up) @ sw_down
            y = y + p
            num = jnp.sum(y * p, -1)
            den = jnp.maximum(jnp.linalg.norm(y, axis=-1), EPS_COS) * jnp.maximum(jnp.linalg.norm(p, axis=-1), EPS_COS)
            closs = CONS_ALPHA * jnp.mean(num / den / (1.0 + COS_TEMP))
            return (y, aux_loss + closs)
        y, _ = _moe_forward(hidden_states, g, wt, wg, w_gate, w_up, w_down, sw_gate, sw_up, sw_down)
        return y

    def _L0_attn_ref(x, Wq, Wk, Wv, Wo):
        import jax, jax.numpy as jnp
        import numpy as np
        B, S, D, K = (4, 1024, 256, 64)
        Q = jax.nn.elu(x @ Wq.T) + 1.0
        Kf = jax.nn.elu(x @ Wk.T) + 1.0
        V = x @ Wv.T
        KV_sum = jnp.cumsum(Kf[..., :, None] * V[..., None, :], axis=1)
        K_sum = jnp.cumsum(Kf, axis=1)
        num = jnp.einsum('bsk,bskm->bsm', Q, KV_sum)
        den = jnp.einsum('bsk,bsk->bs', Q, K_sum)[..., None]
        out = num / (den + 1e-06)
        return out @ Wo.T

    def _L0_cond2_ref(x, mask, g_norm, Wq, Wkv, q_scale, k_scale, null_kv, null_attn_bias, w0, b0, g0, w1, b1, g1, w2, b2, Wout, g_out):
        import jax, jax.numpy as jnp
        import numpy as np
        DIM = 256
        HEADS = 16
        DIM_HEAD = 64
        SCALE = 8.0

        def ln(x, g, eps=1e-05):
            mean = x.mean(axis=-1, keepdims=True)
            var = ((x - mean) ** 2).mean(axis=-1, keepdims=True)
            return (x - mean) * jax.lax.rsqrt(var + eps) * g

        def l2norm(t):
            n = jnp.maximum(jnp.linalg.norm(t, axis=-1, keepdims=True), 1e-12)
            return t / n

        def rel_pos_bias(n, w0, b0, g0, w1, b1, g1, w2, b2, dtype):
            pos = jnp.arange(-n + 1, n, dtype=dtype)[:, None]
            h = jax.nn.silu(ln(pos @ w0 + b0, g0))
            h = jax.nn.silu(ln(h @ w1 + b1, g1))
            h = h @ w2 + b2
            i = jnp.arange(n)
            idx = i[:, None] - i[None, :] + n - 1
            bias = h[idx]
            return jnp.transpose(bias, (2, 0, 1))
        b, n, _ = x.shape
        xn = ln(x, g_norm)
        q = (xn @ Wq).reshape(b, n, HEADS, DIM_HEAD).transpose(0, 2, 1, 3)
        kv = xn @ Wkv
        k, v = (kv[..., :DIM_HEAD], kv[..., DIM_HEAD:])
        nk = jnp.broadcast_to(null_kv[0], (b, 1, DIM_HEAD))
        nv = jnp.broadcast_to(null_kv[1], (b, 1, DIM_HEAD))
        k = jnp.concatenate([nk, k], axis=1)
        v = jnp.concatenate([nv, v], axis=1)
        q = l2norm(q) * q_scale
        k = l2norm(k) * k_scale
        sim = jnp.einsum('bhid,bjd->bhij', q, k) * SCALE
        bias = rel_pos_bias(n, w0, b0, g0, w1, b1, g1, w2, b2, q.dtype)
        null_bias = jnp.broadcast_to(null_attn_bias[:, None, None], (HEADS, n, 1))
        attn_bias = jnp.concatenate([null_bias, bias], axis=-1)
        sim = sim + attn_bias
        neg = -jnp.finfo(sim.dtype).max
        causal = jnp.triu(jnp.ones((n, n + 1), dtype=bool), k=2)
        sim = jnp.where(causal, neg, sim)
        m = jnp.pad(mask, ((0, 0), (1, 0)), constant_values=True)[:, None, None, :]
        sim = jnp.where(m, sim, neg)
        attn = jax.nn.softmax(sim, axis=-1)
        out = jnp.einsum('bhij,bjd->bhid', attn, v)
        out = out.transpose(0, 2, 1, 3).reshape(b, n, HEADS * DIM_HEAD)
        return ln(out @ Wout, g_out)

    def _L0_ffn_ref(x, norm_scale, gate_w, gate_b, mlp1_w, mlp1_b, mlp2_w, mlp2_b):
        import jax, jax.numpy as jnp
        import numpy as np
        B, S, D = (1, 512, 256)
        I = 512
        E = 8
        K = 2
        LIMIT = 7.0
        ALPHA = 1.702
        EPS = 1e-05

        def _swiglu(h):
            x_glu = jnp.minimum(h[..., ::2], LIMIT)
            x_lin = jnp.clip(h[..., 1::2], -LIMIT, LIMIT)
            return x_glu * jax.nn.sigmoid(ALPHA * x_glu) * (x_lin + 1.0)

        def _moe(t, gate_w, gate_b, mlp1_w, mlp1_b, mlp2_w, mlp2_b):
            T = t.shape[0]
            logits = t @ gate_w + gate_b
            top_v, top_i = jax.lax.top_k(logits, K)
            probs = jax.nn.softmax(top_v, axis=-1)
            w = jnp.zeros((T, E), t.dtype).at[jnp.arange(T)[:, None], top_i].set(probs)

            def body(acc, ew):
                w1, b1, w2, b2, we = ew
                h = _swiglu(t @ w1 + b1)
                y = h @ w2 + b2
                return (acc + we[:, None] * y, None)
            acc0 = jnp.zeros((T, t.shape[1]), t.dtype)
            acc, _ = jax.lax.scan(body, acc0, (mlp1_w, mlp1_b, mlp2_w, mlp2_b, w.T))
            return acc
        Bx, Sx, Dx = x.shape
        ms = jnp.mean(x * x, axis=-1, keepdims=True)
        t = (x * jax.lax.rsqrt(ms + EPS) * norm_scale).reshape(Bx * Sx, Dx)
        y = _moe(t, gate_w, gate_b, mlp1_w, mlp1_b, mlp2_w, mlp2_b)
        return x + y.reshape(Bx, Sx, Dx)

    def _L1_cond_ref(x, attn_bias, mask, g_in, null_attn_bias, null_kv, Wq, Wkv, Wo, g_out):
        import jax, jax.numpy as jnp
        import numpy as np
        B, N, DIM, H, DH = (2, 512, 256, 16, 64)
        INNER = H * DH
        EPS = 1e-05

        def layernorm(x, g):
            mean = jnp.mean(x, axis=-1, keepdims=True)
            var = jnp.var(x, axis=-1, keepdims=True)
            return (x - mean) * jax.lax.rsqrt(var + EPS) * g
        b, n, _ = x.shape
        scale = DH ** (-0.5)
        xn = layernorm(x, g_in)
        q = (xn @ Wq).reshape(b, n, H, DH).transpose(0, 2, 1, 3) * scale
        kv = xn @ Wkv
        k, v = (kv[..., :DH], kv[..., DH:])
        nk = jnp.broadcast_to(null_kv[0], (b, 1, DH))
        nv = jnp.broadcast_to(null_kv[1], (b, 1, DH))
        k = jnp.concatenate([nk, k], axis=1)
        v = jnp.concatenate([nv, v], axis=1)
        sim = jnp.einsum('bhid,bjd->bhij', q, k)
        null_col = jnp.broadcast_to(null_attn_bias[:, None, None], (H, n, 1))
        bias = jnp.concatenate([null_col, attn_bias], axis=-1)
        sim = sim + bias
        neg = -jnp.finfo(sim.dtype).max
        j = n + 1
        causal_mask = jnp.triu(jnp.ones((n, j), dtype=bool), k=j - n + 1)
        sim = jnp.where(causal_mask, neg, sim)
        mask_p = jnp.pad(mask, ((0, 0), (1, 0)), constant_values=True)
        sim = jnp.where(mask_p[:, None, None, :], sim, neg)
        attn = jax.nn.softmax(sim, axis=-1)
        out = jnp.einsum('bhij,bjd->bhid', attn, v)
        out = out.transpose(0, 2, 1, 3).reshape(b, n, INNER)
        out = out @ Wo
        return layernorm(out, g_out)

    def _L1_attn_ref(x, Wq, Wk, Wv, Wo):
        import math
        import jax, jax.numpy as jnp
        import numpy as np
        D_MODEL = 256
        N_HEADS = 16
        HEAD_DIM = D_MODEL // N_HEADS
        ROPE_THETA = 10000.0

        def _apply_rope(t, offset=0):
            B, H, T, Dh = t.shape
            inv_freq = 1.0 / ROPE_THETA ** (jnp.arange(0, Dh, 2, dtype=jnp.float32) / Dh)
            pos = jnp.arange(T, dtype=jnp.float32) + offset
            ang = pos[:, None] * inv_freq[None, :]
            cos = jnp.concatenate([jnp.cos(ang), jnp.cos(ang)], axis=-1)
            sin = jnp.concatenate([jnp.sin(ang), jnp.sin(ang)], axis=-1)
            t1, t2 = (t[..., :Dh // 2], t[..., Dh // 2:])
            rot = jnp.concatenate([-t2, t1], axis=-1)
            return t * cos + rot * sin

        def _forward(x, Wq, Wk, Wv, Wo):
            B, T, _ = x.shape
            scale = 1.0 / math.sqrt(HEAD_DIM)

            def split_heads(y):
                return y.reshape(B, T, N_HEADS, HEAD_DIM).transpose(0, 2, 1, 3)
            q = split_heads(x @ Wq.T)
            k = split_heads(x @ Wk.T)
            v = split_heads(x @ Wv.T)
            q = _apply_rope(q)
            k = _apply_rope(k)
            scores = jnp.einsum('bhtd,bhsd->bhts', q, k) * scale
            causal = jnp.triu(jnp.ones((T, T), dtype=bool), k=1)
            scores = jnp.where(causal[None, None], -jnp.inf, scores)
            attn = jax.nn.softmax(scores, axis=-1)
            attn = jnp.nan_to_num(attn, nan=0.0)
            out = jnp.einsum('bhts,bhsd->bhtd', attn, v)
            out = out.transpose(0, 2, 1, 3).reshape(B, T, N_HEADS * HEAD_DIM)
            return out @ Wo.T
        return _forward(x, Wq, Wk, Wv, Wo)

    def _L1_cond2_ref(x, mask, g_norm, Wq, Wkv, q_scale, k_scale, null_kv, null_attn_bias, w0, b0, g0, w1, b1, g1, w2, b2, Wout, g_out):
        import jax, jax.numpy as jnp
        import numpy as np
        DIM = 256
        HEADS = 16
        DIM_HEAD = 64
        SCALE = 8.0

        def ln(x, g, eps=1e-05):
            mean = x.mean(axis=-1, keepdims=True)
            var = ((x - mean) ** 2).mean(axis=-1, keepdims=True)
            return (x - mean) * jax.lax.rsqrt(var + eps) * g

        def l2norm(t):
            n = jnp.maximum(jnp.linalg.norm(t, axis=-1, keepdims=True), 1e-12)
            return t / n

        def rel_pos_bias(n, w0, b0, g0, w1, b1, g1, w2, b2, dtype):
            pos = jnp.arange(-n + 1, n, dtype=dtype)[:, None]
            h = jax.nn.silu(ln(pos @ w0 + b0, g0))
            h = jax.nn.silu(ln(h @ w1 + b1, g1))
            h = h @ w2 + b2
            i = jnp.arange(n)
            idx = i[:, None] - i[None, :] + n - 1
            bias = h[idx]
            return jnp.transpose(bias, (2, 0, 1))
        b, n, _ = x.shape
        xn = ln(x, g_norm)
        q = (xn @ Wq).reshape(b, n, HEADS, DIM_HEAD).transpose(0, 2, 1, 3)
        kv = xn @ Wkv
        k, v = (kv[..., :DIM_HEAD], kv[..., DIM_HEAD:])
        nk = jnp.broadcast_to(null_kv[0], (b, 1, DIM_HEAD))
        nv = jnp.broadcast_to(null_kv[1], (b, 1, DIM_HEAD))
        k = jnp.concatenate([nk, k], axis=1)
        v = jnp.concatenate([nv, v], axis=1)
        q = l2norm(q) * q_scale
        k = l2norm(k) * k_scale
        sim = jnp.einsum('bhid,bjd->bhij', q, k) * SCALE
        bias = rel_pos_bias(n, w0, b0, g0, w1, b1, g1, w2, b2, q.dtype)
        null_bias = jnp.broadcast_to(null_attn_bias[:, None, None], (HEADS, n, 1))
        attn_bias = jnp.concatenate([null_bias, bias], axis=-1)
        sim = sim + attn_bias
        neg = -jnp.finfo(sim.dtype).max
        causal = jnp.triu(jnp.ones((n, n + 1), dtype=bool), k=2)
        sim = jnp.where(causal, neg, sim)
        m = jnp.pad(mask, ((0, 0), (1, 0)), constant_values=True)[:, None, None, :]
        sim = jnp.where(m, sim, neg)
        attn = jax.nn.softmax(sim, axis=-1)
        out = jnp.einsum('bhij,bjd->bhid', attn, v)
        out = out.transpose(0, 2, 1, 3).reshape(b, n, HEADS * DIM_HEAD)
        return ln(out @ Wout, g_out)

    def _L1_ffn_ref(x, clip_x, clip_down, w_gate, w_up, w_down):
        import jax, jax.numpy as jnp
        import numpy as np
        QMAX = 127.0

        def _ste_round(v):
            return v + jax.lax.stop_gradient(jnp.round(v) - v)

        def _act_fake_quant(x, clip_factor):
            scale = jax.nn.sigmoid(clip_factor) * jnp.max(jnp.abs(x)) / QMAX
            return jnp.clip(_ste_round(x / scale), -QMAX - 1.0, QMAX) * scale

        def _weight_fake_quant(w):
            scale = jnp.max(jnp.abs(w), axis=1, keepdims=True) / QMAX
            return jnp.clip(_ste_round(w / scale), -QMAX - 1.0, QMAX) * scale
        xq = _act_fake_quant(x, clip_x[0])
        gate = jnp.einsum('bsh,ih->bsi', xq, _weight_fake_quant(w_gate))
        up = jnp.einsum('bsh,ih->bsi', xq, _weight_fake_quant(w_up))
        h = _act_fake_quant(jax.nn.silu(gate) * up, clip_down[0])
        return jnp.einsum('bsi,hi->bsh', h, _weight_fake_quant(w_down))
    x = x + _L0_attn_ref(_L0_cond_ref(x, cond_64, L0_cond_wt, L0_cond_wg, L0_cond_w_gate, L0_cond_w_up, L0_cond_w_down, L0_cond_sw_gate, L0_cond_sw_up, L0_cond_sw_down), L0_attn_Wq, L0_attn_Wk, L0_attn_Wv, L0_attn_Wo)
    x = x + _L0_ffn_ref(_L0_cond2_ref(x, mask_BxS_bf1, L0_cond2_g_norm, L0_cond2_Wq, L0_cond2_Wkv, L0_cond2_q_scale, L0_cond2_k_scale, cond_64, L0_cond2_null_attn_bias, L0_cond2_w0, L0_cond2_b0, L0_cond2_g0, L0_cond2_w1, L0_cond2_b1, L0_cond2_g1, L0_cond2_w2, L0_cond2_b2, L0_cond2_Wout, L0_cond2_g_out), L0_ffn_norm_scale, L0_ffn_gate_w, L0_ffn_gate_b, L0_ffn_mlp1_w, L0_ffn_mlp1_b, L0_ffn_mlp2_w, L0_ffn_mlp2_b)
    x = x + _L1_attn_ref(_L1_cond_ref(x, fside_16xSxS_0, mask_BxS_bk0, L1_cond_g_in, L1_cond_null_attn_bias, cond_64, L1_cond_Wq, L1_cond_Wkv, L1_cond_Wo, L1_cond_g_out), L1_attn_Wq, L1_attn_Wk, L1_attn_Wv, L1_attn_Wo)
    x = x + _L1_ffn_ref(_L1_cond2_ref(x, mask_BxS_bf1, L1_cond2_g_norm, L1_cond2_Wq, L1_cond2_Wkv, L1_cond2_q_scale, L1_cond2_k_scale, cond_64, L1_cond2_null_attn_bias, L1_cond2_w0, L1_cond2_b0, L1_cond2_g0, L1_cond2_w1, L1_cond2_b1, L1_cond2_g1, L1_cond2_w2, L1_cond2_b2, L1_cond2_Wout, L1_cond2_g_out), L1_ffn_clip_x, L1_ffn_clip_down, L1_ffn_w_gate, L1_ffn_w_up, L1_ffn_w_down)
    return x

_drawn_inputs = setup_inputs


def setup_inputs(seed=0):
    import zlib

    import numpy as np

    out = dict(_drawn_inputs(seed))
    spreads = {'L0_cond2_g_norm': (1.0, 0.2),
     'L0_cond2_q_scale': (1.0, 0.2),
     'L0_cond2_k_scale': (1.0, 0.2),
     'L0_cond2_b0': (0.0, 0.521),
     'L0_cond2_g0': (1.0, 0.6),
     'L0_cond2_b1': (0.0, 0.69),
     'L0_cond2_g1': (1.0, 0.6),
     'L0_cond2_b2': (0.0, 0.608),
     'L0_cond2_g_out': (1.0, 0.2),
     'L0_ffn_norm_scale': (1.0, 0.6),
     'L0_ffn_gate_b': (0.0, 0.1),
     'L0_ffn_mlp1_b': (0.0, 0.725),
     'L0_ffn_mlp2_b': (0.0, 0.1),
     'L1_cond_g_in': (1.0, 0.6),
     'L1_cond_g_out': (1.0, 0.2),
     'L1_cond2_g_norm': (1.0, 0.6),
     'L1_cond2_q_scale': (1.0, 0.6),
     'L1_cond2_k_scale': (1.0, 0.6),
     'L1_cond2_b0': (0.0, 0.8),
     'L1_cond2_g0': (1.0, 0.6),
     'L1_cond2_b1': (0.0, 0.8),
     'L1_cond2_g1': (1.0, 0.6),
     'L1_cond2_b2': (0.0, 0.8),
     'L1_cond2_g_out': (1.0, 0.6)}
    factors = {'fside_16xSxS_0': 22.487,
     'L0_cond_wt': 5.866,
     'L0_cond_wg': 5.436,
     'L0_cond_w_gate': 4.803,
     'L0_cond_w_up': 3.856,
     'L0_cond_w_down': 3.906,
     'L0_cond_sw_gate': 2.679,
     'L0_cond_sw_up': 2.916,
     'L0_cond_sw_down': 2.772,
     'L0_attn_Wq': 8.0,
     'L0_attn_Wk': 8.0,
     'L1_cond_null_attn_bias': 19.098,
     'L1_cond_Wq': 41.108,
     'L1_cond2_Wq': 8.0,
     'L1_cond2_Wkv': 3.747,
     'L1_cond2_null_attn_bias': 8.0,
     'L1_cond2_w0': 8.0,
     'L1_cond2_w1': 8.0,
     'L1_cond2_w2': 8.0,
     'L1_cond2_Wout': 3.275,
     'L1_ffn_w_gate': 3.708,
     'L1_ffn_w_up': 3.419,
     'L1_ffn_w_down': 3.589,
     'L1_attn_Wq': 3.173,
     'L1_attn_Wk': 3.122}
    for name, (base, spread) in spreads.items():
        noise = np.random.default_rng([zlib.crc32(name.encode()), seed]).standard_normal(out[name].shape)
        drawn = base * np.exp(spread * noise) if base else spread * noise
        out[name] = jnp.asarray(drawn.astype(out[name].dtype))
    for name, factor in factors.items():
        out[name] = (out[name] * factor).astype(out[name].dtype)
    return out
```

```python
from contextlib import ExitStack

import numpy as np

import concourse.bass as bass
from concourse import mybir

F32 = mybir.dt.float32
BF16 = mybir.dt.bfloat16
U8 = mybir.dt.uint8
I32 = mybir.dt.int32
U32 = mybir.dt.uint32
ALU = mybir.AluOpType
ACT = mybir.ActivationFunctionType
AX = mybir.AxisListType

P = 128
B, S, D = 4, 512, 256
TB = S // P
NT = B * TB
KD = D // P
H, DH = 16, 64
DR = D // H
E0, M0 = 8, 128
NSH = 2
G0 = 64
E1, I1 = 8, 512
IQ = 704
QMAX = 127.0
NPOS = S + P
MASKED = -1.0e30
EPS = 1e-5
RNE = 12582912.0


FREE = 2


class Steps:

    def __init__(self, eng, sem, base=0, per_loop=None):
        self.eng, self.sem, self.base, self.n, self.per_loop = eng, sem, base, 0, per_loop

    def after(self, ins, apart=False):
        self.n += 1
        ins.then_inc(self.sem, 1)
        self.eng.wait_ge(self.sem, self.base + self.n)
        if apart:
            self.eng.nop(nofuse=True)

    def close(self):
        assert self.per_loop is None or self.n == self.per_loop, (self.n, self.per_loop)


def wait_apart(eng, sem, value):
    eng.wait_ge(sem, value)
    eng.nop(nofuse=True)


def rows(ap, n=P):
    return ap.rearrange("(a d) -> a d", a=1).broadcast_to([n, ap.shape[0]])


def columns(ap, k):
    return ap.rearrange("(k p) -> p k", k=k)


def bias_tables(nc, sem, bank, ident, pos_reversed, layers):
    NR = NPOS // P
    with ExitStack() as ctx:
        def sb(name, shape, dt=F32):
            return ctx.enter_context(nc.sbuf_tensor(name, shape, dt))

        pos = sb("bt_pos", [P, NR])
        row = [sb(f"bt_row{l}", [P, 5, D]) for l in range(2)]
        w1 = [sb(f"bt_w1{l}", [P, KD, D]) for l in range(2)]
        w2 = [sb(f"bt_w2{l}", [P, KD, H]) for l in range(2)]
        b2 = [sb(f"bt_b2{l}", [H, 1]) for l in range(2)]
        hid = sb("bt_hid", [P, NR, D])
        act_out = sb("bt_act", [P, NR, D])
        hid_t = sb("bt_hid_t", [P, KD, NPOS])
        stats = sb("bt_stats", [P, NR, 6])
        mv = sb("bt_mv", [P, NR, 2])
        sd = sb("bt_sd", [P, NR])
        rstd = sb("bt_rstd", [P, NR])
        table = sb("bt_table", [H, NPOS])

        loaded = [sem(f"bt_loaded{l}") for l in range(2)]
        stepped = sem("bt_stepped")
        var_ready = sem("bt_var_ready")
        sd_ready = sem("bt_sd_ready")
        normed = sem("bt_normed")
        activated = sem("bt_activated")
        transposed = sem("bt_transposed")
        hid_t_ready = sem("bt_hid_t_ready")
        projected = sem("bt_projected")
        table_ready = sem("bt_table_ready")
        stored, copied = sem("bt_stored"), sem("bt_copied")
        block = ctx.enter_context(nc.Block())

        @block.sync
        def _(sp):
            for l, lay in enumerate(layers):
                if l == 0:
                    sp.dma_start(pos[:], pos_reversed).then_inc(loaded[l], 16)
                for n, name in enumerate(("w0", "b0", "g0", "b1", "g1")):
                    sp.dma_start(row[l][:, n, :], rows(lay[name])).then_inc(loaded[l], 16)
                sp.dma_start(w1[l][:], lay["w1"].rearrange("(k p) n -> p k n", p=P)).then_inc(loaded[l], 16)
                sp.dma_start(w2[l][:], lay["w2"].rearrange("(k p) n -> p k n", p=P)).then_inc(loaded[l], 16)
                sp.dma_start(b2[l][:], lay["b2"].rearrange("(h a) -> h a", a=1)).then_inc(loaded[l], 16)
            for l, lay in enumerate(layers):
                sp.wait_ge(table_ready, 2 * (l + 1))
                sp.dma_start(lay["table"], table[:]).then_inc(stored, 16)
                sp.wait_ge(stored, 16 * (l + 1))
                line = lay["table"]
                line = bass.AP(tensor=line.tensor, offset=line.offset, ap=[[NPOS, H], [0, P], [1, NPOS]])
                sp.dma_start(lay["copies"], line).then_inc(copied, 16)
            sp.wait_ge(copied, 32)

        @block.vector
        def _(dv):
            st = Steps(dv, stepped)
            for l in range(2):
                dv.wait_ge(loaded[l], 16 * (9 if l == 0 else 8))
                if l == 1:
                    dv.wait_ge(activated, 2)
                for q in range(2):
                    for t in range(NR):
                        if q == 0:
                            ins = nc.vector.scalar_tensor_tensor(
                                hid[:, t, :], row[l][:, 0, :], pos[:, t:t + 1], row[l][:, 1, :], ALU.mult, ALU.add)
                        else:
                            if t == 0:
                                dv.wait_ge(projected, 2 * l + 1)
                            ins = nc.vector.tensor_tensor(
                                hid[:, t, :], bank[3 + t // 2][:, D * (t % 2):D * (t % 2) + D], row[l][:, 3, :], ALU.add)
                    st.after(ins)
                    for t in range(NR):
                        ins = nc.vector.bn_stats(stats[:, t, :], hid[:, t, :])
                    st.after(ins)
                    for t in range(NR):
                        ins = nc.vector.bn_aggr(mv[:, t, :], stats[:, t, :])
                    st.after(ins)
                    nc.vector.tensor_scalar(sd[:], mv[:, :, 1], EPS, None, ALU.add).then_inc(var_ready, 1)
                    dv.wait_ge(sd_ready, 2 * l + q + 1)
                    st.after(nc.vector.reciprocal(rstd[:], sd[:]))
                    for t in range(NR):
                        ins = nc.vector.tensor_scalar(hid[:, t, :], hid[:, t, :], mv[:, t, 0:1], rstd[:, t:t + 1],
                                                      ALU.subtract, ALU.mult)
                    st.after(ins)
                    g = row[l][:, 2 + 2 * q, :].unsqueeze(1).broadcast_to([P, NR, D])
                    nc.vector.tensor_tensor(hid[:], hid[:], g, ALU.mult).then_inc(normed, 1)
                    if q == 0:
                        dv.wait_ge(activated, 2 * l + 1)
                dv.wait_ge(projected, 2 * l + 2)
                if l == 1:
                    dv.wait_ge(stored, 16)
                nc.vector.tensor_scalar(table[:, 0:512], bank[6][0:H, :], b2[l][:], None, ALU.add).then_inc(table_ready, 1)
                nc.vector.tensor_scalar(table[:, 512:NPOS], bank[7][0:H, 0:P], b2[l][:], None, ALU.add).then_inc(table_ready, 1)

        @block.scalar
        def _(ac):
            for n in range(4):
                ac.wait_ge(var_ready, n + 1)
                nc.scalar.activation(sd[:], sd[:], ACT.Sqrt).then_inc(sd_ready, 1)
                ac.wait_ge(normed, n + 1)
                if n:
                    ac.wait_ge(transposed, n)
                nc.scalar.activation(act_out[:], hid[:], ACT.Silu).then_inc(activated, 1)
                ac.wait_ge(transposed, n + 1)
                if n:
                    ac.wait_ge(projected, n)
                nc.scalar.copy(hid_t[:, 0, 0:512], bank[0][:])
                nc.scalar.copy(hid_t[:, 1, 0:512], bank[1][:])
                nc.scalar.copy(hid_t[:, :, 512:NPOS], bank[2][:, 0:D].rearrange("p (k n) -> p k n", k=KD)).then_inc(hid_t_ready, 1)

        @block.tensor
        def _(pe):
            pe.wait_ge(loaded[0], 16 * 9)
            pe.wait_ge(loaded[1], 16 * 8)
            for n in range(4):
                l, q = divmod(n, 2)
                pe.wait_ge(activated, n + 1)
                if n:
                    pe.wait_ge(hid_t_ready, n)
                for t in range(NR):
                    for k in range(KD):
                        dst = bank[k][:, P * t:P * t + P] if t < 4 else bank[2][:, P * k:P * k + P]
                        ins = nc.tensor.transpose(dst, act_out[:, t, P * k:P * k + P], ident[:])
                ins.then_inc(transposed, 1)
                pe.wait_ge(hid_t_ready, n + 1)
                if q == 0:
                    if l:
                        pe.wait_ge(normed, n)
                    for t in range(NR):
                        for k in range(KD):
                            ins = nc.tensor.matmul(bank[3 + t // 2][:, D * (t % 2):D * (t % 2) + D],
                                                   hid_t[:, k, P * t:P * t + P], w1[l][:, k, :], start=k == 0, stop=k == KD - 1)
                else:
                    if l:
                        pe.wait_ge(table_ready, 2)
                    for lo, hi, dst in ((0, 512, bank[6]), (512, NPOS, bank[7])):
                        for k in range(KD):
                            ins = nc.tensor.matmul(dst[0:H, 0:hi - lo], w2[l][:, k, :], hid_t[:, k, lo:hi],
                                                   start=k == 0, stop=k == KD - 1)
                ins.then_inc(projected, 1)


def route(nc, dv, st, logits, ex, zsum, best, best_at, lane, picked, weight, softmax_all, exp_in, exp_ready, exp_done):
    E = E0
    for t in range(NT):
        ins = nc.vector.max(best[:, t, :], logits[:, t, :])
    st.after(ins)
    for t in range(NT):
        ins = nc.vector.max_index(best_at[:, t, :], best[:, t, :], logits[:, t, :])
    st.after(ins)
    top = best[:, :, 0:1].broadcast_to([P, NT, E])
    nc.vector.tensor_tensor(exp_in[:], logits[:], top, ALU.subtract).then_inc(exp_ready, 1)
    at = best_at[:, :, 0:2]
    st.after(nc.vector.tensor_copy(picked[:, :, 0:2], at))
    first = picked[:, :, 0:1].broadcast_to([P, NT, E])
    second = picked[:, :, 1:2].broadcast_to([P, NT, E])
    lanes = lane[:].unsqueeze(1).broadcast_to([P, NT, E])
    nc.vector.tensor_tensor(weight[:], lanes, first, ALU.is_equal)
    st.after(nc.vector.tensor_tensor(logits[:], lanes, second, ALU.is_equal))
    st.after(nc.vector.tensor_tensor(weight[:], weight[:], logits[:], ALU.add))
    dv.wait_ge(exp_done, 1)
    if softmax_all:
        st.after(nc.vector.tensor_reduce(zsum[:], ex[:], AX.X, ALU.add))
        st.after(nc.vector.reciprocal(zsum[:], zsum[:]))
        st.after(nc.vector.tensor_tensor(ex[:], ex[:], zsum[:].unsqueeze(2).broadcast_to([P, NT, E]), ALU.mult))
    st.after(nc.vector.tensor_tensor(ex[:], ex[:], weight[:], ALU.mult))
    st.after(nc.vector.tensor_reduce(zsum[:], ex[:], AX.X, ALU.add))
    if softmax_all:
        st.after(nc.vector.tensor_scalar(zsum[:], zsum[:], 1e-20, None, ALU.add))
    st.after(nc.vector.reciprocal(zsum[:], zsum[:]))
    st.after(nc.vector.tensor_tensor(weight[:], ex[:], zsum[:].unsqueeze(2).broadcast_to([P, NT, E]), ALU.mult))


def moe_conditioning(nc, sem, bank, Y, x_transposed, lane_d, cond_rep, wt_t, wg_t, w_gate, w_up, w_down,
                     sw_gate, sw_up, sw_down):
    NE = E0 + NSH
    with ExitStack() as ctx:
        def sb(name, shape, dt=F32):
            return ctx.enter_context(nc.sbuf_tensor(name, shape, dt))

        xt = sb("mc_xt", [P, B, KD, S])
        wg = sb("mc_wg", [P, KD, NE, M0])
        wu = sb("mc_wu", [P, KD, NE, M0])
        wd = sb("mc_wd", [P, NE, D])
        wtt = sb("mc_wtt", [P, KD, E0])
        wgt = sb("mc_wgt", [G0, E0])
        crep = sb("mc_crep", [G0, B, P])
        lane = sb("mc_lane", [P, E0])
        logits = sb("mc_logits", [P, NT, E0])
        exp_in = sb("mc_exp_in", [P, NT, E0])
        ex = sb("mc_ex", [P, NT, E0])
        zsum = sb("mc_zsum", [P, NT])
        best = sb("mc_best", [P, NT, 8])
        best_at = sb("mc_best_at", [P, NT, 8], U32)
        picked = sb("mc_picked", [P, NT, 2])
        weight = sb("mc_weight", [P, NT, E0])
        gate = sb("mc_gate", [P, 2, S])
        leaky = sb("mc_leaky", [P, 2, S])
        hid = sb("mc_hid", [P, 2, S])

        routing_in = sem("mc_routing_in")
        gate_in, up_in, down_in = sem("mc_gate_in"), sem("mc_up_in"), sem("mc_down_in")
        stepped = sem("mc_stepped")
        logits_done = sem("mc_logits_done")
        exp_ready, exp_done = sem("mc_exp_ready"), sem("mc_exp_done")
        gated, upped, downed = sem("mc_gated"), sem("mc_upped"), sem("mc_downed")
        gate_copied = sem("mc_gate_copied")
        leaked = sem("mc_leaked")
        hid_ready = sem("mc_hid_ready")
        added = sem("mc_added")
        block = ctx.enter_context(nc.Block())

        @block.sync
        def _(sp):
            sp.dma_start(wtt[:], wt_t.rearrange("(k p) e -> p k e", p=P)).then_inc(routing_in, 16)
            sp.dma_start(wgt[:], wg_t).then_inc(routing_in, 16)
            sp.dma_start(crep[:], cond_rep).then_inc(routing_in, 16)
            sp.dma_start(lane[:], lane_d).then_inc(routing_in, 16)
            for b in range(B):
                sp.dma_start(xt[:, b], x_transposed[b].rearrange("(k p) s -> p k s", p=P)).then_inc(routing_in, 16)
            for dst, w, shared, s in ((wg, w_gate, sw_gate, gate_in), (wu, w_up, sw_up, up_in)):
                for k in range(KD):
                    sp.dma_start(dst[:, k, 0:E0, :], w[:, P * k:P * k + P, :].rearrange("e p m -> p e m")).then_inc(s, 16)
                    sp.dma_start(dst[:, k, E0:NE, :].rearrange("p e m -> p (e m)"), shared[P * k:P * k + P, :]).then_inc(s, 16)
            sp.dma_start(wd[:, 0:E0, :], w_down.rearrange("e p n -> p e n")).then_inc(down_in, 16)
            sp.dma_start(wd[:, E0:NE, :], sw_down.rearrange("(e p) n -> p e n", p=P)).then_inc(down_in, 16)

        @block.tensor
        def _(pe):
            pe.sem_inc(downed, 2 * FREE)
            pe.wait_ge(routing_in, 16 * 8)
            for t in range(NT):
                b, i = divmod(t, TB)
                dst = bank[6][:, E0 * t:E0 * t + E0]
                for k in range(KD):
                    nc.tensor.matmul(dst, xt[:, b, k, P * i:P * i + P], wtt[:, k, :], start=k == 0, stop=False)
                ins = nc.tensor.matmul(dst, crep[:, b, :], wgt[:], start=False, stop=True)
            ins.then_inc(logits_done, 1)
            pe.wait_ge(gate_in, 64)
            pe.wait_ge(up_in, 64)
            pe.wait_ge(down_in, 32)

            with pe.Fori(0, B) as it:
                def down(e):
                    n = NE * it + e
                    pe.wait_ge(hid_ready, FREE + n + 1)
                    for j in range(2):
                        pe.wait_ge(added, 2 * n + j + 1)
                        for i in (2 * j, 2 * j + 1):
                            ins = nc.tensor.matmul(bank[4 + j][:, D * (i % 2):D * (i % 2) + D],
                                                   hid[:, e % 2, P * i:P * i + P], wd[:, e, :], start=True, stop=True)
                        ins.then_inc(downed, 1)

                for e in range(NE):
                    n = NE * it + e
                    pe.wait_ge(gate_copied, n + 1)
                    for k in range(KD):
                        ins = nc.tensor.matmul(bank[e % 2][:], wg[:, k, e, :], xt[:, it, k, :], start=k == 0, stop=k == KD - 1)
                    ins.then_inc(gated, 1)
                    pe.wait_ge(hid_ready, n + 1)
                    for k in range(KD):
                        ins = nc.tensor.matmul(bank[2 + e % 2][:], wu[:, k, e, :], xt[:, it, k, :], start=k == 0, stop=k == KD - 1)
                    ins.then_inc(upped, 1)
                    if e:
                        down(e - 1)
                down(NE - 1)

        @block.scalar
        def _(ac):
            ac.sem_inc(gate_copied, FREE)
            ac.wait_ge(exp_ready, 1)
            nc.scalar.activation(ex[:], exp_in[:], ACT.Exp).then_inc(exp_done, 1)
            with ac.Fori(0, B) as it:
                for e in range(NE):
                    n = NE * it + e
                    ac.wait_ge(gated, n + 1)
                    ac.wait_ge(leaked, n + 1)
                    nc.scalar.copy(gate[:, e % 2, :], bank[e % 2][:]).then_inc(gate_copied, 1)

        @block.vector
        def _(dv):
            dv.sem_inc(leaked, FREE)
            dv.sem_inc(hid_ready, FREE)
            dv.sem_inc(added, 2)
            st = Steps(dv, stepped)
            dv.wait_ge(logits_done, 1)
            st.after(nc.vector.tensor_scalar(logits[:], bank[6][:, 0:NT * E0].rearrange("p (t e) -> p t e", e=E0), 0.5, None, ALU.mult))
            route(nc, dv, st, logits, ex, zsum, best, best_at, lane, picked, weight, True, exp_in, exp_ready, exp_done)
            with dv.Fori(0, B) as it:
                def add(e):
                    n = NE * it + e
                    for j in range(2):
                        dv.wait_ge(downed, 2 * FREE + 2 * n + j + 1)
                        if e:
                            dv.wait_ge(added, 2 * n + 2)
                        for i in (2 * j, 2 * j + 1):
                            src = bank[4 + j][:, D * (i % 2):D * (i % 2) + D]
                            y = Y[:, TB * it + i, :]
                            if e == 0:
                                ins = nc.vector.tensor_scalar(y, src, weight[:, TB * it + i, 0:1], None, ALU.mult)
                            else:
                                w = weight[:, TB * it + i, e:e + 1] if e < E0 else 1.0
                                ins = nc.vector.scalar_tensor_tensor(y, src, w, y, ALU.mult, ALU.add)
                        ins.then_inc(added, 1)

                for e in range(NE):
                    n = NE * it + e
                    dv.wait_ge(gate_copied, FREE + n + 1)
                    nc.vector.scalar_tensor_tensor(leaky[:, e % 2, :], gate[:, e % 2, :], 0.01, gate[:, e % 2, :],
                                                   ALU.mult, ALU.max).then_inc(leaked, 1)
                    dv.wait_ge(leaked, FREE + n + 1)
                    dv.wait_ge(upped, n + 1)
                    dv.wait_ge(downed, 2 * n + 2)
                    nc.vector.tensor_tensor(hid[:, e % 2, :], leaky[:, e % 2, :], bank[2 + e % 2][:], ALU.mult).then_inc(hid_ready, 1)
                    if e:
                        add(e - 1)
                add(NE - 1)


def linear_attention(nc, sem, bank, X, Y, ident, keep_upper, wq_t, wk_t, wv_t, wo_t):
    K = 64
    with ExitStack() as ctx:
        def sb(name, shape, dt=F32):
            return ctx.enter_context(nc.sbuf_tensor(name, shape, dt))

        wqk = sb("la_wqk", [P, KD, 2, K])
        wv = sb("la_wv", [P, KD, K])
        wo = sb("la_wo", [K, D])
        keep = sb("la_keep", [P, P])
        y_row = sb("la_y_row", [P, TB, D])
        yt = sb("la_yt", [P, KD, S])
        below = sb("la_below", [K, 2, S])
        expd = sb("la_expd", [K, 2, S])
        qk = sb("la_qk", [K, 2, S])
        v1 = sb("la_v1", [P, TB, K + 1])
        at = sb("la_at", [P, TB, S])
        den = sb("la_den", [P, TB])
        o = sb("la_o", [P, TB, K])
        ot = sb("la_ot", [K, S])

        weights_in = sem("la_weights_in")
        row_copied = sem("la_row_copied")
        row_turned = sem("la_row_turned")
        yt_ready = sem("la_yt_ready")
        projected = sem("la_projected")
        below_ready = sem("la_below_ready")
        exp_ready = sem("la_exp_ready")
        qk_ready = sem("la_qk_ready")
        v1_ready = sem("la_v1_ready")
        ones_set = sem("la_ones_set")
        scored = sem("la_scored")
        at_ready = sem("la_at_ready")
        summed = sem("la_summed")
        den_steps = sem("la_den_steps")
        o_ready = sem("la_o_ready")
        o_turned = sem("la_o_turned")
        ot_ready = sem("la_ot_ready")
        out_done = sem("la_out_done")
        x_added = sem("la_x_added")
        block = ctx.enter_context(nc.Block())
        at_bank = [(5, 0), (6, 0), (7, 0), (6, 384)]

        @block.sync
        def _(sp):
            for n, w in enumerate((wq_t, wk_t)):
                sp.dma_start(wqk[:, :, n, :], w.rearrange("(k p) m -> p k m", p=P)).then_inc(weights_in, 16)
            sp.dma_start(wv[:], wv_t.rearrange("(k p) m -> p k m", p=P)).then_inc(weights_in, 16)
            sp.dma_start(wo[:], wo_t).then_inc(weights_in, 16)
            sp.dma_start(keep[:], keep_upper).then_inc(weights_in, 16)

        @block.gpsimd
        def _(gp):
            nc.gpsimd.memset(v1[:, :, K:K + 1], 1.0).then_inc(ones_set, 1)
            with gp.Fori(0, B) as b:
                gp.wait_ge(row_turned, 1 + b)
                nc.gpsimd.tensor_copy(y_row[:], Y[:, bass.ds(TB * b, TB), :]).then_inc(row_copied, 1)

        @block.tensor
        def _(pe):
            pe.sem_inc(row_turned, 1)
            pe.sem_inc(projected, 1)
            pe.wait_ge(weights_in, 80)
            pe.wait_ge(ones_set, 1)
            with pe.Fori(0, B) as b:
                pe.wait_ge(row_copied, b + 1)
                for k in range(KD):
                    for i in range(TB):
                        ins = nc.tensor.transpose(bank[k][:, P * i:P * i + P], y_row[:, i, P * k:P * k + P], ident[:])
                ins.then_inc(row_turned, 1)
                pe.wait_ge(yt_ready, b + 1)
                for n in range(2):
                    for k in range(KD):
                        nc.tensor.matmul(bank[2 + n][0:K, :], wqk[:, k, n, :], yt[:, k, :], start=k == 0, stop=k == KD - 1)
                for i in range(TB):
                    for k in range(KD):
                        ins = nc.tensor.matmul(bank[4][:, K * i:K * i + K], yt[:, k, P * i:P * i + P], wv[:, k, :],
                                               start=k == 0, stop=k == KD - 1)
                ins.then_inc(projected, 1)
                pe.wait_ge(qk_ready, b + 1)
                pe.wait_ge(x_added, b + 1)
                for c, (n, at_col) in enumerate(at_bank):
                    w = S - P * c
                    ins = nc.tensor.matmul(bank[n][:, at_col:at_col + w], qk[:, 1, P * c:P * c + P], qk[:, 0, P * c:S],
                                           start=True, stop=True)
                ins.then_inc(scored, 1)
                pe.wait_ge(at_ready, b + 1)
                pe.wait_ge(v1_ready, b + 1)
                for r in range(TB):
                    for c in range(r + 1):
                        ins = nc.tensor.matmul(bank[2][:, (K + 1) * r:(K + 1) * (r + 1)], at[:, c, P * r:P * r + P], v1[:, c, :],
                                               start=c == 0, stop=c == r)
                ins.then_inc(summed, 1)
                wait_apart(pe, o_ready, b + 1)
                for r in range(TB):
                    ins = nc.tensor.transpose(bank[3][0:K, P * r:P * r + P], o[:, r, :], ident[:])
                ins.then_inc(o_turned, 1)
                pe.wait_ge(ot_ready, b + 1)
                for r in range(TB):
                    ins = nc.tensor.matmul(bank[5 + r // 2][:, D * (r % 2):D * (r % 2) + D], ot[:, P * r:P * r + P], wo[:],
                                           start=True, stop=True)
                ins.then_inc(out_done, 1)

        @block.scalar
        def _(ac):
            with ac.Fori(0, B) as b:
                ac.wait_ge(row_turned, 2 + b)
                ac.wait_ge(projected, 1 + b)
                for k in range(KD):
                    ins = nc.scalar.copy(yt[:, k, :], bank[k][:])
                ins.then_inc(yt_ready, 1)
                ac.wait_ge(below_ready, b + 1)
                nc.scalar.activation(expd[:], below[:], ACT.Exp).then_inc(exp_ready, 1)
                nc.scalar.copy(v1[:, :, 0:K], bank[4][:, 0:TB * K].rearrange("p (i m) -> p i m", i=TB)).then_inc(v1_ready, 1)
                ac.wait_ge(o_turned, b + 1)
                nc.scalar.copy(ot[:], bank[3][0:K, :]).then_inc(ot_ready, 1)

        @block.vector
        def _(dv):
            dv.sem_inc(x_added, 1)
            dv.wait_ge(weights_in, 80)
            with dv.Fori(0, B) as b:
                dv.wait_ge(projected, 2 + b)
                for n in range(2):
                    ins = nc.vector.tensor_scalar(below[:, n, :], bank[2 + n][0:K, :], 0.0, None, ALU.min)
                ins.then_inc(below_ready, 1)
                dv.wait_ge(exp_ready, b + 1)
                for n in range(2):
                    ins = nc.vector.scalar_tensor_tensor(qk[:, n, :], bank[2 + n][0:K, :], 0.0, expd[:, n, :], ALU.max, ALU.add)
                ins.then_inc(qk_ready, 1)
                dv.wait_ge(scored, b + 1)
                for c, (n, col) in enumerate(at_bank):
                    lo = P * c
                    ins = nc.vector.tensor_tensor(at[:, c, lo:lo + P], bank[n][:, col:col + P], keep[:], ALU.mult)
                    if c < TB - 1:
                        ins = nc.vector.tensor_copy(at[:, c, lo + P:S], bank[n][:, col + P:col + S - lo])
                ins.then_inc(at_ready, 1)
                dv.wait_ge(summed, b + 1)
                sums = bank[2][:, 0:(K + 1) * TB].rearrange("p (r m) -> p r m", r=TB)
                st = Steps(dv, den_steps, 2 * b, 2)
                st.after(nc.vector.tensor_scalar(den[:], sums[:, :, K], 1e-6, None, ALU.add))
                st.after(nc.vector.reciprocal(den[:], den[:]))
                st.close()
                for r in range(TB):
                    ins = nc.vector.tensor_scalar(o[:, r, :], sums[:, r, 0:K], den[:, r:r + 1], None, ALU.mult)
                ins.then_inc(o_ready, 1)
                dv.wait_ge(out_done, b + 1)
                for r in range(TB):
                    x = X[:, TB * b + r, :]
                    ins = nc.vector.tensor_tensor(x, x, bank[5 + r // 2][:, D * (r % 2):D * (r % 2) + D], ALU.add)
                ins.then_inc(x_added, 1)


def attention_inputs(nc, sem, pre, bank, X, ident, w, q_all, kt_all, v_all, null_neg, null_v):
    cosine = "q_scale" in w
    with ExitStack() as ctx:
        def sb(name, shape, dt=F32):
            return ctx.enter_context(nc.sbuf_tensor(pre + name, shape, dt))

        wq = sb("wq", [P, KD, H * DH])
        wkv = sb("wkv", [P, KD, 2 * DH])
        g_norm = sb("g_norm", [P, KD])
        null_k = sb("null_k", [P, DH])
        null_w = sb("null_w", [P, KD, H])
        null_b = sb("null_b", [P, H])
        null_t = sb("null_t", [P, TB, H])
        null_p = sb("null_p", [P, KD, H, DH])
        mask_words = sb("mask_words", [P, B * S // 4], I32)
        mask8 = mask_words[:].bitcast(U8)
        scales = sb("scales", [P, 2, DH])
        kcol = sb("kcol", [DH, 3])
        one = sb("one", [P, 3])
        xn = sb("xn", [P, TB, D])
        xnt = sb("xnt", [P, KD, S])
        stats = sb("stats", [P, TB, 6])
        mv = sb("mv", [P, TB, 2])
        var = sb("var", [P, TB])
        sd = sb("sd", [P, TB])
        rstd = sb("rstd", [P, TB])
        squares = sb("squares", [P, 2, 512])
        k_raw = sb("k_raw", [P, TB, DH])
        k_sq = sb("k_sq", [P, TB, DH])
        k_n = sb("k_n", [P, TB, DH])
        ss = sb("ss", [P, TB * (H + 1)])
        norm = sb("norm", [P, TB * (H + 1)])
        rinv = sb("rinv", [P, TB * (H + 1)])

        params_in = sem(pre + "params_in")
        prologue = sem(pre + "prologue")
        null_ss = sem(pre + "null_ss")
        null_sd = sem(pre + "null_sd")
        stepped = sem(pre + "stepped")
        var_ready = sem(pre + "var_ready")
        sd_ready = sem(pre + "sd_ready")
        xn_ready = sem(pre + "xn_ready")
        xn_turned = sem(pre + "xn_turned")
        xnt_ready = sem(pre + "xnt_ready")
        kv_done = sem(pre + "kv_done")
        k_copied = sem(pre + "k_copied")
        q_done = sem(pre + "q_done")
        q_copied = sem(pre + "q_copied")
        q_summed = sem(pre + "q_summed")
        ss_ready = sem(pre + "ss_ready")
        norm_ready = sem(pre + "norm_ready")
        rinv_ready = sem(pre + "rinv_ready")
        kn_ready = sem(pre + "kn_ready")
        k_turned = sem(pre + "k_turned")
        kt_ready = sem(pre + "kt_ready")
        null_done = sem(pre + "null_done")
        q_scaled = sem(pre + "q_scaled")
        block = ctx.enter_context(nc.Block())
        n_params = 8 + 4 * cosine
        PRO = 11 if cosine else 5
        LOOP = 5 if cosine else 4
        NQ = 2 * TB
        AHEAD = 4

        @block.sync
        def _(sp):
            sp.dma_start(g_norm[:], columns(w["g_norm"], KD)).then_inc(params_in, 16)
            sp.dma_start(wkv[:], w["Wkv"].rearrange("(k p) n -> p k n", p=P)).then_inc(params_in, 16)
            for k in range(KD):
                sp.dma_start(wq[:, k, :], w["Wq"][P * k:P * k + P, :]).then_inc(params_in, 16)
            sp.dma_start(null_k[:], rows(w["cond"][0])).then_inc(params_in, 16)
            for half in range(2):
                sp.dma_start(null_v[DH * half:DH * half + DH, :], w["cond"][1].rearrange("(d a) -> d a", a=1)).then_inc(params_in, 16)
            sp.dma_start(null_b[:], rows(w["null_attn_bias"])).then_inc(params_in, 16)
            sp.dma_start(mask_words[DH:DH + 1, :], w["mask"].rearrange("b s -> (b s)").rearrange("(a n) -> a n", a=1)).then_inc(params_in, 16)
            if cosine:
                for n, name in enumerate(("q_scale", "k_scale")):
                    sp.dma_start(scales[:, n, :], rows(w[name])).then_inc(params_in, 16)
                    sp.dma_start(kcol[:, n:n + 1], w[name].rearrange("(d a) -> d a", a=1)).then_inc(params_in, 16)

        @block.gpsimd
        def _(gp):
            if cosine:
                gp.sem_inc(q_scaled, 1)
                with gp.Fori(0, B) as b:
                    gp.wait_ge(rinv_ready, b + 1)
                    for i in range(TB):
                        q = q_all[:, TB * b + i]
                        r = rinv[:, H * i:H * i + H].unsqueeze(2).broadcast_to([P, H, DH])
                        ins = nc.gpsimd.tensor_tensor(q, q, r, ALU.mult)
                    ins.then_inc(q_scaled, 1)

        @block.tensor
        def _(pe):
            pe.wait_ge(params_in, 16 * (n_params + 1))
            pe.wait_ge(prologue, PRO)
            with pe.Fori(0, B) as b:
                pe.wait_ge(xn_ready, b + 1)
                for k in range(KD):
                    for i in range(TB):
                        ins = nc.tensor.transpose(bank[k][:, P * i:P * i + P], xn[:, i, P * k:P * k + P], ident[:])
                ins.then_inc(xn_turned, 1)
                pe.wait_ge(xnt_ready, b + 1)
                for i in range(TB):
                    for k in range(KD):
                        nc.tensor.matmul(bank[2][:, P * i:P * i + P], xnt[:, k, P * i:P * i + P], wkv[:, k, :],
                                         start=k == 0, stop=k == KD - 1)
                pe.wait_ge(null_done, b + 1)
                for i in range(TB):
                    for k in range(KD):
                        ins = nc.tensor.matmul(bank[3][:, H * i:H * i + H], xnt[:, k, P * i:P * i + P], null_w[:, k, :],
                                               start=k == 0, stop=k == KD - 1)
                ins.then_inc(kv_done, 1)
                for m in range(NQ):
                    i, half = divmod(m, 2)
                    pe.wait_ge(q_copied, NQ * b + m + 1)
                    for k in range(KD):
                        ins = nc.tensor.matmul(bank[4 + m % 4][:], xnt[:, k, P * i:P * i + P],
                                               wq[:, k, 512 * half:512 * half + 512], start=k == 0, stop=k == KD - 1)
                    ins.then_inc(q_done, 1)
                wait_apart(pe, kn_ready, b + 1)
                for i in range(TB):
                    ins = nc.tensor.transpose(bank[2][0:DH, P * i:P * i + P], k_n[:, i, :], ident[:])
                ins.then_inc(k_turned, 1)
                pe.wait_ge(kt_ready, b + 1)

        @block.scalar
        def _(ac):
            ac.sem_inc(q_copied, AHEAD)
            if cosine:
                ac.wait_ge(null_ss, 1)
                nc.scalar.activation(one[:, 2:3], one[:, 1:2], ACT.Sqrt).then_inc(null_sd, 1)
            ac.wait_ge(prologue, PRO)
            with ac.Fori(0, B) as b:
                ac.wait_ge(var_ready, b + 1)
                nc.scalar.activation(sd[:], var[:], ACT.Sqrt).then_inc(sd_ready, 1)
                ac.wait_ge(xn_turned, b + 1)
                for k in range(KD):
                    ins = nc.scalar.activation(xnt[:, k, :], bank[k][:], ACT.Copy, scale=g_norm[:, k:k + 1])
                ins.then_inc(xnt_ready, 1)
                ac.wait_ge(kv_done, b + 1)
                kv = bank[2][:].rearrange("p (i n) -> p i n", i=TB)
                nc.scalar.copy(k_raw[:], kv[:, :, 0:DH]).then_inc(k_copied, 1)
                nc.scalar.copy(v_all[:, bass.ds(TB * b, TB), :], kv[:, :, DH:2 * DH])
                for m in range(NQ):
                    i, half = divmod(m, 2)
                    ac.wait_ge(q_done, NQ * b + m + 1)
                    if cosine:
                        ac.wait_ge(q_summed, NQ * b + m + 1)
                        nc.scalar.activation(squares[:, m % 2, :], bank[4 + m % 4][:], ACT.Square)
                    nc.scalar.copy(q_all[:, TB * b + i, 8 * half:8 * half + 8, :],
                                   bank[4 + m % 4][:].rearrange("p (h d) -> p h d", d=DH)).then_inc(q_copied, 1)
                if cosine:
                    ac.wait_ge(ss_ready, b + 1)
                    nc.scalar.activation(norm[:], ss[:], ACT.Sqrt).then_inc(norm_ready, 1)
                ac.wait_ge(k_turned, b + 1)
                nc.scalar.activation(kt_all[0:DH, b, :], bank[2][0:DH, :], ACT.Copy, scale=kcol[:, 2:3]).then_inc(kt_ready, 1)

        @block.vector
        def _(dv):
            pro = Steps(dv, prologue)
            dv.sem_inc(null_done, 1)
            dv.sem_inc(q_summed, 2)
            dv.wait_ge(params_in, 16 * (n_params + 1))
            mask = kt_all[DH:DH + 1, :, :].rearrange("p b s -> p (b s)")
            pro.after(nc.vector.tensor_scalar(mask, mask8[DH:DH + 1, :], 1.0, -MASKED, ALU.subtract, ALU.mult))
            if cosine:
                pro.after(nc.vector.tensor_tensor_reduce(out=k_sq[:, 0, :], in0=null_k[:], in1=null_k[:], scale=1.0, scalar=0.0,
                                                         op0=ALU.mult, op1=ALU.add, accum_out=one[:, 0:1]))
                nc.vector.tensor_scalar(one[:, 1:2], one[:, 0:1], 1e-24, None, ALU.max).then_inc(null_ss, 1)
                dv.wait_ge(null_sd, 1)
                pro.after(nc.vector.reciprocal(one[:, 0:1], one[:, 2:3]))
                pro.after(nc.vector.tensor_scalar(null_k[:], null_k[:], one[:, 0:1], None, ALU.mult))
                pro.after(nc.vector.tensor_scalar(null_k[:], null_k[:], 8.0, None, ALU.mult))
                pro.after(nc.vector.tensor_tensor(null_k[:], null_k[:], scales[:, 0, :], ALU.mult))
                pro.after(nc.vector.tensor_tensor(null_k[:], null_k[:], scales[:, 1, :], ALU.mult))
                pro.after(nc.vector.tensor_tensor(kcol[:, 2:3], kcol[:, 0:1], kcol[:, 1:2], ALU.mult))
                pro.after(nc.vector.tensor_scalar(kcol[:, 2:3], kcol[:, 2:3], 8.0, None, ALU.mult))
            else:
                pro.after(nc.vector.tensor_scalar(null_k[:], null_k[:], DH ** -0.5, None, ALU.mult))
                pro.after(nc.vector.memset(kcol[:, 2:3], DH ** -0.5))
            for k in range(KD):
                q4 = wq[:, k, :].rearrange("p (h d) -> p h d", h=H)
                ins = nc.vector.tensor_tensor(null_p[:, k], q4, null_k[:].unsqueeze(1).broadcast_to([P, H, DH]), ALU.mult)
            pro.after(ins)
            pro.after(nc.vector.tensor_reduce(null_w[:], null_p[:], AX.X, ALU.add))
            assert pro.n == PRO, pro.n
            with dv.Fori(0, B) as b:
                st = Steps(dv, stepped, LOOP * b, LOOP)
                for i in range(TB):
                    ins = nc.vector.bn_stats(stats[:, i, :], X[:, TB * b + i, :])
                st.after(ins, apart=True)
                for i in range(TB):
                    ins = nc.vector.bn_aggr(mv[:, i, :], stats[:, i, :])
                st.after(ins)
                nc.vector.tensor_scalar(var[:], mv[:, :, 1], EPS, None, ALU.add).then_inc(var_ready, 1)
                dv.wait_ge(sd_ready, b + 1)
                st.after(nc.vector.reciprocal(rstd[:], sd[:]))
                for i in range(TB):
                    ins = nc.vector.tensor_scalar(xn[:, i, :], X[:, TB * b + i, :], mv[:, i, 0:1], rstd[:, i:i + 1],
                                                  ALU.subtract, ALU.mult)
                ins.then_inc(xn_ready, 1)
                dv.wait_ge(k_copied, b + 1)
                null = bank[3][:, 0:TB * H].rearrange("p (i h) -> p i h", i=TB)
                if cosine:
                    st.after(nc.vector.tensor_tensor(k_sq[:], k_raw[:], k_raw[:], ALU.mult))
                    nc.vector.tensor_reduce(ss[:, TB * H:], k_sq[:], AX.X, ALU.add)
                    for m in range(NQ):
                        dv.wait_ge(q_copied, AHEAD + NQ * b + m + 1)
                        nc.vector.tensor_reduce(ss[:, 8 * m:8 * m + 8], squares[:, m % 2, :].rearrange("p (h d) -> p h d", d=DH),
                                                AX.X, ALU.add).then_inc(q_summed, 1)
                    dv.wait_ge(q_summed, 2 + NQ * b + NQ)
                    nc.vector.tensor_scalar(ss[:], ss[:], 1e-24, None, ALU.max).then_inc(ss_ready, 1)
                    dv.wait_ge(norm_ready, b + 1)
                    dv.wait_ge(q_scaled, b + 1)
                    nc.vector.reciprocal(rinv[:], norm[:]).then_inc(rinv_ready, 1)
                    dv.wait_ge(rinv_ready, b + 1)
                    nc.vector.tensor_tensor(k_n[:], k_raw[:], rinv[:, TB * H:].unsqueeze(2).broadcast_to([P, TB, DH]),
                                            ALU.mult).then_inc(kn_ready, 1)
                    dv.wait_ge(kv_done, b + 1)
                    st.after(nc.vector.tensor_tensor(null_t[:], null, rinv[:, 0:TB * H].rearrange("p (i h) -> p i h", i=TB), ALU.mult))
                else:
                    nc.vector.tensor_copy(k_n[:], k_raw[:]).then_inc(kn_ready, 1)
                    dv.wait_ge(kv_done, b + 1)
                    st.after(nc.vector.tensor_copy(null_t[:], null))
                nc.vector.scalar_tensor_tensor(null_neg[:, :, bass.ds(TB * b, TB)], null_t[:].rearrange("p i h -> p h i"), -1.0,
                                               null_b[:].unsqueeze(2).broadcast_to([P, H, TB]), ALU.mult,
                                               ALU.subtract).then_inc(null_done, 1)
                st.close()


def attention_core(nc, sem, pre, bank, ident, w, q_src, kt_all, v_all, null_neg, neg_max, row_sum, o_all):
    rotary = w["bias"] == "none"
    dh = DR if rotary else DH
    kd = dh if rotary else DH + 1
    HU = B * TB
    HT = 2 * HU
    TURNS = H // 2
    with ExitStack() as ctx:
        def sb(name, shape, dt=F32):
            return ctx.enter_context(nc.sbuf_tensor(pre + name, shape, dt))

        full = w["bias"] == "full"
        first_col = [0, P, 3 * P, 6 * P]
        bias = [sb(f"bias{j}", [P, 10 * P if full else S]) for j in range(2)]
        q_row = [sb(f"q_row{j}", [P, TB, 2, dh] if rotary else [P, TB, dh]) for j in range(2)]
        qt = [sb(f"qt{j}", [kd, 2 if rotary else 1, S]) for j in range(2)]
        logit_neg = sb("logit_neg", [P, 2, S])
        prob = sb("prob", [P, 2, S])
        prob_t = sb("prob_t", [P, 2, S])
        null_h = [sb(f"null_h{j}", [P, HU]) for j in range(2)]
        max_h = [sb(f"max_h{j}", [P, HU]) for j in range(2)]
        sum_h = [sb(f"sum_h{j}", [P, HU]) for j in range(2)]

        bias_in = [sem(pre + f"bias_in{j}") for j in range(2)]
        head_ready = sem(pre + "head_ready")
        bias_filled = sem(pre + "bias_filled")
        q_staged = sem(pre + "q_staged")
        q_turned = sem(pre + "q_turned")
        qt_ready = sem(pre + "qt_ready")
        scored = sem(pre + "scored")
        biased = sem(pre + "biased")
        exped = sem(pre + "exped")
        turned = sem(pre + "turned")
        pt_ready = sem(pre + "pt_ready")
        pv_done = sem(pre + "pv_done")
        o_copied = sem(pre + "o_copied")
        sums_kept = sem(pre + "sums_kept")
        block = ctx.enter_context(nc.Block())

        def turns(eng, body):
            body(0, True, False)
            with eng.Fori(1, TURNS - 1) as t:
                body(t, False, False)
            body(TURNS - 1, False, True)

        def bias_of(j, r):
            if full:
                return bias[j][:, first_col[r]:first_col[r] + P * (r + 1)]
            return bias[j][:, P * (TB - 1 - r):S]

        def diagonals(j):
            if full:
                return [bias[j][:, first_col[r] + P * r:first_col[r] + P * (r + 1)] for r in range(TB)]
            return [bias[j][:, P * (TB - 1):S]]

        @block.sync
        def _(sp):
            def load_full(t, first, last):
                for j in range(2):
                    if not first:
                        sp.wait_ge(biased, HT * t - HT + HU * (j + 1))
                    for r in range(TB):
                        sp.dma_start(bias_of(j, r), w["full"][2 * t + j, P * r:P * r + P, 0:P * (r + 1)]).then_inc(bias_in[j], 16)

            if full:
                turns(sp, load_full)
            elif not rotary:
                for h in range(H):
                    if h >= 2:
                        sp.wait_ge(biased, HU * (h - 1))
                    src = w["copies"]
                    skew = bass.AP(tensor=src.tensor, offset=src.offset + P * NPOS * h + P - 1, ap=[[NPOS - 1, P], [1, S]])
                    sp.dma_start(bias[h % 2][:], skew).then_inc(bias_in[h % 2], 16)

        @block.gpsimd
        def _(gp):
            fills = len(diagonals(0))
            n_in = 16 * (TB if full else 1)

            def stage(t, first, blk):
                j, b = divmod(blk, B)
                if not (first and blk < 2):
                    gp.wait_ge(q_turned, 2 * B * t + blk - 1)
                h = 2 * t + j
                if rotary:
                    src = q_src[:, TB * b:TB * b + TB, :, h, :]
                else:
                    src = q_src[:, TB * b:TB * b + TB, h, :]
                nc.gpsimd.tensor_copy(q_row[blk % 2][:], src).then_inc(q_staged, 1)

            def keep_sums(t, j):
                h = 2 * t + j
                gp.wait_ge(exped, HT * t + HU * (j + 1))
                nc.gpsimd.tensor_copy(neg_max[:, h, :], max_h[j][:])
                nc.gpsimd.tensor_copy(row_sum[:, h, :], sum_h[j][:]).then_inc(sums_kept, 1)

            def head(t, first, last):
                for j in range(2):
                    if not first:
                        gp.wait_ge(biased, HT * t - HT + HU * (j + 1))
                    if not rotary:
                        nc.gpsimd.tensor_copy(null_h[j][:], null_neg[:, 2 * t + j, :]).then_inc(head_ready, 1)
                        wait_apart(gp, bias_in[j], n_in * t + n_in)
                        for d in diagonals(j):
                            nc.gpsimd.affine_select(out=d, in_=d, compare_op=ALU.is_ge, fill=MASKED, base=0,
                                                    pattern=[[-1, P]], channel_multiplier=1).then_inc(head_ready, 1)
                    stage(t, first, B * j)
                    stage(t, first, B * j + 1)
                    if j == 1:
                        keep_sums(t, 0)
                    elif not first:
                        keep_sums(t - 1, 1)
                    stage(t, first, B * j + 2)
                    stage(t, first, B * j + 3)
                if last:
                    keep_sums(t, 1)

            if rotary:
                for j in range(2):
                    nc.gpsimd.memset(bias[j][:], 0.0).then_inc(bias_filled, 1)
                gp.wait_ge(bias_filled, 2)
                for j in range(2):
                    for d in diagonals(j):
                        nc.gpsimd.affine_select(out=d, in_=d, compare_op=ALU.is_ge, fill=MASKED, base=0,
                                                pattern=[[-1, P]], channel_multiplier=1).then_inc(head_ready, 1)
            else:
                for j in range(2):
                    nc.gpsimd.memset(qt[j][DH:kd, 0, :], 1.0).then_inc(bias_filled, 1)
                gp.wait_ge(bias_filled, 2)
            turns(gp, head)

        @block.tensor
        def _(pe):
            def turn_q(t, first, blk):
                g = 2 * B * t + blk
                wait_apart(pe, q_staged, g + 1)
                if not (first and blk == 0):
                    wait_apart(pe, qt_ready, g)
                if rotary:
                    for s in range(2):
                        for i in range(TB):
                            ins = nc.tensor.transpose(bank[6 + s][0:dh, P * i:P * i + P], q_row[blk % 2][:, i, s, :], ident[:])
                else:
                    for i in range(TB):
                        ins = nc.tensor.transpose(bank[6][0:dh, P * i:P * i + P], q_row[blk % 2][:, i, :], ident[:])
                ins.then_inc(q_turned, 1)

            def score(t, u):
                blk, r = divmod(u, TB)
                b = blk % B
                if r == 0:
                    pe.wait_ge(qt_ready, 2 * B * t + blk + 1)
                q = qt[blk % 2]
                keys = q[0:kd, 1, 0:P * (r + 1)] if rotary else kt_all[0:kd, b, 0:P * (r + 1)]
                nc.tensor.matmul(bank[u % 2][:, 0:P * (r + 1)], q[0:kd, 0, P * r:P * r + P], keys,
                                 start=True, stop=True).then_inc(scored, 1)

            def turn(t, first, last):
                for u in range(HT):
                    blk, r = divmod(u, TB)
                    b, j = blk % B, blk // B
                    if r == 0 and not (last and blk == 2 * B - 1):
                        nxt = blk + 1
                        turn_q(t, first, nxt) if nxt < 2 * B else turn_q(t + 1, False, 0)
                    pe.wait_ge(exped, HT * t + u + 1)
                    for c in range(r + 1):
                        ins = nc.tensor.transpose(bank[2 + u % 2][:, P * c:P * c + P], prob[:, u % 2, P * c:P * c + P], ident[:])
                    ins.then_inc(turned, 1)
                    if u + 2 < HT:
                        score(t, u + 2)
                    elif not last:
                        score(t + 1, u + 2 - HT)
                    pe.wait_ge(pt_ready, HT * t + u + 1)
                    if r == 0 and not (first and blk < 2):
                        pe.wait_ge(o_copied, 2 * B * t + blk - 1)
                    for c in range(r + 1):
                        v = v_all[:, TB * b + c, bass.ds(dh * (2 * t + j), dh)] if rotary else v_all[:, TB * b + c, :]
                        ins = nc.tensor.matmul(bank[4 + blk % 2][:, dh * r:dh * r + dh], prob_t[:, u % 2, P * c:P * c + P], v,
                                               start=c == 0, stop=c == r)
                    ins.then_inc(pv_done, 1)

            pe.wait_ge(bias_filled, 2)
            turn_q(0, True, 0)
            score(0, 0)
            score(0, 1)
            turns(pe, turn)

        @block.scalar
        def _(ac):
            def copy_qt(t, first, blk):
                g = 2 * B * t + blk
                ac.wait_ge(q_turned, g + 1)
                if not (first and blk < 2):
                    ac.wait_ge(scored, TB * (g - 1))
                for s in range(2 if rotary else 1):
                    ins = nc.scalar.copy(qt[blk % 2][0:dh, s, :], bank[6 + s][0:dh, :])
                ins.then_inc(qt_ready, 1)

            def exp(t, first, u):
                j, n = divmod(u, HU)
                ac.wait_ge(biased, HT * t + u + 1)
                if not (first and u < 2):
                    ac.wait_ge(turned, HT * t + u - 1)
                wd = P * (u % TB + 1)
                nc.scalar.activation(prob[:, u % 2, 0:wd], logit_neg[:, u % 2, 0:wd], ACT.Exp, bias=max_h[j][:, n:n + 1],
                                     scale=-1.0, accum_out=sum_h[j][:, n:n + 1]).then_inc(exped, 1)

            def copy_o(t, blk):
                j, b = divmod(blk, B)
                ac.wait_ge(pv_done, TB * (2 * B * t + blk + 1))
                nc.scalar.copy(o_all[:, TB * b:TB * b + TB, 2 * t + j, :],
                               bank[4 + blk % 2][:, 0:TB * dh].rearrange("p (i d) -> p i d", i=TB)).then_inc(o_copied, 1)

            def turn(t, first, last):
                for u in range(HT):
                    blk, r = divmod(u, TB)
                    if u + 1 < HT:
                        exp(t, first, u + 1)
                    elif not last:
                        exp(t + 1, False, 0)
                    if r == 0 and not (last and blk == 2 * B - 1):
                        copy_qt(t, first, blk + 1) if blk + 1 < 2 * B else copy_qt(t + 1, False, 0)
                    if r == 1 and blk:
                        copy_o(t, blk - 1)
                    elif r == 1 and not first:
                        copy_o(t - 1, 2 * B - 1)
                if last:
                    copy_o(t, 2 * B - 1)

            copy_qt(0, True, 0)
            exp(0, True, 0)
            turns(ac, turn)

        @block.vector
        def _(dv):
            per_head = 1 if rotary else 1 + len(diagonals(0))

            def add_bias(t, first, u):
                j, n = divmod(u, HU)
                if n == 0:
                    if not rotary:
                        dv.wait_ge(head_ready, per_head * (2 * t + j + 1))
                    elif first:
                        dv.wait_ge(head_ready, 2)
                    if not first:
                        dv.wait_ge(sums_kept, 2 * t + j - 1)
                wait_apart(dv, scored, HT * t + u + 1)
                r = n % TB
                wd = P * (r + 1)
                nc.vector.tensor_tensor_reduce(out=logit_neg[:, u % 2, 0:wd], in0=bank[u % 2][:, 0:wd], in1=bias_of(j, r),
                                               scale=-(dh ** -0.5) if rotary else -1.0,
                                               scalar=-MASKED if rotary else null_h[j][:, n:n + 1],
                                               op0=ALU.add, op1=ALU.min, accum_out=max_h[j][:, n:n + 1]).then_inc(biased, 1)

            def copy_pt(t, first, u):
                dv.wait_ge(turned, HT * t + u + 1)
                if not (first and u < 2):
                    dv.wait_ge(pv_done, HT * t + u - 1)
                wd = P * (u % TB + 1)
                nc.vector.tensor_copy(prob_t[:, u % 2, 0:wd], bank[2 + u % 2][:, 0:wd]).then_inc(pt_ready, 1)

            def turn(t, first, last):
                for u in range(HT):
                    if u + 1 < HT:
                        add_bias(t, first, u + 1)
                    elif not last:
                        add_bias(t + 1, False, 0)
                    copy_pt(t, first, u)

            add_bias(0, True, 0)
            turns(dv, turn)


def attention_output(nc, sem, pre, bank, Y, ident, w, o_all, null_neg, null_v, neg_max, row_sum):
    with ExitStack() as ctx:
        def sb(name, shape, dt=F32):
            return ctx.enter_context(nc.sbuf_tensor(pre + name, shape, dt))

        wout = sb("wout", [P, H * DH // P, D])
        g_out = sb("g_out", [P, D])
        null_p = sb("null_p", [P, H, NT])
        rinv = sb("rinv", [P, H, NT])
        spread = sb("spread", [P, H // 2, H])
        null_o = sb("null_o", [H, D])
        os = sb("os", [P, 2, H * DH])
        ps = sb("ps", [P, 2, H])
        ot = sb("ot", [P, 2, H * DH])
        pt = sb("pt", [H, 2, P])
        stats = sb("stats", [P, TB, 6])
        mv = sb("mv", [P, TB, 2])
        var = sb("var", [P, TB])
        sd = sb("sd", [P, TB])
        rstd = sb("rstd", [P, TB])
        yn = sb("yn", [P, TB, D])

        params_in = sem(pre + "params_in")
        pre_steps = sem(pre + "pre_steps")
        null_ready = sem(pre + "null_ready")
        null_exped = sem(pre + "null_exped")
        null_o_done = sem(pre + "null_o_done")
        null_o_ready = sem(pre + "null_o_ready")
        scaled = sem(pre + "scaled")
        turned = sem(pre + "turned")
        ot_ready = sem(pre + "ot_ready")
        projected = sem(pre + "projected")
        stepped = sem(pre + "stepped")
        var_ready = sem(pre + "var_ready")
        sd_ready = sem(pre + "sd_ready")
        y_done = sem(pre + "y_done")
        block = ctx.enter_context(nc.Block())
        NC = H * DH // P

        @block.sync
        def _(sp):
            for half in range(2):
                sp.dma_start(wout[:, 4 * half:4 * half + 4, :],
                             w["Wout"].rearrange("(c p) n -> p c n", p=P)[:, 4 * half:4 * half + 4, :]).then_inc(params_in, 16)
            sp.dma_start(g_out[:], rows(w["g_out"])).then_inc(params_in, 16)

        @block.tensor
        def _(pe):
            pe.sem_inc(turned, 2)
            pe.wait_ge(params_in, 48)
            pe.wait_ge(null_ready, 3)
            for c in range(NC):
                ins = nc.tensor.matmul(bank[3][0:H, 0:D], spread[:, c, :], wout[:, c, :], start=c == 0, stop=c == NC - 1)
            ins.then_inc(null_o_done, 1)
            pe.wait_ge(null_o_ready, 1)
            with pe.Fori(0, B) as b:
                def project(i):
                    n = TB * b + i
                    pe.wait_ge(ot_ready, n + 1)
                    for c in range(NC):
                        nc.tensor.matmul(bank[4 + i][:, 0:D], ot[:, i % 2, P * c:P * c + P], wout[:, c, :], start=c == 0, stop=False)
                    nc.tensor.matmul(bank[4 + i][:, 0:D], pt[:, i % 2, :], null_o[:], start=False, stop=True).then_inc(projected, 1)

                for i in range(TB):
                    n = TB * b + i
                    wait_apart(pe, scaled, 2 + n + 1)
                    if i == 0:
                        wait_apart(pe, y_done, b + 1)
                    else:
                        wait_apart(pe, ot_ready, n)
                    for c in range(NC):
                        nc.tensor.transpose(bank[c // 4][:, P * (c % 4):P * (c % 4) + P], os[:, i % 2, P * c:P * c + P], ident[:])
                    nc.tensor.transpose(bank[2][0:H, 0:P], ps[:, i % 2, :], ident[:]).then_inc(turned, 1)
                    if i:
                        project(i - 1)
                project(TB - 1)

        @block.scalar
        def _(ac):
            ac.wait_ge(null_ready, 1)
            nc.scalar.activation(null_p[:], null_p[:], ACT.Exp).then_inc(null_exped, 1)
            ac.wait_ge(null_o_done, 1)
            nc.scalar.copy(null_o[:], bank[3][0:H, 0:D]).then_inc(null_o_ready, 1)
            ac.sem_inc(sd_ready, 1)
            with ac.Fori(0, B) as b:
                for i in range(TB):
                    n = TB * b + i
                    ac.wait_ge(turned, 2 + n + 1)
                    if i >= 2:
                        ac.wait_ge(projected, n - 1)
                    for c in range(2):
                        nc.scalar.copy(ot[:, i % 2, 512 * c:512 * c + 512], bank[c][:])
                    nc.scalar.copy(pt[:, i % 2, :], bank[2][0:H, 0:P]).then_inc(ot_ready, 1)
                ac.wait_ge(var_ready, b + 1)
                nc.scalar.activation(sd[:], var[:], ACT.Sqrt).then_inc(sd_ready, 1)

        @block.vector
        def _(dv):
            st = Steps(dv, pre_steps)
            dv.sem_inc(scaled, 2)
            dv.sem_inc(y_done, 1)
            nc.vector.tensor_tensor(null_p[:], neg_max[:], null_neg[:], ALU.subtract).then_inc(null_ready, 1)
            st.after(nc.vector.memset(spread[:], 0.0))
            for half in range(2):
                dst = spread[DH * half:DH * half + DH].rearrange("p c h -> p (c h)")[:, half::H + 2]
                nc.vector.tensor_scalar(dst, dst, null_v[DH * half:DH * half + DH, :], None, ALU.add).then_inc(null_ready, 1)
            dv.wait_ge(null_exped, 1)
            st.after(nc.vector.tensor_tensor(rinv[:], row_sum[:], null_p[:], ALU.add))
            st.after(nc.vector.reciprocal(rinv[:], rinv[:]))
            st.after(nc.vector.tensor_tensor(null_p[:], null_p[:], rinv[:], ALU.mult))
            dv.wait_ge(params_in, 48)
            with dv.Fori(0, B) as b:
                st = Steps(dv, stepped, 4 * b, 4)
                for i in range(TB):
                    n = TB * b + i
                    dv.wait_ge(turned, n + 1)
                    nc.vector.tensor_tensor(os[:, i % 2, :].rearrange("p (h d) -> p h d", h=H), o_all[:, n],
                                            rinv[:, :, bass.ds(n, 1)].broadcast_to([P, H, DH]), ALU.mult)
                    nc.vector.tensor_copy(ps[:, i % 2, :], null_p[:, :, n]).then_inc(scaled, 1)
                for i in range(TB):
                    dv.wait_ge(projected, TB * b + i + 1)
                    ins = nc.vector.bn_stats(stats[:, i, :], bank[4 + i][:, 0:D])
                st.after(ins, apart=True)
                for i in range(TB):
                    ins = nc.vector.bn_aggr(mv[:, i, :], stats[:, i, :])
                st.after(ins)
                nc.vector.tensor_scalar(var[:], mv[:, :, 1], EPS, None, ALU.add).then_inc(var_ready, 1)
                dv.wait_ge(sd_ready, 1 + b + 1)
                st.after(nc.vector.reciprocal(rstd[:], sd[:]))
                for i in range(TB):
                    ins = nc.vector.tensor_scalar(yn[:, i, :], bank[4 + i][:, 0:D], mv[:, i, 0:1], rstd[:, i:i + 1],
                                                  ALU.subtract, ALU.mult)
                st.after(ins)
                nc.vector.tensor_tensor(Y[:, bass.ds(TB * b, TB), :], yn[:], g_out[:].unsqueeze(1).broadcast_to([P, TB, D]),
                                        ALU.mult).then_inc(y_done, 1)
                st.close()


def null_key_attention(nc, sem, pre, bank, X, Y, ident, w):
    with ExitStack() as ctx:
        def sb(name, shape, dt=F32):
            return ctx.enter_context(nc.sbuf_tensor(pre + name, shape, dt))

        heads = sb("heads", [P, NT, H, DH])
        v_all = sb("v_all", [P, NT, DH])
        kt_all = sb("kt_all", [DH + 1, B, S])
        null_neg = sb("null_neg", [P, H, NT])
        null_v = sb("null_v", [P, 1])
        neg_max = sb("neg_max", [P, H, NT])
        row_sum = sb("row_sum", [P, H, NT])
        attention_inputs(nc, sem, pre + "i_", bank, X, ident, w, heads, kt_all, v_all, null_neg, null_v)
        attention_core(nc, sem, pre + "c_", bank, ident, w, heads, kt_all, v_all, null_neg, neg_max, row_sum, heads)
        attention_output(nc, sem, pre + "o_", bank, Y, ident, w, heads, null_neg, null_v, neg_max, row_sum)


def moe_ffn(nc, sem, bank, X, Y, ident, lane_d, norm_scale, gate_w, gate_b, w1_d, b1_d, w2_d, b2_d):
    E, J = E1, I1 // P
    LIMIT, ALPHA = 7.0, 1.702
    with ExitStack() as ctx:
        def sb(name, shape, dt=F32):
            return ctx.enter_context(nc.sbuf_tensor("mf_" + name, shape, dt))

        lane = sb("lane", [P, E])
        g_norm = sb("g_norm", [P, KD])
        gw = sb("gw", [P, KD, E])
        gb = sb("gb", [P, E])
        b1 = sb("b1", [P, E, 2, J])
        b2 = sb("b2", [E, D])
        tt = sb("tt", [P, KD, NT * P])
        weight = sb("weight", [P, NT, E])

        params_in = sem("mf_params_in")
        w_in = [sem(f"mf_w_in{j}") for j in range(2)]

        with ExitStack() as inner:
            def tmp(name, shape, dt=F32):
                return inner.enter_context(nc.sbuf_tensor("mf_" + name, shape, dt))

            square = tmp("square", [P, 2, D])
            ms = tmp("ms", [P, NT])
            sd = tmp("sd", [P, NT])
            rms = tmp("rms", [P, NT])
            tn = tmp("tn", [P, 2, TB, D])
            logits = tmp("logits", [P, NT, E])
            exp_in = tmp("exp_in", [P, NT, E])
            ex = tmp("ex", [P, NT, E])
            zsum = tmp("zsum", [P, NT])
            best = tmp("best", [P, NT, 8])
            best_at = tmp("best_at", [P, NT, 8], U32)
            picked = tmp("picked", [P, NT, 2])
            wt = tmp("wt", [E, NT, P])

            stepped = sem("mf_stepped")
            ms_ready, sd_ready = sem("mf_ms_ready"), sem("mf_sd_ready")
            tn_ready, tn_turned, tt_ready = sem("mf_tn_ready"), sem("mf_tn_turned"), sem("mf_tt_ready")
            logits_done = sem("mf_logits_done")
            exp_ready, exp_done = sem("mf_exp_ready"), sem("mf_exp_done")
            weight_ready, weight_turned, wt_ready = sem("mf_weight_ready"), sem("mf_weight_turned"), sem("mf_wt_ready")
            bias_done, x_added = sem("mf_bias_done"), sem("mf_x_added")
            block = inner.enter_context(nc.Block())

            @block.sync
            def _(sp):
                sp.dma_start(lane[:], lane_d).then_inc(params_in, 16)
                sp.dma_start(g_norm[:], columns(norm_scale, KD)).then_inc(params_in, 16)
                sp.dma_start(gw[:], gate_w.rearrange("(k p) e -> p k e", p=P)).then_inc(params_in, 16)
                sp.dma_start(gb[:], rows(gate_b)).then_inc(params_in, 16)
                sp.dma_start(b1[:], b1_d).then_inc(params_in, 16)
                sp.dma_start(b2[:], b2_d).then_inc(params_in, 16)

            @block.gpsimd
            def _(gp):
                nc.gpsimd.tensor_tensor(X[:], X[:], Y[:], ALU.add).then_inc(x_added, 1)

            @block.vector
            def _(dv):
                st = Steps(dv, stepped)
                for t in range(NT):
                    if t >= 2:
                        st.after(ins)
                    ins = nc.vector.tensor_tensor_reduce(out=square[:, t % 2, :], in0=Y[:, t, :], in1=Y[:, t, :], scale=1.0 / D,
                                                         scalar=EPS, op0=ALU.mult, op1=ALU.add, accum_out=ms[:, t:t + 1])
                ins.then_inc(ms_ready, 1)
                dv.wait_ge(sd_ready, 1)
                st.after(nc.vector.reciprocal(rms[:], sd[:]))
                dv.wait_ge(params_in, 96)
                for b in range(B):
                    if b >= 2:
                        dv.wait_ge(tn_turned, b - 1)
                    for i in range(TB):
                        t = TB * b + i
                        ins = nc.vector.tensor_scalar(tn[:, b % 2, i, :], Y[:, t, :], rms[:, t:t + 1], None, ALU.mult)
                    ins.then_inc(tn_ready, 1)
                dv.wait_ge(logits_done, 1)
                st.after(nc.vector.tensor_tensor(logits[:], bank[6][:, 0:NT * E].rearrange("p (t e) -> p t e", e=E),
                                                 gb[:].unsqueeze(1).broadcast_to([P, NT, E]), ALU.add))
                route(nc, dv, st, logits, ex, zsum, best, best_at, lane, picked, weight, False, exp_in, exp_ready, exp_done)
                nc.vector.tensor_copy(exp_in[:], weight[:]).then_inc(weight_ready, 1)
                dv.wait_ge(x_added, 1)
                for t in range(NT):
                    dv.wait_ge(bias_done, t // 8 + 1)
                    src = bank[(t // 2) % 4 + (0 if t < 8 else 4)][:, D * (t % 2):D * (t % 2) + D]
                    nc.vector.tensor_tensor(X[:, t, :], X[:, t, :], src, ALU.add)

            @block.scalar
            def _(ac):
                ac.wait_ge(ms_ready, 1)
                nc.scalar.activation(sd[:], ms[:], ACT.Sqrt).then_inc(sd_ready, 1)
                ac.wait_ge(params_in, 96)
                for b in range(B):
                    ac.wait_ge(tn_turned, b + 1)
                    for k in range(KD):
                        ins = nc.scalar.activation(tt[:, k, S * b:S * b + S], bank[2 * (b % 2) + k][:], ACT.Copy, scale=g_norm[:, k:k + 1])
                    ins.then_inc(tt_ready, 1)
                ac.wait_ge(exp_ready, 1)
                nc.scalar.activation(ex[:], exp_in[:], ACT.Exp).then_inc(exp_done, 1)
                for b in range(B):
                    ac.wait_ge(weight_turned, b + 1)
                    nc.scalar.copy(wt[:, TB * b:TB * b + TB, :], bank[b][0:E, :].rearrange("e (i p) -> e i p", i=TB)).then_inc(wt_ready, 1)

            @block.tensor
            def _(pe):
                pe.wait_ge(params_in, 96)
                for b in range(B):
                    pe.wait_ge(tn_ready, b + 1)
                    if b >= 2:
                        pe.wait_ge(tt_ready, b - 1)
                    for k in range(KD):
                        for i in range(TB):
                            ins = nc.tensor.transpose(bank[2 * (b % 2) + k][:, P * i:P * i + P], tn[:, b % 2, i, P * k:P * k + P], ident[:])
                    ins.then_inc(tn_turned, 1)
                pe.wait_ge(tt_ready, B)
                for t in range(NT):
                    for k in range(KD):
                        ins = nc.tensor.matmul(bank[6][:, E * t:E * t + E], tt[:, k, P * t:P * t + P], gw[:, k, :],
                                               start=k == 0, stop=k == KD - 1)
                ins.then_inc(logits_done, 1)
                pe.wait_ge(weight_ready, 1)
                for b in range(B):
                    for i in range(TB):
                        ins = nc.tensor.transpose(bank[b][0:E, P * i:P * i + P], exp_in[:, TB * b + i, :], ident[:])
                    ins.then_inc(weight_turned, 1)
                pe.wait_ge(wt_ready, B)
                for t in range(NT):
                    dst = bank[(t // 2) % 4 + (0 if t < 8 else 4)][:, D * (t % 2):D * (t % 2) + D]
                    ins = nc.tensor.matmul(dst, wt[:, t, :], b2[:], start=True, stop=True)
                    if t % 8 == 7:
                        ins.then_inc(bias_done, 1)

        w1 = [sb(f"w1{j}", [P, KD, 2, I1]) for j in range(2)]
        w2 = [sb(f"w2{j}", [P, J, D]) for j in range(2)]
        glu = sb("glu", [P, 2, S])
        sig = sb("sig", [P, 2, S])
        gated = sb("gated", [P, 2, S])
        low = sb("low", [P, 2, S])
        lin = sb("lin", [P, 2, S])
        hid = sb("hid", [P, 2, J, S])

        glu_done, lin_done = sem("mf_glu_done"), sem("mf_lin_done")
        glu_ready, low_ready, lin_ready = sem("mf_glu_ready"), sem("mf_low_ready"), sem("mf_lin_ready")
        sig_ready, gated_ready, hid_ready = sem("mf_sig_ready"), sem("mf_gated_ready"), sem("mf_hid_ready")
        downed, added = sem("mf_downed"), sem("mf_added")
        block = ctx.enter_context(nc.Block())
        NU = 2 * B
        CREDIT = 2 * NU + 2

        @block.sync
        def _(sp):
            with sp.Fori(0, E // 2) as t:
                for j in range(2):
                    sp.wait_ge(downed, CREDIT + 2 * NU * t - 2 * B * (1 - j))
                    e = 2 * t + j
                    for k in range(KD):
                        sp.dma_start(w1[j][:, k], w1_d[e, P * k:P * k + P]).then_inc(w_in[j], 16)
                    sp.dma_start(w2[j][:], w2_d[e].rearrange("(j p) n -> p j n", p=P)).then_inc(w_in[j], 16)

        @block.tensor
        def _(pe):
            pe.sem_inc(downed, CREDIT)
            with pe.Fori(0, E // 2) as t:
                def up(u, j):
                    s = J * (NU * t + u) + j
                    e = u // B
                    for half, done, freed in ((0, glu_done, glu_ready), (1, lin_done, low_ready)):
                        pe.wait_ge(freed, s + 1)
                        for k in range(KD):
                            ins = nc.tensor.matmul(bank[2 * half + j % 2][:], w1[e][:, k, half, P * j:P * j + P],
                                                   tt[:, k, S * (u % B):S * (u % B) + S], start=k == 0, stop=k == KD - 1)
                        ins.then_inc(done, 1)

                def down(u):
                    n = NU * t + u
                    pe.wait_ge(hid_ready, FREE + J * (n + 1))
                    for half in range(2):
                        pe.wait_ge(added, 2 * n + half + 1)
                        for i in (2 * half, 2 * half + 1):
                            for j in range(J):
                                ins = nc.tensor.matmul(bank[4 + 2 * (u % 2) + half][:, D * (i % 2):D * (i % 2) + D],
                                                       hid[:, u % 2, j, P * i:P * i + P], w2[u // B][:, j, :], start=j == 0, stop=j == J - 1)
                        ins.then_inc(downed, 1)

                for u in range(NU):
                    if u % B == 0:
                        pe.wait_ge(w_in[u // B], 48 * (t + 1))
                    for j in range(J):
                        up(u, j)
                        if j == 0 and u:
                            down(u - 1)
                down(NU - 1)

        @block.scalar
        def _(ac):
            with ac.Fori(0, E // 2) as t:
                for m in range(J * NU):
                    s = J * NU * t + m
                    ac.wait_ge(glu_ready, FREE + s + 1)
                    ac.wait_ge(gated_ready, s + 1)
                    nc.scalar.activation(sig[:, m % 2, :], glu[:, m % 2, :], ACT.Sigmoid, scale=ALPHA).then_inc(sig_ready, 1)

        @block.gpsimd
        def _(gp):
            gp.sem_inc(gated_ready, FREE)
            with gp.Fori(0, E // 2) as t:
                for m in range(J * NU):
                    s = J * NU * t + m
                    gp.wait_ge(sig_ready, s + 1)
                    gp.wait_ge(hid_ready, s + 1)
                    nc.gpsimd.tensor_tensor(gated[:, m % 2, :], glu[:, m % 2, :], sig[:, m % 2, :], ALU.mult).then_inc(gated_ready, 1)

        @block.vector
        def _(dv):
            for s in (glu_ready, low_ready, hid_ready):
                dv.sem_inc(s, FREE)
            dv.sem_inc(added, 4)
            with dv.Fori(0, E // 2) as t:
                def clip(u, j):
                    s = J * (NU * t + u) + j
                    e = 2 * t + u // B
                    dv.wait_ge(glu_done, s + 1)
                    dv.wait_ge(gated_ready, s + 1)
                    nc.vector.tensor_scalar(glu[:, j % 2, :], bank[j % 2][:], b1[:, e, 0, j:j + 1], LIMIT, ALU.add, ALU.min).then_inc(glu_ready, 1)
                    dv.wait_ge(lin_done, s + 1)
                    nc.vector.tensor_scalar(low[:, j % 2, :], bank[2 + j % 2][:], b1[:, e, 1, j:j + 1], LIMIT, ALU.add, ALU.min).then_inc(low_ready, 1)
                    dv.wait_ge(low_ready, FREE + s + 1)
                    nc.vector.tensor_scalar(lin[:, j % 2, :], low[:, j % 2, :], -LIMIT, 1.0, ALU.max, ALU.add).then_inc(lin_ready, 1)

                def join(u, j):
                    s = J * (NU * t + u) + j
                    dv.wait_ge(gated_ready, FREE + s + 1)
                    dv.wait_ge(lin_ready, s + 1)
                    if j == 0:
                        dv.wait_ge(downed, CREDIT + 2 * (NU * t + u) - 2)
                    nc.vector.tensor_tensor(hid[:, u % 2, j, :], gated[:, j % 2, :], lin[:, j % 2, :], ALU.mult).then_inc(hid_ready, 1)

                def add(u):
                    n = NU * t + u
                    e = 2 * t + u // B
                    for half in range(2):
                        dv.wait_ge(downed, CREDIT + 2 * n + half + 1)
                        for i in (2 * half, 2 * half + 1):
                            x = X[:, TB * (u % B) + i, :]
                            ins = nc.vector.scalar_tensor_tensor(x, bank[4 + 2 * (u % 2) + half][:, D * (i % 2):D * (i % 2) + D],
                                                                 weight[:, TB * (u % B) + i, bass.ds(e, 1)], x, ALU.mult, ALU.add)
                        ins.then_inc(added, 1)

                for u in range(NU):
                    for j in range(J):
                        clip(u, j)
                        if j:
                            join(u, j - 1)
                        elif u:
                            join(u - 1, J - 1)
                        if j == 1 and u:
                            add(u - 1)
                join(NU - 1, J - 1)
                add(NU - 1)


def rotary_attention(nc, sem, bank, X, Y, ident, wqk_t, wv_t, wo_t, cos_d, sin_d):
    with ExitStack() as ctx:
        def sb(name, shape, dt=F32):
            return ctx.enter_context(nc.sbuf_tensor("ra_" + name, shape, dt))

        qk_all = sb("qk_all", [P, NT, 2, H, DR])
        v_all = sb("v_all", [P, NT, D])
        o_all = sb("o_all", [P, NT, H, DR])
        neg_max = sb("neg_max", [P, H, NT])
        row_sum = sb("row_sum", [P, H, NT])
        wo = sb("wo", [P, KD, D])
        weights_in = sem("ra_weights_in")

        with ExitStack() as inner:
            def tmp(name, shape, dt=F32):
                return inner.enter_context(nc.sbuf_tensor("ra_" + name, shape, dt))

            wqk = tmp("wqk", [P, KD, 2 * D])
            wv = tmp("wv", [P, KD, D])
            cos = tmp("cos", [P, TB, DR])
            sin = tmp("sin", [P, TB, DR])
            y_row = tmp("y_row", [P, TB, D])
            yt = tmp("yt", [P, KD, S])
            straight = tmp("straight", [P, 2, 2 * H, DR])
            rotated = tmp("rotated", [P, 2, 2 * H, DR])
            row_copied, row_turned, yt_ready = sem("ra_row_copied"), sem("ra_row_turned"), sem("ra_yt_ready")
            v_done, v_copied = sem("ra_v_done"), sem("ra_v_copied")
            qk_done, turned, joined = sem("ra_qk_done"), sem("ra_turned"), sem("ra_joined")
            block = inner.enter_context(nc.Block())

            @block.sync
            def _(sp):
                sp.dma_start(wqk[:], wqk_t.rearrange("(k p) n -> p k n", p=P)).then_inc(weights_in, 16)
                sp.dma_start(wv[:], wv_t.rearrange("(k p) n -> p k n", p=P)).then_inc(weights_in, 16)
                sp.dma_start(wo[:], wo_t.rearrange("(k p) n -> p k n", p=P)).then_inc(weights_in, 16)
                sp.dma_start(cos[:], cos_d).then_inc(weights_in, 16)
                sp.dma_start(sin[:], sin_d).then_inc(weights_in, 16)

            @block.gpsimd
            def _(gp):
                gp.sem_inc(joined, FREE)
                with gp.Fori(0, B) as b:
                    gp.wait_ge(row_turned, 1 + b)
                    nc.gpsimd.tensor_copy(y_row[:], Y[:, bass.ds(TB * b, TB), :]).then_inc(row_copied, 1)
                    for i in range(TB):
                        gp.wait_ge(turned, TB * b + i + 1)
                        nc.gpsimd.tensor_tensor(qk_all[:, TB * b + i].rearrange("p s h d -> p (s h) d"), straight[:, i % 2],
                                                rotated[:, i % 2], ALU.add).then_inc(joined, 1)

            @block.tensor
            def _(pe):
                pe.sem_inc(row_turned, 1)
                pe.wait_ge(weights_in, 80)
                with pe.Fori(0, B) as b:
                    pe.wait_ge(row_copied, b + 1)
                    for k in range(KD):
                        for i in range(TB):
                            ins = nc.tensor.transpose(bank[k][:, P * i:P * i + P], y_row[:, i, P * k:P * k + P], ident[:])
                    ins.then_inc(row_turned, 1)
                    pe.wait_ge(yt_ready, b + 1)
                    pe.wait_ge(v_copied, b + 1)
                    for i in range(TB):
                        for k in range(KD):
                            ins = nc.tensor.matmul(bank[2 + i // 2][:, D * (i % 2):D * (i % 2) + D], yt[:, k, P * i:P * i + P], wv[:, k, :],
                                                   start=k == 0, stop=k == KD - 1)
                    ins.then_inc(v_done, 1)
                    for i in range(TB):
                        for k in range(KD):
                            ins = nc.tensor.matmul(bank[4 + i][:], yt[:, k, P * i:P * i + P], wqk[:, k, :], start=k == 0, stop=k == KD - 1)
                        ins.then_inc(qk_done, 1)
                    pe.wait_ge(turned, TB * (b + 1))

            @block.scalar
            def _(ac):
                ac.sem_inc(v_copied, 1)
                with ac.Fori(0, B) as b:
                    ac.wait_ge(row_turned, 2 + b)
                    for k in range(KD):
                        ins = nc.scalar.copy(yt[:, k, :], bank[k][:])
                    ins.then_inc(yt_ready, 1)
                    ac.wait_ge(v_done, b + 1)
                    for j in range(2):
                        ins = nc.scalar.copy(v_all[:, bass.ds(TB * b + 2 * j, 2), :], bank[2 + j][:].rearrange("p (i n) -> p i n", i=2))
                    ins.then_inc(v_copied, 1)

            @block.vector
            def _(dv):
                dv.wait_ge(weights_in, 80)
                with dv.Fori(0, B) as b:
                    for i in range(TB):
                        n = TB * b + i
                        HR = DR // 2
                        dv.wait_ge(qk_done, n + 1)
                        dv.wait_ge(joined, n + 1)
                        qk = bank[4 + i][:].rearrange("p (h d) -> p h d", d=DR)
                        c, s = (x[:, i, :].unsqueeze(1).broadcast_to([P, 2 * H, DR]) for x in (cos, sin))
                        nc.vector.tensor_tensor(straight[:, i % 2], qk, c, ALU.mult)
                        nc.vector.tensor_tensor(rotated[:, i % 2, :, 0:HR], qk[:, :, HR:DR], s[:, :, 0:HR], ALU.mult)
                        nc.vector.tensor_tensor(rotated[:, i % 2, :, HR:DR], qk[:, :, 0:HR], s[:, :, HR:DR], ALU.mult).then_inc(turned, 1)

        attention_core(nc, sem, "rc_", bank, ident, {"bias": "none"}, qk_all, None, v_all, None, neg_max, row_sum, o_all)

        os = sb("os", [P, TB, H, DR])
        ot = sb("ot", [P, KD, S])
        rinv_ready, scaled, o_turned, ot_ready = sem("ra_rinv_ready"), sem("ra_scaled"), sem("ra_o_turned"), sem("ra_ot_ready")
        projected, x_added = sem("ra_projected"), sem("ra_x_added")
        block = ctx.enter_context(nc.Block())

        @block.tensor
        def _(pe):
            pe.sem_inc(o_turned, 1)
            pe.wait_ge(weights_in, 80)
            with pe.Fori(0, B) as b:
                pe.wait_ge(scaled, b + 1)
                for k in range(KD):
                    for i in range(TB):
                        src = os[:, i].rearrange("p h d -> p (h d)")[:, P * k:P * k + P]
                        ins = nc.tensor.transpose(bank[k][:, P * i:P * i + P], src, ident[:])
                ins.then_inc(o_turned, 1)
                pe.wait_ge(ot_ready, b + 1)
                pe.wait_ge(x_added, b + 1)
                for i in range(TB):
                    for k in range(KD):
                        ins = nc.tensor.matmul(bank[2 + i // 2][:, D * (i % 2):D * (i % 2) + D], ot[:, k, P * i:P * i + P], wo[:, k, :],
                                               start=k == 0, stop=k == KD - 1)
                ins.then_inc(projected, 1)

        @block.scalar
        def _(ac):
            with ac.Fori(0, B) as b:
                ac.wait_ge(o_turned, 2 + b)
                ac.wait_ge(x_added, b + 1)
                for k in range(KD):
                    ins = nc.scalar.copy(ot[:, k, :], bank[k][:])
                ins.then_inc(ot_ready, 1)

        @block.vector
        def _(dv):
            dv.sem_inc(x_added, 1)
            nc.vector.reciprocal(row_sum[:], row_sum[:]).then_inc(rinv_ready, 1)
            dv.wait_ge(rinv_ready, 1)
            with dv.Fori(0, B) as b:
                dv.wait_ge(o_turned, b + 1)
                for i in range(TB):
                    r = row_sum[:, :, bass.ds(TB * b + i, 1)].broadcast_to([P, H, DR])
                    ins = nc.vector.tensor_tensor(os[:, i], o_all[:, TB * b + i], r, ALU.mult)
                ins.then_inc(scaled, 1)
                dv.wait_ge(projected, b + 1)
                for j in range(2):
                    x = X[:, bass.ds(TB * b + 2 * j, 2), :].rearrange("p i n -> p (i n)")
                    ins = nc.vector.tensor_tensor(x, x, bank[2 + j][:], ALU.add)
                ins.then_inc(x_added, 1)


def quantised_ffn(nc, sem, bank, X, Y, ident, out, clip_x, clip_down, w_gate, w_up, w_down):
    NC = -(-IQ // P)
    LAST = IQ - P * (NC - 1)
    LO, HI = RNE - QMAX - 1.0, RNE + QMAX
    with ExitStack() as ctx:
        def sb(name, shape, dt=F32):
            return ctx.enter_context(nc.sbuf_tensor("qf_" + name, shape, dt))

        clip = sb("clip", [P, 2])
        factor = sb("factor", [P, 2])
        identb = sb("identb", [P, P], BF16)
        wgu_t = sb("wgu_t", [P, 2, KD, NC * P], BF16)
        wd_t = sb("wd_t", [P, NC, D], BF16)
        xq_t = sb("xq_t", [P, KD, NT * P], BF16)
        gu_scale = sb("gu_scale", [P, 2, NC])
        wd_scale = sb("wd_scale", [P, KD])
        hid = sb("hid", [P, NC, NT * P])
        hid_max = sb("hid_max", [P, B * NC])
        loaded = sem("qf_loaded")
        filled = sem("qf_filled")

        with ExitStack() as inner:
            def tmp(name, shape, dt=F32):
                return inner.enter_context(nc.sbuf_tensor("qf_" + name, shape, dt))

            wgu = tmp("wgu", [P, 2, NC, D])
            wd = tmp("wd", [P, KD, IQ])
            xr = tmp("xr", [P, NT, D])
            wgu_q = tmp("wgu_q", [P, 2, NC, D], BF16)
            wd_q = tmp("wd_q", [P, KD, IQ], BF16)
            xq = tmp("xq", [P, NT, D], BF16)
            x_max = tmp("x_max", [P, 1])
            x_maxall = tmp("x_maxall", [P, 1])
            x_scale = tmp("x_scale", [P, 1])
            x_inv = tmp("x_inv", [P, 1])
            gu_inv = tmp("gu_inv", [P, 2, NC])
            wd_inv = tmp("wd_inv", [P, KD])
            stepped, clip_ready = sem("qf_stepped"), sem("qf_clip_ready")
            x_max_ready, x_max_all = sem("qf_x_max_ready"), sem("qf_x_max_all")
            wgu_ready, wd_ready, xq_ready = sem("qf_wgu_ready"), sem("qf_wd_ready"), sem("qf_xq_ready")
            turned, copied = sem("qf_turned"), sem("qf_copied")
            block = inner.enter_context(nc.Block())

            @block.sync
            def _(sp):
                sp.dma_start(clip[:, 0:1], rows(clip_x)).then_inc(loaded, 16)
                sp.dma_start(clip[:, 1:2], rows(clip_down)).then_inc(loaded, 16)
                sp.wait_ge(filled, 1)
                for n, w in enumerate((w_gate, w_up)):
                    full = P * (NC - 1)
                    sp.dma_start(wgu[:, n, 0:NC - 1, :], w[0:full, :].rearrange("(c p) n -> p c n", p=P)).then_inc(loaded, 16)
                    sp.dma_start(wgu[0:LAST, n, NC - 1, :], w[full:IQ, :]).then_inc(loaded, 16)
                sp.dma_start(wd[:], w_down.rearrange("(k p) n -> p k n", p=P)).then_inc(loaded, 16)

            @block.gpsimd
            def _(gp):
                nc.gpsimd.memset(wgu[:, :, NC - 1, :], 1.0).then_inc(filled, 1)
                gp.wait_ge(x_max_ready, 1)
                nc.gpsimd.partition_all_reduce(x_maxall[:], x_max[:], P, bass.bass_isa.ReduceOp.max).then_inc(x_max_all, 1)

            @block.scalar
            def _(ac):
                ac.wait_ge(loaded, 16 * 7)
                nc.scalar.activation(factor[:], clip[:], ACT.Sigmoid).then_inc(clip_ready, 1)
                for n in range(2):
                    ac.wait_ge(turned, n + 1)
                    for k in range(KD):
                        ins = nc.scalar.copy(wgu_t[:, n, k, :], bank[2 * n + k][:].bitcast(BF16)[:, 0:NC * P])
                    ins.then_inc(copied, 1)
                ac.wait_ge(turned, 3)
                nc.scalar.copy(wd_t[:, 0:4, :], bank[4][:].bitcast(BF16).rearrange("p (c n) -> p c n", c=4))
                nc.scalar.copy(wd_t[:, 4, :], bank[5][:].bitcast(BF16)[:, 0:D])
                nc.scalar.copy(wd_t[0:LAST, 5, :], bank[5][0:LAST].bitcast(BF16)[:, D:2 * D]).then_inc(copied, 1)
                for half in range(2):
                    ac.wait_ge(turned, 4 + half)
                    for k in range(KD):
                        ins = nc.scalar.copy(xq_t[:, k, 1024 * half:1024 * half + 1024], bank[6 + k][:].bitcast(BF16))
                    ins.then_inc(copied, 1)

            @block.tensor
            def _(pe):
                pe.wait_ge(wgu_ready, 1)
                for n in range(2):
                    for k in range(KD):
                        dst = bank[2 * n + k][:].bitcast(BF16)
                        for c in range(NC):
                            ins = nc.tensor.transpose(dst[:, P * c:P * c + P], wgu_q[:, n, c, P * k:P * k + P], identb[:])
                    ins.then_inc(turned, 1)
                pe.wait_ge(wd_ready, 1)
                for c in range(NC):
                    m = P if c < NC - 1 else LAST
                    for k in range(KD):
                        dst = bank[4 + c // 4][0:m].bitcast(BF16)
                        col = D * (c % 4) + P * k
                        ins = nc.tensor.transpose(dst[:, col:col + P], wd_q[:, k, P * c:P * c + m], identb[:])
                ins.then_inc(turned, 1)
                pe.wait_ge(xq_ready, 1)
                for half in range(2):
                    if half:
                        pe.wait_ge(copied, 4)
                    for k in range(KD):
                        dst = bank[6 + k][:].bitcast(BF16)
                        for t in range(NT // 2):
                            ins = nc.tensor.transpose(dst[:, P * t:P * t + P], xq[:, NT // 2 * half + t, P * k:P * k + P], identb[:])
                    ins.then_inc(turned, 1)

            @block.vector
            def _(dv):
                st = Steps(dv, stepped)
                nc.vector.memset(hid_max[:], 0.0)
                nc.vector.tensor_reduce(x_max[:], Y[:].rearrange("p t d -> p (t d)"), AX.X, ALU.max, apply_absolute_value=True)\
                    .then_inc(x_max_ready, 1)
                st.after(nc.vector.tensor_copy(identb[:], ident[:]))
                dv.wait_ge(loaded, 16 * 7)

                def round_(dst, mid, src, inv_of, parts):
                    for p in parts:
                        ins = nc.vector.tensor_scalar(mid[p], src[p], inv_of(p), RNE, ALU.mult, ALU.add)
                    st.after(ins)
                    st.after(nc.vector.tensor_scalar(mid[:], mid[:], LO, HI, ALU.max, ALU.min))
                    return nc.vector.tensor_scalar(dst[:], mid[:], RNE, None, ALU.subtract)

                st.after(nc.vector.tensor_reduce(gu_scale[:], wgu[:], AX.X, ALU.max, apply_absolute_value=True))
                st.after(nc.vector.tensor_scalar(gu_scale[:], gu_scale[:], 1.0 / QMAX, None, ALU.mult))
                st.after(nc.vector.reciprocal(gu_inv[:], gu_scale[:]))
                parts = [(slice(None), n, c) for n in range(2) for c in range(NC)]
                round_(wgu_q, wgu, wgu, lambda p: gu_inv[:, p[1], p[2]:p[2] + 1], parts).then_inc(wgu_ready, 1)
                st.after(nc.vector.tensor_reduce(wd_scale[:], wd[:], AX.X, ALU.max, apply_absolute_value=True))
                st.after(nc.vector.tensor_scalar(wd_scale[:], wd_scale[:], 1.0 / QMAX, None, ALU.mult))
                st.after(nc.vector.reciprocal(wd_inv[:], wd_scale[:]))
                parts = [(slice(None), k) for k in range(KD)]
                round_(wd_q, wd, wd, lambda p: wd_inv[:, p[1]:p[1] + 1], parts).then_inc(wd_ready, 1)
                dv.wait_ge(x_max_all, 1)
                dv.wait_ge(clip_ready, 1)
                st.after(nc.vector.tensor_scalar(x_scale[:], x_maxall[:], factor[:, 0:1], None, ALU.mult))
                st.after(nc.vector.tensor_scalar(x_scale[:], x_scale[:], 1.0 / QMAX, None, ALU.mult))
                st.after(nc.vector.reciprocal(x_inv[:], x_scale[:]))
                round_(xq, xr, Y, lambda p: x_inv[:], [(slice(None),)]).then_inc(xq_ready, 1)
                st.after(nc.vector.tensor_scalar(gu_scale[:], gu_scale[:], x_scale[:], None, ALU.mult))

        with ExitStack() as inner:
            act = inner.enter_context(nc.sbuf_tensor("qf_act", [P, 2, S], F32))
            gated, upped, act_ready = sem("qf_gated"), sem("qf_upped"), sem("qf_act_ready")
            hid_ready, maxed = sem("qf_hid_ready"), sem("qf_maxed")
            block = inner.enter_context(nc.Block())

            @block.tensor
            def _(pe):
                with pe.Fori(0, B) as b:
                    for c in range(NC):
                        n = NC * b + c
                        for which, done, freed in ((0, gated, act_ready), (1, upped, hid_ready)):
                            pe.wait_ge(freed, n + 1)
                            for k in range(KD):
                                ins = nc.tensor.matmul(bank[2 * which + c % 2][:], wgu_t[:, which, k, P * c:P * c + P],
                                                       xq_t[:, k, bass.ds(S * b, S)], start=k == 0, stop=k == KD - 1)
                            ins.then_inc(done, 1)

            @block.scalar
            def _(ac):
                ac.sem_inc(act_ready, FREE)
                with ac.Fori(0, B) as b:
                    for c in range(NC):
                        n = NC * b + c
                        ac.wait_ge(gated, n + 1)
                        ac.wait_ge(hid_ready, n + 1)
                        nc.scalar.activation(act[:, c % 2, :], bank[c % 2][:], ACT.Silu, scale=gu_scale[:, 0, c:c + 1]).then_inc(act_ready, 1)

            @block.vector
            def _(dv):
                dv.sem_inc(hid_ready, FREE)
                with dv.Fori(0, B) as b:
                    for c in range(NC):
                        n = NC * b + c
                        m = P if c < NC - 1 else LAST
                        dv.wait_ge(act_ready, FREE + n + 1)
                        dv.wait_ge(upped, n + 1)
                        dst = hid[:, c, bass.ds(S * b, S)]
                        nc.vector.scalar_tensor_tensor(dst, bank[2 + c % 2][:], gu_scale[:, 1, c:c + 1], act[:, c % 2, :],
                                                       ALU.mult, ALU.mult).then_inc(hid_ready, 1)
                        dv.wait_ge(hid_ready, FREE + n + 1)
                        nc.vector.tensor_reduce(hid_max[0:m, bass.ds(n, 1)], hid[0:m, c, bass.ds(S * b, S)], AX.X, ALU.max,
                                                apply_absolute_value=True).then_inc(maxed, 1)

        with ExitStack() as inner:
            def tmp(name, shape, dt=F32):
                return inner.enter_context(nc.sbuf_tensor("qf_" + name, shape, dt))

            hmax = tmp("hmax", [P, 1])
            hmaxall = tmp("hmaxall", [P, 1])
            h_scale = tmp("h_scale", [P, 1])
            h_inv = tmp("h_inv", [P, 1])
            ones = tmp("ones", [P, P])
            diag = tmp("diag", [P, KD, P])
            out_scale = tmp("out_scale", [P, D])
            mid = tmp("mid", [P, NC, S])
            hq = tmp("hq", [P, 2, NC, S], BF16)
            res = tmp("res", [P, 2, TB, D])
            stepped, hmax_ready, hmax_all = sem("qf_c_stepped"), sem("qf_hmax_ready"), sem("qf_hmax_all")
            diag_ready, spread_done = sem("qf_diag_ready"), sem("qf_spread_done")
            hq_ready, down_done, res_ready = sem("qf_hq_ready"), sem("qf_down_done"), sem("qf_res_ready")
            scaled = sem("qf_scaled")
            stored = [sem(f"qf_stored{j}") for j in range(2)]
            block = inner.enter_context(nc.Block())

            @block.gpsimd
            def _(gp):
                gp.wait_ge(hmax_ready, 1)
                nc.gpsimd.partition_all_reduce(hmaxall[:], hmax[:], P, bass.bass_isa.ReduceOp.max).then_inc(hmax_all, 1)

            @block.tensor
            def _(pe):
                pe.wait_ge(diag_ready, 1)
                for k in range(KD):
                    ins = nc.tensor.matmul(bank[6][:, P * k:P * k + P], ones[:], diag[:, k, :], start=True, stop=True)
                ins.then_inc(spread_done, 1)
                for b in range(B):
                    pe.wait_ge(hq_ready, b + 1)
                    if b >= 2:
                        pe.wait_ge(scaled, b - 1)
                    for i in range(TB):
                        for c in range(NC):
                            m = P if c < NC - 1 else LAST
                            ins = nc.tensor.matmul(bank[2 * (b % 2) + i // 2][:, D * (i % 2):D * (i % 2) + D],
                                                   hq[0:m, b % 2, c, P * i:P * i + P], wd_t[0:m, c, :], start=c == 0, stop=c == NC - 1)
                    ins.then_inc(down_done, 1)

            @block.vector
            def _(dv):
                st = Steps(dv, stepped)
                nc.vector.tensor_reduce(hmax[:], hid_max[:], AX.X, ALU.max).then_inc(hmax_ready, 1)
                st.after(nc.vector.memset(ones[:], 1.0))
                for k in range(KD):
                    ins = nc.vector.tensor_scalar(diag[:, k, :], ident[:], wd_scale[:, k:k + 1], None, ALU.mult)
                ins.then_inc(diag_ready, 1)
                dv.wait_ge(hmax_all, 1)
                st.after(nc.vector.tensor_scalar(h_scale[:], hmaxall[:], factor[:, 1:2], None, ALU.mult))
                st.after(nc.vector.tensor_scalar(h_scale[:], h_scale[:], 1.0 / QMAX, None, ALU.mult))
                st.after(nc.vector.reciprocal(h_inv[:], h_scale[:]))
                dv.wait_ge(spread_done, 1)
                st.after(nc.vector.tensor_scalar(out_scale[:], bank[6][:, 0:D], h_scale[:], None, ALU.mult))

                def finish(b):
                    dv.wait_ge(down_done, b + 1)
                    if b >= 2:
                        dv.wait_ge(stored[b % 2], 16 * (b // 2))
                    r = res[:, b % 2]
                    for i in range(TB):
                        ins = nc.vector.tensor_tensor(r[:, i, :], bank[2 * (b % 2) + i // 2][:, D * (i % 2):D * (i % 2) + D], out_scale[:], ALU.mult)
                    ins.then_inc(scaled, 1)
                    dv.wait_ge(scaled, b + 1)
                    nc.vector.tensor_tensor(r, r, X[:, TB * b:TB * b + TB, :], ALU.add).then_inc(res_ready, 1)

                for b in range(B):
                    if b >= 2:
                        dv.wait_ge(down_done, b - 1)
                    if b:
                        dv.wait_ge(hq_ready, b)
                    st.after(nc.vector.tensor_scalar(mid[:], hid[:, :, S * b:S * b + S], h_inv[:], RNE, ALU.mult, ALU.add))
                    st.after(nc.vector.tensor_scalar(mid[:], mid[:], LO, HI, ALU.max, ALU.min))
                    nc.vector.tensor_scalar(hq[:, b % 2], mid[:], RNE, None, ALU.subtract).then_inc(hq_ready, 1)
                    if b:
                        finish(b - 1)
                finish(B - 1)

            @block.sync
            def _(sp):
                for b in range(B):
                    sp.wait_ge(res_ready, b + 1)
                    sp.dma_start(out[b].rearrange("(i p) d -> p i d", p=P), res[:, b % 2]).then_inc(stored[b % 2], 16)
                for j in range(2):
                    sp.wait_ge(stored[j], 16 * (B // 2))


def program(nc, a, out):
    with ExitStack() as ctx:
        stage_semaphores = []

        def sem(name):
            stage_semaphores.append(nc.alloc_semaphore(name=name))
            return stage_semaphores[-1]

        def stage_end():
            nc.clear_and_free_semaphores(list(stage_semaphores))
            stage_semaphores.clear()
            nc.all_engine_barrier()

        ctx.enter_context(nc.allow_non_contiguous_dma(reason="a vector's values, one to a partition"))
        bank = [ctx.enter_context(nc.psum_tensor(f"bank{i}", [P, 512], F32)) for i in range(8)]
        X = ctx.enter_context(nc.sbuf_tensor("X", [P, NT, D], F32))
        Y = ctx.enter_context(nc.sbuf_tensor("Y", [P, NT, D], F32))
        ident = ctx.enter_context(nc.sbuf_tensor("ident", [P, P], F32))
        consts_in = sem("consts_in")
        with nc.Block() as block:
            @block.sync
            def _(sp):
                sp.dma_start(ident[:], a["c_identity"]).then_inc(consts_in, 16)
                sp.dma_start(X[:], a["x"].rearrange("b (i p) d -> p (b i) d", p=P)).then_inc(consts_in, 16)
                sp.wait_ge(consts_in, 32)
        stage_end()
        tables = nc.dram_tensor("bias_tables", (2, H, NPOS), F32, kind="Internal").ap()
        copies = nc.dram_tensor("bias_copies", (2, H, P, NPOS), F32, kind="Internal").ap()
        lay = [{n: a[f"L{l}_cond2_{n}"] for n in ("w0", "b0", "g0", "w1", "b1", "g1", "w2", "b2")} for l in range(2)]
        for l in range(2):
            lay[l]["w0"] = a[f"L{l}_cond2_w0"].rearrange("a d -> (a d)")
            lay[l]["table"] = tables[l]
            lay[l]["copies"] = copies[l]
        bias_tables(nc, sem, bank, ident, a["c_positions"], lay)
        stage_end()
        moe_conditioning(nc, sem, bank, Y, a["c_x_transposed"], a["c_lane"], a["c_cond_rep"], a["c_wt_t"], a["c_wg_t"],
                         *(a["L0_cond_" + n] for n in ("w_gate", "w_up", "w_down", "sw_gate", "sw_up", "sw_down")))
        stage_end()
        linear_attention(nc, sem, bank, X, Y, ident, a["c_keep_upper"], a["c_attn_wq_t"], a["c_attn_wk_t"], a["c_attn_wv_t"],
                         a["c_attn_wo_t"])
        stage_end()
        def cosine(l):
            w = {n: a[f"L{l}_cond2_{n}"] for n in ("g_norm", "Wq", "Wkv", "q_scale", "k_scale", "null_attn_bias", "Wout", "g_out")}
            w.update(cond=a["cond_64"], mask=a["mask_BxS_bf1"], bias="table", copies=copies[l])
            null_key_attention(nc, sem, f"ca{l}_", bank, X, Y, ident, w)
            stage_end()

        cosine(0)
        moe_ffn(nc, sem, bank, X, Y, ident, a["c_lane"], *(a["L0_ffn_" + n] for n in ("norm_scale", "gate_w", "gate_b")),
                a["c_mlp1_w"], a["c_mlp1_b"], a["L0_ffn_mlp2_w"], a["L0_ffn_mlp2_b"])
        stage_end()
        w = {n: a["L1_cond_" + n] for n in ("Wq", "Wkv", "null_attn_bias", "g_out")}
        w.update(g_norm=a["L1_cond_g_in"], Wout=a["L1_cond_Wo"], cond=a["cond_64"], mask=a["mask_BxS_bk0"],
                 bias="full", full=a["fside_16xSxS_0"])
        null_key_attention(nc, sem, "ba_", bank, X, Y, ident, w)
        stage_end()
        rotary_attention(nc, sem, bank, X, Y, ident, a["c_rot_wqk_t"], a["c_rot_wv_t"], a["c_rot_wo_t"], a["c_rot_cos"], a["c_rot_sin"])
        stage_end()
        cosine(1)
        quantised_ffn(nc, sem, bank, X, Y, ident, out, a["L1_ffn_clip_x"], a["L1_ffn_clip_down"], a["L1_ffn_w_gate"],
                      a["L1_ffn_w_up"], a["L1_ffn_w_down"])
        stage_end()


def _layout(inputs):
    a = {k: np.ascontiguousarray(v) for k, v in inputs.items()}
    for k in ("mask_BxS_bf1", "mask_BxS_bk0"):
        a[k] = a[k].view(np.int32)
    a["c_identity"] = np.eye(P, dtype=np.float32)
    a["c_positions"] = (S - 1 - np.arange(NPOS, dtype=np.float32)).reshape(NPOS // P, P).T.copy()
    a["c_lane"] = np.tile(np.arange(E0, dtype=np.float32), (P, 1))
    a["c_x_transposed"] = np.ascontiguousarray(a["x"].transpose(0, 2, 1))
    a["c_cond_rep"] = np.ascontiguousarray(np.broadcast_to(a["cond_64"].T[:, :, None], (G0, B, P)))
    a["c_wt_t"] = np.ascontiguousarray(a.pop("L0_cond_wt").T)
    a["c_wg_t"] = np.ascontiguousarray(a.pop("L0_cond_wg").T)
    a["c_keep_upper"] = np.triu(np.ones((P, P), np.float32))
    for n in ("q", "k", "v", "o"):
        a[f"c_attn_w{n}_t"] = np.ascontiguousarray(a.pop(f"L0_attn_W{n}").T)
    a["c_mlp1_w"] = np.ascontiguousarray(a.pop("L0_ffn_mlp1_w").reshape(E1, D, I1, 2).transpose(0, 1, 3, 2))
    a["c_mlp1_b"] = np.ascontiguousarray(a.pop("L0_ffn_mlp1_b").reshape(E1, I1 // P, P, 2).transpose(2, 0, 3, 1))
    rot = {n: a.pop(f"L1_attn_W{n}").T for n in "qkvo"}
    a["c_rot_wqk_t"] = np.ascontiguousarray(np.concatenate([rot["q"], rot["k"]], axis=1))
    a["c_rot_wv_t"] = np.ascontiguousarray(rot["v"])
    a["c_rot_wo_t"] = np.ascontiguousarray(rot["o"])
    freq = (1.0 / np.float32(10000.0) ** (np.arange(0, DR, 2, dtype=np.float32) / DR)).astype(np.float32)
    angle = np.arange(S, dtype=np.float32)[:, None] * freq
    cos, sin = np.cos(angle).astype(np.float32), np.sin(angle).astype(np.float32)
    a["c_rot_cos"] = np.ascontiguousarray(np.concatenate([cos, cos], axis=1).reshape(TB, P, DR).transpose(1, 0, 2))
    a["c_rot_sin"] = np.ascontiguousarray(np.concatenate([-sin, sin], axis=1).reshape(TB, P, DR).transpose(1, 0, 2))
    return a


def kernel(**inputs):
    import concourse.bacc as bacc
    from concourse.bass_utils import run_bass_kernel_spmd

    nc = bacc.Bacc("TRN2", target_bir_lowering=False, num_devices=1)
    arrays = _layout(inputs)
    aps = {n: nc.dram_tensor(n, v.shape, mybir.dt.from_np(v.dtype), kind="ExternalInput").ap() for n, v in arrays.items()}
    out = nc.dram_tensor("out", (B, S, D), F32, kind="ExternalOutput").ap()
    program(nc, aps, out)
    r = run_bass_kernel_spmd(nc, [arrays], core_ids=[0])
    return r.results[0]["out"]
```

```python
from contextlib import ExitStack

import numpy as np

import concourse.bass as bass
from concourse import mybir

F32 = mybir.dt.float32
BF16 = mybir.dt.bfloat16
U8 = mybir.dt.uint8
I32 = mybir.dt.int32
F32R = mybir.dt.float32r
U32 = mybir.dt.uint32
ALU = mybir.AluOpType
ACT = mybir.ActivationFunctionType
AX = mybir.AxisListType

P = 128
B, S, D = 4, 512, 256
TB = S // P
NT = B * TB
KD = D // P
H, DH = 16, 64
DR = D // H
E0, M0 = 8, 128
NSH = 2
G0 = 64
E1, I1 = 8, 512
IQ = 704
QMAX = 127.0
NPOS = S + P
MASKED = -1.0e30
EPS = 1e-5
HIGH_BITS = -4096
RNE = 12582912.0


FREE = 2


class Steps:

    def __init__(self, eng, sem, base=0, per_loop=None):
        self.eng, self.sem, self.base, self.n, self.per_loop = eng, sem, base, 0, per_loop

    def after(self, ins, apart=False):
        self.n += 1
        ins.then_inc(self.sem, 1)
        self.eng.wait_ge(self.sem, self.base + self.n)
        if apart:
            self.eng.nop(nofuse=True)

    def close(self):
        assert self.per_loop is None or self.n == self.per_loop, (self.n, self.per_loop)


def wait_apart(eng, sem, value):
    eng.wait_ge(sem, value)
    eng.nop(nofuse=True)


def high_part(nc, dst, src):
    return nc.vector.tensor_scalar(dst, src.bitcast(I32), HIGH_BITS, None, ALU.bitwise_and)


def rows(ap, n=P):
    return ap.rearrange("(a d) -> a d", a=1).broadcast_to([n, ap.shape[0]])


def columns(ap, k):
    return ap.rearrange("(k p) -> p k", k=k)


def bias_tables(nc, sem, bank, ident, pos_reversed, layers):
    NR = NPOS // P
    with ExitStack() as ctx:
        def sb(name, shape, dt=F32):
            return ctx.enter_context(nc.sbuf_tensor(name, shape, dt))

        pos = sb("bt_pos", [P, NR])
        row = [sb(f"bt_row{l}", [P, 5, D]) for l in range(2)]
        w1 = [sb(f"bt_w1{l}", [P, KD, D]) for l in range(2)]
        w2 = [sb(f"bt_w2{l}", [P, KD, H]) for l in range(2)]
        b2 = [sb(f"bt_b2{l}", [H, 1]) for l in range(2)]
        hid = sb("bt_hid", [P, NR, D])
        act_out = sb("bt_act", [P, NR, D])
        hid_t = sb("bt_hid_t", [P, KD, NPOS])
        stats = sb("bt_stats", [P, NR, 6])
        mv = sb("bt_mv", [P, NR, 2])
        sd = sb("bt_sd", [P, NR])
        rstd = sb("bt_rstd", [P, NR])
        table = sb("bt_table", [H, NPOS])

        loaded = [sem(f"bt_loaded{l}") for l in range(2)]
        stepped = sem("bt_stepped")
        var_ready = sem("bt_var_ready")
        sd_ready = sem("bt_sd_ready")
        normed = sem("bt_normed")
        activated = sem("bt_activated")
        transposed = sem("bt_transposed")
        hid_t_ready = sem("bt_hid_t_ready")
        projected = sem("bt_projected")
        table_ready = sem("bt_table_ready")
        stored, copied = sem("bt_stored"), sem("bt_copied")
        block = ctx.enter_context(nc.Block())

        @block.sync
        def _(sp):
            for l, lay in enumerate(layers):
                if l == 0:
                    sp.dma_start(pos[:], pos_reversed).then_inc(loaded[l], 16)
                for n, name in enumerate(("w0", "b0", "g0", "b1", "g1")):
                    sp.dma_start(row[l][:, n, :], rows(lay[name])).then_inc(loaded[l], 16)
                sp.dma_start(w1[l][:], lay["w1"].rearrange("(k p) n -> p k n", p=P)).then_inc(loaded[l], 16)
                sp.dma_start(w2[l][:], lay["w2"].rearrange("(k p) n -> p k n", p=P)).then_inc(loaded[l], 16)
                sp.dma_start(b2[l][:], lay["b2"].rearrange("(h a) -> h a", a=1)).then_inc(loaded[l], 16)
            for l, lay in enumerate(layers):
                sp.wait_ge(table_ready, 2 * (l + 1))
                sp.dma_start(lay["table"], table[:]).then_inc(stored, 16)
                sp.wait_ge(stored, 16 * (l + 1))
                line = lay["table"]
                line = bass.AP(tensor=line.tensor, offset=line.offset, ap=[[NPOS, H], [0, P], [1, NPOS]])
                sp.dma_start(lay["copies"], line).then_inc(copied, 16)
            sp.wait_ge(copied, 32)

        @block.vector
        def _(dv):
            st = Steps(dv, stepped)
            for l in range(2):
                dv.wait_ge(loaded[l], 16 * (9 if l == 0 else 8))
                if l == 1:
                    dv.wait_ge(activated, 2)
                for q in range(2):
                    for t in range(NR):
                        if q == 0:
                            ins = nc.vector.scalar_tensor_tensor(
                                hid[:, t, :], row[l][:, 0, :], pos[:, t:t + 1], row[l][:, 1, :], ALU.mult, ALU.add)
                        else:
                            if t == 0:
                                dv.wait_ge(projected, 2 * l + 1)
                            ins = nc.vector.tensor_tensor(
                                hid[:, t, :], bank[3 + t // 2][:, D * (t % 2):D * (t % 2) + D], row[l][:, 3, :], ALU.add)
                    st.after(ins)
                    for t in range(NR):
                        ins = nc.vector.bn_stats(stats[:, t, :], hid[:, t, :])
                    st.after(ins)
                    for t in range(NR):
                        ins = nc.vector.bn_aggr(mv[:, t, :], stats[:, t, :])
                    st.after(ins)
                    nc.vector.tensor_scalar(sd[:], mv[:, :, 1], EPS, None, ALU.add).then_inc(var_ready, 1)
                    dv.wait_ge(sd_ready, 2 * l + q + 1)
                    st.after(nc.vector.reciprocal(rstd[:], sd[:]))
                    for t in range(NR):
                        ins = nc.vector.tensor_scalar(hid[:, t, :], hid[:, t, :], mv[:, t, 0:1], rstd[:, t:t + 1],
                                                      ALU.subtract, ALU.mult)
                    st.after(ins)
                    g = row[l][:, 2 + 2 * q, :].unsqueeze(1).broadcast_to([P, NR, D])
                    nc.vector.tensor_tensor(hid[:], hid[:], g, ALU.mult).then_inc(normed, 1)
                    if q == 0:
                        dv.wait_ge(activated, 2 * l + 1)
                dv.wait_ge(projected, 2 * l + 2)
                if l == 1:
                    dv.wait_ge(stored, 16)
                nc.vector.tensor_scalar(table[:, 0:512], bank[6][0:H, :], b2[l][:], None, ALU.add).then_inc(table_ready, 1)
                nc.vector.tensor_scalar(table[:, 512:NPOS], bank[7][0:H, 0:P], b2[l][:], None, ALU.add).then_inc(table_ready, 1)

        @block.scalar
        def _(ac):
            for n in range(4):
                ac.wait_ge(var_ready, n + 1)
                nc.scalar.activation(sd[:], sd[:], ACT.Sqrt).then_inc(sd_ready, 1)
                ac.wait_ge(normed, n + 1)
                if n:
                    ac.wait_ge(transposed, n)
                nc.scalar.activation(act_out[:], hid[:], ACT.Silu).then_inc(activated, 1)
                ac.wait_ge(transposed, n + 1)
                if n:
                    ac.wait_ge(projected, n)
                nc.scalar.copy(hid_t[:, 0, 0:512], bank[0][:])
                nc.scalar.copy(hid_t[:, 1, 0:512], bank[1][:])
                nc.scalar.copy(hid_t[:, :, 512:NPOS], bank[2][:, 0:D].rearrange("p (k n) -> p k n", k=KD)).then_inc(hid_t_ready, 1)

        @block.tensor
        def _(pe):
            pe.wait_ge(loaded[0], 16 * 9)
            pe.wait_ge(loaded[1], 16 * 8)
            for n in range(4):
                l, q = divmod(n, 2)
                pe.wait_ge(activated, n + 1)
                if n:
                    pe.wait_ge(hid_t_ready, n)
                for t in range(NR):
                    for k in range(KD):
                        dst = bank[k][:, P * t:P * t + P] if t < 4 else bank[2][:, P * k:P * k + P]
                        ins = nc.tensor.transpose(dst, act_out[:, t, P * k:P * k + P], ident[:])
                ins.then_inc(transposed, 1)
                pe.wait_ge(hid_t_ready, n + 1)
                if q == 0:
                    if l:
                        pe.wait_ge(normed, n)
                    for t in range(NR):
                        for k in range(KD):
                            ins = nc.tensor.matmul(bank[3 + t // 2][:, D * (t % 2):D * (t % 2) + D],
                                                   hid_t[:, k, P * t:P * t + P], w1[l][:, k, :], start=k == 0, stop=k == KD - 1)
                else:
                    if l:
                        pe.wait_ge(table_ready, 2)
                    for lo, hi, dst in ((0, 512, bank[6]), (512, NPOS, bank[7])):
                        for k in range(KD):
                            ins = nc.tensor.matmul(dst[0:H, 0:hi - lo], w2[l][:, k, :], hid_t[:, k, lo:hi],
                                                   start=k == 0, stop=k == KD - 1)
                ins.then_inc(projected, 1)


def route(nc, dv, st, logits, ex, zsum, best, best_at, lane, picked, weight, softmax_all, exp_in, exp_ready, exp_done):
    E = E0
    for t in range(NT):
        ins = nc.vector.max(best[:, t, :], logits[:, t, :])
    st.after(ins)
    for t in range(NT):
        ins = nc.vector.max_index(best_at[:, t, :], best[:, t, :], logits[:, t, :])
    st.after(ins)
    top = best[:, :, 0:1].broadcast_to([P, NT, E])
    nc.vector.tensor_tensor(exp_in[:], logits[:], top, ALU.subtract).then_inc(exp_ready, 1)
    at = best_at[:, :, 0:2]
    st.after(nc.vector.tensor_copy(picked[:, :, 0:2], at))
    first = picked[:, :, 0:1].broadcast_to([P, NT, E])
    second = picked[:, :, 1:2].broadcast_to([P, NT, E])
    lanes = lane[:].unsqueeze(1).broadcast_to([P, NT, E])
    nc.vector.tensor_tensor(weight[:], lanes, first, ALU.is_equal)
    st.after(nc.vector.tensor_tensor(logits[:], lanes, second, ALU.is_equal))
    st.after(nc.vector.tensor_tensor(weight[:], weight[:], logits[:], ALU.add))
    dv.wait_ge(exp_done, 1)
    if softmax_all:
        st.after(nc.vector.tensor_reduce(zsum[:], ex[:], AX.X, ALU.add))
        st.after(nc.vector.reciprocal(zsum[:], zsum[:]))
        st.after(nc.vector.tensor_tensor(ex[:], ex[:], zsum[:].unsqueeze(2).broadcast_to([P, NT, E]), ALU.mult))
    st.after(nc.vector.tensor_tensor(ex[:], ex[:], weight[:], ALU.mult))
    st.after(nc.vector.tensor_reduce(zsum[:], ex[:], AX.X, ALU.add))
    if softmax_all:
        st.after(nc.vector.tensor_scalar(zsum[:], zsum[:], 1e-20, None, ALU.add))
    st.after(nc.vector.reciprocal(zsum[:], zsum[:]))
    st.after(nc.vector.tensor_tensor(weight[:], ex[:], zsum[:].unsqueeze(2).broadcast_to([P, NT, E]), ALU.mult))


def moe_conditioning(nc, sem, bank, Y, x_transposed, lane_d, cond_rep, wt_t, wg_t, w_gate, w_up, w_down,
                     sw_gate, sw_up, sw_down):
    NE = E0 + NSH
    with ExitStack() as ctx:
        def sb(name, shape, dt=F32):
            return ctx.enter_context(nc.sbuf_tensor(name, shape, dt))

        xt = sb("mc_xt", [P, B, KD, S])
        wg = sb("mc_wg", [P, KD, NE, M0])
        wu = sb("mc_wu", [P, KD, NE, M0])
        wd = sb("mc_wd", [P, NE, D])
        wtt = sb("mc_wtt", [P, KD, E0])
        wgt = sb("mc_wgt", [G0, E0])
        crep = sb("mc_crep", [G0, B, P])
        lane = sb("mc_lane", [P, E0])
        logits = sb("mc_logits", [P, NT, E0])
        exp_in = sb("mc_exp_in", [P, NT, E0])
        ex = sb("mc_ex", [P, NT, E0])
        zsum = sb("mc_zsum", [P, NT])
        best = sb("mc_best", [P, NT, 8])
        best_at = sb("mc_best_at", [P, NT, 8], U32)
        picked = sb("mc_picked", [P, NT, 2])
        weight = sb("mc_weight", [P, NT, E0])
        gate = sb("mc_gate", [P, 2, S])
        leaky = sb("mc_leaky", [P, 2, S])
        hid = sb("mc_hid", [P, 2, S])

        routing_in = sem("mc_routing_in")
        gate_in, up_in, down_in = sem("mc_gate_in"), sem("mc_up_in"), sem("mc_down_in")
        stepped = sem("mc_stepped")
        logits_done = sem("mc_logits_done")
        exp_ready, exp_done = sem("mc_exp_ready"), sem("mc_exp_done")
        gated, upped, downed = sem("mc_gated"), sem("mc_upped"), sem("mc_downed")
        gate_copied = sem("mc_gate_copied")
        leaked = sem("mc_leaked")
        hid_ready = sem("mc_hid_ready")
        added = sem("mc_added")
        block = ctx.enter_context(nc.Block())

        @block.sync
        def _(sp):
            sp.dma_start(wtt[:], wt_t.rearrange("(k p) e -> p k e", p=P)).then_inc(routing_in, 16)
            sp.dma_start(wgt[:], wg_t).then_inc(routing_in, 16)
            sp.dma_start(crep[:], cond_rep).then_inc(routing_in, 16)
            sp.dma_start(lane[:], lane_d).then_inc(routing_in, 16)
            for b in range(B):
                sp.dma_start(xt[:, b], x_transposed[b].rearrange("(k p) s -> p k s", p=P)).then_inc(routing_in, 16)
            for dst, w, shared, s in ((wg, w_gate, sw_gate, gate_in), (wu, w_up, sw_up, up_in)):
                for k in range(KD):
                    sp.dma_start(dst[:, k, 0:E0, :], w[:, P * k:P * k + P, :].rearrange("e p m -> p e m")).then_inc(s, 16)
                    sp.dma_start(dst[:, k, E0:NE, :].rearrange("p e m -> p (e m)"), shared[P * k:P * k + P, :]).then_inc(s, 16)
            sp.dma_start(wd[:, 0:E0, :], w_down.rearrange("e p n -> p e n")).then_inc(down_in, 16)
            sp.dma_start(wd[:, E0:NE, :], sw_down.rearrange("(e p) n -> p e n", p=P)).then_inc(down_in, 16)

        @block.tensor
        def _(pe):
            pe.sem_inc(downed, 2 * FREE)
            pe.wait_ge(routing_in, 16 * 8)
            for t in range(NT):
                b, i = divmod(t, TB)
                dst = bank[6][:, E0 * t:E0 * t + E0]
                for k in range(KD):
                    nc.tensor.matmul(dst, xt[:, b, k, P * i:P * i + P], wtt[:, k, :], start=k == 0, stop=False)
                ins = nc.tensor.matmul(dst, crep[:, b, :], wgt[:], start=False, stop=True)
            ins.then_inc(logits_done, 1)
            pe.wait_ge(gate_in, 64)
            pe.wait_ge(up_in, 64)
            pe.wait_ge(down_in, 32)

            with pe.Fori(0, B) as it:
                def down(e):
                    n = NE * it + e
                    pe.wait_ge(hid_ready, FREE + n + 1)
                    for j in range(2):
                        pe.wait_ge(added, 2 * n + j + 1)
                        for i in (2 * j, 2 * j + 1):
                            ins = nc.tensor.matmul(bank[4 + j][:, D * (i % 2):D * (i % 2) + D],
                                                   hid[:, e % 2, P * i:P * i + P], wd[:, e, :], start=True, stop=True)
                        ins.then_inc(downed, 1)

                for e in range(NE):
                    n = NE * it + e
                    pe.wait_ge(gate_copied, n + 1)
                    for k in range(KD):
                        ins = nc.tensor.matmul(bank[e % 2][:], wg[:, k, e, :], xt[:, it, k, :], start=k == 0, stop=k == KD - 1)
                    ins.then_inc(gated, 1)
                    pe.wait_ge(hid_ready, n + 1)
                    for k in range(KD):
                        ins = nc.tensor.matmul(bank[2 + e % 2][:], wu[:, k, e, :], xt[:, it, k, :], start=k == 0, stop=k == KD - 1)
                    ins.then_inc(upped, 1)
                    if e:
                        down(e - 1)
                down(NE - 1)

        @block.scalar
        def _(ac):
            ac.sem_inc(gate_copied, FREE)
            ac.wait_ge(exp_ready, 1)
            nc.scalar.activation(ex[:], exp_in[:], ACT.Exp).then_inc(exp_done, 1)
            with ac.Fori(0, B) as it:
                for e in range(NE):
                    n = NE * it + e
                    ac.wait_ge(gated, n + 1)
                    ac.wait_ge(leaked, n + 1)
                    nc.scalar.copy(gate[:, e % 2, :], bank[e % 2][:]).then_inc(gate_copied, 1)

        @block.vector
        def _(dv):
            dv.sem_inc(leaked, FREE)
            dv.sem_inc(hid_ready, FREE)
            dv.sem_inc(added, 2)
            st = Steps(dv, stepped)
            dv.wait_ge(logits_done, 1)
            st.after(nc.vector.tensor_scalar(logits[:], bank[6][:, 0:NT * E0].rearrange("p (t e) -> p t e", e=E0), 0.5, None, ALU.mult))
            route(nc, dv, st, logits, ex, zsum, best, best_at, lane, picked, weight, True, exp_in, exp_ready, exp_done)
            with dv.Fori(0, B) as it:
                def add(e):
                    n = NE * it + e
                    for j in range(2):
                        dv.wait_ge(downed, 2 * FREE + 2 * n + j + 1)
                        if e:
                            dv.wait_ge(added, 2 * n + 2)
                        for i in (2 * j, 2 * j + 1):
                            src = bank[4 + j][:, D * (i % 2):D * (i % 2) + D]
                            y = Y[:, TB * it + i, :]
                            if e == 0:
                                ins = nc.vector.tensor_scalar(y, src, weight[:, TB * it + i, 0:1], None, ALU.mult)
                            else:
                                w = weight[:, TB * it + i, e:e + 1] if e < E0 else 1.0
                                ins = nc.vector.scalar_tensor_tensor(y, src, w, y, ALU.mult, ALU.add)
                        ins.then_inc(added, 1)

                for e in range(NE):
                    n = NE * it + e
                    dv.wait_ge(gate_copied, FREE + n + 1)
                    nc.vector.scalar_tensor_tensor(leaky[:, e % 2, :], gate[:, e % 2, :], 0.01, gate[:, e % 2, :],
                                                   ALU.mult, ALU.max).then_inc(leaked, 1)
                    dv.wait_ge(leaked, FREE + n + 1)
                    dv.wait_ge(upped, n + 1)
                    dv.wait_ge(downed, 2 * n + 2)
                    nc.vector.tensor_tensor(hid[:, e % 2, :], leaky[:, e % 2, :], bank[2 + e % 2][:], ALU.mult).then_inc(hid_ready, 1)
                    if e:
                        add(e - 1)
                add(NE - 1)


def linear_attention(nc, sem, bank, X, Y, ident, keep_upper, wq_t, wk_t, wv_t, wo_t):
    K = 64
    with ExitStack() as ctx:
        def sb(name, shape, dt=F32):
            return ctx.enter_context(nc.sbuf_tensor(name, shape, dt))

        wqk = sb("la_wqk", [P, KD, 2, K])
        wv = sb("la_wv", [P, KD, K])
        wo = sb("la_wo", [K, D])
        keep = sb("la_keep", [P, P])
        y_row = sb("la_y_row", [P, TB, D])
        yt = sb("la_yt", [P, KD, S])
        below = sb("la_below", [K, 2, S])
        expd = sb("la_expd", [K, 2, S])
        qk = sb("la_qk", [K, 2, S])
        v1 = sb("la_v1", [P, TB, K + 1])
        at = sb("la_at", [P, TB, S])
        den = sb("la_den", [P, TB])
        o = sb("la_o", [P, TB, K])
        ot = sb("la_ot", [K, S])

        weights_in = sem("la_weights_in")
        row_copied = sem("la_row_copied")
        row_turned = sem("la_row_turned")
        yt_ready = sem("la_yt_ready")
        projected = sem("la_projected")
        below_ready = sem("la_below_ready")
        exp_ready = sem("la_exp_ready")
        qk_ready = sem("la_qk_ready")
        v1_ready = sem("la_v1_ready")
        ones_set = sem("la_ones_set")
        scored = sem("la_scored")
        at_ready = sem("la_at_ready")
        summed = sem("la_summed")
        den_steps = sem("la_den_steps")
        o_ready = sem("la_o_ready")
        o_turned = sem("la_o_turned")
        ot_ready = sem("la_ot_ready")
        out_done = sem("la_out_done")
        x_added = sem("la_x_added")
        block = ctx.enter_context(nc.Block())
        at_bank = [(5, 0), (6, 0), (7, 0), (6, 384)]

        @block.sync
        def _(sp):
            for n, w in enumerate((wq_t, wk_t)):
                sp.dma_start(wqk[:, :, n, :], w.rearrange("(k p) m -> p k m", p=P)).then_inc(weights_in, 16)
            sp.dma_start(wv[:], wv_t.rearrange("(k p) m -> p k m", p=P)).then_inc(weights_in, 16)
            sp.dma_start(wo[:], wo_t).then_inc(weights_in, 16)
            sp.dma_start(keep[:], keep_upper).then_inc(weights_in, 16)

        @block.gpsimd
        def _(gp):
            nc.gpsimd.memset(v1[:, :, K:K + 1], 1.0).then_inc(ones_set, 1)
            with gp.Fori(0, B) as b:
                gp.wait_ge(row_turned, 1 + b)
                nc.gpsimd.tensor_copy(y_row[:], Y[:, bass.ds(TB * b, TB), :]).then_inc(row_copied, 1)

        @block.tensor
        def _(pe):
            pe.sem_inc(row_turned, 1)
            pe.sem_inc(projected, 1)
            pe.wait_ge(weights_in, 80)
            pe.wait_ge(ones_set, 1)
            with pe.Fori(0, B) as b:
                pe.wait_ge(row_copied, b + 1)
                for k in range(KD):
                    for i in range(TB):
                        ins = nc.tensor.transpose(bank[k][:, P * i:P * i + P], y_row[:, i, P * k:P * k + P], ident[:])
                ins.then_inc(row_turned, 1)
                pe.wait_ge(yt_ready, b + 1)
                for n in range(2):
                    for k in range(KD):
                        nc.tensor.matmul(bank[2 + n][0:K, :], wqk[:, k, n, :], yt[:, k, :], start=k == 0, stop=k == KD - 1)
                for i in range(TB):
                    for k in range(KD):
                        ins = nc.tensor.matmul(bank[4][:, K * i:K * i + K], yt[:, k, P * i:P * i + P], wv[:, k, :],
                                               start=k == 0, stop=k == KD - 1)
                ins.then_inc(projected, 1)
                pe.wait_ge(qk_ready, b + 1)
                pe.wait_ge(x_added, b + 1)
                for c, (n, at_col) in enumerate(at_bank):
                    w = S - P * c
                    ins = nc.tensor.matmul(bank[n][:, at_col:at_col + w], qk[:, 1, P * c:P * c + P], qk[:, 0, P * c:S],
                                           start=True, stop=True)
                ins.then_inc(scored, 1)
                pe.wait_ge(at_ready, b + 1)
                pe.wait_ge(v1_ready, b + 1)
                for r in range(TB):
                    for c in range(r + 1):
                        ins = nc.tensor.matmul(bank[2][:, (K + 1) * r:(K + 1) * (r + 1)], at[:, c, P * r:P * r + P], v1[:, c, :],
                                               start=c == 0, stop=c == r)
                ins.then_inc(summed, 1)
                wait_apart(pe, o_ready, b + 1)
                for r in range(TB):
                    ins = nc.tensor.transpose(bank[3][0:K, P * r:P * r + P], o[:, r, :], ident[:])
                ins.then_inc(o_turned, 1)
                pe.wait_ge(ot_ready, b + 1)
                for r in range(TB):
                    ins = nc.tensor.matmul(bank[5 + r // 2][:, D * (r % 2):D * (r % 2) + D], ot[:, P * r:P * r + P], wo[:],
                                           start=True, stop=True)
                ins.then_inc(out_done, 1)

        @block.scalar
        def _(ac):
            with ac.Fori(0, B) as b:
                ac.wait_ge(row_turned, 2 + b)
                ac.wait_ge(projected, 1 + b)
                for k in range(KD):
                    ins = nc.scalar.copy(yt[:, k, :], bank[k][:])
                ins.then_inc(yt_ready, 1)
                ac.wait_ge(below_ready, b + 1)
                nc.scalar.activation(expd[:], below[:], ACT.Exp).then_inc(exp_ready, 1)
                nc.scalar.copy(v1[:, :, 0:K], bank[4][:, 0:TB * K].rearrange("p (i m) -> p i m", i=TB)).then_inc(v1_ready, 1)
                ac.wait_ge(o_turned, b + 1)
                nc.scalar.copy(ot[:], bank[3][0:K, :]).then_inc(ot_ready, 1)

        @block.vector
        def _(dv):
            dv.sem_inc(x_added, 1)
            dv.wait_ge(weights_in, 80)
            with dv.Fori(0, B) as b:
                dv.wait_ge(projected, 2 + b)
                for n in range(2):
                    ins = nc.vector.tensor_scalar(below[:, n, :], bank[2 + n][0:K, :], 0.0, None, ALU.min)
                ins.then_inc(below_ready, 1)
                dv.wait_ge(exp_ready, b + 1)
                for n in range(2):
                    ins = nc.vector.scalar_tensor_tensor(qk[:, n, :], bank[2 + n][0:K, :], 0.0, expd[:, n, :], ALU.max, ALU.add)
                ins.then_inc(qk_ready, 1)
                dv.wait_ge(scored, b + 1)
                for c, (n, col) in enumerate(at_bank):
                    lo = P * c
                    ins = nc.vector.tensor_tensor(at[:, c, lo:lo + P], bank[n][:, col:col + P], keep[:], ALU.mult)
                    if c < TB - 1:
                        ins = nc.vector.tensor_copy(at[:, c, lo + P:S], bank[n][:, col + P:col + S - lo])
                ins.then_inc(at_ready, 1)
                dv.wait_ge(summed, b + 1)
                sums = bank[2][:, 0:(K + 1) * TB].rearrange("p (r m) -> p r m", r=TB)
                st = Steps(dv, den_steps, 2 * b, 2)
                st.after(nc.vector.tensor_scalar(den[:], sums[:, :, K], 1e-6, None, ALU.add))
                st.after(nc.vector.reciprocal(den[:], den[:]))
                st.close()
                for r in range(TB):
                    ins = nc.vector.tensor_scalar(o[:, r, :], sums[:, r, 0:K], den[:, r:r + 1], None, ALU.mult)
                ins.then_inc(o_ready, 1)
                dv.wait_ge(out_done, b + 1)
                for r in range(TB):
                    x = X[:, TB * b + r, :]
                    ins = nc.vector.tensor_tensor(x, x, bank[5 + r // 2][:, D * (r % 2):D * (r % 2) + D], ALU.add)
                ins.then_inc(x_added, 1)


def attention_inputs(nc, sem, pre, bank, X, ident, w, q_all, kt, v_all, null_neg, null_v):
    cosine = "q_scale" in w
    kt_high, kt_low, mask_row = kt
    with ExitStack() as ctx:
        def sb(name, shape, dt=F32):
            return ctx.enter_context(nc.sbuf_tensor(pre + name, shape, dt))

        wq = sb("wq", [P, KD, H * DH])
        wkv = sb("wkv", [P, KD, 2 * DH])
        g_norm = sb("g_norm", [P, KD])
        null_k = sb("null_k", [P, DH])
        null_w = sb("null_w", [P, KD, H])
        null_b = sb("null_b", [P, H])
        null_t = sb("null_t", [P, TB, H])
        null_p = sb("null_p", [P, KD, H, DH])
        mask_words = sb("mask_words", [1, B * S // 4], I32)
        mask8 = mask_words[:].bitcast(U8)
        scales = sb("scales", [P, 2, DH])
        kt_full = sb("kt_full", [P, B, S])
        kt_bits = sb("kt_bits", [P, B, S], I32)
        kcol = sb("kcol", [P, 3])
        one = sb("one", [P, 3])
        xn = sb("xn", [P, TB, D])
        xnt = sb("xnt", [P, KD, S])
        stats = sb("stats", [P, TB, 6])
        mv = sb("mv", [P, TB, 2])
        var = sb("var", [P, TB])
        sd = sb("sd", [P, TB])
        rstd = sb("rstd", [P, TB])
        squares = sb("squares", [P, 2, 512])
        k_raw = sb("k_raw", [P, TB, DH])
        k_sq = sb("k_sq", [P, TB, DH])
        k_n = sb("k_n", [P, TB, 2, DH])
        ss = sb("ss", [P, TB * (H + 1)])
        norm = sb("norm", [P, TB * (H + 1)])
        rinv = sb("rinv", [P, TB * (H + 1)])

        params_in = sem(pre + "params_in")
        prologue = sem(pre + "prologue")
        null_ss = sem(pre + "null_ss")
        null_sd = sem(pre + "null_sd")
        stepped = sem(pre + "stepped")
        var_ready = sem(pre + "var_ready")
        sd_ready = sem(pre + "sd_ready")
        xn_ready = sem(pre + "xn_ready")
        xn_turned = sem(pre + "xn_turned")
        xnt_ready = sem(pre + "xnt_ready")
        kv_done = sem(pre + "kv_done")
        k_copied = sem(pre + "k_copied")
        q_done = sem(pre + "q_done")
        q_copied = sem(pre + "q_copied")
        q_summed = sem(pre + "q_summed")
        ss_ready = sem(pre + "ss_ready")
        norm_ready = sem(pre + "norm_ready")
        rinv_ready = sem(pre + "rinv_ready")
        kn_ready = sem(pre + "kn_ready")
        k_turned = sem(pre + "k_turned")
        kt_ready = sem(pre + "kt_ready")
        null_done = sem(pre + "null_done")
        q_scaled = sem(pre + "q_scaled")
        k_split = sem(pre + "k_split")
        block = ctx.enter_context(nc.Block())
        n_params = 8 + 6 * cosine
        PRO = 11 if cosine else 5
        LOOP = 5 if cosine else 4
        NQ = 2 * TB
        AHEAD = 4

        @block.sync
        def _(sp):
            sp.dma_start(g_norm[:], columns(w["g_norm"], KD)).then_inc(params_in, 16)
            sp.dma_start(wkv[:], w["Wkv"].rearrange("(k p) n -> p k n", p=P)).then_inc(params_in, 16)
            for k in range(KD):
                sp.dma_start(wq[:, k, :], w["Wq"][P * k:P * k + P, :]).then_inc(params_in, 16)
            sp.dma_start(null_k[:], rows(w["cond"][0])).then_inc(params_in, 16)
            for half in range(2):
                sp.dma_start(null_v[DH * half:DH * half + DH, :], w["cond"][1].rearrange("(d a) -> d a", a=1)).then_inc(params_in, 16)
            sp.dma_start(null_b[:], rows(w["null_attn_bias"])).then_inc(params_in, 16)
            sp.dma_start(mask_words[:], w["mask"].rearrange("b s -> (b s)").rearrange("(a n) -> a n", a=1)).then_inc(params_in, 16)
            if cosine:
                for n, name in enumerate(("q_scale", "k_scale")):
                    sp.dma_start(scales[:, n, :], rows(w[name])).then_inc(params_in, 16)
                    for half in range(2):
                        sp.dma_start(kcol[DH * half:DH * half + DH, n:n + 1], w[name].rearrange("(d a) -> d a", a=1)).then_inc(params_in, 16)

        @block.gpsimd
        def _(gp):
            if cosine:
                gp.sem_inc(q_scaled, 1)
                with gp.Fori(0, B) as b:
                    gp.wait_ge(rinv_ready, b + 1)
                    for i in range(TB):
                        q = q_all[:, TB * b + i]
                        r = rinv[:, H * i:H * i + H].unsqueeze(2).broadcast_to([P, H, DH])
                        ins = nc.gpsimd.tensor_tensor(q, q, r, ALU.mult)
                    ins.then_inc(q_scaled, 1)

        @block.tensor
        def _(pe):
            pe.wait_ge(params_in, 16 * (n_params + 1))
            pe.wait_ge(prologue, PRO)
            with pe.Fori(0, B) as b:
                pe.wait_ge(xn_ready, b + 1)
                for k in range(KD):
                    for i in range(TB):
                        ins = nc.tensor.transpose(bank[k][:, P * i:P * i + P], xn[:, i, P * k:P * k + P], ident[:])
                ins.then_inc(xn_turned, 1)
                pe.wait_ge(xnt_ready, b + 1)
                for i in range(TB):
                    for k in range(KD):
                        nc.tensor.matmul(bank[2][:, P * i:P * i + P], xnt[:, k, P * i:P * i + P], wkv[:, k, :],
                                         start=k == 0, stop=k == KD - 1)
                pe.wait_ge(null_done, b + 1)
                for i in range(TB):
                    for k in range(KD):
                        ins = nc.tensor.matmul(bank[3][:, H * i:H * i + H], xnt[:, k, P * i:P * i + P], null_w[:, k, :],
                                               start=k == 0, stop=k == KD - 1)
                ins.then_inc(kv_done, 1)
                for m in range(NQ):
                    i, half = divmod(m, 2)
                    pe.wait_ge(q_copied, NQ * b + m + 1)
                    for k in range(KD):
                        ins = nc.tensor.matmul(bank[4 + m % 4][:], xnt[:, k, P * i:P * i + P],
                                               wq[:, k, 512 * half:512 * half + 512], start=k == 0, stop=k == KD - 1)
                    ins.then_inc(q_done, 1)
                wait_apart(pe, kn_ready, b + 1)
                for i in range(TB):
                    ins = nc.tensor.transpose(bank[2][:, P * i:P * i + P], k_n[:, i].rearrange("p s d -> p (s d)"), ident[:])
                ins.then_inc(k_turned, 1)
                pe.wait_ge(kt_ready, b + 1)

        @block.scalar
        def _(ac):
            ac.sem_inc(q_copied, AHEAD)
            if cosine:
                ac.wait_ge(null_ss, 1)
                nc.scalar.activation(one[:, 2:3], one[:, 1:2], ACT.Sqrt).then_inc(null_sd, 1)
            ac.wait_ge(prologue, PRO)
            with ac.Fori(0, B) as b:
                ac.wait_ge(var_ready, b + 1)
                nc.scalar.activation(sd[:], var[:], ACT.Sqrt).then_inc(sd_ready, 1)
                ac.wait_ge(xn_turned, b + 1)
                for k in range(KD):
                    ins = nc.scalar.activation(xnt[:, k, :], bank[k][:], ACT.Copy, scale=g_norm[:, k:k + 1])
                ins.then_inc(xnt_ready, 1)
                ac.wait_ge(kv_done, b + 1)
                kv = bank[2][:].rearrange("p (i n) -> p i n", i=TB)
                nc.scalar.copy(k_raw[:], kv[:, :, 0:DH]).then_inc(k_copied, 1)
                nc.scalar.copy(v_all[:, bass.ds(TB * b, TB), :], kv[:, :, DH:2 * DH])
                for m in range(NQ):
                    i, half = divmod(m, 2)
                    ac.wait_ge(q_done, NQ * b + m + 1)
                    if cosine:
                        ac.wait_ge(q_summed, NQ * b + m + 1)
                        nc.scalar.activation(squares[:, m % 2, :], bank[4 + m % 4][:], ACT.Square)
                    nc.scalar.copy(q_all[:, TB * b + i, 8 * half:8 * half + 8, :],
                                   bank[4 + m % 4][:].rearrange("p (h d) -> p h d", d=DH)).then_inc(q_copied, 1)
                if cosine:
                    ac.wait_ge(ss_ready, b + 1)
                    nc.scalar.activation(norm[:], ss[:], ACT.Sqrt).then_inc(norm_ready, 1)
                ac.wait_ge(k_turned, b + 1)
                nc.scalar.activation(kt_full[:, b, :], bank[2][:], ACT.Copy, scale=kcol[:, 2:3]).then_inc(kt_ready, 1)

        @block.vector
        def _(dv):
            pro = Steps(dv, prologue)
            dv.sem_inc(null_done, 1)
            dv.sem_inc(q_summed, 2)
            dv.wait_ge(params_in, 16 * (n_params + 1))
            pro.after(nc.vector.tensor_scalar(mask_row[:], mask8, 1.0, -MASKED, ALU.subtract, ALU.mult))
            if cosine:
                pro.after(nc.vector.tensor_tensor_reduce(out=k_sq[:, 0, :], in0=null_k[:], in1=null_k[:], scale=1.0, scalar=0.0,
                                                         op0=ALU.mult, op1=ALU.add, accum_out=one[:, 0:1]))
                nc.vector.tensor_scalar(one[:, 1:2], one[:, 0:1], 1e-24, None, ALU.max).then_inc(null_ss, 1)
                dv.wait_ge(null_sd, 1)
                pro.after(nc.vector.reciprocal(one[:, 0:1], one[:, 2:3]))
                pro.after(nc.vector.tensor_scalar(null_k[:], null_k[:], one[:, 0:1], None, ALU.mult))
                pro.after(nc.vector.tensor_scalar(null_k[:], null_k[:], 8.0, None, ALU.mult))
                pro.after(nc.vector.tensor_tensor(null_k[:], null_k[:], scales[:, 0, :], ALU.mult))
                pro.after(nc.vector.tensor_tensor(null_k[:], null_k[:], scales[:, 1, :], ALU.mult))
                pro.after(nc.vector.tensor_tensor(kcol[:, 2:3], kcol[:, 0:1], kcol[:, 1:2], ALU.mult))
                pro.after(nc.vector.tensor_scalar(kcol[:, 2:3], kcol[:, 2:3], 8.0, None, ALU.mult))
            else:
                pro.after(nc.vector.tensor_scalar(null_k[:], null_k[:], DH ** -0.5, None, ALU.mult))
                pro.after(nc.vector.memset(kcol[:, 2:3], DH ** -0.5))
            for k in range(KD):
                q4 = wq[:, k, :].rearrange("p (h d) -> p h d", h=H)
                ins = nc.vector.tensor_tensor(null_p[:, k], q4, null_k[:].unsqueeze(1).broadcast_to([P, H, DH]), ALU.mult)
            pro.after(ins)
            pro.after(nc.vector.tensor_reduce(null_w[:], null_p[:], AX.X, ALU.add))
            assert pro.n == PRO, pro.n
            with dv.Fori(0, B) as b:
                st = Steps(dv, stepped, LOOP * b, LOOP)
                for i in range(TB):
                    ins = nc.vector.bn_stats(stats[:, i, :], X[:, TB * b + i, :])
                st.after(ins, apart=True)
                for i in range(TB):
                    ins = nc.vector.bn_aggr(mv[:, i, :], stats[:, i, :])
                st.after(ins)
                nc.vector.tensor_scalar(var[:], mv[:, :, 1], EPS, None, ALU.add).then_inc(var_ready, 1)
                dv.wait_ge(sd_ready, b + 1)
                st.after(nc.vector.reciprocal(rstd[:], sd[:]))
                for i in range(TB):
                    ins = nc.vector.tensor_scalar(xn[:, i, :], X[:, TB * b + i, :], mv[:, i, 0:1], rstd[:, i:i + 1],
                                                  ALU.subtract, ALU.mult)
                ins.then_inc(xn_ready, 1)
                dv.wait_ge(k_copied, b + 1)
                null = bank[3][:, 0:TB * H].rearrange("p (i h) -> p i h", i=TB)
                if cosine:
                    st.after(nc.vector.tensor_tensor(k_sq[:], k_raw[:], k_raw[:], ALU.mult))
                    nc.vector.tensor_reduce(ss[:, TB * H:], k_sq[:], AX.X, ALU.add)
                    for m in range(NQ):
                        dv.wait_ge(q_copied, AHEAD + NQ * b + m + 1)
                        nc.vector.tensor_reduce(ss[:, 8 * m:8 * m + 8], squares[:, m % 2, :].rearrange("p (h d) -> p h d", d=DH),
                                                AX.X, ALU.add).then_inc(q_summed, 1)
                    dv.wait_ge(q_summed, 2 + NQ * b + NQ)
                    nc.vector.tensor_scalar(ss[:], ss[:], 1e-24, None, ALU.max).then_inc(ss_ready, 1)
                    dv.wait_ge(norm_ready, b + 1)
                    dv.wait_ge(q_scaled, b + 1)
                    nc.vector.reciprocal(rinv[:], norm[:]).then_inc(rinv_ready, 1)
                    dv.wait_ge(rinv_ready, b + 1)
                    for half in range(2):
                        ins = nc.vector.tensor_tensor(k_n[:, :, half, :], k_raw[:], rinv[:, TB * H:].unsqueeze(2).broadcast_to([P, TB, DH]),
                                                      ALU.mult)
                    ins.then_inc(kn_ready, 1)
                    dv.wait_ge(kv_done, b + 1)
                    st.after(nc.vector.tensor_tensor(null_t[:], null, rinv[:, 0:TB * H].rearrange("p (i h) -> p i h", i=TB), ALU.mult))
                else:
                    for half in range(2):
                        ins = nc.vector.tensor_copy(k_n[:, :, half, :], k_raw[:])
                    ins.then_inc(kn_ready, 1)
                    dv.wait_ge(kv_done, b + 1)
                    st.after(nc.vector.tensor_copy(null_t[:], null))
                nc.vector.scalar_tensor_tensor(null_neg[:, :, bass.ds(TB * b, TB)], null_t[:].rearrange("p i h -> p h i"), -1.0,
                                               null_b[:].unsqueeze(2).broadcast_to([P, H, TB]), ALU.mult,
                                               ALU.subtract).then_inc(null_done, 1)
                st.close()
            dv.wait_ge(kt_ready, B)
            high_part(nc, kt_bits[:], kt_full[:]).then_inc(k_split, 1)
            dv.wait_ge(k_split, 1)
            nc.vector.tensor_copy(kt_high[:], kt_bits[:].bitcast(F32))
            nc.vector.tensor_tensor(kt_low[:], kt_full[:], kt_bits[:].bitcast(F32), ALU.subtract)




def attention_core(nc, sem, pre, bank, ident, w, q_src, kt, v_all, null_neg, neg_max, row_sum, o_all):
    rotary = w["bias"] == "none"
    dh = DR if rotary else DH
    kd = 4 * DR if rotary else 2 * DH
    HU = B * TB
    HT = 2 * HU
    TURNS = H // 2
    with ExitStack() as ctx:
        def sb(name, shape, dt=F32):
            return ctx.enter_context(nc.sbuf_tensor(pre + name, shape, dt))

        full = w["bias"] == "full"
        first_col = [0, P, 3 * P, 6 * P]
        bias = [sb(f"bias{j}", [P, 10 * P if full else S]) for j in range(2)]
        q_row = [sb(f"q_row{j}", [P, TB, 2, 4, DR] if rotary else [P, TB, 2, DH], F32R) for j in range(2)]
        q_bits = [sb(f"q_bits{j}", [P, TB, 2, DR] if rotary else [P, TB, DH], I32) for j in range(2)]
        qt = [sb(f"qt{j}", [kd, 2 if rotary else 1, S], F32R) for j in range(2)]
        ones = sb("ones", [1, P], F32R)
        unit = sb("unit", [P, P], F32R)
        score_bank = (bank[0], bank[1], bank[7])
        logit_neg = sb("logit_neg", [P, 4, S])
        prob = sb("prob", [P, 4, S])
        prob_t = sb("prob_t", [P, 2, S])
        null_h = [sb(f"null_h{j}", [P, HU]) for j in range(2)]
        max_h = [sb(f"max_h{j}", [P, HU]) for j in range(2)]
        sum_h = [sb(f"sum_h{j}", [P, HU]) for j in range(2)]

        bias_in = [sem(pre + f"bias_in{j}") for j in range(2)]
        head_ready = sem(pre + "head_ready")
        unit_ready = sem(pre + "unit_ready")
        bias_filled = sem(pre + "bias_filled")
        q_high = sem(pre + "q_high")
        q_staged = sem(pre + "q_staged")
        q_turned = sem(pre + "q_turned")
        qt_ready = sem(pre + "qt_ready")
        scored = sem(pre + "scored")
        biased = sem(pre + "biased")
        exped = sem(pre + "exped")
        turned = sem(pre + "turned")
        pt_ready = sem(pre + "pt_ready")
        pv_done = sem(pre + "pv_done")
        o_copied = sem(pre + "o_copied")
        sums_kept = sem(pre + "sums_kept")
        block = ctx.enter_context(nc.Block())

        def turns(eng, body):
            body(0, True, False)
            with eng.Fori(1, TURNS - 1) as t:
                body(t, False, False)
            body(TURNS - 1, False, True)

        def bias_of(j, r):
            if full:
                return bias[j][:, first_col[r]:first_col[r] + P * (r + 1)]
            return bias[j][:, P * (TB - 1 - r):S]

        def diagonals(j):
            if full:
                return [bias[j][:, first_col[r] + P * r:first_col[r] + P * (r + 1)] for r in range(TB)]
            return [bias[j][:, P * (TB - 1):S]]

        @block.sync
        def _(sp):
            def load_full(t, first, last):
                for j in range(2):
                    if not first:
                        sp.wait_ge(biased, HT * t - HT + HU * (j + 1))
                    for r in range(TB):
                        sp.dma_start(bias_of(j, r), w["full"][2 * t + j, P * r:P * r + P, 0:P * (r + 1)]).then_inc(bias_in[j], 16)

            if full:
                turns(sp, load_full)
            elif not rotary:
                for h in range(H):
                    if h >= 2:
                        sp.wait_ge(biased, HU * (h - 1))
                    src = w["copies"]
                    skew = bass.AP(tensor=src.tensor, offset=src.offset + P * NPOS * h + P - 1, ap=[[NPOS - 1, P], [1, S]])
                    sp.dma_start(bias[h % 2][:], skew).then_inc(bias_in[h % 2], 16)

        @block.gpsimd
        def _(gp):
            nc.gpsimd.tensor_copy(unit[:], ident[:]).then_inc(unit_ready, 1)
            fills = len(diagonals(0))
            n_in = 16 * (TB if full else 1)

            def stage(t, first, blk):
                j, b = divmod(blk, B)
                if not (first and blk < 2):
                    gp.wait_ge(q_turned, 2 * B * t + blk - 1)
                gp.wait_ge(q_high, 2 * B * t + blk + 1)
                h = 2 * t + j
                row = q_row[blk % 2]
                if rotary:
                    src = q_src[:, TB * b:TB * b + TB, :, h, :]
                    high = q_bits[blk % 2][:].bitcast(F32)
                    for s, highs, lows in ((0, (0, 1), (2, 3)), (1, (0, 2), (1, 3))):
                        for n in lows:
                            nc.gpsimd.tensor_tensor(row[:, :, s, n, :], src[:, :, s, :], high[:, :, s, :], ALU.subtract)
                        for n in highs:
                            ins = nc.gpsimd.tensor_copy(row[:, :, s, n, :], high[:, :, s, :])
                else:
                    high = q_bits[blk % 2][:].bitcast(F32)
                    nc.gpsimd.tensor_tensor(row[:, :, 1, :], q_src[:, TB * b:TB * b + TB, h, :], high, ALU.subtract)
                    ins = nc.gpsimd.tensor_copy(row[:, :, 0, :], high)
                ins.then_inc(q_staged, 1)

            def keep_sums(t, j):
                h = 2 * t + j
                gp.wait_ge(exped, HT * t + HU * (j + 1))
                nc.gpsimd.tensor_copy(neg_max[:, h, :], max_h[j][:])
                nc.gpsimd.tensor_copy(row_sum[:, h, :], sum_h[j][:]).then_inc(sums_kept, 1)

            def head(t, first, last):
                for j in range(2):
                    if not first:
                        gp.wait_ge(biased, HT * t - HT + HU * (j + 1))
                    if not rotary:
                        nc.gpsimd.tensor_copy(null_h[j][:], null_neg[:, 2 * t + j, :]).then_inc(head_ready, 1)
                        wait_apart(gp, bias_in[j], n_in * t + n_in)
                        for d in diagonals(j):
                            nc.gpsimd.affine_select(out=d, in_=d, compare_op=ALU.is_ge, fill=MASKED, base=0,
                                                    pattern=[[-1, P]], channel_multiplier=1).then_inc(head_ready, 1)
                    stage(t, first, B * j)
                    stage(t, first, B * j + 1)
                    if j == 1:
                        keep_sums(t, 0)
                    elif not first:
                        keep_sums(t - 1, 1)
                    stage(t, first, B * j + 2)
                    stage(t, first, B * j + 3)
                if last:
                    keep_sums(t, 1)

            if rotary:
                for j in range(2):
                    nc.gpsimd.memset(bias[j][:], 0.0).then_inc(bias_filled, 1)
                gp.wait_ge(bias_filled, 2)
                for j in range(2):
                    for d in diagonals(j):
                        nc.gpsimd.affine_select(out=d, in_=d, compare_op=ALU.is_ge, fill=MASKED, base=0,
                                                pattern=[[-1, P]], channel_multiplier=1).then_inc(head_ready, 1)
            else:
                nc.gpsimd.tensor_scalar(ones[:], ident[0:1, :], 0.0, 1.0, ALU.mult, ALU.add).then_inc(bias_filled, 2)
            turns(gp, head)

        @block.tensor
        def _(pe):
            def turn_q(t, first, blk):
                g = 2 * B * t + blk
                wait_apart(pe, q_staged, g + 1)
                if not (first and blk == 0):
                    wait_apart(pe, qt_ready, g)
                for i in range(TB):
                    src = q_row[blk % 2][:, i].rearrange("p s n d -> p (s n d)" if rotary else "p s d -> p (s d)")
                    ins = nc.tensor.transpose(bank[6][:, P * i:P * i + P].bitcast(F32R), src, unit[:])
                ins.then_inc(q_turned, 1)

            def score(t, u):
                blk, r = divmod(u, TB)
                b = blk % B
                if r == 0:
                    pe.wait_ge(qt_ready, 2 * B * t + blk + 1)
                q = qt[blk % 2][:, 0, P * r:P * r + P]
                dst = score_bank[u % 3][:, 0:P * (r + 1)]
                if rotary:
                    ins = nc.tensor.matmul(dst, q, qt[blk % 2][:, 1, 0:P * (r + 1)], start=True, stop=True)
                else:
                    kt_high, kt_low, mask_row = kt
                    nc.tensor.matmul(dst, q, kt_high[:, b, 0:P * (r + 1)], start=True, stop=False)
                    nc.tensor.matmul(dst, q, kt_low[:, b, 0:P * (r + 1)], start=False, stop=False)
                    ins = nc.tensor.matmul(dst, ones[:], mask_row[:, S * b:S * b + P * (r + 1)], start=False, stop=True)
                ins.then_inc(scored, 1)

            def times_v(t, first, u):
                blk, r = divmod(u, TB)
                b, j = blk % B, blk // B
                pe.wait_ge(pt_ready, HT * t + u + 1)
                if r == 0 and not (first and blk < 2):
                    pe.wait_ge(o_copied, 2 * B * t + blk - 1)
                for c in range(r + 1):
                    v = v_all[:, TB * b + c, bass.ds(dh * (2 * t + j), DH)] if rotary else v_all[:, TB * b + c, :]
                    ins = nc.tensor.matmul(bank[4 + blk % 2][:, DH * r:DH * r + DH], prob_t[:, u % 2, P * c:P * c + P], v,
                                           start=c == 0, stop=c == r)
                ins.then_inc(pv_done, 1)

            def turn(t, first, last):
                for u in range(HT):
                    blk, r = divmod(u, TB)
                    if r == 2 and blk + 2 < 2 * B:
                        turn_q(t, first, blk + 2)
                    elif r == 2 and not last:
                        turn_q(t + 1, False, blk + 2 - 2 * B)
                    pe.wait_ge(exped, HT * t + u + 1)
                    for c in range(r + 1):
                        ins = nc.tensor.transpose(bank[2 + u % 2][:, P * c:P * c + P], prob[:, u % 4, P * c:P * c + P], ident[:])
                    ins.then_inc(turned, 1)
                    if u + 3 < HT:
                        score(t, u + 3)
                    elif not last:
                        if u + 3 - HT < HT % 3:
                            pe.wait_ge(biased, HT * t + u + 2)
                        score(t + 1, u + 3 - HT)
                    if u:
                        times_v(t, first, u - 1)
                    elif not first:
                        times_v(t - 1, False, HT - 1)
                if last:
                    times_v(t, False, HT - 1)

            pe.wait_ge(unit_ready, 1)
            pe.wait_ge(bias_filled, 2)
            turn_q(0, True, 0)
            turn_q(0, True, 1)
            for u in range(3):
                score(0, u)
            turns(pe, turn)

        @block.scalar
        def _(ac):
            def copy_qt(t, first, blk):
                g = 2 * B * t + blk
                ac.wait_ge(q_turned, g + 1)
                if not (first and blk < 2):
                    ac.wait_ge(scored, TB * (g - 1))
                for s in range(2 if rotary else 1):
                    ins = nc.scalar.copy(qt[blk % 2][:, s, :], bank[6][kd * s:kd * s + kd, :].bitcast(F32R))
                ins.then_inc(qt_ready, 1)

            def exp(t, first, u):
                j, n = divmod(u, HU)
                ac.wait_ge(biased, HT * t + u + 1)
                if not (first and u < 4):
                    ac.wait_ge(turned, HT * t + u - 3)
                wd = P * (u % TB + 1)
                nc.scalar.activation(prob[:, u % 4, 0:wd], logit_neg[:, u % 4, 0:wd], ACT.Exp, bias=max_h[j][:, n:n + 1],
                                     scale=-1.0, accum_out=sum_h[j][:, n:n + 1]).then_inc(exped, 1)

            def copy_o(t, blk):
                j, b = divmod(blk, B)
                ac.wait_ge(pv_done, TB * (2 * B * t + blk + 1))
                nc.scalar.copy(o_all[:, TB * b:TB * b + TB, 2 * t + j, :],
                               bank[4 + blk % 2][:, 0:TB * DH].rearrange("p (i d) -> p i d", i=TB)[:, :, 0:dh]).then_inc(o_copied, 1)

            def turn(t, first, last):
                for u in range(HT):
                    blk, r = divmod(u, TB)
                    if u + 2 < HT:
                        exp(t, first, u + 2)
                    elif not last:
                        exp(t + 1, False, u + 2 - HT)
                    if r == 2 and blk + 2 < 2 * B:
                        copy_qt(t, first, blk + 2)
                    elif r == 2 and not last:
                        copy_qt(t + 1, False, blk + 2 - 2 * B)
                    if r == 1 and blk:
                        copy_o(t, blk - 1)
                    elif r == 1 and not first:
                        copy_o(t - 1, 2 * B - 1)
                if last:
                    copy_o(t, 2 * B - 1)

            copy_qt(0, True, 0)
            copy_qt(0, True, 1)
            exp(0, True, 0)
            exp(0, True, 1)
            turns(ac, turn)

        @block.vector
        def _(dv):
            per_head = 1 if rotary else 1 + len(diagonals(0))

            def add_bias(t, first, u):
                j, n = divmod(u, HU)
                if n == 0:
                    if not rotary:
                        dv.wait_ge(head_ready, per_head * (2 * t + j + 1))
                    elif first:
                        dv.wait_ge(head_ready, 2)
                    if not first:
                        dv.wait_ge(sums_kept, 2 * t + j - 1)
                wait_apart(dv, scored, HT * t + u + 1)
                r = n % TB
                wd = P * (r + 1)
                nc.vector.tensor_tensor_reduce(out=logit_neg[:, u % 4, 0:wd], in0=score_bank[u % 3][:, 0:wd], in1=bias_of(j, r),
                                               scale=-(dh ** -0.5) if rotary else -1.0,
                                               scalar=-MASKED if rotary else null_h[j][:, n:n + 1],
                                               op0=ALU.add, op1=ALU.min, accum_out=max_h[j][:, n:n + 1]).then_inc(biased, 1)

            def split_q(t, first, blk):
                j, b = divmod(blk, B)
                h = 2 * t + j
                if not (first and blk < 2):
                    dv.wait_ge(q_staged, 2 * B * t + blk - 1)
                src = q_src[:, TB * b:TB * b + TB, :, h, :] if rotary else q_src[:, TB * b:TB * b + TB, h, :]
                high_part(nc, q_bits[blk % 2][:], src).then_inc(q_high, 1)

            def copy_pt(t, first, u):
                dv.wait_ge(turned, HT * t + u + 1)
                if not (first and u < 2):
                    dv.wait_ge(pv_done, HT * t + u - 1)
                wd = P * (u % TB + 1)
                nc.vector.tensor_copy(prob_t[:, u % 2, 0:wd], bank[2 + u % 2][:, 0:wd]).then_inc(pt_ready, 1)

            def turn(t, first, last):
                for u in range(HT):
                    if u + 2 < HT:
                        add_bias(t, first, u + 2)
                    elif not last:
                        add_bias(t + 1, False, u + 2 - HT)
                    copy_pt(t, first, u)
                    ahead = u // TB + 3
                    if u % TB == 1 and ahead < 2 * B:
                        split_q(t, first, ahead)
                    elif u % TB == 1 and not last:
                        split_q(t + 1, False, ahead - 2 * B)

            for blk in range(3):
                split_q(0, True, blk)
            add_bias(0, True, 0)
            add_bias(0, True, 1)
            turns(dv, turn)


def attention_output(nc, sem, pre, bank, Y, ident, w, o_all, null_neg, null_v, neg_max, row_sum):
    with ExitStack() as ctx:
        def sb(name, shape, dt=F32):
            return ctx.enter_context(nc.sbuf_tensor(pre + name, shape, dt))

        wout = sb("wout", [P, H * DH // P, D])
        g_out = sb("g_out", [P, D])
        null_p = sb("null_p", [P, H, NT])
        rinv = sb("rinv", [P, H, NT])
        spread = sb("spread", [P, H // 2, H])
        null_o = sb("null_o", [H, D])
        os = sb("os", [P, 2, H * DH])
        ps = sb("ps", [P, 2, H])
        ot = sb("ot", [P, 2, H * DH])
        pt = sb("pt", [H, 2, P])
        stats = sb("stats", [P, TB, 6])
        mv = sb("mv", [P, TB, 2])
        var = sb("var", [P, TB])
        sd = sb("sd", [P, TB])
        rstd = sb("rstd", [P, TB])
        yn = sb("yn", [P, TB, D])

        params_in = sem(pre + "params_in")
        pre_steps = sem(pre + "pre_steps")
        null_ready = sem(pre + "null_ready")
        null_exped = sem(pre + "null_exped")
        null_o_done = sem(pre + "null_o_done")
        null_o_ready = sem(pre + "null_o_ready")
        scaled = sem(pre + "scaled")
        turned = sem(pre + "turned")
        ot_ready = sem(pre + "ot_ready")
        projected = sem(pre + "projected")
        stepped = sem(pre + "stepped")
        var_ready = sem(pre + "var_ready")
        sd_ready = sem(pre + "sd_ready")
        y_done = sem(pre + "y_done")
        block = ctx.enter_context(nc.Block())
        NC = H * DH // P

        @block.sync
        def _(sp):
            for half in range(2):
                sp.dma_start(wout[:, 4 * half:4 * half + 4, :],
                             w["Wout"].rearrange("(c p) n -> p c n", p=P)[:, 4 * half:4 * half + 4, :]).then_inc(params_in, 16)
            sp.dma_start(g_out[:], rows(w["g_out"])).then_inc(params_in, 16)

        @block.tensor
        def _(pe):
            pe.sem_inc(turned, 2)
            pe.wait_ge(params_in, 48)
            pe.wait_ge(null_ready, 3)
            for c in range(NC):
                ins = nc.tensor.matmul(bank[3][0:H, 0:D], spread[:, c, :], wout[:, c, :], start=c == 0, stop=c == NC - 1)
            ins.then_inc(null_o_done, 1)
            pe.wait_ge(null_o_ready, 1)
            with pe.Fori(0, B) as b:
                def project(i):
                    n = TB * b + i
                    pe.wait_ge(ot_ready, n + 1)
                    for c in range(NC):
                        nc.tensor.matmul(bank[4 + i][:, 0:D], ot[:, i % 2, P * c:P * c + P], wout[:, c, :], start=c == 0, stop=False)
                    nc.tensor.matmul(bank[4 + i][:, 0:D], pt[:, i % 2, :], null_o[:], start=False, stop=True).then_inc(projected, 1)

                for i in range(TB):
                    n = TB * b + i
                    wait_apart(pe, scaled, 2 + n + 1)
                    if i == 0:
                        wait_apart(pe, y_done, b + 1)
                    else:
                        wait_apart(pe, ot_ready, n)
                    for c in range(NC):
                        nc.tensor.transpose(bank[c // 4][:, P * (c % 4):P * (c % 4) + P], os[:, i % 2, P * c:P * c + P], ident[:])
                    nc.tensor.transpose(bank[2][0:H, 0:P], ps[:, i % 2, :], ident[:]).then_inc(turned, 1)
                    if i:
                        project(i - 1)
                project(TB - 1)

        @block.scalar
        def _(ac):
            ac.wait_ge(null_ready, 1)
            nc.scalar.activation(null_p[:], null_p[:], ACT.Exp).then_inc(null_exped, 1)
            ac.wait_ge(null_o_done, 1)
            nc.scalar.copy(null_o[:], bank[3][0:H, 0:D]).then_inc(null_o_ready, 1)
            ac.sem_inc(sd_ready, 1)
            with ac.Fori(0, B) as b:
                for i in range(TB):
                    n = TB * b + i
                    ac.wait_ge(turned, 2 + n + 1)
                    if i >= 2:
                        ac.wait_ge(projected, n - 1)
                    for c in range(2):
                        nc.scalar.copy(ot[:, i % 2, 512 * c:512 * c + 512], bank[c][:])
                    nc.scalar.copy(pt[:, i % 2, :], bank[2][0:H, 0:P]).then_inc(ot_ready, 1)
                ac.wait_ge(var_ready, b + 1)
                nc.scalar.activation(sd[:], var[:], ACT.Sqrt).then_inc(sd_ready, 1)

        @block.vector
        def _(dv):
            st = Steps(dv, pre_steps)
            dv.sem_inc(scaled, 2)
            dv.sem_inc(y_done, 1)
            nc.vector.tensor_tensor(null_p[:], neg_max[:], null_neg[:], ALU.subtract).then_inc(null_ready, 1)
            st.after(nc.vector.memset(spread[:], 0.0))
            for half in range(2):
                dst = spread[DH * half:DH * half + DH].rearrange("p c h -> p (c h)")[:, half::H + 2]
                nc.vector.tensor_scalar(dst, dst, null_v[DH * half:DH * half + DH, :], None, ALU.add).then_inc(null_ready, 1)
            dv.wait_ge(null_exped, 1)
            st.after(nc.vector.tensor_tensor(rinv[:], row_sum[:], null_p[:], ALU.add))
            st.after(nc.vector.reciprocal(rinv[:], rinv[:]))
            st.after(nc.vector.tensor_tensor(null_p[:], null_p[:], rinv[:], ALU.mult))
            dv.wait_ge(params_in, 48)
            with dv.Fori(0, B) as b:
                st = Steps(dv, stepped, 4 * b, 4)
                for i in range(TB):
                    n = TB * b + i
                    dv.wait_ge(turned, n + 1)
                    nc.vector.tensor_tensor(os[:, i % 2, :].rearrange("p (h d) -> p h d", h=H), o_all[:, n],
                                            rinv[:, :, bass.ds(n, 1)].broadcast_to([P, H, DH]), ALU.mult)
                    nc.vector.tensor_copy(ps[:, i % 2, :], null_p[:, :, n]).then_inc(scaled, 1)
                for i in range(TB):
                    dv.wait_ge(projected, TB * b + i + 1)
                    ins = nc.vector.bn_stats(stats[:, i, :], bank[4 + i][:, 0:D])
                st.after(ins, apart=True)
                for i in range(TB):
                    ins = nc.vector.bn_aggr(mv[:, i, :], stats[:, i, :])
                st.after(ins)
                nc.vector.tensor_scalar(var[:], mv[:, :, 1], EPS, None, ALU.add).then_inc(var_ready, 1)
                dv.wait_ge(sd_ready, 1 + b + 1)
                st.after(nc.vector.reciprocal(rstd[:], sd[:]))
                for i in range(TB):
                    ins = nc.vector.tensor_scalar(yn[:, i, :], bank[4 + i][:, 0:D], mv[:, i, 0:1], rstd[:, i:i + 1],
                                                  ALU.subtract, ALU.mult)
                st.after(ins)
                nc.vector.tensor_tensor(Y[:, bass.ds(TB * b, TB), :], yn[:], g_out[:].unsqueeze(1).broadcast_to([P, TB, D]),
                                        ALU.mult).then_inc(y_done, 1)
                st.close()


def null_key_attention(nc, sem, pre, bank, X, Y, ident, w):
    with ExitStack() as ctx:
        def sb(name, shape, dt=F32):
            return ctx.enter_context(nc.sbuf_tensor(pre + name, shape, dt))

        heads = sb("heads", [P, NT, H, DH])
        v_all = sb("v_all", [P, NT, DH])
        kt = (sb("kt_high", [P, B, S], F32R), sb("kt_low", [P, B, S], F32R), sb("mask_row", [1, B * S], F32R))
        null_neg = sb("null_neg", [P, H, NT])
        null_v = sb("null_v", [P, 1])
        neg_max = sb("neg_max", [P, H, NT])
        row_sum = sb("row_sum", [P, H, NT])
        attention_inputs(nc, sem, pre + "i_", bank, X, ident, w, heads, kt, v_all, null_neg, null_v)
        attention_core(nc, sem, pre + "c_", bank, ident, w, heads, kt, v_all, null_neg, neg_max, row_sum, heads)
        attention_output(nc, sem, pre + "o_", bank, Y, ident, w, heads, null_neg, null_v, neg_max, row_sum)


def moe_ffn(nc, sem, bank, X, Y, ident, lane_d, norm_scale, gate_w, gate_b, w1_d, b1_d, w2_d, b2_d):
    E, J = E1, I1 // P
    LIMIT, ALPHA = 7.0, 1.702
    with ExitStack() as ctx:
        def sb(name, shape, dt=F32):
            return ctx.enter_context(nc.sbuf_tensor("mf_" + name, shape, dt))

        lane = sb("lane", [P, E])
        g_norm = sb("g_norm", [P, KD])
        gw = sb("gw", [P, KD, E])
        gb = sb("gb", [P, E])
        b1 = sb("b1", [P, E, 2, J])
        b2 = sb("b2", [E, D])
        tt_high = sb("tt_high", [P, KD, NT * P], F32R)
        tt_low = sb("tt_low", [P, KD, NT * P], F32R)
        weight = sb("weight", [P, NT, E])

        params_in = sem("mf_params_in")
        w_in = [sem(f"mf_w_in{j}") for j in range(2)]

        with ExitStack() as inner:
            def tmp(name, shape, dt=F32):
                return inner.enter_context(nc.sbuf_tensor("mf_" + name, shape, dt))

            square = tmp("square", [P, 2, D])
            ms = tmp("ms", [P, NT])
            sd = tmp("sd", [P, NT])
            rms = tmp("rms", [P, NT])
            tn = tmp("tn", [P, 2, TB, D])
            logits = tmp("logits", [P, NT, E])
            exp_in = tmp("exp_in", [P, NT, E])
            ex = tmp("ex", [P, NT, E])
            zsum = tmp("zsum", [P, NT])
            best = tmp("best", [P, NT, 8])
            best_at = tmp("best_at", [P, NT, 8], U32)
            picked = tmp("picked", [P, NT, 2])
            wt = tmp("wt", [E, NT, P])
            tt = tmp("tt", [P, KD, NT * P])
            tt_bits = tmp("tt_bits", [P, KD, NT * P], I32)

            stepped = sem("mf_stepped")
            ms_ready, sd_ready = sem("mf_ms_ready"), sem("mf_sd_ready")
            tn_ready, tn_turned, tt_ready = sem("mf_tn_ready"), sem("mf_tn_turned"), sem("mf_tt_ready")
            logits_done = sem("mf_logits_done")
            exp_ready, exp_done = sem("mf_exp_ready"), sem("mf_exp_done")
            weight_ready, weight_turned, wt_ready = sem("mf_weight_ready"), sem("mf_weight_turned"), sem("mf_wt_ready")
            bias_done, x_added, tt_split = sem("mf_bias_done"), sem("mf_x_added"), sem("mf_tt_split")
            block = inner.enter_context(nc.Block())

            @block.sync
            def _(sp):
                sp.dma_start(lane[:], lane_d).then_inc(params_in, 16)
                sp.dma_start(g_norm[:], columns(norm_scale, KD)).then_inc(params_in, 16)
                sp.dma_start(gw[:], gate_w.rearrange("(k p) e -> p k e", p=P)).then_inc(params_in, 16)
                sp.dma_start(gb[:], rows(gate_b)).then_inc(params_in, 16)
                sp.dma_start(b1[:], b1_d).then_inc(params_in, 16)
                sp.dma_start(b2[:], b2_d).then_inc(params_in, 16)

            @block.gpsimd
            def _(gp):
                nc.gpsimd.tensor_tensor(X[:], X[:], Y[:], ALU.add).then_inc(x_added, 1)
                gp.wait_ge(tt_split, 1)
                nc.gpsimd.tensor_tensor(tt_low[:], tt[:], tt_bits[:].bitcast(F32), ALU.subtract)

            @block.vector
            def _(dv):
                st = Steps(dv, stepped)
                for t in range(NT):
                    if t >= 2:
                        st.after(ins)
                    ins = nc.vector.tensor_tensor_reduce(out=square[:, t % 2, :], in0=Y[:, t, :], in1=Y[:, t, :], scale=1.0 / D,
                                                         scalar=EPS, op0=ALU.mult, op1=ALU.add, accum_out=ms[:, t:t + 1])
                ins.then_inc(ms_ready, 1)
                dv.wait_ge(sd_ready, 1)
                st.after(nc.vector.reciprocal(rms[:], sd[:]))
                dv.wait_ge(params_in, 96)
                for b in range(B):
                    if b >= 2:
                        dv.wait_ge(tn_turned, b - 1)
                    for i in range(TB):
                        t = TB * b + i
                        ins = nc.vector.tensor_scalar(tn[:, b % 2, i, :], Y[:, t, :], rms[:, t:t + 1], None, ALU.mult)
                    ins.then_inc(tn_ready, 1)
                dv.wait_ge(tt_ready, B)
                high_part(nc, tt_bits[:], tt[:]).then_inc(tt_split, 1)
                dv.wait_ge(logits_done, 1)
                st.after(nc.vector.tensor_tensor(logits[:], bank[6][:, 0:NT * E].rearrange("p (t e) -> p t e", e=E),
                                                 gb[:].unsqueeze(1).broadcast_to([P, NT, E]), ALU.add))
                route(nc, dv, st, logits, ex, zsum, best, best_at, lane, picked, weight, False, exp_in, exp_ready, exp_done)
                nc.vector.tensor_copy(exp_in[:], weight[:]).then_inc(weight_ready, 1)
                dv.wait_ge(x_added, 1)
                for t in range(NT):
                    dv.wait_ge(bias_done, t // 8 + 1)
                    src = bank[(t // 2) % 4 + (0 if t < 8 else 4)][:, D * (t % 2):D * (t % 2) + D]
                    nc.vector.tensor_tensor(X[:, t, :], X[:, t, :], src, ALU.add)

            @block.scalar
            def _(ac):
                ac.wait_ge(ms_ready, 1)
                nc.scalar.activation(sd[:], ms[:], ACT.Sqrt).then_inc(sd_ready, 1)
                ac.wait_ge(params_in, 96)
                for b in range(B):
                    ac.wait_ge(tn_turned, b + 1)
                    for k in range(KD):
                        ins = nc.scalar.activation(tt[:, k, S * b:S * b + S], bank[2 * (b % 2) + k][:], ACT.Copy, scale=g_norm[:, k:k + 1])
                    ins.then_inc(tt_ready, 1)
                ac.wait_ge(tt_split, 1)
                nc.scalar.copy(tt_high[:], tt_bits[:].bitcast(F32))
                ac.wait_ge(exp_ready, 1)
                nc.scalar.activation(ex[:], exp_in[:], ACT.Exp).then_inc(exp_done, 1)
                for b in range(B):
                    ac.wait_ge(weight_turned, b + 1)
                    nc.scalar.copy(wt[:, TB * b:TB * b + TB, :], bank[b][0:E, :].rearrange("e (i p) -> e i p", i=TB)).then_inc(wt_ready, 1)

            @block.tensor
            def _(pe):
                pe.wait_ge(params_in, 96)
                for b in range(B):
                    pe.wait_ge(tn_ready, b + 1)
                    if b >= 2:
                        pe.wait_ge(tt_ready, b - 1)
                    for k in range(KD):
                        for i in range(TB):
                            ins = nc.tensor.transpose(bank[2 * (b % 2) + k][:, P * i:P * i + P], tn[:, b % 2, i, P * k:P * k + P], ident[:])
                    ins.then_inc(tn_turned, 1)
                pe.wait_ge(tt_ready, B)
                for t in range(NT):
                    for k in range(KD):
                        ins = nc.tensor.matmul(bank[6][:, E * t:E * t + E], tt[:, k, P * t:P * t + P], gw[:, k, :],
                                               start=k == 0, stop=k == KD - 1)
                ins.then_inc(logits_done, 1)
                pe.wait_ge(weight_ready, 1)
                for b in range(B):
                    for i in range(TB):
                        ins = nc.tensor.transpose(bank[b][0:E, P * i:P * i + P], exp_in[:, TB * b + i, :], ident[:])
                    ins.then_inc(weight_turned, 1)
                pe.wait_ge(wt_ready, B)
                for t in range(NT):
                    dst = bank[(t // 2) % 4 + (0 if t < 8 else 4)][:, D * (t % 2):D * (t % 2) + D]
                    ins = nc.tensor.matmul(dst, wt[:, t, :], b2[:], start=True, stop=True)
                    if t % 8 == 7:
                        ins.then_inc(bias_done, 1)

        raw = [Y[:, NT // 2 * j:NT // 2 * j + NT // 2, :].rearrange("p i d -> p (i d)") for j in range(2)]
        W1, W2 = KD * 2 * I1, J * D
        raw2 = [sb(f"raw2{j}", [P, W2]) for j in range(2)]
        w_bits = sb("w_bits", [P, W1 + W2], I32)
        w_high = [sb(f"w_high{j}", [P, W1 + W2], F32R) for j in range(2)]
        w_low = [sb(f"w_low{j}", [P, W1 + W2], F32R) for j in range(2)]
        glu = sb("glu", [P, 2, S])
        sig = sb("sig", [P, 2, S])
        gated = sb("gated", [P, 2, S])
        low = sb("low", [P, 2, S])
        lin = sb("lin", [P, 2, S])
        hid = sb("hid", [P, 2, S])
        hid_bits = sb("hid_bits", [P, 2, S], I32)
        hid_high = sb("hid_high", [P, 2, J, S], F32R)
        hid_low = sb("hid_low", [P, 2, J, S], F32R)

        def w1_of(w, k, half, j):
            return w[:, (2 * k + half) * I1 + P * j:(2 * k + half) * I1 + P * j + P]

        def w2_of(w, j):
            return w[:, W1 + D * j:W1 + D * j + D]

        glu_done, lin_done = sem("mf_glu_done"), sem("mf_lin_done")
        glu_ready, low_ready, lin_ready = sem("mf_glu_ready"), sem("mf_low_ready"), sem("mf_lin_ready")
        sig_ready, gated_ready, hid_ready = sem("mf_sig_ready"), sem("mf_gated_ready"), sem("mf_hid_ready")
        bits_ready, high_ready, low_part_ready = sem("mf_bits_ready"), sem("mf_high_ready"), sem("mf_low_part_ready")
        w_bits_ready, w_high_ready, w_low_ready = sem("mf_w_bits_ready"), sem("mf_w_high_ready"), sem("mf_w_low_ready")
        downed, added = sem("mf_downed"), sem("mf_added")
        block = ctx.enter_context(nc.Block())
        NU = 2 * B
        SUB = J * NU
        PAIRS = E // 2
        CREDIT = 4

        def turns(eng, body):
            body(0, True, False)
            with eng.Fori(1, PAIRS - 1) as t:
                body(t, False, False)
            body(PAIRS - 1, False, True)

        def quarter(q):
            return slice(W1 // 4 * q, W1 // 4 * (q + 1)), slice(W1 + W2 // 4 * q, W1 + W2 // 4 * (q + 1))

        def split_points(t, last, u):
            if u == 2:
                return (t, 1, NU * t)
            if u == B + 2 and not last:
                return (t + 1, 0, NU * t + B)
            return None

        @block.sync
        def _(sp):
            def load(t, j):
                e = 2 * t + j
                for k in range(KD):
                    dst = raw[j][:, 2 * I1 * k:2 * I1 * k + 2 * I1].rearrange("p (s n) -> p s n", s=2)
                    sp.dma_start(dst, w1_d[e, P * k:P * k + P]).then_inc(w_in[j], 16)
                sp.dma_start(raw2[j][:].rearrange("p (j n) -> p j n", j=J),
                             w2_d[e].rearrange("(j p) n -> p j n", p=P)).then_inc(w_in[j], 16)

            for j in range(2):
                load(0, j)
            with sp.Fori(0, PAIRS - 1) as t:
                for j in range(2):
                    sp.wait_ge(w_low_ready, 2 * t + j + 1)
                    load(t + 1, j)

        @block.tensor
        def _(pe):
            pe.sem_inc(downed, CREDIT)

            def up(t, u, j):
                s = SUB * t + J * u + j
                h, l = w_high[u // B], w_low[u // B]
                cols = slice(S * (u % B), S * (u % B) + S)
                for half, done, freed in ((0, glu_done, glu_ready), (1, lin_done, low_ready)):
                    pe.wait_ge(freed, s + 1)
                    parts = [(w1_of(w, k, half, j), x[:, k, cols]) for k in range(KD) for w, x in ((h, tt_high), (l, tt_high), (h, tt_low))]
                    for n, (w, x) in enumerate(parts):
                        ins = nc.tensor.matmul(bank[2 * half + j % 2][:], w, x, start=n == 0, stop=n == len(parts) - 1)
                    ins.then_inc(done, 1)

            def down(t, u, i):
                n = NU * t + u
                h, l = w_high[u // B], w_low[u // B]
                if i == 0:
                    pe.wait_ge(high_ready, FREE + J * (n + 1))
                    pe.wait_ge(low_part_ready, FREE + J * (n + 1))
                if i % 2 == 0:
                    pe.wait_ge(added, 2 * n + i // 2 + 1)
                parts = [(x[:, u % 2, j, P * i:P * i + P], w2_of(w, j)) for j in range(J)
                         for x, w in ((hid_high, h), (hid_low, h), (hid_high, l))]
                for m, (x, w) in enumerate(parts):
                    ins = nc.tensor.matmul(bank[4 + 2 * (u % 2) + i // 2][:, D * (i % 2):D * (i % 2) + D], x, w,
                                           start=m == 0, stop=m == len(parts) - 1)
                if i % 2:
                    ins.then_inc(downed, 1)

            def turn(t, first, last):
                for u in range(NU):
                    if u % B == 0:
                        pe.wait_ge(w_high_ready, 2 * t + u // B + 1)
                        pe.wait_ge(w_low_ready, 2 * t + u // B + 1)
                    for j in range(J):
                        up(t, u, j)
                        of, i = (u - 1, j - 2) if j >= 2 else (u - 2, j + 2)
                        if of >= 0:
                            down(t, of, i)
                        elif not first:
                            down(t - 1, NU + of, i)
                if last:
                    for of, i in ((NU - 2, 2), (NU - 2, 3), (NU - 1, 0), (NU - 1, 1), (NU - 1, 2), (NU - 1, 3)):
                        down(t, of, i)

            turns(pe, turn)

        @block.scalar
        def _(ac):
            ac.sem_inc(high_ready, FREE)

            def split_w(t, j, over, q):
                if q == 0:
                    ac.wait_ge(w_bits_ready, 2 * t + j + 1)
                    ac.wait_ge(downed, CREDIT + 2 * over)
                for cols in quarter(q):
                    ins = nc.scalar.copy(w_high[j][:, cols], w_bits[:, cols].bitcast(F32))
                if q == 3:
                    ins.then_inc(w_high_ready, 1)

            def high(t, m):
                s = SUB * t + m
                ac.wait_ge(bits_ready, s + 1)
                if m % J == 0:
                    ac.wait_ge(downed, CREDIT + 2 * (NU * t + m // J) - 2)
                nc.scalar.copy(hid_high[:, m // J % 2, m % J, :], hid_bits[:, m % 2, :].bitcast(F32)).then_inc(high_ready, 1)

            def turn(t, first, last):
                for m in range(SUB):
                    s = SUB * t + m
                    ac.wait_ge(glu_ready, FREE + s + 1)
                    ac.wait_ge(gated_ready, s + 1)
                    nc.scalar.activation(sig[:, m % 2, :], glu[:, m % 2, :], ACT.Sigmoid, scale=ALPHA).then_inc(sig_ready, 1)
                    if m >= 2:
                        high(t, m - 2)
                    elif not first:
                        high(t - 1, SUB + m - 2)
                    point = split_points(t, last, m // J)
                    if point:
                        split_w(*point, m % J)
                if last:
                    high(t, SUB - 2)
                    high(t, SUB - 1)

            for q in range(4):
                split_w(0, 0, 0, q)
            turns(ac, turn)

        @block.gpsimd
        def _(gp):
            gp.sem_inc(gated_ready, FREE)
            gp.sem_inc(low_part_ready, FREE)

            def split_w(t, j, over, q):
                if q == 0:
                    gp.wait_ge(w_bits_ready, 2 * t + j + 1)
                    gp.wait_ge(downed, CREDIT + 2 * over)
                one, two = quarter(q)
                nc.gpsimd.tensor_tensor(w_low[j][:, one], raw[j][:, one], w_bits[:, one].bitcast(F32), ALU.subtract)
                ins = nc.gpsimd.tensor_tensor(w_low[j][:, two], raw2[j][:, two.start - W1:two.stop - W1], w_bits[:, two].bitcast(F32),
                                              ALU.subtract)
                if q == 3:
                    ins.then_inc(w_low_ready, 1)

            def low_part(t, m):
                s = SUB * t + m
                gp.wait_ge(bits_ready, s + 1)
                if m % J == 0:
                    gp.wait_ge(downed, CREDIT + 2 * (NU * t + m // J) - 2)
                nc.gpsimd.tensor_tensor(hid_low[:, m // J % 2, m % J, :], hid[:, m % 2, :], hid_bits[:, m % 2, :].bitcast(F32),
                                        ALU.subtract).then_inc(low_part_ready, 1)

            def turn(t, first, last):
                for m in range(SUB):
                    s = SUB * t + m
                    gp.wait_ge(sig_ready, s + 1)
                    gp.wait_ge(hid_ready, s + 1)
                    nc.gpsimd.tensor_tensor(gated[:, m % 2, :], glu[:, m % 2, :], sig[:, m % 2, :], ALU.mult).then_inc(gated_ready, 1)
                    if m >= 2:
                        low_part(t, m - 2)
                    elif not first:
                        low_part(t - 1, SUB + m - 2)
                    point = split_points(t, last, m // J)
                    if point:
                        split_w(*point, m % J)
                if last:
                    low_part(t, SUB - 2)
                    low_part(t, SUB - 1)

            for q in range(4):
                split_w(0, 0, 0, q)
            turns(gp, turn)

        @block.vector
        def _(dv):
            for s in (glu_ready, low_ready, hid_ready):
                dv.sem_inc(s, FREE)
            dv.sem_inc(added, 4)

            def split_w(t, j, first):
                n = 2 * t + j
                if not first:
                    dv.wait_ge(w_high_ready, n)
                    dv.wait_ge(w_low_ready, n)
                dv.wait_ge(w_in[j], 16 * (KD + 1) * (t + 1))
                high_part(nc, w_bits[:, 0:W1], raw[j])
                high_part(nc, w_bits[:, W1:], raw2[j][:]).then_inc(w_bits_ready, 1)

            def clip(t, u, j):
                s = SUB * t + J * u + j
                e = 2 * t + u // B
                b1_glu, b1_lin = (b1[:, bass.ds(e, 1), h, j] for h in range(2))
                dv.wait_ge(glu_done, s + 1)
                dv.wait_ge(gated_ready, s + 1)
                nc.vector.tensor_scalar(glu[:, j % 2, :], bank[j % 2][:], b1_glu, LIMIT, ALU.add, ALU.min).then_inc(glu_ready, 1)
                dv.wait_ge(lin_done, s + 1)
                nc.vector.tensor_scalar(low[:, j % 2, :], bank[2 + j % 2][:], b1_lin, LIMIT, ALU.add, ALU.min).then_inc(low_ready, 1)
                dv.wait_ge(low_ready, FREE + s + 1)
                nc.vector.tensor_scalar(lin[:, j % 2, :], low[:, j % 2, :], -LIMIT, 1.0, ALU.max, ALU.add).then_inc(lin_ready, 1)

            def join(t, m):
                s = SUB * t + m
                dv.wait_ge(gated_ready, FREE + s + 1)
                dv.wait_ge(lin_ready, s + 1)
                dv.wait_ge(low_part_ready, s + 1)
                nc.vector.tensor_tensor(hid[:, m % 2, :], gated[:, m % 2, :], lin[:, m % 2, :], ALU.mult).then_inc(hid_ready, 1)

            def bits(t, m):
                s = SUB * t + m
                dv.wait_ge(hid_ready, FREE + s + 1)
                dv.wait_ge(high_ready, s + 1)
                dv.wait_ge(low_part_ready, s + 1)
                high_part(nc, hid_bits[:, m % 2, :], hid[:, m % 2, :]).then_inc(bits_ready, 1)

            def add(t, u, half):
                n = NU * t + u
                e = 2 * t + u // B
                dv.wait_ge(downed, CREDIT + 2 * n + half + 1)
                for i in (2 * half, 2 * half + 1):
                    x = X[:, TB * (u % B) + i, :]
                    ins = nc.vector.scalar_tensor_tensor(x, bank[4 + 2 * (u % 2) + half][:, D * (i % 2):D * (i % 2) + D],
                                                         weight[:, TB * (u % B) + i, bass.ds(e, 1)], x, ALU.mult, ALU.add)
                ins.then_inc(added, 1)

            def turn(t, first, last):
                for m in range(SUB):
                    u, j = divmod(m, J)
                    if m >= 2:
                        bits(t, m - 2)
                    elif not first:
                        bits(t - 1, SUB + m - 2)
                    clip(t, u, j)
                    if m:
                        join(t, m - 1)
                    elif not first:
                        join(t - 1, SUB - 1)
                    if j % 2 == 0:
                        if u >= 2:
                            add(t, u - 2, j // 2)
                        elif not first:
                            add(t - 1, NU + u - 2, j // 2)
                    point = split_points(t, last, u) if j == 0 else None
                    if point:
                        split_w(point[0], point[1], False)
                if last:
                    bits(t, SUB - 2)
                    join(t, SUB - 1)
                    bits(t, SUB - 1)
                    for u in (NU - 2, NU - 1):
                        for half in range(2):
                            add(t, u, half)

            split_w(0, 0, True)
            turns(dv, turn)


def rotary_attention(nc, sem, bank, X, Y, ident, wqk_t, wv_t, wo_t, cos_d, sin_d):
    with ExitStack() as ctx:
        def sb(name, shape, dt=F32):
            return ctx.enter_context(nc.sbuf_tensor("ra_" + name, shape, dt))

        qk_all = sb("qk_all", [P, NT, 2, H, DR])
        v_all = sb("v_all", [P, NT, D + DH - DR])
        o_all = sb("o_all", [P, NT, H, DR])
        neg_max = sb("neg_max", [P, H, NT])
        row_sum = sb("row_sum", [P, H, NT])
        wo = sb("wo", [P, KD, D])
        weights_in = sem("ra_weights_in")

        with ExitStack() as inner:
            def tmp(name, shape, dt=F32):
                return inner.enter_context(nc.sbuf_tensor("ra_" + name, shape, dt))

            wqk = tmp("wqk", [P, KD, 2 * D])
            wv = tmp("wv", [P, KD, D])
            cos = tmp("cos", [P, TB, DR])
            sin = tmp("sin", [P, TB, DR])
            y_row = tmp("y_row", [P, TB, D])
            yt = tmp("yt", [P, KD, S])
            straight = tmp("straight", [P, 2, 2 * H, DR])
            rotated = tmp("rotated", [P, 2, 2 * H, DR])
            row_copied, row_turned, yt_ready = sem("ra_row_copied"), sem("ra_row_turned"), sem("ra_yt_ready")
            v_done, v_copied = sem("ra_v_done"), sem("ra_v_copied")
            qk_done, turned, joined = sem("ra_qk_done"), sem("ra_turned"), sem("ra_joined")
            block = inner.enter_context(nc.Block())

            @block.sync
            def _(sp):
                sp.dma_start(wqk[:], wqk_t.rearrange("(k p) n -> p k n", p=P)).then_inc(weights_in, 16)
                sp.dma_start(wv[:], wv_t.rearrange("(k p) n -> p k n", p=P)).then_inc(weights_in, 16)
                sp.dma_start(wo[:], wo_t.rearrange("(k p) n -> p k n", p=P)).then_inc(weights_in, 16)
                sp.dma_start(cos[:], cos_d).then_inc(weights_in, 16)
                sp.dma_start(sin[:], sin_d).then_inc(weights_in, 16)

            @block.gpsimd
            def _(gp):
                gp.sem_inc(joined, FREE)
                nc.gpsimd.memset(v_all[:, :, D:], 0.0)
                with gp.Fori(0, B) as b:
                    gp.wait_ge(row_turned, 1 + b)
                    nc.gpsimd.tensor_copy(y_row[:], Y[:, bass.ds(TB * b, TB), :]).then_inc(row_copied, 1)
                    for i in range(TB):
                        gp.wait_ge(turned, TB * b + i + 1)
                        nc.gpsimd.tensor_tensor(qk_all[:, TB * b + i].rearrange("p s h d -> p (s h) d"), straight[:, i % 2],
                                                rotated[:, i % 2], ALU.add).then_inc(joined, 1)

            @block.tensor
            def _(pe):
                pe.sem_inc(row_turned, 1)
                pe.wait_ge(weights_in, 80)
                with pe.Fori(0, B) as b:
                    pe.wait_ge(row_copied, b + 1)
                    for k in range(KD):
                        for i in range(TB):
                            ins = nc.tensor.transpose(bank[k][:, P * i:P * i + P], y_row[:, i, P * k:P * k + P], ident[:])
                    ins.then_inc(row_turned, 1)
                    pe.wait_ge(yt_ready, b + 1)
                    pe.wait_ge(v_copied, b + 1)
                    for i in range(TB):
                        for k in range(KD):
                            ins = nc.tensor.matmul(bank[2 + i // 2][:, D * (i % 2):D * (i % 2) + D], yt[:, k, P * i:P * i + P], wv[:, k, :],
                                                   start=k == 0, stop=k == KD - 1)
                    ins.then_inc(v_done, 1)
                    for i in range(TB):
                        for k in range(KD):
                            ins = nc.tensor.matmul(bank[4 + i][:], yt[:, k, P * i:P * i + P], wqk[:, k, :], start=k == 0, stop=k == KD - 1)
                        ins.then_inc(qk_done, 1)
                    pe.wait_ge(turned, TB * (b + 1))

            @block.scalar
            def _(ac):
                ac.sem_inc(v_copied, 1)
                with ac.Fori(0, B) as b:
                    ac.wait_ge(row_turned, 2 + b)
                    for k in range(KD):
                        ins = nc.scalar.copy(yt[:, k, :], bank[k][:])
                    ins.then_inc(yt_ready, 1)
                    ac.wait_ge(v_done, b + 1)
                    for j in range(2):
                        ins = nc.scalar.copy(v_all[:, bass.ds(TB * b + 2 * j, 2), 0:D], bank[2 + j][:].rearrange("p (i n) -> p i n", i=2))
                    ins.then_inc(v_copied, 1)

            @block.vector
            def _(dv):
                dv.wait_ge(weights_in, 80)
                with dv.Fori(0, B) as b:
                    for i in range(TB):
                        n = TB * b + i
                        HR = DR // 2
                        dv.wait_ge(qk_done, n + 1)
                        dv.wait_ge(joined, n + 1)
                        qk = bank[4 + i][:].rearrange("p (h d) -> p h d", d=DR)
                        c, s = (x[:, i, :].unsqueeze(1).broadcast_to([P, 2 * H, DR]) for x in (cos, sin))
                        nc.vector.tensor_tensor(straight[:, i % 2], qk, c, ALU.mult)
                        nc.vector.tensor_tensor(rotated[:, i % 2, :, 0:HR], qk[:, :, HR:DR], s[:, :, 0:HR], ALU.mult)
                        nc.vector.tensor_tensor(rotated[:, i % 2, :, HR:DR], qk[:, :, 0:HR], s[:, :, HR:DR], ALU.mult).then_inc(turned, 1)

        attention_core(nc, sem, "rc_", bank, ident, {"bias": "none"}, qk_all, None, v_all, None, neg_max, row_sum, o_all)

        os = sb("os", [P, TB, H, DR])
        ot = sb("ot", [P, KD, S])
        rinv_ready, scaled, o_turned, ot_ready = sem("ra_rinv_ready"), sem("ra_scaled"), sem("ra_o_turned"), sem("ra_ot_ready")
        projected, x_added = sem("ra_projected"), sem("ra_x_added")
        block = ctx.enter_context(nc.Block())

        @block.tensor
        def _(pe):
            pe.sem_inc(o_turned, 1)
            pe.wait_ge(weights_in, 80)
            with pe.Fori(0, B) as b:
                pe.wait_ge(scaled, b + 1)
                for k in range(KD):
                    for i in range(TB):
                        src = os[:, i].rearrange("p h d -> p (h d)")[:, P * k:P * k + P]
                        ins = nc.tensor.transpose(bank[k][:, P * i:P * i + P], src, ident[:])
                ins.then_inc(o_turned, 1)
                pe.wait_ge(ot_ready, b + 1)
                pe.wait_ge(x_added, b + 1)
                for i in range(TB):
                    for k in range(KD):
                        ins = nc.tensor.matmul(bank[2 + i // 2][:, D * (i % 2):D * (i % 2) + D], ot[:, k, P * i:P * i + P], wo[:, k, :],
                                               start=k == 0, stop=k == KD - 1)
                ins.then_inc(projected, 1)

        @block.scalar
        def _(ac):
            with ac.Fori(0, B) as b:
                ac.wait_ge(o_turned, 2 + b)
                ac.wait_ge(x_added, b + 1)
                for k in range(KD):
                    ins = nc.scalar.copy(ot[:, k, :], bank[k][:])
                ins.then_inc(ot_ready, 1)

        @block.vector
        def _(dv):
            dv.sem_inc(x_added, 1)
            nc.vector.reciprocal(row_sum[:], row_sum[:]).then_inc(rinv_ready, 1)
            dv.wait_ge(rinv_ready, 1)
            with dv.Fori(0, B) as b:
                dv.wait_ge(o_turned, b + 1)
                for i in range(TB):
                    r = row_sum[:, :, bass.ds(TB * b + i, 1)].broadcast_to([P, H, DR])
                    ins = nc.vector.tensor_tensor(os[:, i], o_all[:, TB * b + i], r, ALU.mult)
                ins.then_inc(scaled, 1)
                dv.wait_ge(projected, b + 1)
                for j in range(2):
                    x = X[:, bass.ds(TB * b + 2 * j, 2), :].rearrange("p i n -> p (i n)")
                    ins = nc.vector.tensor_tensor(x, x, bank[2 + j][:], ALU.add)
                ins.then_inc(x_added, 1)


def quantised_ffn(nc, sem, bank, X, Y, ident, out, clip_x, clip_down, w_gate, w_up, w_down):
    NC = -(-IQ // P)
    LAST = IQ - P * (NC - 1)
    LO, HI = RNE - QMAX - 1.0, RNE + QMAX
    with ExitStack() as ctx:
        def sb(name, shape, dt=F32):
            return ctx.enter_context(nc.sbuf_tensor("qf_" + name, shape, dt))

        clip = sb("clip", [P, 2])
        factor = sb("factor", [P, 2])
        identb = sb("identb", [P, P], BF16)
        wgu_t = sb("wgu_t", [P, 2, KD, NC * P], BF16)
        wd_t = sb("wd_t", [P, NC, D], BF16)
        xq_t = sb("xq_t", [P, KD, NT * P], BF16)
        gu_scale = sb("gu_scale", [P, 2, NC])
        wd_scale = sb("wd_scale", [P, KD])
        hid = sb("hid", [P, NC, NT * P])
        hid_max = sb("hid_max", [P, B * NC])
        loaded = sem("qf_loaded")
        filled = sem("qf_filled")

        with ExitStack() as inner:
            def tmp(name, shape, dt=F32):
                return inner.enter_context(nc.sbuf_tensor("qf_" + name, shape, dt))

            wgu = tmp("wgu", [P, 2, NC, D])
            wd = tmp("wd", [P, KD, IQ])
            xr = tmp("xr", [P, NT, D])
            wgu_q = tmp("wgu_q", [P, 2, NC, D], BF16)
            wd_q = tmp("wd_q", [P, KD, IQ], BF16)
            xq = tmp("xq", [P, NT, D], BF16)
            x_max = tmp("x_max", [P, 1])
            x_maxall = tmp("x_maxall", [P, 1])
            x_scale = tmp("x_scale", [P, 1])
            x_inv = tmp("x_inv", [P, 1])
            gu_inv = tmp("gu_inv", [P, 2, NC])
            wd_inv = tmp("wd_inv", [P, KD])
            stepped, clip_ready = sem("qf_stepped"), sem("qf_clip_ready")
            x_max_ready, x_max_all = sem("qf_x_max_ready"), sem("qf_x_max_all")
            wgu_ready, wd_ready, xq_ready = sem("qf_wgu_ready"), sem("qf_wd_ready"), sem("qf_xq_ready")
            turned, copied = sem("qf_turned"), sem("qf_copied")
            block = inner.enter_context(nc.Block())

            @block.sync
            def _(sp):
                sp.dma_start(clip[:, 0:1], rows(clip_x)).then_inc(loaded, 16)
                sp.dma_start(clip[:, 1:2], rows(clip_down)).then_inc(loaded, 16)
                sp.wait_ge(filled, 1)
                for n, w in enumerate((w_gate, w_up)):
                    full = P * (NC - 1)
                    sp.dma_start(wgu[:, n, 0:NC - 1, :], w[0:full, :].rearrange("(c p) n -> p c n", p=P)).then_inc(loaded, 16)
                    sp.dma_start(wgu[0:LAST, n, NC - 1, :], w[full:IQ, :]).then_inc(loaded, 16)
                sp.dma_start(wd[:], w_down.rearrange("(k p) n -> p k n", p=P)).then_inc(loaded, 16)

            @block.gpsimd
            def _(gp):
                nc.gpsimd.memset(wgu[:, :, NC - 1, :], 1.0).then_inc(filled, 1)
                gp.wait_ge(x_max_ready, 1)
                nc.gpsimd.partition_all_reduce(x_maxall[:], x_max[:], P, bass.bass_isa.ReduceOp.max).then_inc(x_max_all, 1)

            @block.scalar
            def _(ac):
                ac.wait_ge(loaded, 16 * 7)
                nc.scalar.activation(factor[:], clip[:], ACT.Sigmoid).then_inc(clip_ready, 1)
                for n in range(2):
                    ac.wait_ge(turned, n + 1)
                    for k in range(KD):
                        ins = nc.scalar.copy(wgu_t[:, n, k, :], bank[2 * n + k][:].bitcast(BF16)[:, 0:NC * P])
                    ins.then_inc(copied, 1)
                ac.wait_ge(turned, 3)
                nc.scalar.copy(wd_t[:, 0:4, :], bank[4][:].bitcast(BF16).rearrange("p (c n) -> p c n", c=4))
                nc.scalar.copy(wd_t[:, 4, :], bank[5][:].bitcast(BF16)[:, 0:D])
                nc.scalar.copy(wd_t[0:LAST, 5, :], bank[5][0:LAST].bitcast(BF16)[:, D:2 * D]).then_inc(copied, 1)
                for half in range(2):
                    ac.wait_ge(turned, 4 + half)
                    for k in range(KD):
                        ins = nc.scalar.copy(xq_t[:, k, 1024 * half:1024 * half + 1024], bank[6 + k][:].bitcast(BF16))
                    ins.then_inc(copied, 1)

            @block.tensor
            def _(pe):
                pe.wait_ge(wgu_ready, 1)
                for n in range(2):
                    for k in range(KD):
                        dst = bank[2 * n + k][:].bitcast(BF16)
                        for c in range(NC):
                            ins = nc.tensor.transpose(dst[:, P * c:P * c + P], wgu_q[:, n, c, P * k:P * k + P], identb[:])
                    ins.then_inc(turned, 1)
                pe.wait_ge(wd_ready, 1)
                for c in range(NC):
                    m = P if c < NC - 1 else LAST
                    for k in range(KD):
                        dst = bank[4 + c // 4][0:m].bitcast(BF16)
                        col = D * (c % 4) + P * k
                        ins = nc.tensor.transpose(dst[:, col:col + P], wd_q[:, k, P * c:P * c + m], identb[:])
                ins.then_inc(turned, 1)
                pe.wait_ge(xq_ready, 1)
                for half in range(2):
                    if half:
                        pe.wait_ge(copied, 4)
                    for k in range(KD):
                        dst = bank[6 + k][:].bitcast(BF16)
                        for t in range(NT // 2):
                            ins = nc.tensor.transpose(dst[:, P * t:P * t + P], xq[:, NT // 2 * half + t, P * k:P * k + P], identb[:])
                    ins.then_inc(turned, 1)

            @block.vector
            def _(dv):
                st = Steps(dv, stepped)
                nc.vector.memset(hid_max[:], 0.0)
                nc.vector.tensor_reduce(x_max[:], Y[:].rearrange("p t d -> p (t d)"), AX.X, ALU.max, apply_absolute_value=True)\
                    .then_inc(x_max_ready, 1)
                st.after(nc.vector.tensor_copy(identb[:], ident[:]))
                dv.wait_ge(loaded, 16 * 7)

                def round_(dst, mid, src, inv_of, parts):
                    for p in parts:
                        ins = nc.vector.tensor_scalar(mid[p], src[p], inv_of(p), RNE, ALU.mult, ALU.add)
                    st.after(ins)
                    st.after(nc.vector.tensor_scalar(mid[:], mid[:], LO, HI, ALU.max, ALU.min))
                    return nc.vector.tensor_scalar(dst[:], mid[:], RNE, None, ALU.subtract)

                st.after(nc.vector.tensor_reduce(gu_scale[:], wgu[:], AX.X, ALU.max, apply_absolute_value=True))
                st.after(nc.vector.tensor_scalar(gu_scale[:], gu_scale[:], 1.0 / QMAX, None, ALU.mult))
                st.after(nc.vector.reciprocal(gu_inv[:], gu_scale[:]))
                parts = [(slice(None), n, c) for n in range(2) for c in range(NC)]
                round_(wgu_q, wgu, wgu, lambda p: gu_inv[:, p[1], p[2]:p[2] + 1], parts).then_inc(wgu_ready, 1)
                st.after(nc.vector.tensor_reduce(wd_scale[:], wd[:], AX.X, ALU.max, apply_absolute_value=True))
                st.after(nc.vector.tensor_scalar(wd_scale[:], wd_scale[:], 1.0 / QMAX, None, ALU.mult))
                st.after(nc.vector.reciprocal(wd_inv[:], wd_scale[:]))
                parts = [(slice(None), k) for k in range(KD)]
                round_(wd_q, wd, wd, lambda p: wd_inv[:, p[1]:p[1] + 1], parts).then_inc(wd_ready, 1)
                dv.wait_ge(x_max_all, 1)
                dv.wait_ge(clip_ready, 1)
                st.after(nc.vector.tensor_scalar(x_scale[:], x_maxall[:], factor[:, 0:1], None, ALU.mult))
                st.after(nc.vector.tensor_scalar(x_scale[:], x_scale[:], 1.0 / QMAX, None, ALU.mult))
                st.after(nc.vector.reciprocal(x_inv[:], x_scale[:]))
                round_(xq, xr, Y, lambda p: x_inv[:], [(slice(None),)]).then_inc(xq_ready, 1)
                st.after(nc.vector.tensor_scalar(gu_scale[:], gu_scale[:], x_scale[:], None, ALU.mult))

        with ExitStack() as inner:
            act = inner.enter_context(nc.sbuf_tensor("qf_act", [P, 2, S], F32))
            gated, upped, act_ready = sem("qf_gated"), sem("qf_upped"), sem("qf_act_ready")
            hid_ready, maxed = sem("qf_hid_ready"), sem("qf_maxed")
            block = inner.enter_context(nc.Block())

            @block.tensor
            def _(pe):
                with pe.Fori(0, B) as b:
                    for c in range(NC):
                        n = NC * b + c
                        for which, done, freed in ((0, gated, act_ready), (1, upped, hid_ready)):
                            pe.wait_ge(freed, n + 1)
                            for k in range(KD):
                                ins = nc.tensor.matmul(bank[2 * which + c % 2][:], wgu_t[:, which, k, P * c:P * c + P],
                                                       xq_t[:, k, bass.ds(S * b, S)], start=k == 0, stop=k == KD - 1)
                            ins.then_inc(done, 1)

            @block.scalar
            def _(ac):
                ac.sem_inc(act_ready, FREE)
                with ac.Fori(0, B) as b:
                    for c in range(NC):
                        n = NC * b + c
                        ac.wait_ge(gated, n + 1)
                        ac.wait_ge(hid_ready, n + 1)
                        nc.scalar.activation(act[:, c % 2, :], bank[c % 2][:], ACT.Silu, scale=gu_scale[:, 0, c:c + 1]).then_inc(act_ready, 1)

            @block.vector
            def _(dv):
                dv.sem_inc(hid_ready, FREE)
                with dv.Fori(0, B) as b:
                    for c in range(NC):
                        n = NC * b + c
                        m = P if c < NC - 1 else LAST
                        dv.wait_ge(act_ready, FREE + n + 1)
                        dv.wait_ge(upped, n + 1)
                        dst = hid[:, c, bass.ds(S * b, S)]
                        nc.vector.scalar_tensor_tensor(dst, bank[2 + c % 2][:], gu_scale[:, 1, c:c + 1], act[:, c % 2, :],
                                                       ALU.mult, ALU.mult).then_inc(hid_ready, 1)
                        dv.wait_ge(hid_ready, FREE + n + 1)
                        nc.vector.tensor_reduce(hid_max[0:m, bass.ds(n, 1)], hid[0:m, c, bass.ds(S * b, S)], AX.X, ALU.max,
                                                apply_absolute_value=True).then_inc(maxed, 1)

        with ExitStack() as inner:
            def tmp(name, shape, dt=F32):
                return inner.enter_context(nc.sbuf_tensor("qf_" + name, shape, dt))

            hmax = tmp("hmax", [P, 1])
            hmaxall = tmp("hmaxall", [P, 1])
            h_scale = tmp("h_scale", [P, 1])
            h_inv = tmp("h_inv", [P, 1])
            ones = tmp("ones", [P, P])
            diag = tmp("diag", [P, KD, P])
            out_scale = tmp("out_scale", [P, D])
            mid = tmp("mid", [P, NC, S])
            hq = tmp("hq", [P, 2, NC, S], BF16)
            res = tmp("res", [P, 2, TB, D])
            stepped, hmax_ready, hmax_all = sem("qf_c_stepped"), sem("qf_hmax_ready"), sem("qf_hmax_all")
            diag_ready, spread_done = sem("qf_diag_ready"), sem("qf_spread_done")
            hq_ready, down_done, res_ready = sem("qf_hq_ready"), sem("qf_down_done"), sem("qf_res_ready")
            scaled = sem("qf_scaled")
            stored = [sem(f"qf_stored{j}") for j in range(2)]
            block = inner.enter_context(nc.Block())

            @block.gpsimd
            def _(gp):
                gp.wait_ge(hmax_ready, 1)
                nc.gpsimd.partition_all_reduce(hmaxall[:], hmax[:], P, bass.bass_isa.ReduceOp.max).then_inc(hmax_all, 1)

            @block.tensor
            def _(pe):
                pe.wait_ge(diag_ready, 1)
                for k in range(KD):
                    ins = nc.tensor.matmul(bank[6][:, P * k:P * k + P], ones[:], diag[:, k, :], start=True, stop=True)
                ins.then_inc(spread_done, 1)
                for b in range(B):
                    pe.wait_ge(hq_ready, b + 1)
                    if b >= 2:
                        pe.wait_ge(scaled, b - 1)
                    for i in range(TB):
                        for c in range(NC):
                            m = P if c < NC - 1 else LAST
                            ins = nc.tensor.matmul(bank[2 * (b % 2) + i // 2][:, D * (i % 2):D * (i % 2) + D],
                                                   hq[0:m, b % 2, c, P * i:P * i + P], wd_t[0:m, c, :], start=c == 0, stop=c == NC - 1)
                    ins.then_inc(down_done, 1)

            @block.vector
            def _(dv):
                st = Steps(dv, stepped)
                nc.vector.tensor_reduce(hmax[:], hid_max[:], AX.X, ALU.max).then_inc(hmax_ready, 1)
                st.after(nc.vector.memset(ones[:], 1.0))
                for k in range(KD):
                    ins = nc.vector.tensor_scalar(diag[:, k, :], ident[:], wd_scale[:, k:k + 1], None, ALU.mult)
                ins.then_inc(diag_ready, 1)
                dv.wait_ge(hmax_all, 1)
                st.after(nc.vector.tensor_scalar(h_scale[:], hmaxall[:], factor[:, 1:2], None, ALU.mult))
                st.after(nc.vector.tensor_scalar(h_scale[:], h_scale[:], 1.0 / QMAX, None, ALU.mult))
                st.after(nc.vector.reciprocal(h_inv[:], h_scale[:]))
                dv.wait_ge(spread_done, 1)
                st.after(nc.vector.tensor_scalar(out_scale[:], bank[6][:, 0:D], h_scale[:], None, ALU.mult))

                def finish(b):
                    dv.wait_ge(down_done, b + 1)
                    if b >= 2:
                        dv.wait_ge(stored[b % 2], 16 * (b // 2))
                    r = res[:, b % 2]
                    for i in range(TB):
                        ins = nc.vector.tensor_tensor(r[:, i, :], bank[2 * (b % 2) + i // 2][:, D * (i % 2):D * (i % 2) + D], out_scale[:], ALU.mult)
                    ins.then_inc(scaled, 1)
                    dv.wait_ge(scaled, b + 1)
                    nc.vector.tensor_tensor(r, r, X[:, TB * b:TB * b + TB, :], ALU.add).then_inc(res_ready, 1)

                for b in range(B):
                    if b >= 2:
                        dv.wait_ge(down_done, b - 1)
                    if b:
                        dv.wait_ge(hq_ready, b)
                    st.after(nc.vector.tensor_scalar(mid[:], hid[:, :, S * b:S * b + S], h_inv[:], RNE, ALU.mult, ALU.add))
                    st.after(nc.vector.tensor_scalar(mid[:], mid[:], LO, HI, ALU.max, ALU.min))
                    nc.vector.tensor_scalar(hq[:, b % 2], mid[:], RNE, None, ALU.subtract).then_inc(hq_ready, 1)
                    if b:
                        finish(b - 1)
                finish(B - 1)

            @block.sync
            def _(sp):
                for b in range(B):
                    sp.wait_ge(res_ready, b + 1)
                    sp.dma_start(out[b].rearrange("(i p) d -> p i d", p=P), res[:, b % 2]).then_inc(stored[b % 2], 16)
                for j in range(2):
                    sp.wait_ge(stored[j], 16 * (B // 2))


def program(nc, a, out):
    with ExitStack() as ctx:
        stage_semaphores = []

        def sem(name):
            stage_semaphores.append(nc.alloc_semaphore(name=name))
            return stage_semaphores[-1]

        def stage_end():
            nc.clear_and_free_semaphores(list(stage_semaphores))
            stage_semaphores.clear()
            nc.all_engine_barrier()

        ctx.enter_context(nc.allow_non_contiguous_dma(reason="a vector's values, one to a partition"))
        bank = [ctx.enter_context(nc.psum_tensor(f"bank{i}", [P, 512], F32)) for i in range(8)]
        X = ctx.enter_context(nc.sbuf_tensor("X", [P, NT, D], F32))
        Y = ctx.enter_context(nc.sbuf_tensor("Y", [P, NT, D], F32))
        ident = ctx.enter_context(nc.sbuf_tensor("ident", [P, P], F32))
        consts_in = sem("consts_in")
        with nc.Block() as block:
            @block.sync
            def _(sp):
                sp.dma_start(ident[:], a["c_identity"]).then_inc(consts_in, 16)
                sp.dma_start(X[:], a["x"].rearrange("b (i p) d -> p (b i) d", p=P)).then_inc(consts_in, 16)
                sp.wait_ge(consts_in, 32)
        stage_end()
        tables = nc.dram_tensor("bias_tables", (2, H, NPOS), F32, kind="Internal").ap()
        copies = nc.dram_tensor("bias_copies", (2, H, P, NPOS), F32, kind="Internal").ap()
        lay = [{n: a[f"L{l}_cond2_{n}"] for n in ("w0", "b0", "g0", "w1", "b1", "g1", "w2", "b2")} for l in range(2)]
        for l in range(2):
            lay[l]["w0"] = a[f"L{l}_cond2_w0"].rearrange("a d -> (a d)")
            lay[l]["table"] = tables[l]
            lay[l]["copies"] = copies[l]
        bias_tables(nc, sem, bank, ident, a["c_positions"], lay)
        stage_end()
        moe_conditioning(nc, sem, bank, Y, a["c_x_transposed"], a["c_lane"], a["c_cond_rep"], a["c_wt_t"], a["c_wg_t"],
                         *(a["L0_cond_" + n] for n in ("w_gate", "w_up", "w_down", "sw_gate", "sw_up", "sw_down")))
        stage_end()
        linear_attention(nc, sem, bank, X, Y, ident, a["c_keep_upper"], a["c_attn_wq_t"], a["c_attn_wk_t"], a["c_attn_wv_t"],
                         a["c_attn_wo_t"])
        stage_end()
        def cosine(l):
            w = {n: a[f"L{l}_cond2_{n}"] for n in ("g_norm", "Wq", "Wkv", "q_scale", "k_scale", "null_attn_bias", "Wout", "g_out")}
            w.update(cond=a["cond_64"], mask=a["mask_BxS_bf1"], bias="table", copies=copies[l])
            null_key_attention(nc, sem, f"ca{l}_", bank, X, Y, ident, w)
            stage_end()

        cosine(0)
        moe_ffn(nc, sem, bank, X, Y, ident, a["c_lane"], *(a["L0_ffn_" + n] for n in ("norm_scale", "gate_w", "gate_b")),
                a["c_mlp1_w"], a["c_mlp1_b"], a["L0_ffn_mlp2_w"], a["L0_ffn_mlp2_b"])
        stage_end()
        w = {n: a["L1_cond_" + n] for n in ("Wq", "Wkv", "null_attn_bias", "g_out")}
        w.update(g_norm=a["L1_cond_g_in"], Wout=a["L1_cond_Wo"], cond=a["cond_64"], mask=a["mask_BxS_bk0"],
                 bias="full", full=a["fside_16xSxS_0"])
        null_key_attention(nc, sem, "ba_", bank, X, Y, ident, w)
        stage_end()
        rotary_attention(nc, sem, bank, X, Y, ident, a["c_rot_wqk_t"], a["c_rot_wv_t"], a["c_rot_wo_t"], a["c_rot_cos"], a["c_rot_sin"])
        stage_end()
        cosine(1)
        quantised_ffn(nc, sem, bank, X, Y, ident, out, a["L1_ffn_clip_x"], a["L1_ffn_clip_down"], a["L1_ffn_w_gate"],
                      a["L1_ffn_w_up"], a["L1_ffn_w_down"])
        stage_end()


def _layout(inputs):
    a = {k: np.ascontiguousarray(v) for k, v in inputs.items()}
    for k in ("mask_BxS_bf1", "mask_BxS_bk0"):
        a[k] = a[k].view(np.int32)
    a["c_identity"] = np.eye(P, dtype=np.float32)
    a["c_positions"] = (S - 1 - np.arange(NPOS, dtype=np.float32)).reshape(NPOS // P, P).T.copy()
    a["c_lane"] = np.tile(np.arange(E0, dtype=np.float32), (P, 1))
    a["c_x_transposed"] = np.ascontiguousarray(a["x"].transpose(0, 2, 1))
    a["c_cond_rep"] = np.ascontiguousarray(np.broadcast_to(a["cond_64"].T[:, :, None], (G0, B, P)))
    a["c_wt_t"] = np.ascontiguousarray(a.pop("L0_cond_wt").T)
    a["c_wg_t"] = np.ascontiguousarray(a.pop("L0_cond_wg").T)
    a["c_keep_upper"] = np.triu(np.ones((P, P), np.float32))
    for n in ("q", "k", "v", "o"):
        a[f"c_attn_w{n}_t"] = np.ascontiguousarray(a.pop(f"L0_attn_W{n}").T)
    a["c_mlp1_w"] = np.ascontiguousarray(a.pop("L0_ffn_mlp1_w").reshape(E1, D, I1, 2).transpose(0, 1, 3, 2))
    a["c_mlp1_b"] = np.ascontiguousarray(a.pop("L0_ffn_mlp1_b").reshape(E1, I1 // P, P, 2).transpose(2, 0, 3, 1))
    rot = {n: a.pop(f"L1_attn_W{n}").T for n in "qkvo"}
    a["c_rot_wqk_t"] = np.ascontiguousarray(np.concatenate([rot["q"], rot["k"]], axis=1))
    a["c_rot_wv_t"] = np.ascontiguousarray(rot["v"])
    a["c_rot_wo_t"] = np.ascontiguousarray(rot["o"])
    freq = (1.0 / np.float32(10000.0) ** (np.arange(0, DR, 2, dtype=np.float32) / DR)).astype(np.float32)
    angle = np.arange(S, dtype=np.float32)[:, None] * freq
    cos, sin = np.cos(angle).astype(np.float32), np.sin(angle).astype(np.float32)
    a["c_rot_cos"] = np.ascontiguousarray(np.concatenate([cos, cos], axis=1).reshape(TB, P, DR).transpose(1, 0, 2))
    a["c_rot_sin"] = np.ascontiguousarray(np.concatenate([-sin, sin], axis=1).reshape(TB, P, DR).transpose(1, 0, 2))
    return a


def kernel(**inputs):
    import concourse.bacc as bacc
    from concourse.bass_utils import run_bass_kernel_spmd

    nc = bacc.Bacc("TRN2", target_bir_lowering=False, num_devices=1)
    arrays = _layout(inputs)
    aps = {n: nc.dram_tensor(n, v.shape, mybir.dt.from_np(v.dtype), kind="ExternalInput").ap() for n, v in arrays.items()}
    out = nc.dram_tensor("out", (B, S, D), F32, kind="ExternalOutput").ap()
    program(nc, aps, out)
    r = run_bass_kernel_spmd(nc, [arrays], core_ids=[0])
    return r.results[0]["out"]
```

```python
from contextlib import ExitStack

import numpy as np

import concourse.bass as bass
from concourse import mybir

F32 = mybir.dt.float32
BF16 = mybir.dt.bfloat16
U8 = mybir.dt.uint8
I32 = mybir.dt.int32
F32R = mybir.dt.float32r
U32 = mybir.dt.uint32
ALU = mybir.AluOpType
ACT = mybir.ActivationFunctionType
AX = mybir.AxisListType

P = 128
B, S, D = 4, 512, 256
TB = S // P
NT = B * TB
KD = D // P
H, DH = 16, 64
DR = D // H
E0, M0 = 8, 128
NSH = 2
G0 = 64
E1, I1 = 8, 512
IQ = 704
QMAX = 127.0
NPOS = S + P
MASKED = -1.0e30
EPS = 1e-5
HIGH_BITS = -4096
RNE = 12582912.0


FREE = 2


class Steps:

    def __init__(self, eng, sem, base=0, per_loop=None):
        self.eng, self.sem, self.base, self.n, self.per_loop = eng, sem, base, 0, per_loop

    def after(self, ins, apart=False):
        self.n += 1
        ins.then_inc(self.sem, 1)
        self.eng.wait_ge(self.sem, self.base + self.n)
        if apart:
            self.eng.nop(nofuse=True)

    def close(self):
        assert self.per_loop is None or self.n == self.per_loop, (self.n, self.per_loop)


def wait_apart(eng, sem, value):
    eng.wait_ge(sem, value)
    eng.nop(nofuse=True)


def high_part(nc, dst, src):
    return nc.vector.tensor_scalar(dst, src.bitcast(I32), HIGH_BITS, None, ALU.bitwise_and)


def rows(ap, n=P):
    return ap.rearrange("(a d) -> a d", a=1).broadcast_to([n, ap.shape[0]])


def columns(ap, k):
    return ap.rearrange("(k p) -> p k", k=k)


def bias_tables(nc, sem, bank, ident, pos_reversed, layers):
    NR = NPOS // P
    with ExitStack() as ctx:
        def sb(name, shape, dt=F32):
            return ctx.enter_context(nc.sbuf_tensor(name, shape, dt))

        pos = sb("bt_pos", [P, NR])
        row = [sb(f"bt_row{l}", [P, 5, D]) for l in range(2)]
        w1 = [sb(f"bt_w1{l}", [P, KD, D]) for l in range(2)]
        w2 = [sb(f"bt_w2{l}", [P, KD, H]) for l in range(2)]
        b2 = [sb(f"bt_b2{l}", [H, 1]) for l in range(2)]
        hid = [sb(f"bt_hid{l}", [P, NR, D]) for l in range(2)]
        act_out = [sb(f"bt_act{l}", [P, NR, D]) for l in range(2)]
        hid_t = [sb(f"bt_hid_t{l}", [P, KD, NPOS]) for l in range(2)]
        stats = sb("bt_stats", [P, NR, 6])
        mv = sb("bt_mv", [P, NR, 2])
        sd = sb("bt_sd", [P, NR])
        rstd = sb("bt_rstd", [P, NR])
        table = [sb(f"bt_table{l}", [H, NPOS]) for l in range(2)]
        phases = [(0, 0), (1, 0), (0, 1), (1, 1)]

        loaded = [sem(f"bt_loaded{l}") for l in range(2)]
        stepped = sem("bt_stepped")
        var_ready = sem("bt_var_ready")
        sd_ready = sem("bt_sd_ready")
        biased = sem("bt_biased")
        normed = sem("bt_normed")
        activated = sem("bt_activated")
        transposed = sem("bt_transposed")
        hid_t_ready = sem("bt_hid_t_ready")
        projected = sem("bt_projected")
        table_ready = sem("bt_table_ready")
        stored = sem("bt_stored")
        block = ctx.enter_context(nc.Block())

        @block.sync
        def _(sp):
            for l, lay in enumerate(layers):
                if l == 0:
                    sp.dma_start(pos[:], pos_reversed).then_inc(loaded[l], 16)
                for n, name in enumerate(("w0", "b0", "g0", "b1", "g1")):
                    sp.dma_start(row[l][:, n, :], rows(lay[name])).then_inc(loaded[l], 16)
                sp.dma_start(w1[l][:], lay["w1"].rearrange("(k p) n -> p k n", p=P)).then_inc(loaded[l], 16)
                sp.dma_start(w2[l][:], lay["w2"].rearrange("(k p) n -> p k n", p=P)).then_inc(loaded[l], 16)
                sp.dma_start(b2[l][:], lay["b2"].rearrange("(h a) -> h a", a=1)).then_inc(loaded[l], 16)
            for l, lay in enumerate(layers):
                sp.wait_ge(table_ready, 2 * (l + 1))
                sp.dma_start(lay["table"], table[l][:]).then_inc(stored, 16)
            sp.wait_ge(stored, 32)

        @block.vector
        def _(dv):
            st = Steps(dv, stepped)
            for n, (l, q) in enumerate(phases):
                x = hid[l]
                if q == 0:
                    dv.wait_ge(loaded[l], 16 * (9 if l == 0 else 8))
                    for t in range(NR):
                        ins = nc.vector.scalar_tensor_tensor(
                            x[:, t, :], row[l][:, 0, :], pos[:, t:t + 1], row[l][:, 1, :], ALU.mult, ALU.add)
                    st.after(ins)
                else:
                    dv.wait_ge(activated, l + 1)
                    dv.wait_ge(projected, l + 1)
                    for t in range(NR):
                        ins = nc.vector.tensor_tensor(
                            x[:, t, :], bank[3 + t // 2][:, D * (t % 2):D * (t % 2) + D], row[l][:, 3, :], ALU.add)
                    ins.then_inc(biased, 1)
                    dv.wait_ge(biased, l + 1)
                for t in range(NR):
                    ins = nc.vector.bn_stats(stats[:, t, :], x[:, t, :])
                st.after(ins)
                for t in range(NR):
                    ins = nc.vector.bn_aggr(mv[:, t, :], stats[:, t, :])
                st.after(ins)
                nc.vector.tensor_scalar(sd[:], mv[:, :, 1], EPS, None, ALU.add).then_inc(var_ready, 1)
                dv.wait_ge(sd_ready, n + 1)
                st.after(nc.vector.reciprocal(rstd[:], sd[:]))
                for t in range(NR):
                    ins = nc.vector.tensor_scalar(x[:, t, :], x[:, t, :], mv[:, t, 0:1], rstd[:, t:t + 1],
                                                  ALU.subtract, ALU.mult)
                st.after(ins)
                g = row[l][:, 2 + 2 * q, :].unsqueeze(1).broadcast_to([P, NR, D])
                nc.vector.tensor_tensor(x[:], x[:], g, ALU.mult).then_inc(normed, 1)
            for l in range(2):
                dv.wait_ge(projected, 3 + l)
                nc.vector.tensor_scalar(table[l][:, 0:512], bank[6][0:H, :], b2[l][:], None, ALU.add).then_inc(table_ready, 1)
                nc.vector.tensor_scalar(table[l][:, 512:NPOS], bank[7][0:H, 0:P], b2[l][:], None, ALU.add).then_inc(table_ready, 1)

        @block.scalar
        def _(ac):
            def root(n):
                ac.wait_ge(var_ready, n + 1)
                nc.scalar.activation(sd[:], sd[:], ACT.Sqrt).then_inc(sd_ready, 1)

            def activate(n):
                l, q = phases[n]
                ac.wait_ge(normed, n + 1)
                if q:
                    ac.wait_ge(transposed, l + 1)
                nc.scalar.activation(act_out[l][:], hid[l][:], ACT.Silu).then_inc(activated, 1)

            def copy_t(n):
                l, q = phases[n]
                ac.wait_ge(transposed, n + 1)
                if q:
                    ac.wait_ge(projected, l + 1)
                nc.scalar.copy(hid_t[l][:, 0, 0:512], bank[0][:])
                nc.scalar.copy(hid_t[l][:, 1, 0:512], bank[1][:])
                nc.scalar.copy(hid_t[l][:, :, 512:NPOS], bank[2][:, 0:D].rearrange("p (k n) -> p k n", k=KD)).then_inc(hid_t_ready, 1)

            for n in range(len(phases)):
                root(n)
                activate(n)
                copy_t(n)

        @block.tensor
        def _(pe):
            pe.wait_ge(loaded[0], 16 * 9)
            pe.wait_ge(loaded[1], 16 * 8)
            for n, (l, q) in enumerate(phases):
                pe.wait_ge(activated, n + 1)
                if n:
                    pe.wait_ge(hid_t_ready, n)
                for t in range(NR):
                    for k in range(KD):
                        dst = bank[k][:, P * t:P * t + P] if t < 4 else bank[2][:, P * k:P * k + P]
                        ins = nc.tensor.transpose(dst, act_out[l][:, t, P * k:P * k + P], ident[:])
                ins.then_inc(transposed, 1)
                pe.wait_ge(hid_t_ready, n + 1)
                if q == 0:
                    if l:
                        pe.wait_ge(biased, 1)
                    for t in range(NR):
                        for k in range(KD):
                            ins = nc.tensor.matmul(bank[3 + t // 2][:, D * (t % 2):D * (t % 2) + D],
                                                   hid_t[l][:, k, P * t:P * t + P], w1[l][:, k, :], start=k == 0, stop=k == KD - 1)
                else:
                    if l:
                        pe.wait_ge(table_ready, 2)
                    for lo, hi, dst in ((0, 512, bank[6]), (512, NPOS, bank[7])):
                        for k in range(KD):
                            ins = nc.tensor.matmul(dst[0:H, 0:hi - lo], w2[l][:, k, :], hid_t[l][:, k, lo:hi],
                                                   start=k == 0, stop=k == KD - 1)
                ins.then_inc(projected, 1)


def route(nc, dv, st, logits, ex, zsum, best, best_at, lane, picked, weight, softmax_all, exp_in, exp_ready, exp_done):
    E = E0
    for t in range(NT):
        ins = nc.vector.max(best[:, t, :], logits[:, t, :])
    st.after(ins)
    for t in range(NT):
        ins = nc.vector.max_index(best_at[:, t, :], best[:, t, :], logits[:, t, :])
    st.after(ins)
    top = best[:, :, 0:1].broadcast_to([P, NT, E])
    nc.vector.tensor_tensor(exp_in[:], logits[:], top, ALU.subtract).then_inc(exp_ready, 1)
    at = best_at[:, :, 0:2]
    st.after(nc.vector.tensor_copy(picked[:, :, 0:2], at))
    first = picked[:, :, 0:1].broadcast_to([P, NT, E])
    second = picked[:, :, 1:2].broadcast_to([P, NT, E])
    lanes = lane[:].unsqueeze(1).broadcast_to([P, NT, E])
    nc.vector.tensor_tensor(weight[:], lanes, first, ALU.is_equal)
    st.after(nc.vector.tensor_tensor(logits[:], lanes, second, ALU.is_equal))
    st.after(nc.vector.tensor_tensor(weight[:], weight[:], logits[:], ALU.add))
    dv.wait_ge(exp_done, 1)
    if softmax_all:
        st.after(nc.vector.tensor_reduce(zsum[:], ex[:], AX.X, ALU.add))
        st.after(nc.vector.reciprocal(zsum[:], zsum[:]))
        st.after(nc.vector.tensor_tensor(ex[:], ex[:], zsum[:].unsqueeze(2).broadcast_to([P, NT, E]), ALU.mult))
    st.after(nc.vector.tensor_tensor(ex[:], ex[:], weight[:], ALU.mult))
    st.after(nc.vector.tensor_reduce(zsum[:], ex[:], AX.X, ALU.add))
    if softmax_all:
        st.after(nc.vector.tensor_scalar(zsum[:], zsum[:], 1e-20, None, ALU.add))
    st.after(nc.vector.reciprocal(zsum[:], zsum[:]))
    st.after(nc.vector.tensor_tensor(weight[:], ex[:], zsum[:].unsqueeze(2).broadcast_to([P, NT, E]), ALU.mult))


def moe_conditioning(nc, sem, bank, Y, x_transposed, lane_d, cond_rep, wt_t, wg_t, w_gate, w_up, w_down,
                     sw_gate, sw_up, sw_down, layers, copied):
    NE = E0 + NSH
    WC = KD * M0
    with ExitStack() as ctx:
        def sb(name, shape, dt=F32):
            return ctx.enter_context(nc.sbuf_tensor(name, shape, dt))

        xt = sb("mc_xt", [P, B, KD * S])
        xt_high = sb("mc_xt_high", [P, B, KD, S], F32R)
        xt_low = sb("mc_xt_low", [P, B, KD, S], F32R)
        xt_bits = sb("mc_xt_bits", [P, KD * S], I32)
        w = sb("mc_w", [P, NE, 2 * WC + D])
        w_bits = sb("mc_w_bits", [P, 2, 2 * WC + D], I32)
        w_high = sb("mc_w_high", [P, NE, 2 * WC + D], F32R)
        w_low = sb("mc_w_low", [P, NE, 2 * WC + D], F32R)
        wtt = sb("mc_wtt", [P, KD, E0])
        wgt = sb("mc_wgt", [G0, E0])
        crep = sb("mc_crep", [G0, B, P])
        lane = sb("mc_lane", [P, E0])
        logits = sb("mc_logits", [P, NT, E0])
        exp_in = sb("mc_exp_in", [P, NT, E0])
        ex = sb("mc_ex", [P, NT, E0])
        zsum = sb("mc_zsum", [P, NT])
        best = sb("mc_best", [P, NT, 8])
        best_at = sb("mc_best_at", [P, NT, 8], U32)
        picked = sb("mc_picked", [P, NT, 2])
        weight = sb("mc_weight", [P, NT, E0])
        gate = sb("mc_gate", [P, 2, S])
        hid = sb("mc_hid", [P, 2, S])
        hid_bits = sb("mc_hid_bits", [P, 2, S], I32)
        hid_high = sb("mc_hid_high", [P, 2, S], F32R)
        hid_low = sb("mc_hid_low", [P, 2, S], F32R)

        routing_in = sem("mc_routing_in")
        x_in = [sem(f"mc_x_in{b}") for b in range(B)]
        w_in = [sem(f"mc_w_in{e}") for e in range(NE)]
        stepped = sem("mc_stepped")
        logits_done = sem("mc_logits_done")
        exp_ready, exp_done = sem("mc_exp_ready"), sem("mc_exp_done")
        gated, upped, downed = sem("mc_gated"), sem("mc_upped"), sem("mc_downed")
        gate_copied = sem("mc_gate_copied")
        leaked = sem("mc_leaked")
        hid_ready = sem("mc_hid_ready")
        bits_ready, high_ready, low_ready = sem("mc_bits_ready"), sem("mc_high_ready"), sem("mc_low_ready")
        x_bits_ready, x_high_ready, x_low_ready = sem("mc_x_bits_ready"), sem("mc_x_high_ready"), sem("mc_x_low_ready")
        w_bits_ready, w_high_ready, w_low_ready = sem("mc_w_bits_ready"), sem("mc_w_high_ready"), sem("mc_w_low_ready")
        added = sem("mc_added")
        block = ctx.enter_context(nc.Block())

        def rows_of(eng, body):
            body(0, True, False)
            with eng.Fori(1, B - 1) as it:
                body(it, False, False)
            body(B - 1, False, True)

        def three(lhs, rhs):
            return [(lhs[0], rhs[0]), (lhs[1], rhs[0]), (lhs[0], rhs[1])]

        @block.sync
        def _(sp):
            def load_x(b):
                sp.dma_start(xt[:, b].rearrange("p (k s) -> p k s", k=KD),
                             x_transposed[b].rearrange("(k p) s -> p k s", p=P)).then_inc(x_in[b], 16)

            load_x(0)
            for e in range(NE):
                one = slice(M0 * (e - E0), M0 * (e - E0) + M0)
                gate_d, up_d = (w_gate[e], w_up[e]) if e < E0 else (sw_gate[:, one], sw_up[:, one])
                for n, src in enumerate((gate_d, up_d)):
                    sp.dma_start(w[:, e, WC * n:WC * n + WC].rearrange("p (k m) -> p k m", k=KD),
                                 src.rearrange("(k p) m -> p k m", p=P)).then_inc(w_in[e], 16)
                sp.dma_start(w[:, e, 2 * WC:], w_down[e] if e < E0 else sw_down[one, :]).then_inc(w_in[e], 16)
                if e == 1:
                    sp.dma_start(wtt[:], wt_t.rearrange("(k p) e -> p k e", p=P)).then_inc(routing_in, 16)
                    sp.dma_start(wgt[:], wg_t).then_inc(routing_in, 16)
                    sp.dma_start(crep[:], cond_rep).then_inc(routing_in, 16)
                    sp.dma_start(lane[:], lane_d).then_inc(routing_in, 16)
                    for b in range(1, B):
                        load_x(b)
            for l, lay in enumerate(layers):
                line = lay["table"]
                line = bass.AP(tensor=line.tensor, offset=line.offset, ap=[[NPOS, H], [0, P], [1, NPOS]])
                sp.dma_start(lay["copies"], line).then_inc(copied, 16)

        @block.tensor
        def _(pe):
            def up(it, first, e):
                n = NE * it + e
                cols = [(xt_high[:, it, k, :], xt_low[:, it, k, :]) for k in range(KD)]
                if first:
                    pe.wait_ge(w_high_ready, e + 1)
                    pe.wait_ge(w_low_ready, e + 1)
                if e == 0:
                    pe.wait_ge(x_high_ready, it + 1)
                    pe.wait_ge(x_low_ready, it + 1)
                for part, dst, freed, done in ((0, bank[e % 2], gate_copied, gated), (1, bank[2 + e % 2], hid_ready, upped)):
                    pe.wait_ge(freed, n + 1)
                    pairs = []
                    for k in range(KD):
                        at = slice(WC * part + M0 * k, WC * part + M0 * k + M0)
                        pairs += three((w_high[:, e, at], w_low[:, e, at]), cols[k])
                    for m, (l, r) in enumerate(pairs):
                        ins = nc.tensor.matmul(dst[:], l, r, start=m == 0, stop=m == len(pairs) - 1)
                    ins.then_inc(done, 1)

            def down(it, e):
                n = NE * it + e
                pe.wait_ge(high_ready, FREE + n + 1)
                pe.wait_ge(low_ready, FREE + n + 1)
                for j in range(2):
                    pe.wait_ge(added, 2 * n + j + 1)
                    for i in (2 * j, 2 * j + 1):
                        tile = slice(P * i, P * i + P)
                        pairs = three((hid_high[:, e % 2, tile], hid_low[:, e % 2, tile]), (w_high[:, e, 2 * WC:], w_low[:, e, 2 * WC:]))
                        for m, (l, r) in enumerate(pairs):
                            ins = nc.tensor.matmul(bank[4 + 2 * (e % 2) + j][:, D * (i % 2):D * (i % 2) + D], l, r,
                                                   start=m == 0, stop=m == 2)
                    ins.then_inc(downed, 1)

            def routing():
                pe.wait_ge(routing_in, 64)
                for t in range(NT):
                    b, i = divmod(t, TB)
                    if i == 0:
                        pe.wait_ge(x_in[b], 16)
                    dst = bank[6][:, E0 * t:E0 * t + E0]
                    for k in range(KD):
                        nc.tensor.matmul(dst, xt[:, b, S * k + P * i:S * k + P * i + P], wtt[:, k, :], start=k == 0, stop=False)
                    ins = nc.tensor.matmul(dst, crep[:, b, :], wgt[:], start=False, stop=True)
                ins.then_inc(logits_done, 1)

            def row(it, first, last):
                for e in range(NE):
                    up(it, first, e)
                    if first and e == 1:
                        routing()
                    if first and e == 2:
                        pe.wait_ge(exp_ready, 1)
                    if e >= 2:
                        down(it, e - 2)
                    elif not first:
                        down(it - 1, NE + e - 2)
                if last:
                    down(it, NE - 2)
                    down(it, NE - 1)

            pe.sem_inc(downed, 2 * FREE)
            rows_of(pe, row)

        @block.scalar
        def _(ac):
            def high(it, e):
                n = NE * it + e
                ac.wait_ge(bits_ready, n + 1)
                ac.wait_ge(downed, 2 * n + 2)
                nc.scalar.copy(hid_high[:, e % 2, :], hid_bits[:, e % 2, :].bitcast(F32)).then_inc(high_ready, 1)

            def split_x(it):
                ac.wait_ge(x_bits_ready, it + 1)
                nc.scalar.copy(xt_high[:, bass.ds(it, 1)].rearrange("p b k s -> p (b k s)"), xt_bits[:].bitcast(F32)).then_inc(x_high_ready, 1)

            def split_w(e):
                ac.wait_ge(w_bits_ready, e + 1)
                nc.scalar.copy(w_high[:, e, :], w_bits[:, e % 2, :].bitcast(F32)).then_inc(w_high_ready, 1)

            def row(it, first, last):
                for e in range(NE):
                    n = NE * it + e
                    if first and e + 1 < NE:
                        split_w(e + 1)
                    if e == 4 and not last:
                        split_x(it + 1)
                    ac.wait_ge(gated, n + 1)
                    ac.wait_ge(leaked, n + 1)
                    nc.scalar.copy(gate[:, e % 2, :], bank[e % 2][:]).then_inc(gate_copied, 1)
                    if e:
                        high(it, e - 1)
                    elif not first:
                        high(it - 1, NE - 1)
                    if first and e == 1:
                        ac.wait_ge(exp_ready, 1)
                        nc.scalar.activation(ex[:], exp_in[:], ACT.Exp).then_inc(exp_done, 1)
                if last:
                    high(it, NE - 1)

            ac.sem_inc(gate_copied, FREE)
            ac.sem_inc(high_ready, FREE)
            split_x(0)
            split_w(0)
            rows_of(ac, row)

        @block.gpsimd
        def _(gp):
            def low(it, e):
                n = NE * it + e
                gp.wait_ge(bits_ready, n + 1)
                gp.wait_ge(downed, 2 * n + 2)
                nc.gpsimd.tensor_tensor(hid_low[:, e % 2, :], hid[:, e % 2, :], hid_bits[:, e % 2, :].bitcast(F32),
                                        ALU.subtract).then_inc(low_ready, 1)

            def split_x(it):
                gp.wait_ge(x_bits_ready, it + 1)
                nc.gpsimd.tensor_tensor(xt_low[:, bass.ds(it, 1)].rearrange("p b k s -> p (b k s)"),
                                        xt[:, bass.ds(it, 1)].rearrange("p b n -> p (b n)"), xt_bits[:].bitcast(F32),
                                        ALU.subtract).then_inc(x_low_ready, 1)

            def split_w(e):
                gp.wait_ge(w_bits_ready, e + 1)
                nc.gpsimd.tensor_tensor(w_low[:, e, :], w[:, e, :], w_bits[:, e % 2, :].bitcast(F32), ALU.subtract).then_inc(w_low_ready, 1)

            def row(it, first, last):
                for e in range(NE):
                    if first and e + 1 < NE:
                        split_w(e + 1)
                    if e == 4 and not last:
                        split_x(it + 1)
                    if e:
                        low(it, e - 1)
                    elif not first:
                        low(it - 1, NE - 1)
                if last:
                    low(it, NE - 1)

            gp.sem_inc(low_ready, FREE)
            split_x(0)
            split_w(0)
            rows_of(gp, row)

        @block.vector
        def _(dv):
            st = Steps(dv, stepped)

            def split_x(it, first=False):
                if not first:
                    dv.wait_ge(x_high_ready, it)
                    dv.wait_ge(x_low_ready, it)
                high_part(nc, xt_bits[:], xt[:, bass.ds(it, 1)].rearrange("p b n -> p (b n)")).then_inc(x_bits_ready, 1)

            def split_w(e):
                dv.wait_ge(w_in[e], 48)
                if e >= 2:
                    dv.wait_ge(w_high_ready, e - 1)
                    dv.wait_ge(w_low_ready, e - 1)
                high_part(nc, w_bits[:, e % 2, :], w[:, e, :]).then_inc(w_bits_ready, 1)

            def bits(it, e):
                n = NE * it + e
                dv.wait_ge(hid_ready, FREE + n + 1)
                dv.wait_ge(high_ready, n + 1)
                dv.wait_ge(low_ready, n + 1)
                high_part(nc, hid_bits[:, e % 2, :], hid[:, e % 2, :]).then_inc(bits_ready, 1)

            def add(it, e):
                n = NE * it + e
                for j in range(2):
                    dv.wait_ge(downed, 2 * FREE + 2 * n + j + 1)
                    if e:
                        dv.wait_ge(added, FREE * 2 + 2 * n - 2 + j + 1)
                    for i in (2 * j, 2 * j + 1):
                        src = bank[4 + 2 * (e % 2) + j][:, D * (i % 2):D * (i % 2) + D]
                        y = Y[:, TB * it + i, :]
                        if e == 0:
                            ins = nc.vector.tensor_scalar(y, src, weight[:, TB * it + i, 0:1], None, ALU.mult)
                        else:
                            by = weight[:, TB * it + i, e:e + 1] if e < E0 else 1.0
                            ins = nc.vector.scalar_tensor_tensor(y, src, by, y, ALU.mult, ALU.add)
                    ins.then_inc(added, 1)

            def row(it, first, last):
                for e in range(NE):
                    n = NE * it + e
                    if first and e + 1 < NE:
                        split_w(e + 1)
                    if e == 4 and first:
                        for b in range(1, B):
                            dv.wait_ge(x_in[b], 16)
                    if e == 4 and not last:
                        split_x(it + 1)
                    dv.wait_ge(gate_copied, FREE + n + 1)
                    dv.wait_ge(low_ready, n + 1)
                    nc.vector.scalar_tensor_tensor(hid[:, e % 2, :], gate[:, e % 2, :], 0.01, gate[:, e % 2, :],
                                                   ALU.mult, ALU.max).then_inc(leaked, 1)
                    dv.wait_ge(leaked, FREE + n + 1)
                    dv.wait_ge(upped, n + 1)
                    nc.vector.tensor_tensor(hid[:, e % 2, :], hid[:, e % 2, :], bank[2 + e % 2][:], ALU.mult).then_inc(hid_ready, 1)
                    bits(it, e)
                    if first and e == 1:
                        dv.wait_ge(logits_done, 1)
                        st.after(nc.vector.tensor_scalar(logits[:], bank[6][:, 0:NT * E0].rearrange("p (t e) -> p t e", e=E0), 0.5, None, ALU.mult))
                        route(nc, dv, st, logits, ex, zsum, best, best_at, lane, picked, weight, True, exp_in, exp_ready, exp_done)
                    if e >= 3:
                        add(it, e - 3)
                    elif not first:
                        add(it - 1, NE + e - 3)
                if last:
                    for e in (NE - 3, NE - 2, NE - 1):
                        add(it, e)

            dv.sem_inc(leaked, FREE)
            dv.sem_inc(hid_ready, FREE)
            dv.sem_inc(added, 2 * FREE)
            dv.wait_ge(x_in[0], 16)
            split_x(0, True)
            split_w(0)
            rows_of(dv, row)


def linear_attention(nc, sem, x_loaded, bank, X, Y, ident, keep_upper, wq_t, wk_t, wv_t, wo_t):
    K = 64
    with ExitStack() as ctx:
        def sb(name, shape, dt=F32):
            return ctx.enter_context(nc.sbuf_tensor(name, shape, dt))

        wqk = sb("la_wqk", [P, KD, 2, K])
        wv = sb("la_wv", [P, KD, K])
        wo = sb("la_wo", [K, D])
        keep = sb("la_keep", [P, P])
        yt = sb("la_yt", [P, KD, S])
        below = sb("la_below", [2 * K, S])
        expd = sb("la_expd", [2 * K, S])
        qk = sb("la_qk", [K, 2, S])
        v1 = sb("la_v1", [P, TB, K + 1])
        at = sb("la_at", [P, TB, S])
        den = sb("la_den", [P, TB])
        o = sb("la_o", [P, TB, K])
        ot = sb("la_ot", [K, S])

        weights_in = sem("la_weights_in")
        row_turned = sem("la_row_turned")
        yt_ready = sem("la_yt_ready")
        projected = sem("la_projected")
        below_ready = sem("la_below_ready")
        exp_ready = sem("la_exp_ready")
        qk_ready = sem("la_qk_ready")
        v1_ready = sem("la_v1_ready")
        ones_set = sem("la_ones_set")
        scored = sem("la_scored")
        at_ready = sem("la_at_ready")
        summed = sem("la_summed")
        den_steps = sem("la_den_steps")
        o_ready = sem("la_o_ready")
        o_turned = sem("la_o_turned")
        ot_ready = sem("la_ot_ready")
        out_done = sem("la_out_done")
        x_added = sem("la_x_added")
        block = ctx.enter_context(nc.Block())
        at_bank = [(5, 0), (6, 0), (7, 0), (6, 384)]

        @block.sync
        def _(sp):
            for n, w in enumerate((wq_t, wk_t)):
                sp.dma_start(wqk[:, :, n, :], w.rearrange("(k p) m -> p k m", p=P)).then_inc(weights_in, 16)
            sp.dma_start(wv[:], wv_t.rearrange("(k p) m -> p k m", p=P)).then_inc(weights_in, 16)
            sp.dma_start(wo[:], wo_t).then_inc(weights_in, 16)
            sp.dma_start(keep[:], keep_upper).then_inc(weights_in, 16)

        @block.gpsimd
        def _(gp):
            nc.gpsimd.memset(v1[:, :, K:K + 1], 1.0).then_inc(ones_set, 1)

        @block.tensor
        def _(pe):
            def project(b):
                if b:
                    pe.wait_ge(v1_ready, b)
                for k in range(KD):
                    for i in range(TB):
                        ins = nc.tensor.transpose(bank[k][:, P * i:P * i + P], Y[:, TB * b + i, P * k:P * k + P], ident[:])
                ins.then_inc(row_turned, 1)
                pe.wait_ge(yt_ready, b + 1)
                for k in range(KD):
                    nc.tensor.matmul(bank[2][:], wqk[:, k].rearrange("p n m -> p (n m)"), yt[:, k, :], start=k == 0, stop=k == KD - 1)
                for i in range(TB):
                    for k in range(KD):
                        ins = nc.tensor.matmul(bank[4][:, K * i:K * i + K], yt[:, k, P * i:P * i + P], wv[:, k, :],
                                               start=k == 0, stop=k == KD - 1)
                ins.then_inc(projected, 1)

            pe.wait_ge(weights_in, 80)
            pe.wait_ge(ones_set, 1)
            project(0)
            for b in range(B):
                pe.wait_ge(qk_ready, b + 1)
                if b:
                    pe.wait_ge(x_added, b)
                for c, (n, at_col) in enumerate(at_bank):
                    w = S - P * c
                    ins = nc.tensor.matmul(bank[n][:, at_col:at_col + w], qk[:, 1, P * c:P * c + P], qk[:, 0, P * c:S],
                                           start=True, stop=True)
                ins.then_inc(scored, 1)
                if b + 1 < B:
                    project(b + 1)
                pe.wait_ge(at_ready, b + 1)
                pe.wait_ge(v1_ready, b + 1)
                for r in range(TB):
                    for c in range(r + 1):
                        ins = nc.tensor.matmul(bank[7][:, (K + 1) * r:(K + 1) * (r + 1)], at[:, c, P * r:P * r + P], v1[:, c, :],
                                               start=c == 0, stop=c == r)
                ins.then_inc(summed, 1)
                pe.wait_ge(o_ready, b + 1)
                for r in range(TB):
                    ins = nc.tensor.transpose(bank[7][0:K, P * r:P * r + P], o[:, r, :], ident[:])
                ins.then_inc(o_turned, 1)
                pe.wait_ge(ot_ready, b + 1)
                for r in range(TB):
                    ins = nc.tensor.matmul(bank[5 + r // 2][:, D * (r % 2):D * (r % 2) + D], ot[:, P * r:P * r + P], wo[:],
                                           start=True, stop=True)
                ins.then_inc(out_done, 1)

        @block.scalar
        def _(ac):
            def copy_yt(b):
                ac.wait_ge(row_turned, b + 1)
                if b:
                    ac.wait_ge(projected, b)
                for k in range(KD):
                    ins = nc.scalar.copy(yt[:, k, :], bank[k][:])
                ins.then_inc(yt_ready, 1)

            def exp_qk(b):
                ac.wait_ge(below_ready, b + 1)
                nc.scalar.activation(expd[:], below[:], ACT.Exp).then_inc(exp_ready, 1)
                if b:
                    ac.wait_ge(summed, b)
                nc.scalar.copy(v1[:, :, 0:K], bank[4][:, 0:TB * K].rearrange("p (i m) -> p i m", i=TB)).then_inc(v1_ready, 1)

            copy_yt(0)
            exp_qk(0)
            for b in range(B):
                if b + 1 < B:
                    copy_yt(b + 1)
                    exp_qk(b + 1)
                ac.wait_ge(o_turned, b + 1)
                nc.scalar.copy(ot[:], bank[7][0:K, :]).then_inc(ot_ready, 1)

        @block.vector
        def _(dv):
            st = Steps(dv, den_steps)

            def clamp(b):
                dv.wait_ge(projected, b + 1)
                nc.vector.tensor_scalar(below[:], bank[2][:], 0.0, None, ALU.min).then_inc(below_ready, 1)

            def elu(b):
                dv.wait_ge(exp_ready, b + 1)
                for n in range(2):
                    at_n = slice(K * n, K * n + K)
                    ins = nc.vector.scalar_tensor_tensor(qk[:, n, :], bank[2][at_n, :], 0.0, expd[at_n, :], ALU.max, ALU.add)
                ins.then_inc(qk_ready, 1)

            dv.wait_ge(weights_in, 80)
            dv.wait_ge(x_loaded, 16)
            clamp(0)
            elu(0)
            for b in range(B):
                dv.wait_ge(scored, b + 1)
                for c, (n, col) in enumerate(at_bank):
                    lo = P * c
                    ins = nc.vector.tensor_tensor(at[:, c, lo:lo + P], bank[n][:, col:col + P], keep[:], ALU.mult)
                    if c < TB - 1:
                        ins = nc.vector.tensor_copy(at[:, c, lo + P:S], bank[n][:, col + P:col + S - lo])
                ins.then_inc(at_ready, 1)
                if b + 1 < B:
                    clamp(b + 1)
                dv.wait_ge(summed, b + 1)
                sums = bank[7][:, 0:(K + 1) * TB].rearrange("p (r m) -> p r m", r=TB)
                st.after(nc.vector.tensor_scalar(den[:], sums[:, :, K], 1e-6, None, ALU.add))
                st.after(nc.vector.reciprocal(den[:], den[:]))
                for r in range(TB):
                    ins = nc.vector.tensor_scalar(o[:, r, :], sums[:, r, 0:K], den[:, r:r + 1], None, ALU.mult)
                ins.then_inc(o_ready, 1)
                if b + 1 < B:
                    elu(b + 1)
                dv.wait_ge(out_done, b + 1)
                for j in range(2):
                    x = X[:, TB * b + 2 * j:TB * b + 2 * j + 2, :].rearrange("p i n -> p (i n)")
                    ins = nc.vector.tensor_tensor(x, x, bank[5 + j][:], ALU.add)
                ins.then_inc(x_added, 1)


def attention_inputs(nc, sem, pre, bank, X, ident, w, q_all, kt, v_all, null_neg, null_v):
    cosine = "q_scale" in w
    kt_high, kt_low = kt
    with ExitStack() as ctx:
        def sb(name, shape, dt=F32):
            return ctx.enter_context(nc.sbuf_tensor(pre + name, shape, dt))

        wq = sb("wq", [P, KD, H * DH])
        NKV = 2 * DH + H
        wkv = sb("wkv", [P, KD, NKV])
        g_norm = sb("g_norm", [P, KD])
        null_k = sb("null_k", [P, DH])
        null_w = wkv[:, :, 2 * DH:]
        null_b = sb("null_b", [P, H])
        null_t = sb("null_t", [P, TB, H])
        null_p = sb("null_p", [P, KD, H, DH])
        mask_words = sb("mask_words", [P, B * S // 4], I32)
        mask8 = mask_words[:].bitcast(U8)
        scales = sb("scales", [P, 2, DH])
        kt_full = sb("kt_full", [P, B, S])
        kcol = sb("kcol", [P, 3])
        one = sb("one", [P, 3])
        xn = sb("xn", [P, TB, D])
        xnt = sb("xnt", [P, KD, S])
        xnt_bits = sb("xnt_bits", [P, KD, S], I32)
        xnt_high = sb("xnt_high", [P, KD, S], F32R)
        xnt_low = sb("xnt_low", [P, KD, S], F32R)
        wq_bits = sb("wq_bits", [P, KD, H * DH], I32)
        wq_high = sb("wq_high", [P, KD, H * DH], F32R)
        wq_low = sb("wq_low", [P, KD, H * DH], F32R)
        stats = sb("stats", [P, TB, 6])
        mv = sb("mv", [P, TB, 2])
        var = sb("var", [P, TB])
        sd = sb("sd", [P, TB])
        rstd = sb("rstd", [P, TB])
        squares = sb("squares", [P, 2, 512])
        k_raw = sb("k_raw", [P, TB, DH])
        k_sq = sb("k_sq", [P, TB, DH])
        k_n = sb("k_n", [P, TB, 2, DH])
        ss = sb("ss", [P, TB * (H + 1)])
        norm = sb("norm", [P, TB * (H + 1)])
        rinv = sb("rinv", [P, TB * (H + 1)])

        params_in = sem(pre + "params_in")
        prologue = sem(pre + "prologue")
        null_ss = sem(pre + "null_ss")
        null_sd = sem(pre + "null_sd")
        stepped = sem(pre + "stepped")
        var_ready = sem(pre + "var_ready")
        sd_ready = sem(pre + "sd_ready")
        xn_ready = sem(pre + "xn_ready")
        xn_turned = sem(pre + "xn_turned")
        xnt_ready = sem(pre + "xnt_ready")
        kv_done = sem(pre + "kv_done")
        k_copied = sem(pre + "k_copied")
        q_done = sem(pre + "q_done")
        q_copied = sem(pre + "q_copied")
        q_summed = sem(pre + "q_summed")
        ss_ready = sem(pre + "ss_ready")
        norm_ready = sem(pre + "norm_ready")
        rinv_ready = sem(pre + "rinv_ready")
        kn_ready = sem(pre + "kn_ready")
        k_turned = sem(pre + "k_turned")
        kt_ready = sem(pre + "kt_ready")
        null_done = sem(pre + "null_done")
        q_scaled = sem(pre + "q_scaled")
        k_split = sem(pre + "k_split")
        xnt_split, xnt_high_ready, xnt_low_ready = sem(pre + "xnt_split"), sem(pre + "xnt_high_ready"), sem(pre + "xnt_low_ready")
        wq_split, wq_high_ready, wq_low_ready = sem(pre + "wq_split"), sem(pre + "wq_high_ready"), sem(pre + "wq_low_ready")
        block = ctx.enter_context(nc.Block())
        n_params = 8 + 6 * cosine
        PRO = 11 if cosine else 5
        NQ = 2 * TB
        AHEAD = 4

        @block.sync
        def _(sp):
            sp.dma_start(g_norm[:], columns(w["g_norm"], KD)).then_inc(params_in, 16)
            sp.dma_start(wkv[:, :, 0:2 * DH], w["Wkv"].rearrange("(k p) n -> p k n", p=P)).then_inc(params_in, 16)
            for k in range(KD):
                sp.dma_start(wq[:, k, :], w["Wq"][P * k:P * k + P, :]).then_inc(params_in, 16)
            sp.dma_start(null_k[:], rows(w["cond"][0])).then_inc(params_in, 16)
            for half in range(2):
                sp.dma_start(null_v[DH * half:DH * half + DH, :], w["cond"][1].rearrange("(d a) -> d a", a=1)).then_inc(params_in, 16)
            sp.dma_start(null_b[:], rows(w["null_attn_bias"])).then_inc(params_in, 16)
            sp.dma_start(mask_words[DH:DH + 1, :], w["mask"].rearrange("b s -> (b s)").rearrange("(a n) -> a n", a=1)).then_inc(params_in, 16)
            if cosine:
                for n, name in enumerate(("q_scale", "k_scale")):
                    sp.dma_start(scales[:, n, :], rows(w[name])).then_inc(params_in, 16)
                    for half in range(2):
                        sp.dma_start(kcol[DH * half:DH * half + DH, n:n + 1], w[name].rearrange("(d a) -> d a", a=1)).then_inc(params_in, 16)

        @block.gpsimd
        def _(gp):
            gp.wait_ge(wq_split, 1)
            nc.gpsimd.tensor_tensor(wq_low[:], wq[:], wq_bits[:].bitcast(F32), ALU.subtract).then_inc(wq_low_ready, 1)
            if cosine:
                gp.sem_inc(q_scaled, 1)

            def low_part(b):
                gp.wait_ge(xnt_split, b + 1)
                if b:
                    gp.wait_ge(q_done, NQ * b)
                nc.gpsimd.tensor_tensor(xnt_low[:], xnt[:], xnt_bits[:].bitcast(F32), ALU.subtract).then_inc(xnt_low_ready, 1)

            low_part(0)
            for b in range(B):
                if b + 1 < B:
                    low_part(b + 1)
                if cosine:
                    gp.wait_ge(rinv_ready, b + 1)
                    for i in range(TB):
                        q = q_all[:, TB * b + i]
                        r = rinv[:, H * i:H * i + H].unsqueeze(2).broadcast_to([P, H, DH])
                        ins = nc.gpsimd.tensor_tensor(q, q, r, ALU.mult)
                    ins.then_inc(q_scaled, 1)

        @block.tensor
        def _(pe):
            def turn_k(b):
                pe.wait_ge(kn_ready, b + 1)
                for i in range(TB):
                    ins = nc.tensor.transpose(bank[0][:, P * i:P * i + P], k_n[:, i].rearrange("p s d -> p (s d)"), ident[:])
                ins.then_inc(k_turned, 1)

            for b in range(B):
                pe.wait_ge(xn_ready, b + 1)
                if b >= 2:
                    pe.wait_ge(kt_ready, b - 1)
                for k in range(KD):
                    for i in range(TB):
                        ins = nc.tensor.transpose(bank[k][:, P * i:P * i + P], xn[:, i, P * k:P * k + P], ident[:])
                ins.then_inc(xn_turned, 1)
                if b == 0:
                    pe.wait_ge(params_in, 16 * (n_params + 1))
                    pe.wait_ge(prologue, PRO)
                pe.wait_ge(xnt_ready, b + 1)
                pe.wait_ge(null_done, b + 1)
                for i in range(TB):
                    for k in range(KD):
                        ins = nc.tensor.matmul(bank[2 + i // 2][:, NKV * (i % 2):NKV * (i % 2) + NKV], xnt[:, k, P * i:P * i + P],
                                               wkv[:, k, :], start=k == 0, stop=k == KD - 1)
                ins.then_inc(kv_done, 1)
                if b:
                    turn_k(b - 1)
                if b == 0:
                    pe.wait_ge(wq_high_ready, 1)
                    pe.wait_ge(wq_low_ready, 1)
                pe.wait_ge(xnt_high_ready, b + 1)
                pe.wait_ge(xnt_low_ready, b + 1)
                for m in range(NQ):
                    i, half = divmod(m, 2)
                    pe.wait_ge(q_copied, NQ * b + m + 1)
                    tile, cols = slice(P * i, P * i + P), slice(512 * half, 512 * half + 512)
                    pairs = [(x[:, k, tile], y[:, k, cols]) for k in range(KD)
                             for x, y in ((xnt_high, wq_high), (xnt_low, wq_high), (xnt_high, wq_low))]
                    for n, (x, y) in enumerate(pairs):
                        ins = nc.tensor.matmul(bank[4 + m % 4][:], x, y, start=n == 0, stop=n == len(pairs) - 1)
                    ins.then_inc(q_done, 1)
            turn_k(B - 1)

        @block.scalar
        def _(ac):
            ac.sem_inc(q_copied, AHEAD)
            def root(b):
                ac.wait_ge(var_ready, b + 1)
                nc.scalar.activation(sd[:], var[:], ACT.Sqrt).then_inc(sd_ready, 1)

            def copy_kt(b):
                ac.wait_ge(k_turned, b + 1)
                if b == 0:
                    ac.wait_ge(prologue, PRO)
                nc.scalar.activation(kt_full[:, b, :], bank[0][:], ACT.Copy, scale=kcol[:, 2:3]).then_inc(kt_ready, 1)

            root(0)
            if cosine:
                ac.wait_ge(null_ss, 1)
                nc.scalar.activation(one[:, 2:3], one[:, 1:2], ACT.Sqrt).then_inc(null_sd, 1)
            ac.wait_ge(params_in, 16 * (n_params + 1))
            for b in range(B):
                ac.wait_ge(xn_turned, b + 1)
                if b:
                    ac.wait_ge(xnt_low_ready, b)
                for k in range(KD):
                    ins = nc.scalar.activation(xnt[:, k, :], bank[k][:], ACT.Copy, scale=g_norm[:, k:k + 1])
                ins.then_inc(xnt_ready, 1)
                if b == 0:
                    ac.wait_ge(wq_split, 1)
                    nc.scalar.copy(wq_high[:], wq_bits[:].bitcast(F32)).then_inc(wq_high_ready, 1)
                ac.wait_ge(xnt_split, b + 1)
                nc.scalar.copy(xnt_high[:], xnt_bits[:].bitcast(F32)).then_inc(xnt_high_ready, 1)
                ac.wait_ge(kv_done, b + 1)
                for j in range(2):
                    kv = bank[2 + j][:, 0:2 * NKV].rearrange("p (i n) -> p i n", i=2)
                    nc.scalar.copy(k_raw[:, 2 * j:2 * j + 2, :], kv[:, :, 0:DH])
                    ins = nc.scalar.copy(v_all[:, TB * b + 2 * j:TB * b + 2 * j + 2, :], kv[:, :, DH:2 * DH])
                ins.then_inc(k_copied, 1)
                if b + 1 < B:
                    root(b + 1)
                if b:
                    copy_kt(b - 1)
                for m in range(NQ):
                    i, half = divmod(m, 2)
                    ac.wait_ge(q_done, NQ * b + m + 1)
                    if cosine:
                        ac.wait_ge(q_summed, NQ * b + m + 1)
                        nc.scalar.activation(squares[:, m % 2, :], bank[4 + m % 4][:], ACT.Square)
                    nc.scalar.copy(q_all[:, TB * b + i, 8 * half:8 * half + 8, :],
                                   bank[4 + m % 4][:].rearrange("p (h d) -> p h d", d=DH)).then_inc(q_copied, 1)
                if cosine:
                    ac.wait_ge(ss_ready, b + 1)
                    nc.scalar.activation(norm[:], ss[:], ACT.Sqrt).then_inc(norm_ready, 1)
            copy_kt(B - 1)

        @block.vector
        def _(dv):
            pro = Steps(dv, prologue)
            dv.sem_inc(null_done, 1)
            dv.sem_inc(q_summed, 2)
            st = Steps(dv, stepped)

            def norm_x(b):
                for i in range(TB):
                    ins = nc.vector.bn_stats(stats[:, i, :], X[:, TB * b + i, :])
                st.after(ins)
                for i in range(TB):
                    ins = nc.vector.bn_aggr(mv[:, i, :], stats[:, i, :])
                st.after(ins)
                nc.vector.tensor_scalar(var[:], mv[:, :, 1], EPS, None, ALU.add).then_inc(var_ready, 1)
                dv.wait_ge(sd_ready, b + 1)
                st.after(nc.vector.reciprocal(rstd[:], sd[:]))
                if b:
                    dv.wait_ge(xn_turned, b)
                for i in range(TB):
                    ins = nc.vector.tensor_scalar(xn[:, i, :], X[:, TB * b + i, :], mv[:, i, 0:1], rstd[:, i:i + 1],
                                                  ALU.subtract, ALU.mult)
                ins.then_inc(xn_ready, 1)

            norm_x(0)
            dv.wait_ge(params_in, 16 * (n_params + 1))
            high_part(nc, wq_bits[:], wq[:]).then_inc(wq_split, 1)
            mask_row = kt_low[DH:DH + 1].rearrange("p b s -> p (b s)")
            pro.after(nc.vector.tensor_scalar(mask_row, mask8[DH:DH + 1, :], 1.0, -MASKED, ALU.subtract, ALU.mult))
            if cosine:
                pro.after(nc.vector.tensor_tensor_reduce(out=k_sq[:, 0, :], in0=null_k[:], in1=null_k[:], scale=1.0, scalar=0.0,
                                                         op0=ALU.mult, op1=ALU.add, accum_out=one[:, 0:1]))
                nc.vector.tensor_scalar(one[:, 1:2], one[:, 0:1], 1e-24, None, ALU.max).then_inc(null_ss, 1)
                dv.wait_ge(null_sd, 1)
                pro.after(nc.vector.reciprocal(one[:, 0:1], one[:, 2:3]))
                pro.after(nc.vector.tensor_scalar(null_k[:], null_k[:], one[:, 0:1], None, ALU.mult))
                pro.after(nc.vector.tensor_scalar(null_k[:], null_k[:], 8.0, None, ALU.mult))
                pro.after(nc.vector.tensor_tensor(null_k[:], null_k[:], scales[:, 0, :], ALU.mult))
                pro.after(nc.vector.tensor_tensor(null_k[:], null_k[:], scales[:, 1, :], ALU.mult))
                pro.after(nc.vector.tensor_tensor(kcol[:, 2:3], kcol[:, 0:1], kcol[:, 1:2], ALU.mult))
                pro.after(nc.vector.tensor_scalar(kcol[:, 2:3], kcol[:, 2:3], 8.0, None, ALU.mult))
            else:
                pro.after(nc.vector.tensor_scalar(null_k[:], null_k[:], DH ** -0.5, None, ALU.mult))
                pro.after(nc.vector.memset(kcol[:, 2:3], DH ** -0.5))
            for k in range(KD):
                q4 = wq[:, k, :].rearrange("p (h d) -> p h d", h=H)
                ins = nc.vector.tensor_tensor(null_p[:, k], q4, null_k[:].unsqueeze(1).broadcast_to([P, H, DH]), ALU.mult)
            pro.after(ins)
            pro.after(nc.vector.tensor_reduce(null_w, null_p[:], AX.X, ALU.add))
            assert pro.n == PRO, pro.n
            for b in range(B):
                dv.wait_ge(xnt_ready, b + 1)
                if b:
                    dv.wait_ge(xnt_high_ready, b)
                    dv.wait_ge(xnt_low_ready, b)
                high_part(nc, xnt_bits[:], xnt[:]).then_inc(xnt_split, 1)
                if b + 1 < B:
                    norm_x(b + 1)
                dv.wait_ge(k_copied, b + 1)
                null = [bank[2 + j][:, 0:2 * NKV].rearrange("p (i n) -> p i n", i=2)[:, :, 2 * DH:] for j in range(2)]
                if cosine:
                    st.after(nc.vector.tensor_tensor(k_sq[:], k_raw[:], k_raw[:], ALU.mult))
                    nc.vector.tensor_reduce(ss[:, TB * H:], k_sq[:], AX.X, ALU.add)
                    for m in range(NQ):
                        dv.wait_ge(q_copied, AHEAD + NQ * b + m + 1)
                        nc.vector.tensor_reduce(ss[:, 8 * m:8 * m + 8], squares[:, m % 2, :].rearrange("p (h d) -> p h d", d=DH),
                                                AX.X, ALU.add).then_inc(q_summed, 1)
                    dv.wait_ge(q_summed, 2 + NQ * b + NQ)
                    nc.vector.tensor_scalar(ss[:], ss[:], 1e-24, None, ALU.max).then_inc(ss_ready, 1)
                    dv.wait_ge(norm_ready, b + 1)
                    dv.wait_ge(q_scaled, b + 1)
                    nc.vector.reciprocal(rinv[:], norm[:]).then_inc(rinv_ready, 1)
                    dv.wait_ge(rinv_ready, b + 1)
                    if b:
                        dv.wait_ge(k_turned, b)
                    for half in range(2):
                        ins = nc.vector.tensor_tensor(k_n[:, :, half, :], k_raw[:], rinv[:, TB * H:].unsqueeze(2).broadcast_to([P, TB, DH]),
                                                      ALU.mult)
                    ins.then_inc(kn_ready, 1)
                    dv.wait_ge(kv_done, b + 1)
                    for j in range(2):
                        ins = nc.vector.tensor_tensor(null_t[:, 2 * j:2 * j + 2, :], null[j],
                                                      rinv[:, 2 * H * j:2 * H * j + 2 * H].rearrange("p (i h) -> p i h", i=2), ALU.mult)
                    st.after(ins)
                else:
                    if b:
                        dv.wait_ge(k_turned, b)
                    for half in range(2):
                        ins = nc.vector.tensor_copy(k_n[:, :, half, :], k_raw[:])
                    ins.then_inc(kn_ready, 1)
                    dv.wait_ge(kv_done, b + 1)
                    for j in range(2):
                        ins = nc.vector.tensor_copy(null_t[:, 2 * j:2 * j + 2, :], null[j])
                    st.after(ins)
                nc.vector.scalar_tensor_tensor(null_neg[:, :, TB * b:TB * b + TB], null_t[:].rearrange("p i h -> p h i"), -1.0,
                                               null_b[:].unsqueeze(2).broadcast_to([P, H, TB]), ALU.mult,
                                               ALU.subtract).then_inc(null_done, 1)
                st.close()
            dv.wait_ge(kt_ready, B)
            dv.wait_ge(wq_high_ready, 1)
            dv.wait_ge(wq_low_ready, 1)
            kt_bits = wq_bits[:].rearrange("p k n -> p (k n)").rearrange("p (b s) -> p b s", b=B)
            high_part(nc, kt_bits, kt_full[:]).then_inc(k_split, 1)
            dv.wait_ge(k_split, 1)
            nc.vector.tensor_copy(kt_high[:], kt_bits.bitcast(F32))
            nc.vector.tensor_tensor(kt_low[0:DH], kt_full[0:DH], kt_bits[0:DH].bitcast(F32), ALU.subtract)




def attention_core(nc, sem, pre, bank, ident, w, q_src, kt, v_all, null_neg, neg_max, row_sum, o_all):
    rotary = w["bias"] == "none"
    dh = DR if rotary else DH
    kd = 4 * DR if rotary else 2 * DH
    HU = B * TB
    HT = 2 * HU
    TURNS = H // 2
    with ExitStack() as ctx:
        def sb(name, shape, dt=F32):
            return ctx.enter_context(nc.sbuf_tensor(pre + name, shape, dt))

        full = w["bias"] == "full"
        first_col = [0, P, 3 * P, 6 * P]
        bias = [sb(f"bias{j}", [P, 10 * P if full else S]) for j in range(2)]
        q_row = [sb(f"q_row{j}", [P, TB, 2, 4, DR] if rotary else [P, TB, 2, DH], F32R) for j in range(2)]
        q_bits = [sb(f"q_bits{j}", [P, TB, 2, DR] if rotary else [P, TB, DH], I32) for j in range(2)]
        qt = [sb(f"qt{j}", [kd, 2 if rotary else 1, S], F32R) for j in range(2)]
        qt_high = [sb(f"qt_high{j}", [DH + 1, S], F32R) for j in range(0 if rotary else 2)]
        unit = sb("unit", [P, P], F32R)
        score_bank = (bank[0], bank[1], bank[7])
        logit_neg = sb("logit_neg", [P, 4, S])
        prob = sb("prob", [P, 4, S])
        prob_t = sb("prob_t", [P, 2, S])
        null_h = [sb(f"null_h{j}", [P, HU]) for j in range(2)]
        max_h = [sb(f"max_h{j}", [P, HU]) for j in range(2)]
        sum_h = [sb(f"sum_h{j}", [P, HU]) for j in range(2)]

        bias_in = [sem(pre + f"bias_in{j}") for j in range(2)]
        head_ready = sem(pre + "head_ready")
        unit_ready = sem(pre + "unit_ready")
        bias_filled = sem(pre + "bias_filled")
        ones_set = sem(pre + "ones_set")
        q_high = sem(pre + "q_high")
        q_staged = sem(pre + "q_staged")
        q_turned = sem(pre + "q_turned")
        qt_ready = sem(pre + "qt_ready")
        scored = sem(pre + "scored")
        biased = sem(pre + "biased")
        exped = sem(pre + "exped")
        turned = sem(pre + "turned")
        pt_ready = sem(pre + "pt_ready")
        pv_done = sem(pre + "pv_done")
        o_copied = sem(pre + "o_copied")
        sums_kept = sem(pre + "sums_kept")
        block = ctx.enter_context(nc.Block())

        def turns(eng, body):
            body(0, True, False)
            with eng.Fori(1, TURNS - 1) as t:
                body(t, False, False)
            body(TURNS - 1, False, True)

        def bias_of(j, r):
            if full:
                return bias[j][:, first_col[r]:first_col[r] + P * (r + 1)]
            return bias[j][:, P * (TB - 1 - r):S]

        def diagonals(j):
            if full:
                return [bias[j][:, first_col[r] + P * r:first_col[r] + P * (r + 1)] for r in range(TB)]
            return [bias[j][:, P * (TB - 1):S]]

        @block.sync
        def _(sp):
            def load_full(t, first, last):
                for j in range(2):
                    if not first:
                        sp.wait_ge(biased, HT * t - HT + HU * (j + 1))
                    for r in range(TB):
                        sp.dma_start(bias_of(j, r), w["full"][2 * t + j, P * r:P * r + P, 0:P * (r + 1)]).then_inc(bias_in[j], 16)

            if full:
                turns(sp, load_full)
            elif not rotary:
                sp.wait_ge(w["copied"], 32)
                for h in range(H):
                    if h >= 2:
                        sp.wait_ge(biased, HU * (h - 1))
                    src = w["copies"]
                    skew = bass.AP(tensor=src.tensor, offset=src.offset + P * NPOS * h + P - 1, ap=[[NPOS - 1, P], [1, S]])
                    sp.dma_start(bias[h % 2][:], skew).then_inc(bias_in[h % 2], 16)

        @block.gpsimd
        def _(gp):
            nc.gpsimd.tensor_copy(unit[:], ident[:]).then_inc(unit_ready, 1)
            fills = len(diagonals(0))
            n_in = 16 * (TB if full else 1)

            def stage(t, first, blk):
                j, b = divmod(blk, B)
                if not (first and blk < 2):
                    gp.wait_ge(q_turned, 2 * B * t + blk - 1)
                gp.wait_ge(q_high, 2 * B * t + blk + 1)
                h = 2 * t + j
                row = q_row[blk % 2]
                if rotary:
                    src = q_src[:, TB * b:TB * b + TB, :, h, :]
                    high = q_bits[blk % 2][:].bitcast(F32)
                    for s, highs, lows in ((0, (0, 1), (2, 3)), (1, (0, 2), (1, 3))):
                        for n in lows:
                            nc.gpsimd.tensor_tensor(row[:, :, s, n, :], src[:, :, s, :], high[:, :, s, :], ALU.subtract)
                        for n in highs:
                            ins = nc.gpsimd.tensor_copy(row[:, :, s, n, :], high[:, :, s, :])
                else:
                    high = q_bits[blk % 2][:].bitcast(F32)
                    nc.gpsimd.tensor_tensor(row[:, :, 1, :], q_src[:, TB * b:TB * b + TB, h, :], high, ALU.subtract)
                    ins = nc.gpsimd.tensor_copy(row[:, :, 0, :], high)
                ins.then_inc(q_staged, 1)

            def keep_sums(t, j):
                h = 2 * t + j
                gp.wait_ge(exped, HT * t + HU * (j + 1))
                nc.gpsimd.tensor_copy(neg_max[:, h, :], max_h[j][:])
                nc.gpsimd.tensor_copy(row_sum[:, h, :], sum_h[j][:]).then_inc(sums_kept, 1)

            def head(t, first, last):
                for j in range(2):
                    if not first:
                        gp.wait_ge(biased, HT * t - HT + HU * (j + 1))
                    if not rotary:
                        nc.gpsimd.tensor_copy(null_h[j][:], null_neg[:, 2 * t + j, :]).then_inc(head_ready, 1)
                        wait_apart(gp, bias_in[j], n_in * t + n_in)
                        for d in diagonals(j):
                            nc.gpsimd.affine_select(out=d, in_=d, compare_op=ALU.is_ge, fill=MASKED, base=0,
                                                    pattern=[[-1, P]], channel_multiplier=1).then_inc(head_ready, 1)
                    stage(t, first, B * j)
                    stage(t, first, B * j + 1)
                    if j == 1:
                        keep_sums(t, 0)
                    elif not first:
                        keep_sums(t - 1, 1)
                    stage(t, first, B * j + 2)
                    stage(t, first, B * j + 3)
                if last:
                    keep_sums(t, 1)

            if rotary:
                for j in range(2):
                    nc.gpsimd.memset(bias[j][:], 0.0).then_inc(bias_filled, 1)
                gp.wait_ge(bias_filled, 2)
                for j in range(2):
                    for d in diagonals(j):
                        nc.gpsimd.affine_select(out=d, in_=d, compare_op=ALU.is_ge, fill=MASKED, base=0,
                                                pattern=[[-1, P]], channel_multiplier=1).then_inc(head_ready, 1)
            turns(gp, head)

        @block.tensor
        def _(pe):
            def turn_q(t, first, blk):
                g = 2 * B * t + blk
                wait_apart(pe, q_staged, g + 1)
                if not (first and blk == 0):
                    wait_apart(pe, qt_ready, g)
                for i in range(TB):
                    src = q_row[blk % 2][:, i].rearrange("p s n d -> p (s n d)" if rotary else "p s d -> p (s d)")
                    ins = nc.tensor.transpose(bank[6][:, P * i:P * i + P].bitcast(F32R), src, unit[:])
                ins.then_inc(q_turned, 1)

            def score(t, u):
                blk, r = divmod(u, TB)
                b = blk % B
                if r == 0:
                    pe.wait_ge(qt_ready, 2 * B * t + blk + 1)
                q = qt[blk % 2][:, 0, P * r:P * r + P]
                dst = score_bank[u % 3][:, 0:P * (r + 1)]
                if rotary:
                    ins = nc.tensor.matmul(dst, q, qt[blk % 2][:, 1, 0:P * (r + 1)], start=True, stop=True)
                else:
                    kt_high, kt_low = kt
                    nc.tensor.matmul(dst, q, kt_high[:, b, 0:P * (r + 1)], start=True, stop=False)
                    ins = nc.tensor.matmul(dst, qt_high[blk % 2][:, P * r:P * r + P], kt_low[:, b, 0:P * (r + 1)], start=False, stop=True)
                ins.then_inc(scored, 1)

            def times_v(t, first, u):
                blk, r = divmod(u, TB)
                b, j = blk % B, blk // B
                pe.wait_ge(pt_ready, HT * t + u + 1)
                if r == 0 and not (first and blk < 2):
                    pe.wait_ge(o_copied, 2 * B * t + blk - 1)
                for c in range(r + 1):
                    v = v_all[:, TB * b + c, bass.ds(dh * (2 * t + j), DH)] if rotary else v_all[:, TB * b + c, :]
                    ins = nc.tensor.matmul(bank[4 + blk % 2][:, DH * r:DH * r + DH], prob_t[:, u % 2, P * c:P * c + P], v,
                                           start=c == 0, stop=c == r)
                ins.then_inc(pv_done, 1)

            def turn(t, first, last):
                for u in range(HT):
                    blk, r = divmod(u, TB)
                    if r == 2 and blk + 2 < 2 * B:
                        turn_q(t, first, blk + 2)
                    elif r == 2 and not last:
                        turn_q(t + 1, False, blk + 2 - 2 * B)
                    pe.wait_ge(exped, HT * t + u + 1)
                    for c in range(r + 1):
                        ins = nc.tensor.transpose(bank[2 + u % 2][:, P * c:P * c + P], prob[:, u % 4, P * c:P * c + P], ident[:])
                    ins.then_inc(turned, 1)
                    if u + 3 < HT:
                        score(t, u + 3)
                    elif not last:
                        if u + 3 - HT < HT % 3:
                            pe.wait_ge(biased, HT * t + u + 2)
                        score(t + 1, u + 3 - HT)
                    if u:
                        times_v(t, first, u - 1)
                    elif not first:
                        times_v(t - 1, False, HT - 1)
                if last:
                    times_v(t, False, HT - 1)

            pe.wait_ge(unit_ready, 1)
            if not rotary:
                pe.wait_ge(ones_set, 2)
            turn_q(0, True, 0)
            turn_q(0, True, 1)
            for u in range(3):
                score(0, u)
            turns(pe, turn)

        @block.scalar
        def _(ac):
            def copy_qt(t, first, blk):
                g = 2 * B * t + blk
                ac.wait_ge(q_turned, g + 1)
                if not (first and blk < 2):
                    ac.wait_ge(scored, TB * (g - 1))
                for s in range(2 if rotary else 1):
                    ins = nc.scalar.copy(qt[blk % 2][:, s, :], bank[6][kd * s:kd * s + kd, :].bitcast(F32R))
                if not rotary:
                    ins = nc.scalar.copy(qt_high[blk % 2][0:DH, :], bank[6][0:DH, :].bitcast(F32R))
                ins.then_inc(qt_ready, 1)

            def exp(t, first, u):
                j, n = divmod(u, HU)
                ac.wait_ge(biased, HT * t + u + 1)
                if not (first and u < 4):
                    ac.wait_ge(turned, HT * t + u - 3)
                wd = P * (u % TB + 1)
                nc.scalar.activation(prob[:, u % 4, 0:wd], logit_neg[:, u % 4, 0:wd], ACT.Exp, bias=max_h[j][:, n:n + 1],
                                     scale=-1.0, accum_out=sum_h[j][:, n:n + 1]).then_inc(exped, 1)

            def copy_o(t, blk):
                j, b = divmod(blk, B)
                ac.wait_ge(pv_done, TB * (2 * B * t + blk + 1))
                nc.scalar.copy(o_all[:, TB * b:TB * b + TB, 2 * t + j, :],
                               bank[4 + blk % 2][:, 0:TB * DH].rearrange("p (i d) -> p i d", i=TB)[:, :, 0:dh]).then_inc(o_copied, 1)

            def turn(t, first, last):
                for u in range(HT):
                    blk, r = divmod(u, TB)
                    if u + 2 < HT:
                        exp(t, first, u + 2)
                    elif not last:
                        exp(t + 1, False, u + 2 - HT)
                    if r == 2 and blk + 2 < 2 * B:
                        copy_qt(t, first, blk + 2)
                    elif r == 2 and not last:
                        copy_qt(t + 1, False, blk + 2 - 2 * B)
                    if r == 1 and blk:
                        copy_o(t, blk - 1)
                    elif r == 1 and not first:
                        copy_o(t - 1, 2 * B - 1)
                if last:
                    copy_o(t, 2 * B - 1)

            copy_qt(0, True, 0)
            copy_qt(0, True, 1)
            exp(0, True, 0)
            exp(0, True, 1)
            turns(ac, turn)

        @block.vector
        def _(dv):
            per_head = 1 if rotary else 1 + len(diagonals(0))

            def add_bias(t, first, u):
                j, n = divmod(u, HU)
                if n == 0:
                    if not rotary:
                        dv.wait_ge(head_ready, per_head * (2 * t + j + 1))
                    elif first:
                        dv.wait_ge(head_ready, 2)
                    if not first:
                        dv.wait_ge(sums_kept, 2 * t + j - 1)
                wait_apart(dv, scored, HT * t + u + 1)
                r = n % TB
                wd = P * (r + 1)
                nc.vector.tensor_tensor_reduce(out=logit_neg[:, u % 4, 0:wd], in0=score_bank[u % 3][:, 0:wd], in1=bias_of(j, r),
                                               scale=-(dh ** -0.5) if rotary else -1.0,
                                               scalar=-MASKED if rotary else null_h[j][:, n:n + 1],
                                               op0=ALU.add, op1=ALU.min, accum_out=max_h[j][:, n:n + 1]).then_inc(biased, 1)

            def split_q(t, first, blk):
                j, b = divmod(blk, B)
                h = 2 * t + j
                if not (first and blk < 2):
                    dv.wait_ge(q_staged, 2 * B * t + blk - 1)
                src = q_src[:, TB * b:TB * b + TB, :, h, :] if rotary else q_src[:, TB * b:TB * b + TB, h, :]
                high_part(nc, q_bits[blk % 2][:], src).then_inc(q_high, 1)

            def copy_pt(t, first, u):
                dv.wait_ge(turned, HT * t + u + 1)
                if not (first and u < 2):
                    dv.wait_ge(pv_done, HT * t + u - 1)
                wd = P * (u % TB + 1)
                nc.vector.tensor_copy(prob_t[:, u % 2, 0:wd], bank[2 + u % 2][:, 0:wd]).then_inc(pt_ready, 1)

            def turn(t, first, last):
                for u in range(HT):
                    if u + 2 < HT:
                        add_bias(t, first, u + 2)
                    elif not last:
                        add_bias(t + 1, False, u + 2 - HT)
                    copy_pt(t, first, u)
                    ahead = u // TB + 3
                    if u % TB == 1 and ahead < 2 * B:
                        split_q(t, first, ahead)
                    elif u % TB == 1 and not last:
                        split_q(t + 1, False, ahead - 2 * B)

            if not rotary:
                for j in range(2):
                    one = ident[DH:DH + 1, :].unsqueeze(1).broadcast_to([1, TB, P])
                    nc.vector.tensor_scalar(qt_high[j][DH:DH + 1, :].rearrange("p (i n) -> p i n", i=TB), one, 0.0, 1.0,
                                            ALU.mult, ALU.add).then_inc(ones_set, 1)
            for blk in range(3):
                split_q(0, True, blk)
            add_bias(0, True, 0)
            add_bias(0, True, 1)
            turns(dv, turn)


def attention_output(nc, sem, pre, bank, Y, ident, w, o_all, null_neg, null_v, neg_max, row_sum):
    with ExitStack() as ctx:
        def sb(name, shape, dt=F32):
            return ctx.enter_context(nc.sbuf_tensor(pre + name, shape, dt))

        wout = sb("wout", [P, H * DH // P, D])
        g_out = sb("g_out", [P, D])
        null_p = sb("null_p", [P, H, NT])
        rinv = sb("rinv", [P, H, NT])
        spread = sb("spread", [P, H // 2, H])
        null_o = sb("null_o", [H, D])
        os = sb("os", [P, 2, H * DH])
        ps = sb("ps", [P, 2, H])
        ot = sb("ot", [P, 2, H * DH])
        pt = sb("pt", [H, 4, P])
        ot_bits = sb("ot_bits", [P, 2, H * DH], I32)
        ot_high = sb("ot_high", [P, 2, H * DH], F32R)
        ot_low = sb("ot_low", [P, 2, H * DH], F32R)
        wout_bits = sb("wout_bits", [P, H * DH // P, D], I32)
        wout_high = sb("wout_high", [P, H * DH // P, D], F32R)
        wout_low = sb("wout_low", [P, H * DH // P, D], F32R)
        stats = sb("stats", [P, TB, 6])
        mv = sb("mv", [P, TB, 2])
        var = sb("var", [P, TB])
        sd = sb("sd", [P, TB])
        rstd = sb("rstd", [P, TB])
        yn = sb("yn", [P, TB, D])

        params_in = sem(pre + "params_in")
        pre_steps = sem(pre + "pre_steps")
        null_ready = sem(pre + "null_ready")
        null_exped = sem(pre + "null_exped")
        null_o_done = sem(pre + "null_o_done")
        null_o_ready = sem(pre + "null_o_ready")
        scaled = sem(pre + "scaled")
        turned = sem(pre + "turned")
        ot_ready = sem(pre + "ot_ready")
        projected = sem(pre + "projected")
        stepped = sem(pre + "stepped")
        var_ready = sem(pre + "var_ready")
        sd_ready = sem(pre + "sd_ready")
        y_done = sem(pre + "y_done")
        wout_split, wout_high_ready, wout_low_ready = sem(pre + "wout_split"), sem(pre + "wout_high_ready"), sem(pre + "wout_low_ready")
        ot_split, high_ready, low_ready = sem(pre + "ot_split"), sem(pre + "high_ready"), sem(pre + "low_ready")
        block = ctx.enter_context(nc.Block())
        NC = H * DH // P

        def y_of(n):
            b, i = divmod(n, TB)
            return bank[4 + 2 * (b % 2) + i // 2][:, D * (i % 2):D * (i % 2) + D]

        @block.sync
        def _(sp):
            for half in range(2):
                sp.dma_start(wout[:, 4 * half:4 * half + 4, :],
                             w["Wout"].rearrange("(c p) n -> p c n", p=P)[:, 4 * half:4 * half + 4, :]).then_inc(params_in, 16)
            sp.dma_start(g_out[:], rows(w["g_out"])).then_inc(params_in, 16)

        @block.tensor
        def _(pe):
            pe.sem_inc(turned, 2)
            pe.wait_ge(params_in, 48)
            pe.wait_ge(null_ready, 3)
            for c in range(NC):
                ins = nc.tensor.matmul(bank[3][0:H, 0:D], spread[:, c, :], wout[:, c, :], start=c == 0, stop=c == NC - 1)
            ins.then_inc(null_o_done, 1)
            pe.wait_ge(null_o_ready, 1)

            def project(n):
                if n == 0:
                    pe.wait_ge(wout_high_ready, 1)
                    pe.wait_ge(wout_low_ready, 1)
                if n % TB == 0:
                    pe.wait_ge(y_done, n // TB + 1)
                pe.wait_ge(high_ready, n + 1)
                pe.wait_ge(low_ready, n + 1)
                dst = y_of(n)
                pairs = [(x[:, n % 2, P * c:P * c + P], y[:, c, :]) for c in range(NC)
                         for x, y in ((ot_high, wout_high), (ot_low, wout_high), (ot_high, wout_low))]
                for m, (x, y) in enumerate(pairs):
                    nc.tensor.matmul(dst, x, y, start=m == 0, stop=False)
                nc.tensor.matmul(dst, pt[:, n % 4, :], null_o[:], start=False, stop=True).then_inc(projected, 1)

            for n in range(NT):
                pe.wait_ge(scaled, 2 + n + 1)
                if n:
                    pe.wait_ge(ot_ready, n)
                for c in range(NC):
                    nc.tensor.transpose(bank[c // 4][:, P * (c % 4):P * (c % 4) + P], os[:, n % 2, P * c:P * c + P], ident[:])
                nc.tensor.transpose(bank[2][0:H, 0:P], ps[:, n % 2, :], ident[:]).then_inc(turned, 1)
                if n >= 2:
                    project(n - 2)
            project(NT - 2)
            project(NT - 1)

        @block.gpsimd
        def _(gp):
            gp.wait_ge(wout_split, 1)
            nc.gpsimd.tensor_tensor(wout_low[:], wout[:], wout_bits[:].bitcast(F32), ALU.subtract).then_inc(wout_low_ready, 1)
            for n in range(NT):
                gp.wait_ge(ot_split, n + 1)
                if n >= 2:
                    gp.wait_ge(projected, n - 1)
                nc.gpsimd.tensor_tensor(ot_low[:, n % 2, :], ot[:, n % 2, :], ot_bits[:, n % 2, :].bitcast(F32),
                                        ALU.subtract).then_inc(low_ready, 1)

        @block.scalar
        def _(ac):
            ac.wait_ge(null_ready, 1)
            nc.scalar.activation(null_p[:], null_p[:], ACT.Exp).then_inc(null_exped, 1)
            ac.wait_ge(null_o_done, 1)
            nc.scalar.copy(null_o[:], bank[3][0:H, 0:D]).then_inc(null_o_ready, 1)
            ac.sem_inc(sd_ready, 1)

            def root(b):
                ac.wait_ge(var_ready, b + 1)
                nc.scalar.activation(sd[:], var[:], ACT.Sqrt).then_inc(sd_ready, 1)

            def high(n):
                ac.wait_ge(ot_split, n + 1)
                if n >= 2:
                    ac.wait_ge(projected, n - 1)
                nc.scalar.copy(ot_high[:, n % 2, :], ot_bits[:, n % 2, :].bitcast(F32)).then_inc(high_ready, 1)

            ac.wait_ge(wout_split, 1)
            nc.scalar.copy(wout_high[:], wout_bits[:].bitcast(F32)).then_inc(wout_high_ready, 1)
            for n in range(NT):
                b, i = divmod(n, TB)
                ac.wait_ge(turned, 2 + n + 1)
                if n >= 2:
                    ac.wait_ge(low_ready, n - 1)
                for c in range(2):
                    nc.scalar.copy(ot[:, n % 2, 512 * c:512 * c + 512], bank[c][:])
                if n >= 4:
                    ac.wait_ge(projected, n - 3)
                nc.scalar.copy(pt[:, n % 4, :], bank[2][0:H, 0:P]).then_inc(ot_ready, 1)
                if n:
                    high(n - 1)
                if b and i == 2:
                    root(b - 1)
            high(NT - 1)
            root(B - 1)

        @block.vector
        def _(dv):
            st = Steps(dv, pre_steps)
            dv.sem_inc(scaled, 2)
            dv.sem_inc(y_done, FREE)
            nc.vector.tensor_tensor(null_p[:], neg_max[:], null_neg[:], ALU.subtract).then_inc(null_ready, 1)
            st.after(nc.vector.memset(spread[:], 0.0))
            for half in range(2):
                dst = spread[DH * half:DH * half + DH].rearrange("p c h -> p (c h)")[:, half::H + 2]
                nc.vector.tensor_scalar(dst, dst, null_v[DH * half:DH * half + DH, :], None, ALU.add).then_inc(null_ready, 1)
            dv.wait_ge(null_exped, 1)
            st.after(nc.vector.tensor_tensor(rinv[:], row_sum[:], null_p[:], ALU.add))
            st.after(nc.vector.reciprocal(rinv[:], rinv[:]))
            st.after(nc.vector.tensor_tensor(null_p[:], null_p[:], rinv[:], ALU.mult))
            dv.wait_ge(params_in, 48)
            high_part(nc, wout_bits[:], wout[:]).then_inc(wout_split, 1)
            st = Steps(dv, stepped)

            def split_o(n):
                dv.wait_ge(ot_ready, n + 1)
                if n >= 2:
                    dv.wait_ge(high_ready, n - 1)
                    dv.wait_ge(low_ready, n - 1)
                high_part(nc, ot_bits[:, n % 2, :], ot[:, n % 2, :]).then_inc(ot_split, 1)

            def variance(b):
                dv.wait_ge(projected, TB * b + TB)
                for i in range(TB):
                    ins = nc.vector.bn_stats(stats[:, i, :], y_of(TB * b + i))
                st.after(ins)
                for i in range(TB):
                    ins = nc.vector.bn_aggr(mv[:, i, :], stats[:, i, :])
                st.after(ins)
                nc.vector.tensor_scalar(var[:], mv[:, :, 1], EPS, None, ALU.add).then_inc(var_ready, 1)

            def norm_y(b):
                dv.wait_ge(sd_ready, 1 + b + 1)
                st.after(nc.vector.reciprocal(rstd[:], sd[:]))
                for i in range(TB):
                    ins = nc.vector.tensor_scalar(yn[:, i, :], y_of(TB * b + i), mv[:, i, 0:1], rstd[:, i:i + 1],
                                                  ALU.subtract, ALU.mult)
                st.after(ins)
                nc.vector.tensor_tensor(Y[:, TB * b:TB * b + TB, :], yn[:], g_out[:].unsqueeze(1).broadcast_to([P, TB, D]),
                                        ALU.mult).then_inc(y_done, 1)

            for n in range(NT):
                b, i = divmod(n, TB)
                dv.wait_ge(turned, n + 1)
                nc.vector.tensor_tensor(os[:, n % 2, :].rearrange("p (h d) -> p h d", h=H), o_all[:, n],
                                        rinv[:, :, n:n + 1].broadcast_to([P, H, DH]), ALU.mult)
                nc.vector.tensor_copy(ps[:, n % 2, :], null_p[:, :, n]).then_inc(scaled, 1)
                if n:
                    split_o(n - 1)
                if b and i == 2:
                    variance(b - 1)
                elif b and i == 3:
                    norm_y(b - 1)
            split_o(NT - 1)
            variance(B - 1)
            norm_y(B - 1)


def null_key_attention(nc, sem, pre, bank, X, Y, ident, w):
    with ExitStack() as ctx:
        def sb(name, shape, dt=F32):
            return ctx.enter_context(nc.sbuf_tensor(pre + name, shape, dt))

        heads = sb("heads", [P, NT, H, DH])
        v_all = sb("v_all", [P, NT, DH])
        kt = (sb("kt_high", [P, B, S], F32R), sb("kt_low", [DH + 1, B, S], F32R))
        null_neg = sb("null_neg", [P, H, NT])
        null_v = sb("null_v", [P, 1])
        neg_max = sb("neg_max", [P, H, NT])
        row_sum = sb("row_sum", [P, H, NT])
        attention_inputs(nc, sem, pre + "i_", bank, X, ident, w, heads, kt, v_all, null_neg, null_v)
        attention_core(nc, sem, pre + "c_", bank, ident, w, heads, kt, v_all, null_neg, neg_max, row_sum, heads)
        attention_output(nc, sem, pre + "o_", bank, Y, ident, w, heads, null_neg, null_v, neg_max, row_sum)


def moe_ffn(nc, sem, bank, X, Y, ident, lane_d, norm_scale, gate_w, gate_b, w1_d, b1_d, w2_d, b2_d):
    E, J = E1, I1 // P
    LIMIT, ALPHA = 7.0, 1.702
    with ExitStack() as ctx:
        def sb(name, shape, dt=F32):
            return ctx.enter_context(nc.sbuf_tensor("mf_" + name, shape, dt))

        lane = sb("lane", [P, E])
        g_norm = sb("g_norm", [P, KD])
        gw = sb("gw", [P, KD, E])
        gb = sb("gb", [P, E])
        b1 = sb("b1", [P, E, 2, J])
        b2 = sb("b2", [E, D])
        tt_high = sb("tt_high", [P, KD, NT * P], F32R)
        tt_low = sb("tt_low", [P, KD, NT * P], F32R)
        weight = sb("weight", [P, NT, E])

        params_in = sem("mf_params_in")
        w_in = [sem(f"mf_w_in{j}") for j in range(2)]

        with ExitStack() as inner:
            def tmp(name, shape, dt=F32):
                return inner.enter_context(nc.sbuf_tensor("mf_" + name, shape, dt))

            square = tmp("square", [P, 2, D])
            ms = tmp("ms", [P, NT])
            sd = tmp("sd", [P, NT])
            rms = tmp("rms", [P, NT])
            tn = tmp("tn", [P, 2, TB, D])
            logits = tmp("logits", [P, NT, E])
            exp_in = tmp("exp_in", [P, NT, E])
            ex = tmp("ex", [P, NT, E])
            zsum = tmp("zsum", [P, NT])
            best = tmp("best", [P, NT, 8])
            best_at = tmp("best_at", [P, NT, 8], U32)
            picked = tmp("picked", [P, NT, 2])
            wt = tmp("wt", [E, NT, P])
            tt = tmp("tt", [P, KD, NT * P])
            tt_bits = tmp("tt_bits", [P, KD, NT * P], I32)

            stepped = sem("mf_stepped")
            ms_ready, sd_ready = sem("mf_ms_ready"), sem("mf_sd_ready")
            tn_ready, tn_turned, tt_ready = sem("mf_tn_ready"), sem("mf_tn_turned"), sem("mf_tt_ready")
            logits_done = sem("mf_logits_done")
            exp_ready, exp_done = sem("mf_exp_ready"), sem("mf_exp_done")
            weight_ready, weight_turned, wt_ready = sem("mf_weight_ready"), sem("mf_weight_turned"), sem("mf_wt_ready")
            bias_done, x_added, tt_split = sem("mf_bias_done"), sem("mf_x_added"), sem("mf_tt_split")
            block = inner.enter_context(nc.Block())

            @block.sync
            def _(sp):
                sp.dma_start(lane[:], lane_d).then_inc(params_in, 16)
                sp.dma_start(g_norm[:], columns(norm_scale, KD)).then_inc(params_in, 16)
                sp.dma_start(gw[:], gate_w.rearrange("(k p) e -> p k e", p=P)).then_inc(params_in, 16)
                sp.dma_start(gb[:], rows(gate_b)).then_inc(params_in, 16)
                sp.dma_start(b1[:], b1_d).then_inc(params_in, 16)
                sp.dma_start(b2[:], b2_d).then_inc(params_in, 16)

            @block.gpsimd
            def _(gp):
                nc.gpsimd.tensor_tensor(X[:], X[:], Y[:], ALU.add).then_inc(x_added, 1)
                gp.wait_ge(tt_split, 1)
                nc.gpsimd.tensor_tensor(tt_low[:], tt[:], tt_bits[:].bitcast(F32), ALU.subtract)

            @block.vector
            def _(dv):
                st = Steps(dv, stepped)
                for t in range(NT):
                    if t >= 2:
                        st.after(ins)
                    ins = nc.vector.tensor_tensor_reduce(out=square[:, t % 2, :], in0=Y[:, t, :], in1=Y[:, t, :], scale=1.0 / D,
                                                         scalar=EPS, op0=ALU.mult, op1=ALU.add, accum_out=ms[:, t:t + 1])
                ins.then_inc(ms_ready, 1)
                dv.wait_ge(sd_ready, 1)
                st.after(nc.vector.reciprocal(rms[:], sd[:]))
                dv.wait_ge(params_in, 96)
                for b in range(B):
                    if b >= 2:
                        dv.wait_ge(tn_turned, b - 1)
                    for i in range(TB):
                        t = TB * b + i
                        ins = nc.vector.tensor_scalar(tn[:, b % 2, i, :], Y[:, t, :], rms[:, t:t + 1], None, ALU.mult)
                    ins.then_inc(tn_ready, 1)
                dv.wait_ge(tt_ready, B)
                high_part(nc, tt_bits[:], tt[:]).then_inc(tt_split, 1)
                dv.wait_ge(logits_done, 1)
                st.after(nc.vector.tensor_tensor(logits[:], bank[6][:, 0:NT * E].rearrange("p (t e) -> p t e", e=E),
                                                 gb[:].unsqueeze(1).broadcast_to([P, NT, E]), ALU.add))
                route(nc, dv, st, logits, ex, zsum, best, best_at, lane, picked, weight, False, exp_in, exp_ready, exp_done)
                nc.vector.tensor_copy(exp_in[:], weight[:]).then_inc(weight_ready, 1)
                dv.wait_ge(x_added, 1)
                for t in range(NT):
                    dv.wait_ge(bias_done, t // 8 + 1)
                    src = bank[(t // 2) % 4 + (0 if t < 8 else 4)][:, D * (t % 2):D * (t % 2) + D]
                    nc.vector.tensor_tensor(X[:, t, :], X[:, t, :], src, ALU.add)

            @block.scalar
            def _(ac):
                ac.wait_ge(ms_ready, 1)
                nc.scalar.activation(sd[:], ms[:], ACT.Sqrt).then_inc(sd_ready, 1)
                ac.wait_ge(params_in, 96)
                for b in range(B):
                    ac.wait_ge(tn_turned, b + 1)
                    for k in range(KD):
                        ins = nc.scalar.activation(tt[:, k, S * b:S * b + S], bank[2 * (b % 2) + k][:], ACT.Copy, scale=g_norm[:, k:k + 1])
                    ins.then_inc(tt_ready, 1)
                ac.wait_ge(tt_split, 1)
                nc.scalar.copy(tt_high[:], tt_bits[:].bitcast(F32))
                ac.wait_ge(exp_ready, 1)
                nc.scalar.activation(ex[:], exp_in[:], ACT.Exp).then_inc(exp_done, 1)
                for b in range(B):
                    ac.wait_ge(weight_turned, b + 1)
                    nc.scalar.copy(wt[:, TB * b:TB * b + TB, :], bank[b][0:E, :].rearrange("e (i p) -> e i p", i=TB)).then_inc(wt_ready, 1)

            @block.tensor
            def _(pe):
                pe.wait_ge(params_in, 96)
                for b in range(B):
                    pe.wait_ge(tn_ready, b + 1)
                    if b >= 2:
                        pe.wait_ge(tt_ready, b - 1)
                    for k in range(KD):
                        for i in range(TB):
                            ins = nc.tensor.transpose(bank[2 * (b % 2) + k][:, P * i:P * i + P], tn[:, b % 2, i, P * k:P * k + P], ident[:])
                    ins.then_inc(tn_turned, 1)
                pe.wait_ge(tt_ready, B)
                for t in range(NT):
                    for k in range(KD):
                        ins = nc.tensor.matmul(bank[6][:, E * t:E * t + E], tt[:, k, P * t:P * t + P], gw[:, k, :],
                                               start=k == 0, stop=k == KD - 1)
                ins.then_inc(logits_done, 1)
                pe.wait_ge(weight_ready, 1)
                for b in range(B):
                    for i in range(TB):
                        ins = nc.tensor.transpose(bank[b][0:E, P * i:P * i + P], exp_in[:, TB * b + i, :], ident[:])
                    ins.then_inc(weight_turned, 1)
                pe.wait_ge(wt_ready, B)
                for t in range(NT):
                    dst = bank[(t // 2) % 4 + (0 if t < 8 else 4)][:, D * (t % 2):D * (t % 2) + D]
                    ins = nc.tensor.matmul(dst, wt[:, t, :], b2[:], start=True, stop=True)
                    if t % 8 == 7:
                        ins.then_inc(bias_done, 1)

        raw = [Y[:, NT // 2 * j:NT // 2 * j + NT // 2, :].rearrange("p i d -> p (i d)") for j in range(2)]
        W1, W2 = KD * 2 * I1, J * D
        raw2 = [sb(f"raw2{j}", [P, W2]) for j in range(2)]
        w_bits = sb("w_bits", [P, W1 + W2], I32)
        w_high = [sb(f"w_high{j}", [P, W1 + W2], F32R) for j in range(2)]
        w_low = [sb(f"w_low{j}", [P, W1 + W2], F32R) for j in range(2)]
        glu = sb("glu", [P, 2, S])
        sig = sb("sig", [P, 2, S])
        gated = sb("gated", [P, 2, S])
        low = sb("low", [P, 2, S])
        lin = sb("lin", [P, 2, S])
        hid = sb("hid", [P, 2, S])
        hid_bits = sb("hid_bits", [P, 2, S], I32)
        hid_high = sb("hid_high", [P, 2, J, S], F32R)
        hid_low = sb("hid_low", [P, 2, J, S], F32R)

        def w1_of(w, k, half, j):
            return w[:, (2 * k + half) * I1 + P * j:(2 * k + half) * I1 + P * j + P]

        def w2_of(w, j):
            return w[:, W1 + D * j:W1 + D * j + D]

        glu_done, lin_done = sem("mf_glu_done"), sem("mf_lin_done")
        glu_ready, low_ready, lin_ready = sem("mf_glu_ready"), sem("mf_low_ready"), sem("mf_lin_ready")
        sig_ready, gated_ready, hid_ready = sem("mf_sig_ready"), sem("mf_gated_ready"), sem("mf_hid_ready")
        bits_ready, high_ready, low_part_ready = sem("mf_bits_ready"), sem("mf_high_ready"), sem("mf_low_part_ready")
        w_bits_ready, w_high_ready, w_low_ready = sem("mf_w_bits_ready"), sem("mf_w_high_ready"), sem("mf_w_low_ready")
        downed, added = sem("mf_downed"), sem("mf_added")
        block = ctx.enter_context(nc.Block())
        NU = 2 * B
        SUB = J * NU
        PAIRS = E // 2
        CREDIT = 4

        def turns(eng, body):
            body(0, True, False)
            with eng.Fori(1, PAIRS - 1) as t:
                body(t, False, False)
            body(PAIRS - 1, False, True)

        def quarter(q):
            return slice(W1 // 4 * q, W1 // 4 * (q + 1)), slice(W1 + W2 // 4 * q, W1 + W2 // 4 * (q + 1))

        def split_points(t, last, u):
            if u == 2:
                return (t, 1, NU * t)
            if u == B + 2 and not last:
                return (t + 1, 0, NU * t + B)
            return None

        @block.sync
        def _(sp):
            def load(t, j):
                e = 2 * t + j
                for k in range(KD):
                    dst = raw[j][:, 2 * I1 * k:2 * I1 * k + 2 * I1].rearrange("p (s n) -> p s n", s=2)
                    sp.dma_start(dst, w1_d[e, P * k:P * k + P]).then_inc(w_in[j], 16)
                sp.dma_start(raw2[j][:].rearrange("p (j n) -> p j n", j=J),
                             w2_d[e].rearrange("(j p) n -> p j n", p=P)).then_inc(w_in[j], 16)

            for j in range(2):
                load(0, j)
            with sp.Fori(0, PAIRS - 1) as t:
                for j in range(2):
                    sp.wait_ge(w_low_ready, 2 * t + j + 1)
                    load(t + 1, j)

        @block.tensor
        def _(pe):
            pe.sem_inc(downed, CREDIT)

            def up(t, u, j):
                s = SUB * t + J * u + j
                h, l = w_high[u // B], w_low[u // B]
                cols = slice(S * (u % B), S * (u % B) + S)
                for half, done, freed in ((0, glu_done, glu_ready), (1, lin_done, low_ready)):
                    pe.wait_ge(freed, s + 1)
                    parts = [(w1_of(w, k, half, j), x[:, k, cols]) for k in range(KD) for w, x in ((h, tt_high), (l, tt_high), (h, tt_low))]
                    for n, (w, x) in enumerate(parts):
                        ins = nc.tensor.matmul(bank[2 * half + j % 2][:], w, x, start=n == 0, stop=n == len(parts) - 1)
                    ins.then_inc(done, 1)

            def down(t, u, i):
                n = NU * t + u
                h, l = w_high[u // B], w_low[u // B]
                if i == 0:
                    pe.wait_ge(high_ready, FREE + J * (n + 1))
                    pe.wait_ge(low_part_ready, FREE + J * (n + 1))
                if i % 2 == 0:
                    pe.wait_ge(added, 2 * n + i // 2 + 1)
                parts = [(x[:, u % 2, j, P * i:P * i + P], w2_of(w, j)) for j in range(J)
                         for x, w in ((hid_high, h), (hid_low, h), (hid_high, l))]
                for m, (x, w) in enumerate(parts):
                    ins = nc.tensor.matmul(bank[4 + 2 * (u % 2) + i // 2][:, D * (i % 2):D * (i % 2) + D], x, w,
                                           start=m == 0, stop=m == len(parts) - 1)
                if i % 2:
                    ins.then_inc(downed, 1)

            def turn(t, first, last):
                for u in range(NU):
                    if u % B == 0:
                        pe.wait_ge(w_high_ready, 2 * t + u // B + 1)
                        pe.wait_ge(w_low_ready, 2 * t + u // B + 1)
                    for j in range(J):
                        up(t, u, j)
                        of, i = (u - 1, j - 2) if j >= 2 else (u - 2, j + 2)
                        if of >= 0:
                            down(t, of, i)
                        elif not first:
                            down(t - 1, NU + of, i)
                if last:
                    for of, i in ((NU - 2, 2), (NU - 2, 3), (NU - 1, 0), (NU - 1, 1), (NU - 1, 2), (NU - 1, 3)):
                        down(t, of, i)

            turns(pe, turn)

        @block.scalar
        def _(ac):
            ac.sem_inc(high_ready, FREE)

            def split_w(t, j, over, q):
                if q == 0:
                    ac.wait_ge(w_bits_ready, 2 * t + j + 1)
                    ac.wait_ge(downed, CREDIT + 2 * over)
                for cols in quarter(q):
                    ins = nc.scalar.copy(w_high[j][:, cols], w_bits[:, cols].bitcast(F32))
                if q == 3:
                    ins.then_inc(w_high_ready, 1)

            def high(t, m):
                s = SUB * t + m
                ac.wait_ge(bits_ready, s + 1)
                if m % J == 0:
                    ac.wait_ge(downed, CREDIT + 2 * (NU * t + m // J) - 2)
                nc.scalar.copy(hid_high[:, m // J % 2, m % J, :], hid_bits[:, m % 2, :].bitcast(F32)).then_inc(high_ready, 1)

            def turn(t, first, last):
                for m in range(SUB):
                    s = SUB * t + m
                    ac.wait_ge(glu_ready, FREE + s + 1)
                    ac.wait_ge(gated_ready, s + 1)
                    nc.scalar.activation(sig[:, m % 2, :], glu[:, m % 2, :], ACT.Sigmoid, scale=ALPHA).then_inc(sig_ready, 1)
                    if m >= 2:
                        high(t, m - 2)
                    elif not first:
                        high(t - 1, SUB + m - 2)
                    point = split_points(t, last, m // J)
                    if point:
                        split_w(*point, m % J)
                if last:
                    high(t, SUB - 2)
                    high(t, SUB - 1)

            for q in range(4):
                split_w(0, 0, 0, q)
            turns(ac, turn)

        @block.gpsimd
        def _(gp):
            gp.sem_inc(gated_ready, FREE)
            gp.sem_inc(low_part_ready, FREE)

            def split_w(t, j, over, q):
                if q == 0:
                    gp.wait_ge(w_bits_ready, 2 * t + j + 1)
                    gp.wait_ge(downed, CREDIT + 2 * over)
                one, two = quarter(q)
                nc.gpsimd.tensor_tensor(w_low[j][:, one], raw[j][:, one], w_bits[:, one].bitcast(F32), ALU.subtract)
                ins = nc.gpsimd.tensor_tensor(w_low[j][:, two], raw2[j][:, two.start - W1:two.stop - W1], w_bits[:, two].bitcast(F32),
                                              ALU.subtract)
                if q == 3:
                    ins.then_inc(w_low_ready, 1)

            def low_part(t, m):
                s = SUB * t + m
                gp.wait_ge(bits_ready, s + 1)
                if m % J == 0:
                    gp.wait_ge(downed, CREDIT + 2 * (NU * t + m // J) - 2)
                nc.gpsimd.tensor_tensor(hid_low[:, m // J % 2, m % J, :], hid[:, m % 2, :], hid_bits[:, m % 2, :].bitcast(F32),
                                        ALU.subtract).then_inc(low_part_ready, 1)

            def turn(t, first, last):
                for m in range(SUB):
                    s = SUB * t + m
                    gp.wait_ge(sig_ready, s + 1)
                    gp.wait_ge(hid_ready, s + 1)
                    nc.gpsimd.tensor_tensor(gated[:, m % 2, :], glu[:, m % 2, :], sig[:, m % 2, :], ALU.mult).then_inc(gated_ready, 1)
                    if m >= 2:
                        low_part(t, m - 2)
                    elif not first:
                        low_part(t - 1, SUB + m - 2)
                    point = split_points(t, last, m // J)
                    if point:
                        split_w(*point, m % J)
                if last:
                    low_part(t, SUB - 2)
                    low_part(t, SUB - 1)

            for q in range(4):
                split_w(0, 0, 0, q)
            turns(gp, turn)

        @block.vector
        def _(dv):
            for s in (glu_ready, low_ready, hid_ready):
                dv.sem_inc(s, FREE)
            dv.sem_inc(added, 4)

            def split_w(t, j, first):
                n = 2 * t + j
                if not first:
                    dv.wait_ge(w_high_ready, n)
                    dv.wait_ge(w_low_ready, n)
                dv.wait_ge(w_in[j], 16 * (KD + 1) * (t + 1))
                high_part(nc, w_bits[:, 0:W1], raw[j])
                high_part(nc, w_bits[:, W1:], raw2[j][:]).then_inc(w_bits_ready, 1)

            def clip(t, u, j):
                s = SUB * t + J * u + j
                e = 2 * t + u // B
                b1_glu, b1_lin = (b1[:, bass.ds(e, 1), h, j] for h in range(2))
                dv.wait_ge(glu_done, s + 1)
                dv.wait_ge(gated_ready, s + 1)
                nc.vector.tensor_scalar(glu[:, j % 2, :], bank[j % 2][:], b1_glu, LIMIT, ALU.add, ALU.min).then_inc(glu_ready, 1)
                dv.wait_ge(lin_done, s + 1)
                nc.vector.tensor_scalar(low[:, j % 2, :], bank[2 + j % 2][:], b1_lin, LIMIT, ALU.add, ALU.min).then_inc(low_ready, 1)
                dv.wait_ge(low_ready, FREE + s + 1)
                nc.vector.tensor_scalar(lin[:, j % 2, :], low[:, j % 2, :], -LIMIT, 1.0, ALU.max, ALU.add).then_inc(lin_ready, 1)

            def join(t, m):
                s = SUB * t + m
                dv.wait_ge(gated_ready, FREE + s + 1)
                dv.wait_ge(lin_ready, s + 1)
                dv.wait_ge(low_part_ready, s + 1)
                nc.vector.tensor_tensor(hid[:, m % 2, :], gated[:, m % 2, :], lin[:, m % 2, :], ALU.mult).then_inc(hid_ready, 1)

            def bits(t, m):
                s = SUB * t + m
                dv.wait_ge(hid_ready, FREE + s + 1)
                dv.wait_ge(high_ready, s + 1)
                dv.wait_ge(low_part_ready, s + 1)
                high_part(nc, hid_bits[:, m % 2, :], hid[:, m % 2, :]).then_inc(bits_ready, 1)

            def add(t, u, half):
                n = NU * t + u
                e = 2 * t + u // B
                dv.wait_ge(downed, CREDIT + 2 * n + half + 1)
                for i in (2 * half, 2 * half + 1):
                    x = X[:, TB * (u % B) + i, :]
                    ins = nc.vector.scalar_tensor_tensor(x, bank[4 + 2 * (u % 2) + half][:, D * (i % 2):D * (i % 2) + D],
                                                         weight[:, TB * (u % B) + i, bass.ds(e, 1)], x, ALU.mult, ALU.add)
                ins.then_inc(added, 1)

            def turn(t, first, last):
                for m in range(SUB):
                    u, j = divmod(m, J)
                    if m >= 2:
                        bits(t, m - 2)
                    elif not first:
                        bits(t - 1, SUB + m - 2)
                    clip(t, u, j)
                    if m:
                        join(t, m - 1)
                    elif not first:
                        join(t - 1, SUB - 1)
                    if j % 2 == 0:
                        if u >= 2:
                            add(t, u - 2, j // 2)
                        elif not first:
                            add(t - 1, NU + u - 2, j // 2)
                    point = split_points(t, last, u) if j == 0 else None
                    if point:
                        split_w(point[0], point[1], False)
                if last:
                    bits(t, SUB - 2)
                    join(t, SUB - 1)
                    bits(t, SUB - 1)
                    for u in (NU - 2, NU - 1):
                        for half in range(2):
                            add(t, u, half)

            split_w(0, 0, True)
            turns(dv, turn)


def rotary_attention(nc, sem, bank, X, Y, ident, wqk_t, wv_t, wo_t, cos_d, sin_d):
    with ExitStack() as ctx:
        def sb(name, shape, dt=F32):
            return ctx.enter_context(nc.sbuf_tensor("ra_" + name, shape, dt))

        qk_all = sb("qk_all", [P, NT, 2, H, DR])
        v_all = sb("v_all", [P, NT, D + DH - DR])
        o_all = sb("o_all", [P, NT, H, DR])
        neg_max = sb("neg_max", [P, H, NT])
        row_sum = sb("row_sum", [P, H, NT])
        wo = sb("wo", [P, KD, D])
        weights_in = sem("ra_weights_in")

        with ExitStack() as inner:
            def tmp(name, shape, dt=F32):
                return inner.enter_context(nc.sbuf_tensor("ra_" + name, shape, dt))

            wqk = tmp("wqk", [P, KD, 2 * D])
            wv = tmp("wv", [P, KD, D])
            cos = tmp("cos", [P, TB, DR])
            sin = tmp("sin", [P, TB, DR])
            yt = tmp("yt", [P, 2, KD, S])
            straight = tmp("straight", [P, 2, 2 * H, DR])
            rotated = tmp("rotated", [P, 2, 2 * H, DR])
            row_turned, yt_ready = sem("ra_row_turned"), sem("ra_yt_ready")
            v_done, v_copied = sem("ra_v_done"), sem("ra_v_copied")
            qk_done, turned, joined = sem("ra_qk_done"), sem("ra_turned"), sem("ra_joined")
            block = inner.enter_context(nc.Block())

            @block.sync
            def _(sp):
                sp.dma_start(wqk[:], wqk_t.rearrange("(k p) n -> p k n", p=P)).then_inc(weights_in, 16)
                sp.dma_start(wv[:], wv_t.rearrange("(k p) n -> p k n", p=P)).then_inc(weights_in, 16)
                sp.dma_start(wo[:], wo_t.rearrange("(k p) n -> p k n", p=P)).then_inc(weights_in, 16)
                sp.dma_start(cos[:], cos_d).then_inc(weights_in, 16)
                sp.dma_start(sin[:], sin_d).then_inc(weights_in, 16)

            @block.gpsimd
            def _(gp):
                gp.sem_inc(joined, FREE)
                nc.gpsimd.memset(v_all[:, :, D:], 0.0)
                with gp.Fori(0, B) as b:
                    for i in range(TB):
                        gp.wait_ge(turned, TB * b + i + 1)
                        nc.gpsimd.tensor_tensor(qk_all[:, TB * b + i].rearrange("p s h d -> p (s h) d"), straight[:, i % 2],
                                                rotated[:, i % 2], ALU.add).then_inc(joined, 1)

            @block.tensor
            def _(pe):
                def turn_y(b):
                    if b:
                        pe.wait_ge(yt_ready, b)
                    for k in range(KD):
                        for i in range(TB):
                            ins = nc.tensor.transpose(bank[k][:, P * i:P * i + P], Y[:, TB * b + i, P * k:P * k + P], ident[:])
                    ins.then_inc(row_turned, 1)

                turn_y(0)
                pe.wait_ge(weights_in, 80)
                for b in range(B):
                    if b + 1 < B:
                        turn_y(b + 1)
                    pe.wait_ge(yt_ready, b + 1)
                    if b:
                        pe.wait_ge(v_copied, b)
                    for i in range(TB):
                        for k in range(KD):
                            ins = nc.tensor.matmul(bank[2 + i // 2][:, D * (i % 2):D * (i % 2) + D], yt[:, b % 2, k, P * i:P * i + P], wv[:, k, :],
                                                   start=k == 0, stop=k == KD - 1)
                    ins.then_inc(v_done, 1)
                    for i in range(TB):
                        if b:
                            pe.wait_ge(turned, TB * (b - 1) + i + 1)
                        for k in range(KD):
                            ins = nc.tensor.matmul(bank[4 + i][:], yt[:, b % 2, k, P * i:P * i + P], wqk[:, k, :], start=k == 0, stop=k == KD - 1)
                        ins.then_inc(qk_done, 1)

            @block.scalar
            def _(ac):
                def copy_yt(b):
                    ac.wait_ge(row_turned, b + 1)
                    if b >= 2:
                        ac.wait_ge(qk_done, TB * (b - 1))
                    for k in range(KD):
                        ins = nc.scalar.copy(yt[:, b % 2, k, :], bank[k][:])
                    ins.then_inc(yt_ready, 1)

                copy_yt(0)
                for b in range(B):
                    if b + 1 < B:
                        copy_yt(b + 1)
                    ac.wait_ge(v_done, b + 1)
                    for j in range(2):
                        ins = nc.scalar.copy(v_all[:, TB * b + 2 * j:TB * b + 2 * j + 2, 0:D], bank[2 + j][:].rearrange("p (i n) -> p i n", i=2))
                    ins.then_inc(v_copied, 1)

            @block.vector
            def _(dv):
                dv.wait_ge(weights_in, 80)
                with dv.Fori(0, B) as b:
                    for i in range(TB):
                        n = TB * b + i
                        HR = DR // 2
                        dv.wait_ge(qk_done, n + 1)
                        dv.wait_ge(joined, n + 1)
                        qk = bank[4 + i][:].rearrange("p (h d) -> p h d", d=DR)
                        c, s = (x[:, i, :].unsqueeze(1).broadcast_to([P, 2 * H, DR]) for x in (cos, sin))
                        nc.vector.tensor_tensor(straight[:, i % 2], qk, c, ALU.mult)
                        nc.vector.tensor_tensor(rotated[:, i % 2, :, 0:HR], qk[:, :, HR:DR], s[:, :, 0:HR], ALU.mult)
                        nc.vector.tensor_tensor(rotated[:, i % 2, :, HR:DR], qk[:, :, 0:HR], s[:, :, HR:DR], ALU.mult).then_inc(turned, 1)

        attention_core(nc, sem, "rc_", bank, ident, {"bias": "none"}, qk_all, None, v_all, None, neg_max, row_sum, o_all)

        os = sb("os", [P, 2, TB, H, DR])
        ot = sb("ot", [P, 2, KD, S])
        rinv_ready, scaled, o_turned, ot_ready = sem("ra_rinv_ready"), sem("ra_scaled"), sem("ra_o_turned"), sem("ra_ot_ready")
        projected, x_added = sem("ra_projected"), sem("ra_x_added")
        block = ctx.enter_context(nc.Block())

        @block.tensor
        def _(pe):
            def turn_o(b):
                pe.wait_ge(scaled, b + 1)
                if b:
                    pe.wait_ge(ot_ready, b)
                for k in range(KD):
                    for i in range(TB):
                        src = os[:, b % 2, i].rearrange("p h d -> p (h d)")[:, P * k:P * k + P]
                        ins = nc.tensor.transpose(bank[k][:, P * i:P * i + P], src, ident[:])
                ins.then_inc(o_turned, 1)

            pe.wait_ge(weights_in, 80)
            turn_o(0)
            for b in range(B):
                if b + 1 < B:
                    turn_o(b + 1)
                pe.wait_ge(ot_ready, b + 1)
                if b >= 2:
                    pe.wait_ge(x_added, b - 1)
                for i in range(TB):
                    for k in range(KD):
                        ins = nc.tensor.matmul(bank[2 + 2 * (b % 2) + i // 2][:, D * (i % 2):D * (i % 2) + D],
                                               ot[:, b % 2, k, P * i:P * i + P], wo[:, k, :], start=k == 0, stop=k == KD - 1)
                ins.then_inc(projected, 1)

        @block.scalar
        def _(ac):
            for b in range(B):
                ac.wait_ge(o_turned, b + 1)
                if b >= 2:
                    ac.wait_ge(projected, b - 1)
                for k in range(KD):
                    ins = nc.scalar.copy(ot[:, b % 2, k, :], bank[k][:])
                ins.then_inc(ot_ready, 1)

        @block.vector
        def _(dv):
            nc.vector.reciprocal(row_sum[:], row_sum[:]).then_inc(rinv_ready, 1)
            dv.wait_ge(rinv_ready, 1)

            def scale(b):
                if b >= 2:
                    dv.wait_ge(o_turned, b - 1)
                for i in range(TB):
                    r = row_sum[:, :, TB * b + i:TB * b + i + 1].broadcast_to([P, H, DR])
                    ins = nc.vector.tensor_tensor(os[:, b % 2, i], o_all[:, TB * b + i], r, ALU.mult)
                ins.then_inc(scaled, 1)

            scale(0)
            for b in range(B):
                if b + 1 < B:
                    scale(b + 1)
                dv.wait_ge(projected, b + 1)
                for j in range(2):
                    x = X[:, TB * b + 2 * j:TB * b + 2 * j + 2, :].rearrange("p i n -> p (i n)")
                    ins = nc.vector.tensor_tensor(x, x, bank[2 + 2 * (b % 2) + j][:], ALU.add)
                ins.then_inc(x_added, 1)


def quantised_ffn(nc, sem, bank, X, Y, ident, out, clip_x, clip_down, w_gate, w_up, w_down):
    NC = -(-IQ // P)
    LAST = IQ - P * (NC - 1)
    LO, HI = RNE - QMAX - 1.0, RNE + QMAX
    with ExitStack() as ctx:
        def sb(name, shape, dt=F32):
            return ctx.enter_context(nc.sbuf_tensor("qf_" + name, shape, dt))

        clip = sb("clip", [P, 2])
        factor = sb("factor", [P, 2])
        identb = sb("identb", [P, P], BF16)
        wgu_t = sb("wgu_t", [P, 2, KD, NC * P], BF16)
        wd_t = sb("wd_t", [P, NC, D], BF16)
        xq_t = sb("xq_t", [P, KD, NT * P], BF16)
        gu_scale = sb("gu_scale", [P, 2, NC])
        wd_scale = sb("wd_scale", [P, KD])
        hid = sb("hid", [P, NC, NT * P])
        hid_max = sb("hid_max", [P, B * NC])
        loaded = sem("qf_loaded")
        filled = sem("qf_filled")

        with ExitStack() as inner:
            def tmp(name, shape, dt=F32):
                return inner.enter_context(nc.sbuf_tensor("qf_" + name, shape, dt))

            wgu = tmp("wgu", [P, 2, NC, D])
            wd = tmp("wd", [P, KD, IQ])
            xr = tmp("xr", [P, NT, D])
            wgu_q = tmp("wgu_q", [P, 2, NC, D], BF16)
            wd_q = tmp("wd_q", [P, KD, IQ], BF16)
            xq = tmp("xq", [P, NT, D], BF16)
            x_max = tmp("x_max", [P, 1])
            x_maxall = tmp("x_maxall", [P, 1])
            x_scale = tmp("x_scale", [P, 1])
            x_inv = tmp("x_inv", [P, 1])
            gu_inv = tmp("gu_inv", [P, 2, NC])
            wd_inv = tmp("wd_inv", [P, KD])
            stepped, clip_ready = sem("qf_stepped"), sem("qf_clip_ready")
            x_max_ready, x_max_all = sem("qf_x_max_ready"), sem("qf_x_max_all")
            wgu_ready, wd_ready, xq_ready = sem("qf_wgu_ready"), sem("qf_wd_ready"), sem("qf_xq_ready")
            turned, copied = sem("qf_turned"), sem("qf_copied")
            block = inner.enter_context(nc.Block())

            @block.sync
            def _(sp):
                sp.dma_start(clip[:, 0:1], rows(clip_x)).then_inc(loaded, 16)
                sp.dma_start(clip[:, 1:2], rows(clip_down)).then_inc(loaded, 16)
                sp.wait_ge(filled, 1)
                for n, w in enumerate((w_gate, w_up)):
                    full = P * (NC - 1)
                    sp.dma_start(wgu[:, n, 0:NC - 1, :], w[0:full, :].rearrange("(c p) n -> p c n", p=P)).then_inc(loaded, 16)
                    sp.dma_start(wgu[0:LAST, n, NC - 1, :], w[full:IQ, :]).then_inc(loaded, 16)
                sp.dma_start(wd[:], w_down.rearrange("(k p) n -> p k n", p=P)).then_inc(loaded, 16)

            @block.gpsimd
            def _(gp):
                nc.gpsimd.memset(wgu[:, :, NC - 1, :], 1.0).then_inc(filled, 1)
                gp.wait_ge(x_max_ready, 1)
                nc.gpsimd.partition_all_reduce(x_maxall[:], x_max[:], P, bass.bass_isa.ReduceOp.max).then_inc(x_max_all, 1)

            @block.scalar
            def _(ac):
                ac.wait_ge(loaded, 16 * 7)
                nc.scalar.activation(factor[:], clip[:], ACT.Sigmoid).then_inc(clip_ready, 1)
                for n in range(2):
                    ac.wait_ge(turned, n + 1)
                    for k in range(KD):
                        ins = nc.scalar.copy(wgu_t[:, n, k, :], bank[2 * n + k][:].bitcast(BF16)[:, 0:NC * P])
                    ins.then_inc(copied, 1)
                ac.wait_ge(turned, 3)
                nc.scalar.copy(wd_t[:, 0:4, :], bank[4][:].bitcast(BF16).rearrange("p (c n) -> p c n", c=4))
                nc.scalar.copy(wd_t[:, 4, :], bank[5][:].bitcast(BF16)[:, 0:D])
                nc.scalar.copy(wd_t[0:LAST, 5, :], bank[5][0:LAST].bitcast(BF16)[:, D:2 * D]).then_inc(copied, 1)
                for half in range(2):
                    ac.wait_ge(turned, 4 + half)
                    for k in range(KD):
                        ins = nc.scalar.copy(xq_t[:, k, 1024 * half:1024 * half + 1024], bank[6 + k][:].bitcast(BF16))
                    ins.then_inc(copied, 1)

            @block.tensor
            def _(pe):
                pe.wait_ge(wgu_ready, 1)
                for n in range(2):
                    for k in range(KD):
                        dst = bank[2 * n + k][:].bitcast(BF16)
                        for c in range(NC):
                            ins = nc.tensor.transpose(dst[:, P * c:P * c + P], wgu_q[:, n, c, P * k:P * k + P], identb[:])
                    ins.then_inc(turned, 1)
                pe.wait_ge(wd_ready, 1)
                for c in range(NC):
                    m = P if c < NC - 1 else LAST
                    for k in range(KD):
                        dst = bank[4 + c // 4][0:m].bitcast(BF16)
                        col = D * (c % 4) + P * k
                        ins = nc.tensor.transpose(dst[:, col:col + P], wd_q[:, k, P * c:P * c + m], identb[:])
                ins.then_inc(turned, 1)
                pe.wait_ge(xq_ready, 1)
                for half in range(2):
                    if half:
                        pe.wait_ge(copied, 4)
                    for k in range(KD):
                        dst = bank[6 + k][:].bitcast(BF16)
                        for t in range(NT // 2):
                            ins = nc.tensor.transpose(dst[:, P * t:P * t + P], xq[:, NT // 2 * half + t, P * k:P * k + P], identb[:])
                    ins.then_inc(turned, 1)

            @block.vector
            def _(dv):
                st = Steps(dv, stepped)
                nc.vector.memset(hid_max[:], 0.0)
                nc.vector.tensor_reduce(x_max[:], Y[:].rearrange("p t d -> p (t d)"), AX.X, ALU.max, apply_absolute_value=True)\
                    .then_inc(x_max_ready, 1)
                st.after(nc.vector.tensor_copy(identb[:], ident[:]))
                dv.wait_ge(loaded, 16 * 7)

                def round_(dst, mid, src, inv_of, parts):
                    for p in parts:
                        ins = nc.vector.tensor_scalar(mid[p], src[p], inv_of(p), RNE, ALU.mult, ALU.add)
                    st.after(ins)
                    st.after(nc.vector.tensor_scalar(mid[:], mid[:], LO, HI, ALU.max, ALU.min))
                    return nc.vector.tensor_scalar(dst[:], mid[:], RNE, None, ALU.subtract)

                st.after(nc.vector.tensor_reduce(gu_scale[:], wgu[:], AX.X, ALU.max, apply_absolute_value=True))
                st.after(nc.vector.tensor_scalar(gu_scale[:], gu_scale[:], 1.0 / QMAX, None, ALU.mult))
                st.after(nc.vector.reciprocal(gu_inv[:], gu_scale[:]))
                parts = [(slice(None), n, c) for n in range(2) for c in range(NC)]
                round_(wgu_q, wgu, wgu, lambda p: gu_inv[:, p[1], p[2]:p[2] + 1], parts).then_inc(wgu_ready, 1)
                st.after(nc.vector.tensor_reduce(wd_scale[:], wd[:], AX.X, ALU.max, apply_absolute_value=True))
                st.after(nc.vector.tensor_scalar(wd_scale[:], wd_scale[:], 1.0 / QMAX, None, ALU.mult))
                st.after(nc.vector.reciprocal(wd_inv[:], wd_scale[:]))
                parts = [(slice(None), k) for k in range(KD)]
                round_(wd_q, wd, wd, lambda p: wd_inv[:, p[1]:p[1] + 1], parts).then_inc(wd_ready, 1)
                dv.wait_ge(x_max_all, 1)
                dv.wait_ge(clip_ready, 1)
                st.after(nc.vector.tensor_scalar(x_scale[:], x_maxall[:], factor[:, 0:1], None, ALU.mult))
                st.after(nc.vector.tensor_scalar(x_scale[:], x_scale[:], 1.0 / QMAX, None, ALU.mult))
                st.after(nc.vector.reciprocal(x_inv[:], x_scale[:]))
                round_(xq, xr, Y, lambda p: x_inv[:], [(slice(None),)]).then_inc(xq_ready, 1)
                st.after(nc.vector.tensor_scalar(gu_scale[:], gu_scale[:], x_scale[:], None, ALU.mult))

        with ExitStack() as inner:
            act = inner.enter_context(nc.sbuf_tensor("qf_act", [P, 2, S], F32))
            gated, upped, act_ready = sem("qf_gated"), sem("qf_upped"), sem("qf_act_ready")
            hid_ready, maxed = sem("qf_hid_ready"), sem("qf_maxed")
            block = inner.enter_context(nc.Block())

            @block.tensor
            def _(pe):
                with pe.Fori(0, B) as b:
                    for c in range(NC):
                        n = NC * b + c
                        for which, done, freed in ((0, gated, act_ready), (1, upped, hid_ready)):
                            pe.wait_ge(freed, n + 1)
                            for k in range(KD):
                                ins = nc.tensor.matmul(bank[2 * which + c % 2][:], wgu_t[:, which, k, P * c:P * c + P],
                                                       xq_t[:, k, bass.ds(S * b, S)], start=k == 0, stop=k == KD - 1)
                            ins.then_inc(done, 1)

            @block.scalar
            def _(ac):
                ac.sem_inc(act_ready, FREE)
                with ac.Fori(0, B) as b:
                    for c in range(NC):
                        n = NC * b + c
                        ac.wait_ge(gated, n + 1)
                        ac.wait_ge(hid_ready, n + 1)
                        nc.scalar.activation(act[:, c % 2, :], bank[c % 2][:], ACT.Silu, scale=gu_scale[:, 0, c:c + 1]).then_inc(act_ready, 1)

            @block.vector
            def _(dv):
                dv.sem_inc(hid_ready, FREE)
                with dv.Fori(0, B) as b:
                    for c in range(NC):
                        n = NC * b + c
                        m = P if c < NC - 1 else LAST
                        dv.wait_ge(act_ready, FREE + n + 1)
                        dv.wait_ge(upped, n + 1)
                        dst = hid[:, c, bass.ds(S * b, S)]
                        nc.vector.scalar_tensor_tensor(dst, bank[2 + c % 2][:], gu_scale[:, 1, c:c + 1], act[:, c % 2, :],
                                                       ALU.mult, ALU.mult).then_inc(hid_ready, 1)
                        dv.wait_ge(hid_ready, FREE + n + 1)
                        nc.vector.tensor_reduce(hid_max[0:m, bass.ds(n, 1)], hid[0:m, c, bass.ds(S * b, S)], AX.X, ALU.max,
                                                apply_absolute_value=True).then_inc(maxed, 1)

        with ExitStack() as inner:
            def tmp(name, shape, dt=F32):
                return inner.enter_context(nc.sbuf_tensor("qf_" + name, shape, dt))

            hmax = tmp("hmax", [P, 1])
            hmaxall = tmp("hmaxall", [P, 1])
            h_scale = tmp("h_scale", [P, 1])
            h_inv = tmp("h_inv", [P, 1])
            ones = tmp("ones", [P, P])
            diag = tmp("diag", [P, KD, P])
            out_scale = tmp("out_scale", [P, D])
            shift = tmp("shift", [P, 1])
            hq = tmp("hq", [P, 2, NC, S], BF16)
            res = tmp("res", [P, 2, TB, D])
            stepped, hmax_ready, hmax_all = sem("qf_c_stepped"), sem("qf_hmax_ready"), sem("qf_hmax_all")
            diag_ready, spread_done = sem("qf_diag_ready"), sem("qf_spread_done")
            rounded, shift_ready = sem("qf_rounded"), sem("qf_shift_ready")
            hq_ready, down_done, res_ready = sem("qf_hq_ready"), sem("qf_down_done"), sem("qf_res_ready")
            scaled = sem("qf_scaled")
            stored = [sem(f"qf_stored{j}") for j in range(2)]
            block = inner.enter_context(nc.Block())

            @block.gpsimd
            def _(gp):
                gp.wait_ge(hmax_ready, 1)
                nc.gpsimd.partition_all_reduce(hmaxall[:], hmax[:], P, bass.bass_isa.ReduceOp.max).then_inc(hmax_all, 1)

            @block.tensor
            def _(pe):
                pe.wait_ge(diag_ready, 1)
                for k in range(KD):
                    ins = nc.tensor.matmul(bank[6][:, P * k:P * k + P], ones[:], diag[:, k, :], start=True, stop=True)
                ins.then_inc(spread_done, 1)
                for b in range(B):
                    pe.wait_ge(hq_ready, b + 1)
                    if b >= 2:
                        pe.wait_ge(scaled, b - 1)
                    for i in range(TB):
                        for c in range(NC):
                            m = P if c < NC - 1 else LAST
                            ins = nc.tensor.matmul(bank[2 * (b % 2) + i // 2][:, D * (i % 2):D * (i % 2) + D],
                                                   hq[0:m, b % 2, c, P * i:P * i + P], wd_t[0:m, c, :], start=c == 0, stop=c == NC - 1)
                    ins.then_inc(down_done, 1)

            @block.scalar
            def _(ac):
                nc.scalar.activation(shift[:], ident[:, 0:1], ACT.Copy, scale=0.0, bias=-RNE).then_inc(shift_ready, 1)
                ac.wait_ge(shift_ready, 1)
                for b in range(B):
                    ac.wait_ge(rounded, b + 1)
                    if b >= 2:
                        ac.wait_ge(down_done, b - 1)
                    nc.scalar.activation(hq[:, b % 2], hid[:, :, S * b:S * b + S], ACT.Identity, bias=shift[:]).then_inc(hq_ready, 1)

            @block.vector
            def _(dv):
                st = Steps(dv, stepped)
                nc.vector.tensor_reduce(hmax[:], hid_max[:], AX.X, ALU.max).then_inc(hmax_ready, 1)
                st.after(nc.vector.memset(ones[:], 1.0))
                for k in range(KD):
                    ins = nc.vector.tensor_scalar(diag[:, k, :], ident[:], wd_scale[:, k:k + 1], None, ALU.mult)
                ins.then_inc(diag_ready, 1)
                dv.wait_ge(hmax_all, 1)
                st.after(nc.vector.tensor_scalar(h_scale[:], hmaxall[:], factor[:, 1:2], None, ALU.mult))
                st.after(nc.vector.tensor_scalar(h_scale[:], h_scale[:], 1.0 / QMAX, None, ALU.mult))
                st.after(nc.vector.reciprocal(h_inv[:], h_scale[:]))
                dv.wait_ge(spread_done, 1)
                st.after(nc.vector.tensor_scalar(out_scale[:], bank[6][:, 0:D], h_scale[:], None, ALU.mult))

                def finish(b):
                    dv.wait_ge(down_done, b + 1)
                    if b >= 2:
                        dv.wait_ge(stored[b % 2], 16 * (b // 2))
                    r = res[:, b % 2]
                    for i in range(TB):
                        ins = nc.vector.tensor_tensor(r[:, i, :], bank[2 * (b % 2) + i // 2][:, D * (i % 2):D * (i % 2) + D], out_scale[:], ALU.mult)
                    ins.then_inc(scaled, 1)
                    dv.wait_ge(scaled, b + 1)
                    nc.vector.tensor_tensor(r, r, X[:, TB * b:TB * b + TB, :], ALU.add).then_inc(res_ready, 1)

                for b in range(B):
                    h = hid[:, :, S * b:S * b + S]
                    st.after(nc.vector.tensor_scalar(h, h, h_inv[:], RNE, ALU.mult, ALU.add))
                    nc.vector.tensor_scalar(h, h, LO, HI, ALU.max, ALU.min).then_inc(rounded, 1)
                    if b:
                        finish(b - 1)
                finish(B - 1)

            @block.sync
            def _(sp):
                for b in range(B):
                    sp.wait_ge(res_ready, b + 1)
                    sp.dma_start(out[b].rearrange("(i p) d -> p i d", p=P), res[:, b % 2]).then_inc(stored[b % 2], 16)
                for j in range(2):
                    sp.wait_ge(stored[j], 16 * (B // 2))


def program(nc, a, out):
    with ExitStack() as ctx:
        stage_semaphores = []

        def sem(name):
            stage_semaphores.append(nc.alloc_semaphore(name=name))
            return stage_semaphores[-1]

        def stage_end():
            nc.clear_and_free_semaphores(list(stage_semaphores))
            stage_semaphores.clear()
            nc.all_engine_barrier()

        ctx.enter_context(nc.allow_non_contiguous_dma(reason="a vector's values, one to a partition"))
        bank = [ctx.enter_context(nc.psum_tensor(f"bank{i}", [P, 512], F32)) for i in range(8)]
        X = ctx.enter_context(nc.sbuf_tensor("X", [P, NT, D], F32))
        Y = ctx.enter_context(nc.sbuf_tensor("Y", [P, NT, D], F32))
        ident = ctx.enter_context(nc.sbuf_tensor("ident", [P, P], F32))
        consts_in = sem("consts_in")
        copied = nc.alloc_semaphore(name="bias_copied")
        x_loaded = nc.alloc_semaphore(name="x_loaded")
        with nc.Block() as block:
            @block.sync
            def _(sp):
                sp.dma_start(ident[:], a["c_identity"]).then_inc(consts_in, 16)
                sp.dma_start(X[:], a["x"].rearrange("b (i p) d -> p (b i) d", p=P)).then_inc(x_loaded, 16)
                sp.wait_ge(consts_in, 16)
        stage_end()
        tables = nc.dram_tensor("bias_tables", (2, H, NPOS), F32, kind="Internal").ap()
        copies = nc.dram_tensor("bias_copies", (2, H, P, NPOS), F32, kind="Internal").ap()
        lay = [{n: a[f"L{l}_cond2_{n}"] for n in ("w0", "b0", "g0", "w1", "b1", "g1", "w2", "b2")} for l in range(2)]
        for l in range(2):
            lay[l]["w0"] = a[f"L{l}_cond2_w0"].rearrange("a d -> (a d)")
            lay[l]["table"] = tables[l]
            lay[l]["copies"] = copies[l]
        bias_tables(nc, sem, bank, ident, a["c_positions"], lay)
        stage_end()
        moe_conditioning(nc, sem, bank, Y, a["c_x_transposed"], a["c_lane"], a["c_cond_rep"], a["c_wt_t"], a["c_wg_t"],
                         *(a["L0_cond_" + n] for n in ("w_gate", "w_up", "w_down", "sw_gate", "sw_up", "sw_down")), lay, copied)
        stage_end()
        linear_attention(nc, sem, x_loaded, bank, X, Y, ident, a["c_keep_upper"], a["c_attn_wq_t"], a["c_attn_wk_t"], a["c_attn_wv_t"],
                         a["c_attn_wo_t"])
        stage_end()
        def cosine(l):
            w = {n: a[f"L{l}_cond2_{n}"] for n in ("g_norm", "Wq", "Wkv", "q_scale", "k_scale", "null_attn_bias", "Wout", "g_out")}
            w.update(cond=a["cond_64"], mask=a["mask_BxS_bf1"], bias="table", copies=copies[l], copied=copied)
            null_key_attention(nc, sem, f"ca{l}_", bank, X, Y, ident, w)
            stage_end()

        cosine(0)
        moe_ffn(nc, sem, bank, X, Y, ident, a["c_lane"], *(a["L0_ffn_" + n] for n in ("norm_scale", "gate_w", "gate_b")),
                a["c_mlp1_w"], a["c_mlp1_b"], a["L0_ffn_mlp2_w"], a["L0_ffn_mlp2_b"])
        stage_end()
        w = {n: a["L1_cond_" + n] for n in ("Wq", "Wkv", "null_attn_bias", "g_out")}
        w.update(g_norm=a["L1_cond_g_in"], Wout=a["L1_cond_Wo"], cond=a["cond_64"], mask=a["mask_BxS_bk0"],
                 bias="full", full=a["fside_16xSxS_0"])
        null_key_attention(nc, sem, "ba_", bank, X, Y, ident, w)
        stage_end()
        rotary_attention(nc, sem, bank, X, Y, ident, a["c_rot_wqk_t"], a["c_rot_wv_t"], a["c_rot_wo_t"], a["c_rot_cos"], a["c_rot_sin"])
        stage_end()
        cosine(1)
        quantised_ffn(nc, sem, bank, X, Y, ident, out, a["L1_ffn_clip_x"], a["L1_ffn_clip_down"], a["L1_ffn_w_gate"],
                      a["L1_ffn_w_up"], a["L1_ffn_w_down"])
        stage_end()


def _layout(inputs):
    a = {k: np.ascontiguousarray(v) for k, v in inputs.items()}
    for k in ("mask_BxS_bf1", "mask_BxS_bk0"):
        a[k] = a[k].view(np.int32)
    a["c_identity"] = np.eye(P, dtype=np.float32)
    a["c_positions"] = (S - 1 - np.arange(NPOS, dtype=np.float32)).reshape(NPOS // P, P).T.copy()
    a["c_lane"] = np.tile(np.arange(E0, dtype=np.float32), (P, 1))
    a["c_x_transposed"] = np.ascontiguousarray(a["x"].transpose(0, 2, 1))
    a["c_cond_rep"] = np.ascontiguousarray(np.broadcast_to(a["cond_64"].T[:, :, None], (G0, B, P)))
    a["c_wt_t"] = np.ascontiguousarray(a.pop("L0_cond_wt").T)
    a["c_wg_t"] = np.ascontiguousarray(a.pop("L0_cond_wg").T)
    a["c_keep_upper"] = np.triu(np.ones((P, P), np.float32))
    for n in ("q", "k", "v", "o"):
        a[f"c_attn_w{n}_t"] = np.ascontiguousarray(a.pop(f"L0_attn_W{n}").T)
    a["c_mlp1_w"] = np.ascontiguousarray(a.pop("L0_ffn_mlp1_w").reshape(E1, D, I1, 2).transpose(0, 1, 3, 2))
    a["c_mlp1_b"] = np.ascontiguousarray(a.pop("L0_ffn_mlp1_b").reshape(E1, I1 // P, P, 2).transpose(2, 0, 3, 1))
    rot = {n: a.pop(f"L1_attn_W{n}").T for n in "qkvo"}
    a["c_rot_wqk_t"] = np.ascontiguousarray(np.concatenate([rot["q"], rot["k"]], axis=1))
    a["c_rot_wv_t"] = np.ascontiguousarray(rot["v"])
    a["c_rot_wo_t"] = np.ascontiguousarray(rot["o"])
    freq = (1.0 / np.float32(10000.0) ** (np.arange(0, DR, 2, dtype=np.float32) / DR)).astype(np.float32)
    angle = np.arange(S, dtype=np.float32)[:, None] * freq
    cos, sin = np.cos(angle).astype(np.float32), np.sin(angle).astype(np.float32)
    a["c_rot_cos"] = np.ascontiguousarray(np.concatenate([cos, cos], axis=1).reshape(TB, P, DR).transpose(1, 0, 2))
    a["c_rot_sin"] = np.ascontiguousarray(np.concatenate([-sin, sin], axis=1).reshape(TB, P, DR).transpose(1, 0, 2))
    return a


def kernel(**inputs):
    import concourse.bacc as bacc
    from concourse.bass_utils import run_bass_kernel_spmd

    nc = bacc.Bacc("TRN2", target_bir_lowering=False, num_devices=1)
    arrays = _layout(inputs)
    aps = {n: nc.dram_tensor(n, v.shape, mybir.dt.from_np(v.dtype), kind="ExternalInput").ap() for n, v in arrays.items()}
    out = nc.dram_tensor("out", (B, S, D), F32, kind="ExternalOutput").ap()
    program(nc, aps, out)
    r = run_bass_kernel_spmd(nc, [arrays], core_ids=[0])
    return r.results[0]["out"]
```
